# Optimizing a Trainium2 kernel written in Bass

```python
import numpy as np
import jax
import jax.numpy as jnp

def _softmax(x, axis=-1):
    return jax.nn.softmax(x, axis=axis)

def _gelu(x):
    return jax.nn.gelu(x, approximate=True)

def _silu(x):
    return jax.nn.silu(x)

def _sigmoid(x):
    return jax.nn.sigmoid(x)

def _layernorm(x, axis=-1, eps=1e-05):
    m = jnp.mean(x, axis=axis, keepdims=True)
    v = jnp.var(x, axis=axis, keepdims=True)
    return (x - m) / jnp.sqrt(v + eps)

def _scatter_add(tgt, idx, src, axis=0):
    return tgt.at[idx].add(src)

def _segment_sum(src, seg, n):
    return jax.ops.segment_sum(src, seg, n)
kernel_name = 'mk_gps_d2_gnn_r8_e82bf4'

def setup_inputs(seed: int=0):
    np.random.seed(seed)
    _w = jnp.asarray

    def _rec_inputs():
        import jax
        import jax.numpy as jnp
        _gk = jax.random.key(seed)
        x = -0.0003713 + 1 * jax.random.normal(jax.random.fold_in(_gk, 1), (6250, 256), jnp.float32)
        _s = jax.random.randint(jax.random.fold_in(_gk, 2), (50000,), 0, 6250, jnp.int32)
        _d = jax.random.randint(jax.random.fold_in(_gk, 3), (50000,), 0, 6250, jnp.int32)
        _loop = jnp.arange(6250, dtype=jnp.int32)
        src = jnp.concatenate([_s, _d, _loop])
        dst = jnp.concatenate([_d, _s, _loop])
        _o = jnp.argsort(dst, stable=True)
        src = src[_o]
        dst = dst[_o]
        return (x, src, dst)
    x, src, dst = _rec_inputs()

    def _L0_gnn_setup():
        import jax, jax.numpy as jnp
        import numpy as np
        N, E, D_IN, D_OUT = (6250, 200000, 256, 256)
        key = jax.random.key(seed)
        k1, k2, k3, k4, k5, k6 = jax.random.split(key, 6)
        x = jax.random.normal(k1, (N, D_IN), dtype=jnp.float32)
        edge_index = jax.random.randint(k2, (2, E), 0, N, dtype=jnp.int64)
        s = 1.0 / np.sqrt(D_IN)
        W1 = jax.random.uniform(k3, (D_OUT, D_IN), minval=-s, maxval=s, dtype=jnp.float32)
        b1 = jax.random.uniform(k4, (D_OUT,), minval=-s, maxval=s, dtype=jnp.float32)
        W2 = jax.random.uniform(k5, (D_OUT, D_IN), minval=-s, maxval=s, dtype=jnp.float32)
        b2 = jax.random.uniform(k6, (D_OUT,), minval=-s, maxval=s, dtype=jnp.float32)
        return {'x': x, 'W1': W1, 'b1': b1, 'W2': W2, 'b2': b2, 'edge_index': edge_index}
    _L0_gnn_all = _L0_gnn_setup()
    _L0_gnn_in = {k: v for k, v in _L0_gnn_all.items() if k in ('W1', 'b1', 'W2', 'b2')}
    del _L0_gnn_all

    def _L0_mix_setup():
        import jax, jax.numpy as jnp
        import numpy as np
        A, Bc, Cc = (0.5, 1.0, 1.0)
        H = 8
        EPS = 1e-12

        def _normalize(t):
            n = jnp.linalg.norm(t, axis=-1, keepdims=True)
            return t / jnp.maximum(n, EPS)
        key = jax.random.key(seed)
        ks = jax.random.split(key, 5)
        B, N, C = (8, 256, 256)
        D = C // H
        x = jax.random.normal(ks[0], (B, N, C), dtype=jnp.float32)
        Wqkv = jax.random.normal(ks[1], (3 * H * D, C), dtype=jnp.float32) * 0.02
        bqkv = jnp.zeros((3 * H * D,), dtype=jnp.float32)
        Wproj = jax.random.normal(ks[2], (C, H * D), dtype=jnp.float32) * 0.02
        bproj = jnp.zeros((C,), dtype=jnp.float32)
        temperature = jnp.ones((1, H, 1, 1), dtype=jnp.float32)
        return {'x': x, 'Wqkv': Wqkv, 'bqkv': bqkv, 'Wproj': Wproj, 'bproj': bproj, 'temperature': temperature}
    _L0_mix_all = _L0_mix_setup()
    _L0_mix_in = {k: v for k, v in _L0_mix_all.items() if k in ('Wqkv', 'bqkv', 'Wproj', 'bproj', 'temperature')}
    del _L0_mix_all

    def _L0_ffn_setup():
        import jax, jax.numpy as jnp
        import numpy as np
        B, K, D = (512, 16, 256)
        E = 32
        H = int(D * 0.25)
        key = jax.random.key(seed)
        ks = jax.random.split(key, 7)
        d_rs = D ** (-0.5)
        h_rs = H ** (-0.5)
        x = jax.random.normal(ks[0], (B, K, D), dtype=jnp.float32)
        router_w = jax.random.uniform(ks[1], (E, D), jnp.float32, -d_rs, d_rs)
        router_b = jax.random.uniform(ks[2], (E,), jnp.float32, -d_rs, d_rs)
        W1 = jax.random.uniform(ks[3], (E, D, H), jnp.float32, -h_rs, h_rs)
        b1 = jax.random.uniform(ks[4], (E, H), jnp.float32, -h_rs, h_rs)
        W2 = jax.random.uniform(ks[5], (E, H, D), jnp.float32, -d_rs, d_rs)
        b2 = jax.random.uniform(ks[6], (E, D), jnp.float32, -d_rs, d_rs)
        return {'x': x, 'router_w': router_w, 'router_b': router_b, 'W1': W1, 'b1': b1, 'W2': W2, 'b2': b2}
    _L0_ffn_all = _L0_ffn_setup()
    _L0_ffn_in = {k: v for k, v in _L0_ffn_all.items() if k in ('router_w', 'router_b', 'W1', 'b1', 'W2', 'b2')}
    del _L0_ffn_all

    def _L1_gnn_setup():
        import jax, jax.numpy as jnp
        import numpy as np
        N = 6250
        E = 100000
        IN_C = 256
        HEADS = 8
        OUT_C = 32
        key = jax.random.key(seed)
        k1, k2, k3, k4, k5 = jax.random.split(key, 5)
        x = jax.random.normal(k1, (N, IN_C), dtype=jnp.float32)
        edge_index = jax.random.randint(k2, (2, E), 0, N, dtype=jnp.int64)
        lim_W = float(np.sqrt(6.0 / (IN_C + HEADS * OUT_C)))
        lim_a = float(np.sqrt(6.0 / (HEADS + OUT_C)))
        W = jax.random.uniform(k3, (IN_C, HEADS * OUT_C), minval=-lim_W, maxval=lim_W, dtype=jnp.float32)
        a_src = jax.random.uniform(k4, (HEADS, OUT_C), minval=-lim_a, maxval=lim_a, dtype=jnp.float32)
        a_dst = jax.random.uniform(k5, (HEADS, OUT_C), minval=-lim_a, maxval=lim_a, dtype=jnp.float32)
        return {'x': x, 'edge_index': edge_index, 'W': W, 'a_src': a_src, 'a_dst': a_dst}
    _L1_gnn_all = _L1_gnn_setup()
    _L1_gnn_in = {k: v for k, v in _L1_gnn_all.items() if k in ('W', 'a_src', 'a_dst')}
    del _L1_gnn_all

    def _L1_mix_setup():
        import math
        import jax, jax.numpy as jnp
        import numpy as np
        EPS_DIV = 1e-07
        EPS_NORM = 1e-12

        def _l2_normalize(x, axis):
            n = jnp.sqrt(jnp.sum(x * x, axis=axis, keepdims=True))
            return x / jnp.maximum(n, EPS_NORM)
        key = jax.random.key(seed)
        ks = jax.random.split(key, 5)
        b, N, C = (8, 512, 256)
        x = jax.random.normal(ks[0], (b, N, C), dtype=jnp.float32)
        W_qkv = jax.random.normal(ks[1], (C, 3 * C), dtype=jnp.float32) * (1.0 / math.sqrt(C))
        b_qkv = jax.random.normal(ks[2], (3 * C,), dtype=jnp.float32) * 0.02
        W_out = jax.random.normal(ks[3], (C, C), dtype=jnp.float32) * (1.0 / math.sqrt(C))
        b_out = jax.random.normal(ks[4], (C,), dtype=jnp.float32) * 0.02
        return {'x': x, 'W_qkv': W_qkv, 'b_qkv': b_qkv, 'W_out': W_out, 'b_out': b_out}
    _L1_mix_all = _L1_mix_setup()
    _L1_mix_in = {k: v for k, v in _L1_mix_all.items() if k in ('W_qkv', 'b_qkv', 'W_out', 'b_out')}
    del _L1_mix_all

    def _L1_ffn_setup():
        import jax, jax.numpy as jnp
        import numpy as np
        B, T, D, H, E = (16, 512, 256, 512, 8)
        key = jax.random.key(seed)
        ks = jax.random.split(key, 5)
        x = jax.random.normal(ks[0], (B, T, D), dtype=jnp.float32)
        gate_w = jax.random.normal(ks[1], (D, E), dtype=jnp.float32) * 0.02
        gate_b = jnp.zeros((E,), dtype=jnp.float32)
        W1 = jax.random.normal(ks[2], (E, D, H), dtype=jnp.float32) * 0.02
        b1 = jnp.zeros((E, H), dtype=jnp.float32)
        W2 = jax.random.normal(ks[3], (E, H, D), dtype=jnp.float32) * 0.02
        b2 = jnp.zeros((E, D), dtype=jnp.float32)
        return {'x': x, 'gate_w': gate_w, 'gate_b': gate_b, 'W1': W1, 'b1': b1, 'W2': W2, 'b2': b2}
    _L1_ffn_all = _L1_ffn_setup()
    _L1_ffn_in = {k: v for k, v in _L1_ffn_all.items() if k in ('gate_w', 'gate_b', 'W1', 'b1', 'W2', 'b2')}
    del _L1_ffn_all
    return {'x': x, 'src': src, 'dst': dst, 'L0_gnn_W1': _L0_gnn_in['W1'], 'L0_gnn_b1': _L0_gnn_in['b1'], 'L0_gnn_W2': _L0_gnn_in['W2'], 'L0_gnn_b2': _L0_gnn_in['b2'], 'L0_mix_Wqkv': _L0_mix_in['Wqkv'], 'L0_mix_bqkv': _L0_mix_in['bqkv'], 'L0_mix_Wproj': _L0_mix_in['Wproj'], 'L0_mix_bproj': _L0_mix_in['bproj'], 'L0_mix_temperature': _L0_mix_in['temperature'], 'L0_ffn_router_w': _L0_ffn_in['router_w'], 'L0_ffn_router_b': _L0_ffn_in['router_b'], 'L0_ffn_W1': _L0_ffn_in['W1'], 'L0_ffn_b1': _L0_ffn_in['b1'], 'L0_ffn_W2': _L0_ffn_in['W2'], 'L0_ffn_b2': _L0_ffn_in['b2'], 'L1_gnn_W': _L1_gnn_in['W'], 'L1_gnn_a_src': _L1_gnn_in['a_src'], 'L1_gnn_a_dst': _L1_gnn_in['a_dst'], 'L1_mix_W_qkv': _L1_mix_in['W_qkv'], 'L1_mix_b_qkv': _L1_mix_in['b_qkv'], 'L1_mix_W_out': _L1_mix_in['W_out'], 'L1_mix_b_out': _L1_mix_in['b_out'], 'L1_ffn_gate_w': _L1_ffn_in['gate_w'], 'L1_ffn_gate_b': _L1_ffn_in['gate_b'], 'L1_ffn_W1': _L1_ffn_in['W1'], 'L1_ffn_b1': _L1_ffn_in['b1'], 'L1_ffn_W2': _L1_ffn_in['W2'], 'L1_ffn_b2': _L1_ffn_in['b2']}

def reference(x, src, dst, L0_gnn_W1, L0_gnn_b1, L0_gnn_W2, L0_gnn_b2, L0_mix_Wqkv, L0_mix_bqkv, L0_mix_Wproj, L0_mix_bproj, L0_mix_temperature, L0_ffn_router_w, L0_ffn_router_b, L0_ffn_W1, L0_ffn_b1, L0_ffn_W2, L0_ffn_b2, L1_gnn_W, L1_gnn_a_src, L1_gnn_a_dst, L1_mix_W_qkv, L1_mix_b_qkv, L1_mix_W_out, L1_mix_b_out, L1_ffn_gate_w, L1_ffn_gate_b, L1_ffn_W1, L1_ffn_b1, L1_ffn_W2, L1_ffn_b2):
    import jax
    import jax.numpy as jnp

    def _L0_gnn_ref(x, W1, b1, W2, b2, edge_index):
        import jax, jax.numpy as jnp
        import numpy as np
        N, E, D_IN, D_OUT = (6250, 200000, 256, 256)
        dst = edge_index[0]
        nbr = edge_index[1]
        n = x.shape[0]
        agg = jax.ops.segment_sum(x[nbr], dst, num_segments=n)
        cnt = jax.ops.segment_sum(jnp.ones((nbr.shape[0],), x.dtype), dst, num_segments=n)
        mean = agg / jnp.maximum(cnt, 1.0)[:, None]
        return x @ W1.T + b1 + mean @ W2.T + b2

    def _L0_mix_ref(x, Wqkv, bqkv, Wproj, bproj, temperature):
        import jax, jax.numpy as jnp
        import numpy as np
        A, Bc, Cc = (0.5, 1.0, 1.0)
        H = 8
        EPS = 1e-12

        def _normalize(t):
            n = jnp.linalg.norm(t, axis=-1, keepdims=True)
            return t / jnp.maximum(n, EPS)
        B, N, C = x.shape
        D = C // H
        scale = float(D) ** 0.25
        qkv = (x @ Wqkv.T + bqkv).reshape(B, N, 3, H, D)
        qkv = jnp.transpose(qkv, (2, 0, 3, 1, 4))
        q, k, v = (qkv[0], qkv[1], qkv[2])
        q = q * scale
        v1 = jnp.concatenate([jnp.ones((B, H, N, 1), dtype=v.dtype), v], axis=-1)
        qn = _normalize(q) * (scale * temperature)
        kn = _normalize(k) * scale
        vN = v1 / N
        kv_mod = jnp.einsum('bhni,bhnj,bhne->bhije', kn, kn, vN)
        kv = jnp.einsum('bhnd,bhne->bhde', kn, vN)
        vsum = jnp.sum(vN, axis=-2)[:, :, None, :]
        y = A * jnp.einsum('bhni,bhnj,bhije->bhne', qn, qn, kv_mod) + scale ** 2 * Bc * jnp.einsum('bhnd,bhde->bhne', qn, kv) + scale ** 4 * Cc * vsum
        y_norm, y = (y[..., :1], y[..., 1:])
        y = y / y_norm
        out = jnp.transpose(y, (0, 2, 1, 3)).reshape(B, N, H * D)
        return out @ Wproj.T + bproj

    def _L0_ffn_ref(x, router_w, router_b, W1, b1, W2, b2):
        import jax, jax.numpy as jnp
        import numpy as np
        B, K, D = (512, 16, 256)
        E = 32
        H = int(D * 0.25)
        xf = x.reshape(-1, D)
        logits = xf @ router_w.T + router_b
        idx = jnp.argmax(logits, axis=-1)
        w1t = jnp.take(W1, idx, axis=0)
        h = jnp.einsum('nd,ndh->nh', xf, w1t) + jnp.take(b1, idx, axis=0)
        h = jax.nn.relu(h)
        w2t = jnp.take(W2, idx, axis=0)
        out = jnp.einsum('nh,nhd->nd', h, w2t) + jnp.take(b2, idx, axis=0)
        out = jax.nn.relu(out)
        return out.reshape(x.shape)

    def _L1_gnn_ref(x, edge_index, W, a_src, a_dst):
        import jax, jax.numpy as jnp
        import numpy as np
        N = 6250
        E = 100000
        IN_C = 256
        HEADS = 8
        OUT_C = 32
        n = x.shape[0]
        H, D = a_src.shape
        x_proj = (x @ W).reshape(n, H, D)
        alpha_src = jnp.einsum('nhd,hd->nh', x_proj, a_src)
        alpha_dst = jnp.einsum('nhd,hd->nh', x_proj, a_dst)
        row, col = (edge_index[0], edge_index[1])
        e = alpha_src[row] + alpha_dst[col]
        m = jax.ops.segment_max(e, col, num_segments=n)
        m = jnp.where(jnp.isfinite(m), m, 0.0)
        e_exp = jnp.exp(e - m[col])
        s = jax.ops.segment_sum(e_exp, col, num_segments=n)
        att = e_exp / (s[col] + 1e-16)
        out = jax.ops.segment_sum(att[:, :, None] * x_proj[row], col, num_segments=n)
        return out.reshape(n, H * D)

    def _L1_mix_ref(x, W_qkv, b_qkv, W_out, b_out):
        import math
        import jax, jax.numpy as jnp
        import numpy as np
        EPS_DIV = 1e-07
        EPS_NORM = 1e-12

        def _l2_normalize(x, axis):
            n = jnp.sqrt(jnp.sum(x * x, axis=axis, keepdims=True))
            return x / jnp.maximum(n, EPS_NORM)
        b, N, C = x.shape
        qkv = x @ W_qkv + b_qkv
        q, k, v = jnp.split(qkv, 3, axis=2)
        q = q - jnp.mean(q, axis=2, keepdims=True)
        k = k - jnp.mean(k, axis=2, keepdims=True)
        q2 = q * q
        k2 = k * k
        q2s = jnp.sum(q2, axis=2, keepdims=True)
        k2s = jnp.sum(k2, axis=2, keepdims=True)
        k2 = _l2_normalize(k2 / (k2s + EPS_DIV), axis=-2)
        q2 = _l2_normalize(q2 / (q2s + EPS_DIV), axis=-1)
        kv = jnp.einsum('bnc,bnd->bcd', k2, v)
        t2 = jnp.einsum('bnc,bcd->bnd', q2, kv) / math.sqrt(N)
        attn = v + t2
        return attn @ W_out + b_out

    def _L1_ffn_ref(x, gate_w, gate_b, W1, b1, W2, b2):
        import jax, jax.numpy as jnp
        import numpy as np
        B, T, D, H, E = (16, 512, 256, 512, 8)
        Bb, Tt, Dd = x.shape
        Ee = gate_w.shape[1]
        xf = x.reshape(-1, Dd)
        N = xf.shape[0]
        logits = xf @ gate_w + gate_b
        probs = jax.nn.softmax(logits, axis=-1)
        top2_vals, top2_idx = jax.lax.top_k(probs, 2)
        cw = jnp.zeros((N, Ee), dtype=xf.dtype).at[jnp.arange(N)[:, None], top2_idx].add(top2_vals)

        def step(acc, params):
            w1, bb1, w2, bb2, we = params
            h = jax.nn.gelu(xf @ w1 + bb1, approximate=False)
            y = h @ w2 + bb2
            return (acc + we[:, None] * y, None)
        out, _ = jax.lax.scan(step, jnp.zeros_like(xf), (W1, b1, W2, b2, cw.T))
        return out.reshape(Bb, Tt, Dd)
    edge_index = jnp.stack([src, dst])
    xn = _layernorm(x, axis=-1)
    x = x + _L0_gnn_ref(xn, L0_gnn_W1, L0_gnn_b1, L0_gnn_W2, L0_gnn_b2, edge_index) + _L0_mix_ref(xn[None], L0_mix_Wqkv, L0_mix_bqkv, L0_mix_Wproj, L0_mix_bproj, L0_mix_temperature)[0]
    x = x + _L0_ffn_ref(_layernorm(x, axis=-1)[None], L0_ffn_router_w, L0_ffn_router_b, L0_ffn_W1, L0_ffn_b1, L0_ffn_W2, L0_ffn_b2)[0]
    xn = _layernorm(x, axis=-1)
    x = x + _L1_gnn_ref(xn, edge_index, L1_gnn_W, L1_gnn_a_src, L1_gnn_a_dst) + _L1_mix_ref(xn[None], L1_mix_W_qkv, L1_mix_b_qkv, L1_mix_W_out, L1_mix_b_out)[0]
    x = x + _L1_ffn_ref(_layernorm(x, axis=-1)[None], L1_ffn_gate_w, L1_ffn_gate_b, L1_ffn_W1, L1_ffn_b1, L1_ffn_W2, L1_ffn_b2)[0]
    return x

_drawn_inputs = setup_inputs


def setup_inputs(seed=0):
    import zlib

    import numpy as np

    out = dict(_drawn_inputs(seed))
    spreads = {'L0_mix_bqkv': (0.0, 0.1),
     'L0_mix_bproj': (0.0, 0.1),
     'L0_mix_temperature': (1.0, 0.6),
     'L1_ffn_gate_b': (0.0, 0.8),
     'L1_ffn_b1': (0.0, 0.8),
     'L1_ffn_b2': (0.0, 0.563)}
    factors = {'L0_mix_Wqkv': 8.0,
     'L0_ffn_b1': 6.824,
     'L1_gnn_a_dst': 8.0,
     'L1_mix_b_out': 5.316,
     'L1_ffn_gate_w': 3.409,
     'L1_ffn_W1': 4.926,
     'L1_ffn_W2': 4.609}
    for name, (base, spread) in spreads.items():
        noise = np.random.default_rng([zlib.crc32(name.encode()), seed]).standard_normal(out[name].shape)
        drawn = base * np.exp(spread * noise) if base else spread * noise
        out[name] = jnp.asarray(drawn.astype(out[name].dtype))
    for name, factor in factors.items():
        out[name] = (out[name] * factor).astype(out[name].dtype)
    return out
```

```python
from collections import namedtuple
from contextlib import ExitStack, contextmanager

import concourse.bass as bass
from concourse import mybir

F32 = mybir.dt.float32
BF16 = mybir.dt.bfloat16
I32 = mybir.dt.int32
U32 = mybir.dt.uint32
ALU = mybir.AluOpType
ACT = mybir.ActivationFunctionType
AX = mybir.AxisListType

P = 128
N = 6250
D = 256
T = 50
NP = T * P
FULL = N // P
REST = N - FULL * P
H, HD = 8, 32
E = 106250
ET = -(-E // (16 * P)) * 16
EP = ET * P
WIN = -(-N // P)
STEPS = ET + WIN - 1
SROWS = -(-STEPS // P) * P
PAD_NODE = WIN * P - 1
GW = 260
AW = GW + 4
LN_EPS = 1e-5
NEG = -1.0e30


def cut(buf, at, *dims):
    whole = buf[tuple([slice(None)] * len(buf.shape))]
    return bass.AP(whole.tensor, whole.offset + at, [list(whole.ap[0]), *[list(d) for d in dims]])


def sub(ap, at, *dims):
    return bass.AP(ap.tensor, ap.offset + at, [list(ap.ap[0]), *[list(d) for d in dims]])


def flat(buf, at, *dims):
    whole = buf[tuple([slice(None)] * len(buf.shape))]
    return bass.AP(whole.tensor, whole.offset + at, [list(d) for d in dims])


def own(nc, name):
    return f"{name}_{nc.next_id()}"


def done(n):
    return n + 3


def landed(i, k=1):
    return 16 * k * (i + 2)


def pool_sems(nc, names):
    return [nc.alloc_semaphore(own(nc, n)) for n in names]


@contextmanager
def phase(nc, names, dma_names=()):
    with ExitStack() as held:
        sems = [held.enter_context(nc.semaphore(own(nc, n))) for n in (*names, *dma_names)]
        yield held, sems
        with nc.Block() as block:
            @block.gpsimd
            def _(pool):
                for s in sems:
                    pool.sem_clear(s)


def setup_phase(nc, g, x, src, dst):
    names = ["s_x0", "s_iota", "s_pad", "s_f", "s_const"]
    with phase(nc, names, ["s_in", "s_edge"]) as (held, sems):
        s_x0, s_iota, s_pad, s_f, s_const, s_in, s_edge = sems
        iota_i = held.enter_context(nc.sbuf_tensor(own(nc, "iota_i"), [P, P], I32))
        col_i = held.enter_context(nc.sbuf_tensor(own(nc, "col_i"), [P, 1], I32))
        node_i = held.enter_context(nc.sbuf_tensor(own(nc, "node_i"), [P, T], I32))
        node_f = held.enter_context(nc.sbuf_tensor(own(nc, "node_f"), [P, T], F32))
        pad_i = held.enter_context(nc.sbuf_tensor(own(nc, "pad_i"), [1, EP - E], I32))
        with nc.Block() as block:
            @block.sync
            def _(sp):
                for t in range(0, FULL, 12):
                    sp.dma_start(g.X[:, t:t + 12, :],
                                 x[t * P:(t + 12) * P, :].rearrange("(t p) d -> p t d", p=P)).then_inc(s_in, 16)
                sp.wait_ge(s_x0, 1)
                sp.dma_start(g.X[0:REST, FULL, :], x[FULL * P:N, :]).then_inc(s_in, 16)
                for to, of in ((g.esrc, src), (g.edst, dst)):
                    sp.dma_start(flat(to, 0, [E // 10, 10], [1, E // 10]),
                                 of.rearrange("(a b) -> a b", a=10)).then_inc(s_edge, 16)
                sp.wait_ge(s_pad, 1)
                for to in (g.esrc, g.edst):
                    sp.dma_start(flat(to, E, [EP - E, 1], [1, EP - E]), pad_i[:, :]).then_inc(s_edge, 16)
                sp.wait_ge(s_in, 16 * (FULL // 12 + 1))
                sp.wait_ge(s_edge, 64)

            @block.gpsimd
            def _(pool):
                pool.iota(iota_i[:, :], pattern=[[1, P]], base=0, channel_multiplier=0).then_inc(s_iota, 1)
                pool.iota(col_i[:, :], pattern=[[1, 1]], base=0, channel_multiplier=1).then_inc(s_iota, 1)
                pool.iota(node_i[:, :], pattern=[[P, T]], base=0, channel_multiplier=1).then_inc(s_iota, 1)
                pool.memset(pad_i[:, :], PAD_NODE).then_inc(s_pad, 1)

            @block.vector
            def _(dve):
                dve.memset(g.X[:, FULL:T, :], 0.0).then_inc(s_x0, 1)
                dve.memset(cut(g.XN, D, [GW, T], [1, 1]), 1.0)
                dve.memset(cut(g.XN, D + 1, [GW, T], [1, GW - D - 1]), 0.0)
                dve.memset(g.eps[:, :], LN_EPS)
                dve.memset(g.zero[:, :], 0.0)
                dve.memset(g.zrow[:, :], 0.0)
                dve.memset(g.ones[:, :], 1.0)
                dve.wait_ge(s_iota, 3)
                dve.tensor_copy(g.iota[:, :], iota_i[:, :]).then_inc(s_f, 1)
                dve.tensor_copy(g.pcol[:, :], col_i[:, :]).then_inc(s_f, 1)
                dve.tensor_copy(node_f[:, :], node_i[:, :]).then_inc(s_f, 1)
                dve.wait_ge(s_f, 3)
                dve.tensor_scalar(out=g.ident[:, :], in0=g.iota[:, :], scalar1=g.pcol[:, 0:1], scalar2=None,
                                  op0=ALU.is_equal)
                dve.tensor_scalar(out=g.lower[:, :], in0=g.iota[:, :], scalar1=g.pcol[:, 0:1], scalar2=None,
                                  op0=ALU.is_lt)
                dve.tensor_scalar(out=g.valid[:, :], in0=node_f[:, :], scalar1=float(N), scalar2=None,
                                  op0=ALU.is_lt).then_inc(s_const, 1)
                dve.wait_ge(s_const, 1)


def qkv0_phase(nc, g, w):
    names = ["s_st", "s_mv", "s_sd", "s_rs", "s_xs", "s_keep", "s_xtp", "s_xt", "s_qkvp", "s_qkv", "s_sq", "s_ss",
             "s_sc", "s_nm", "s_fac", "s_fac2", "s_fac3", "s_qk", "s_qtp", "s_qt", "s_bias", "s_cf", "s_root", "s_turn"]
    with phase(nc, names, ["s_w", "s_kv0", "s_kv1", "s_qo0", "s_qo1"]) as (held, sems):
        (s_st, s_mv, s_sd, s_rs, s_xs, s_keep, s_xtp, s_xt, s_qkvp, s_qkv, s_sq, s_ss, s_sc, s_nm, s_fac, s_fac2,
         s_fac3, s_qk, s_qtp, s_qt, s_bias, s_cf, s_root, s_turn, s_w, s_kv0, s_kv1, s_qo0, s_qo1) = sems
        s_kv, s_qo = (s_kv0, s_kv1), (s_qo0, s_qo1)

        def sb(name, shape, dt=F32):
            return held.enter_context(nc.sbuf_tensor(own(nc, name), shape, dt))

        W = sb("w_qkv", [P, 2, 4 * D])
        B = sb("b_qkv", [P, 3 * D])
        RB = sb("res_bias", [P, 3, D])
        C = sb("ss_scale", [P, 2 * H])
        F = sb("norm_scale", [P, 2 * H])
        ST = sb("st", [P, 2, 6])
        MV = sb("mv", [P, 2, 2])
        SD = sb("sd", [P, 2, 1])
        RS = sb("rs", [P, 2, 1])
        XS = sb("xs", [P, 2, D])
        XT = sb("xt", [P, 2, D])
        QKV = sb("qkv", [P, 2, 3 * D])
        SQ = sb("sq", [P, 2, 2 * D])
        SS = sb("ss", [P, 2, 2 * H])
        SC = sb("sc", [P, 2, 2 * H])
        NM = sb("nm", [P, 2, 2 * H])
        FA = sb("fa", [P, 2, 2 * H])
        FB = sb("fb", [P, 2, 2 * H])
        QK = sb("qk", [P, 2, 2 * D])
        QT = sb("qt", [P, 2, D])
        pt = held.enter_context(nc.psum_tensor(own(nc, "pt"), [P, 2, 512], F32))
        pq = held.enter_context(nc.psum_tensor(own(nc, "pq"), [P, 2, 1024], F32))
        pr = held.enter_context(nc.psum_tensor(own(nc, "pr"), [P, 2, 512], F32))
        QSCALE = float(HD) ** 0.25
        NW = 16 * 7
        with nc.Block() as block:
            @block.sync
            def _(sp):
                for s in (*s_kv, *s_qo):
                    sp.sem_inc(s, 32)
                sp.dma_start(W[:, :, 0:3 * D], w.L0_mix_Wqkv.rearrange("(c p) o -> p c o", p=P)).then_inc(s_w, 16)
                sp.dma_start(W[:, :, 3 * D:4 * D], w.L0_gnn_W1.rearrange("(c p) o -> p c o", p=P)).then_inc(s_w, 16)
                sp.dma_start(B[:, :], w.L0_mix_bqkv.partition_broadcast(P)).then_inc(s_w, 16)
                for k, b in enumerate((w.L0_gnn_b1, w.L0_gnn_b2, w.L0_mix_bproj)):
                    sp.dma_start(RB[:, k, :], b.partition_broadcast(P)).then_inc(s_w, 16)
                sp.dma_start(C[:, 0:H], w.L0_mix_temperature.partition_broadcast(P)).then_inc(s_w, 16)
                with sp.Fori(0, T // 2) as i:
                    for u in (0, 1):
                        n = i * 2 + u
                        sp.wait_ge(s_qk, done(n))
                        sp.dma_start(flat(g.kv, n * (P * 2 * D), [2 * D, P], [1, D]),
                                     QK[:, u, D:2 * D]).then_inc(s_kv[u], 16)
                        sp.dma_start(flat(g.kv, n * (P * 2 * D) + D, [2 * D, P], [1, D]),
                                     QKV[:, u, 2 * D:3 * D]).then_inc(s_kv[u], 16)
                        sp.wait_ge(s_qt, done(n))
                        for c in (0, 1):
                            sp.dma_start(flat(g.qT, c * P * NP + n * P, [NP, P], [1, P]),
                                         QT[:, u, c * P:(c + 1) * P]).then_inc(s_qo[u], 16)
                for s in (*s_kv, *s_qo):
                    sp.wait_ge(s, landed(T // 2 - 1, 2))

            @block.vector
            def _(dve):
                for s in (s_root, s_st, s_mv, s_rs, s_xs, s_qkv, s_ss, s_sc, s_fac, s_fac2, s_fac3, s_qk):
                    dve.sem_inc(s, 2)
                dve.wait_ge(s_w, NW)
                dve.tensor_scalar(out=F[:, 0:H], in0=C[:, 0:H], scalar1=QSCALE * QSCALE, scalar2=None,
                                  op0=ALU.mult).then_inc(s_cf, 1)
                dve.memset(F[:, H:2 * H], QSCALE)
                dve.wait_ge(s_cf, 1)
                dve.memset(C[:, 0:H], QSCALE * QSCALE)
                dve.memset(C[:, H:2 * H], 1.0)
                dve.tensor_tensor(out=RB[:, 0, :], in0=RB[:, 0, :], in1=RB[:, 1, :], op=ALU.add).then_inc(s_cf, 1)
                dve.wait_ge(s_cf, 2)
                dve.tensor_tensor(out=RB[:, 0, :], in0=RB[:, 0, :], in1=RB[:, 2, :], op=ALU.add).then_inc(s_bias, 1)
                with dve.Fori(0, T // 2) as i:
                    for u in (0, 1):
                        n = i * 2 + u
                        dve.bn_stats(out=ST[:, u, :], in_=cut(g.X, n * D, [1, D])).then_inc(s_st, 1)
                    for u in (0, 1):
                        n = i * 2 + u
                        dve.wait_ge(s_st, done(n))
                        dve.sem_inc(s_turn, 1)
                        dve.bn_aggr(out=MV[:, u, :], in_=ST[:, u, :]).then_inc(s_mv, 1)
                    for u in (0, 1):
                        n = i * 2 + u
                        dve.wait_ge(s_sd, done(n))
                        dve.reciprocal(RS[:, u, :], SD[:, u, :]).then_inc(s_rs, 1)
                    for u in (0, 1):
                        n = i * 2 + u
                        dve.wait_ge(s_rs, done(n))
                        dve.wait_ge(s_keep, done(n - 2))
                        dve.wait_ge(s_xtp, done(n - 2))
                        dve.tensor_scalar(out=XS[:, u, :], in0=cut(g.X, n * D, [1, D]), scalar1=MV[:, u, 0:1],
                                          scalar2=RS[:, u, 0:1], op0=ALU.subtract, op1=ALU.mult).then_inc(s_xs, 1)
                    for u in (0, 1):
                        n = i * 2 + u
                        dve.wait_ge(s_qkvp, done(n))
                        dve.wait_ge(s_kv[u], landed(i - 1, 2))
                        dve.tensor_tensor(out=QKV[:, u, :], in0=pq[:, u, 0:3 * D], in1=B[:, :],
                                          op=ALU.add).then_inc(s_qkv, 1)
                    for u in (0, 1):
                        n = i * 2 + u
                        dve.tensor_tensor(out=cut(g.X, n * D, [1, D]), in0=pq[:, u, 3 * D:4 * D],
                                          in1=cut(g.X, n * D, [1, D]), op=ALU.add).then_inc(s_root, 1)
                    for u in (0, 1):
                        n = i * 2 + u
                        dve.wait_ge(s_sq, done(n))
                        dve.tensor_reduce(out=SS[:, u, :], in_=SQ[:, u, :].rearrange("p (h d) -> p h d", d=HD),
                                          axis=AX.X, op=ALU.add).then_inc(s_ss, 1)
                    for u in (0, 1):
                        n = i * 2 + u
                        dve.wait_ge(s_ss, done(n))
                        dve.tensor_tensor(out=SC[:, u, :], in0=SS[:, u, :], in1=C[:, :], op=ALU.mult).then_inc(s_sc, 1)
                    for u in (0, 1):
                        n = i * 2 + u
                        dve.wait_ge(s_sc, done(n))
                        dve.tensor_scalar(out=SS[:, u, :], in0=SC[:, u, :], scalar1=1e-24, scalar2=None,
                                          op0=ALU.max).then_inc(s_fac, 1)
                    for u in (0, 1):
                        n = i * 2 + u
                        dve.wait_ge(s_nm, done(n))
                        dve.reciprocal(FA[:, u, :], NM[:, u, :]).then_inc(s_fac2, 1)
                    for u in (0, 1):
                        n = i * 2 + u
                        dve.wait_ge(s_fac2, done(n))
                        dve.tensor_tensor(out=FB[:, u, 0:H], in0=FA[:, u, 0:H], in1=F[:, 0:H], op=ALU.mult)
                        dve.scalar_tensor_tensor(out=FB[:, u, H:2 * H], in0=FA[:, u, H:2 * H],
                                                 scalar=cut(g.valid, n, [1, 1]), in1=F[:, H:2 * H],
                                                 op0=ALU.mult, op1=ALU.mult).then_inc(s_fac3, 1)
                    for u in (0, 1):
                        n = i * 2 + u
                        dve.wait_ge(s_fac3, done(n))
                        dve.wait_ge(s_qtp, done(n - 2))
                        dve.tensor_tensor(out=QK[:, u, :].rearrange("p (h d) -> p h d", d=HD),
                                          in0=QKV[:, u, 0:2 * D].rearrange("p (h d) -> p h d", d=HD),
                                          in1=cut(FB, u * 2 * H, [1, 2 * H], [0, HD]), op=ALU.mult).then_inc(s_qk, 1)
                dve.wait_ge(s_qk, done(T - 1))

            @block.scalar
            def _(act):
                for s in (s_sd, s_xt, s_sq, s_nm, s_qt):
                    act.sem_inc(s, 2)
                with act.Fori(0, T // 2) as i:
                    for u in (0, 1):
                        n = i * 2 + u
                        act.wait_ge(s_mv, done(n))
                        act.activation(SD[:, u, :], MV[:, u, 1:2], ACT.Sqrt, bias=g.eps[:, 0:1]).then_inc(s_sd, 1)
                    for u in (0, 1):
                        n = i * 2 + u
                        act.wait_ge(s_xtp, done(n))
                        act.activation(XT[:, u, :], pt[:, u, 0:D], ACT.Copy).then_inc(s_xt, 1)
                    for u in (0, 1):
                        n = i * 2 + u
                        act.wait_ge(s_qkv, done(n))
                        act.activation(SQ[:, u, :], QKV[:, u, 0:2 * D], ACT.Square).then_inc(s_sq, 1)
                    for u in (0, 1):
                        n = i * 2 + u
                        act.wait_ge(s_fac, done(n))
                        act.activation(NM[:, u, :], SS[:, u, :], ACT.Sqrt, bias=g.zero[:, 0:1]).then_inc(s_nm, 1)
                    for u in (0, 1):
                        n = i * 2 + u
                        act.wait_ge(s_qtp, done(n))
                        act.wait_ge(s_qo[u], landed(i - 1, 2))
                        act.activation(QT[:, u, :], pr[:, u, 0:D], ACT.Copy).then_inc(s_qt, 1)
                act.wait_ge(s_qt, done(T - 1))

            @block.gpsimd
            def _(pool):
                pool.sem_inc(s_keep, 2)
                pool.wait_ge(s_bias, 1)
                with pool.Fori(0, T // 2) as i:
                    for u in (0, 1):
                        n = i * 2 + u
                        pool.wait_ge(s_xs, done(n))
                        pool.tensor_copy(cut(g.XN, n * GW, [1, D]), XS[:, u, :])
                        pool.wait_ge(s_root, done(n))
                        pool.tensor_tensor(out=cut(g.X, n * D, [1, D]), in0=cut(g.X, n * D, [1, D]),
                                           in1=RB[:, 0, :], op=ALU.add).then_inc(s_keep, 1)
                pool.wait_ge(s_keep, done(T - 1))

            @block.tensor
            def _(pe):
                for s in (s_xtp, s_qkvp, s_qtp):
                    pe.sem_inc(s, 2)
                pe.wait_ge(s_w, NW)
                with pe.Fori(0, T // 2) as i:
                    for u in (0, 1):
                        n = i * 2 + u
                        pe.wait_ge(s_xs, done(n))
                        pe.wait_ge(s_xt, done(n - 2))
                        for c in (0, 1):
                            last = pe.transpose(pt[:, u, c * P:(c + 1) * P], XS[:, u, c * P:(c + 1) * P], g.ident[:, :])
                        last.then_inc(s_xtp, 1)
                    for u in (0, 1):
                        n = i * 2 + u
                        pe.wait_ge(s_xt, done(n))
                        pe.wait_ge(s_qkv, done(n - 2))
                        pe.wait_ge(s_root, done(n - 2))
                        for c in (0, 1):
                            for a, b in ((0, 512), (512, 1024)):
                                last = pe.matmul(pq[:, u, a:b], XT[:, u, c * P:(c + 1) * P], W[:, c, a:b],
                                                 start=c == 0, stop=c == 1)
                        last.then_inc(s_qkvp, 1)
                    for u in (0, 1):
                        n = i * 2 + u
                        pe.wait_ge(s_qk, done(n))
                        pe.wait_ge(s_qt, done(n - 2))
                        for c in (0, 1):
                            last = pe.transpose(pr[:, u, c * P:(c + 1) * P], QK[:, u, c * P:(c + 1) * P], g.ident[:, :])
                        last.then_inc(s_qtp, 1)

SHIFTS = [(0, 0)] + [(a, b) for b in (4, 8, 12, 16) for a in range(4)]
PAIRS = len(SHIFTS)
TURNED = [0, 1, 2, 3, 4, 8, 12, 16]
SECOND = 0.5
GH = H // 2


def pair_weight(a, b):
    return 1.0 if b - a in (0, 16) else 2.0


def keys0_phase(nc, g):
    names = ["s_dup", "s_z", "s_acc", "s_zero", "s_out", "s_tp", "s_m", "s_blk"]
    with phase(nc, names, ["s_l0", "s_l1"]) as (held, sems):
        s_dup, s_z, s_acc, s_zero, s_out, s_tp, s_m, s_blk, s_l0, s_l1 = sems
        s_l = (s_l0, s_l1)

        def sb(name, shape, dt=F32):
            return held.enter_context(nc.sbuf_tensor(own(nc, name), shape, dt))

        ZW = PAIRS * P + P + 1
        KV = sb("kv_in", [P, 2, 2, P])
        KD = sb("k_twice", [P, 2, GH, 2, HD])
        Z = sb("z", [P, 2, ZW + 3])
        S = sb("sums", [P, ZW + 3])
        SG = sb("gram", [P, P + 4])
        blk_i = sb("blk_i", [P, P], I32)
        row_i = sb("row_i", [P, 1], I32)
        acc = held.enter_context(nc.psum_tensor(own(nc, "acc"), [P, 2560], F32))
        gram = held.enter_context(nc.psum_tensor(own(nc, "pgram"), [P, 512], F32))
        tp = held.enter_context(nc.psum_tensor(own(nc, "ptp"), [P, 2, 512], F32))
        LAST = PAIRS * P
        KT = T // 2
        with nc.Block() as block:
            @block.sync
            def _(sp):
                for s in s_l:
                    sp.sem_inc(s, 32)
                for q in (0, 1):
                    with sp.Fori(0, KT) as i:
                        for u in (0, 1):
                            n = i * 2 + u
                            sp.wait_ge(s_acc, done(q * T + n - 2))
                            for c in (0, 1):
                                sp.dma_start(KV[:, u, c, :], flat(g.kv, n * (P * 2 * D) + c * D + q * P,
                                                                  [2 * D, P], [1, P])).then_inc(s_l[u], 16)

            @block.scalar
            def _(act):
                act.sem_inc(s_dup, 2)
                for q in (0, 1):
                    with act.Fori(0, KT) as i:
                        for u in (0, 1):
                            n = i * 2 + u + q * T
                            act.wait_ge(s_l[u], landed(i + q * KT, 2))
                            act.wait_ge(s_z, done(n - 2))
                            act.wait_ge(s_acc, done(n - 2))
                            act.activation(KD[:, u, :, :, :], cut(KV, u * 2 * P, [HD, GH], [0, 2], [1, HD]), ACT.Copy)
                            act.activation(Z[:, u, LAST:LAST + P], KV[:, u, 0, :], ACT.Copy)
                            act.activation(Z[:, u, LAST + P:LAST + P + 1], cut(g.valid, i * 2 + u, [1, 1]),
                                           ACT.Copy).then_inc(s_dup, 1)

            @block.gpsimd
            def _(pool):
                pool.iota(blk_i[:, :], pattern=[[1, P]], base=0, channel_multiplier=0).then_inc(s_blk, 1)
                pool.iota(row_i[:, :], pattern=[[1, 1]], base=0, channel_multiplier=1).then_inc(s_blk, 1)

            @block.vector
            def _(dve):
                dve.wait_ge(s_blk, 2)
                dve.tensor_scalar(out=blk_i[:, :], in0=blk_i[:, :], scalar1=5, scalar2=None,
                                  op0=ALU.logical_shift_right)
                dve.tensor_scalar(out=row_i[:, :], in0=row_i[:, :], scalar1=5, scalar2=None,
                                  op0=ALU.logical_shift_right).then_inc(s_blk, 1)
                dve.wait_ge(s_blk, 3)
                dve.tensor_copy(g.blk[:, :], blk_i[:, :])
                dve.tensor_copy(g.head[:, :], row_i[:, :]).then_inc(s_blk, 1)
                dve.wait_ge(s_blk, 4)
                dve.tensor_scalar(out=g.blk[:, :], in0=g.blk[:, :], scalar1=g.head[:, 0:1], scalar2=None,
                                  op0=ALU.is_equal).then_inc(s_blk, 1)
                dve.wait_ge(s_blk, 5)
                dve.sem_inc(s_z, 2)
                for q in (0, 1):
                    with dve.Fori(0, KT) as i:
                        for u in (0, 1):
                            n = i * 2 + u + q * T
                            dve.wait_ge(s_dup, done(n))
                            dve.wait_ge(s_acc, done(n - 2))
                            dve.tensor_tensor(out=Z[:, u, 0:P].rearrange("p (h d) -> p h d", d=HD),
                                              in0=KD[:, u, :, 0, :], in1=KD[:, u, :, 0, :], op=ALU.mult)
                            for k, b in enumerate((4, 8, 12, 16)):
                                at = u * GH * 2 * HD
                                last = dve.tensor_tensor(
                                    out=Z[:, u, (1 + 4 * k) * P:(5 + 4 * k) * P].rearrange("p (a h d) -> p a h d", a=4, d=HD),
                                    in0=cut(KD, at, [1, 4], [2 * HD, GH], [1, HD]),
                                    in1=cut(KD, at + b, [0, 4], [2 * HD, GH], [1, HD]), op=ALU.mult)
                            last.then_inc(s_z, 1)
                    dve.wait_ge(s_zero, 2 * q + 2)
                    dve.tensor_copy(S[:, 0:LAST + P + 1], acc[:, 0:LAST + P + 1]).then_inc(s_out, 1)
                    dve.tensor_copy(SG[:, 0:P + 1], gram[:, 0:P + 1]).then_inc(s_out, 1)
                    dve.wait_ge(s_out, 3 * q + 2)
                    for f in range(PAIRS + 1):
                        c = (SECOND * pair_weight(*SHIFTS[f]) if f < PAIRS else float(HD) ** 0.5) / N
                        dve.wait_ge(s_tp, q * (PAIRS + 1) + f + 1)
                        dve.scalar_tensor_tensor(out=g.WS[:, q, f, :], in0=tp[:, f % 2, 0:P], scalar=c,
                                                 in1=g.blk[:, :], op0=ALU.mult, op1=ALU.mult).then_inc(s_m, 1)
                    dve.scalar_tensor_tensor(out=g.GS[:, q, :], in0=SG[:, 0:P], scalar=SECOND / N,
                                             in1=g.blk[:, :], op0=ALU.mult, op1=ALU.mult)
                    dve.tensor_scalar(out=g.ks[:, q:q + 1], in0=SG[:, P:P + 1], scalar1=float(HD) ** 0.5 / N,
                                      scalar2=None, op0=ALU.mult)
                    dve.tensor_scalar(out=g.vs[:, q:q + 1], in0=S[:, LAST + P:LAST + P + 1], scalar1=float(HD) / N,
                                      scalar2=None, op0=ALU.mult).then_inc(s_out, 1)

            @block.tensor
            def _(pe):
                pe.sem_inc(s_acc, 2)
                for q in (0, 1):
                    if q:
                        pe.wait_ge(s_out, 2)
                    def zero(start, stop):
                        for b in range(5):
                            pe.matmul(acc[:, b * 512:(b + 1) * 512], g.zrow[0:1, 0:P], g.zrow[0:1, :],
                                      start=start, stop=stop)
                        return pe.matmul(gram[:, :], g.zrow[0:1, 0:P], g.zrow[0:1, :], start=start, stop=stop)
                    zero(True, False).then_inc(s_zero, 1)
                    with pe.Fori(0, KT) as i:
                        for u in (0, 1):
                            n = i * 2 + u + q * T
                            pe.wait_ge(s_z, done(n))
                            for b in range(5):
                                z0, z1 = b * 512, min(b * 512 + 512, LAST + P + 1)
                                pe.matmul(acc[:, z0:z1], KV[:, u, 1, :], Z[:, u, z0:z1], start=False, stop=False)
                            pe.matmul(gram[:, 0:P + 1], KV[:, u, 0, :], Z[:, u, LAST:LAST + P + 1],
                                      start=False, stop=False).then_inc(s_acc, 1)
                    zero(False, True).then_inc(s_zero, 1)
                    pe.wait_ge(s_out, 3 * q + 2)
                    for f in range(PAIRS + 1):
                        k = q * (PAIRS + 1) + f
                        if k >= 2:
                            pe.wait_ge(s_m, k - 1)
                        pe.transpose(tp[:, f % 2, 0:P], S[:, f * P:(f + 1) * P], g.ident[:, :]).then_inc(s_tp, 1)


def queries0_phase(nc, g, w):
    names = ["s_go", "s_turn", "s_z", "s_y", "s_u", "s_t", "s_d", "s_d2", "s_rec", "s_ot", "s_pp", "s_add"]
    with phase(nc, names, ["s_w", "s_l0", "s_l1"]) as (held, sems):
        s_go, s_turn, s_z, s_y, s_u, s_t, s_d, s_d2, s_rec, s_ot, s_pp, s_add, s_w, s_l0, s_l1 = sems
        s_l = (s_l0, s_l1)

        def sb(name, shape, dt=F32):
            return held.enter_context(nc.sbuf_tensor(own(nc, name), shape, dt))

        M = 2 * P
        WP = sb("w_proj", [P, 2, D])
        R = sb("turned", [P, 2, len(TURNED), M])
        Z = sb("z", [P, 2, PAIRS, M])
        TT = sb("t", [P, 2, M])
        DE = sb("den", [P, 2, M])
        DR = sb("rec", [P, 2, M])
        OT = sb("ot", [P, 2, M])
        py = held.enter_context(nc.psum_tensor(own(nc, "py"), [P, 2, 512], F32))
        pu = held.enter_context(nc.psum_tensor(own(nc, "pu"), [P, 2, 512], F32))
        pd = held.enter_context(nc.psum_tensor(own(nc, "pd"), [P, 2, 512], F32))
        pp = held.enter_context(nc.psum_tensor(own(nc, "pp"), [P, 2, 512], F32))
        with nc.Block() as block:
            @block.sync
            def _(sp):
                for s in s_l:
                    sp.sem_inc(s, 16)
                sp.dma_start(WP[:, :, :], w.L0_mix_Wproj.rearrange("(c p) o -> p c o", p=P)).then_inc(s_w, 16)
                with sp.Fori(0, T // 2) as i:
                    for q in (0, 1):
                        n = i * 2 + q
                        sp.wait_ge(s_t, done(n - 2))
                        sp.wait_ge(s_y, done(n - 2))
                        sp.wait_ge(s_z, done(n - 2))
                        sp.dma_start(R[:, q, 0, :], flat(g.qT, q * P * NP + i * M, [NP, P], [1, M])).then_inc(s_l[q], 16)

            @block.vector
            def _(dve):
                for s in (s_turn, s_z, s_t, s_d2, s_rec, s_ot, s_add):
                    dve.sem_inc(s, 2)
                with dve.Fori(0, T // 2) as i:
                    for q in (0, 1):
                        n = i * 2 + q
                        dve.wait_ge(s_l[q], landed(i))
                        dve.sem_inc(s_go, 1)
                        for k, r in enumerate(TURNED[1:]):
                            last = dve.stream_shuffle(out=R[:, q, k + 1, :], in_=R[:, q, 0, :],
                                                      mask=[(j + r) % HD for j in range(HD)])
                        last.then_inc(s_turn, 1)
                        dve.wait_ge(s_turn, done(n))
                        dve.wait_ge(s_y, done(n - 2))
                        dve.tensor_tensor(out=Z[:, q, 0, :], in0=R[:, q, 0, :], in1=R[:, q, 0, :], op=ALU.mult)
                        for k in range(4):
                            last = dve.tensor_tensor(out=Z[:, q, 1 + 4 * k:5 + 4 * k, :], in0=R[:, q, 0:4, :],
                                                     in1=cut(R, (q * 8 + 4 + k) * M, [0, 4], [1, M]), op=ALU.mult)
                        last.then_inc(s_z, 1)
                        dve.wait_ge(s_u, done(n))
                        dve.wait_ge(s_d, done(n - 2))
                        dve.scalar_tensor_tensor(out=TT[:, q, :], in0=pu[:, q, 0:M], scalar=g.ks[:, q:q + 1],
                                                 in1=R[:, q, 0, :], op0=ALU.add, op1=ALU.mult).then_inc(s_t, 1)
                    for q in (0, 1):
                        n = i * 2 + q
                        dve.wait_ge(s_d, done(n))
                        dve.tensor_scalar(out=DE[:, q, :], in0=pd[:, q, 0:M], scalar1=float(HD), scalar2=None,
                                          op0=ALU.add).then_inc(s_d2, 1)
                    for q in (0, 1):
                        n = i * 2 + q
                        dve.wait_ge(s_d2, done(n))
                        dve.reciprocal(DR[:, q, :], DE[:, q, :]).then_inc(s_rec, 1)
                    for q in (0, 1):
                        n = i * 2 + q
                        dve.wait_ge(s_rec, done(n))
                        dve.wait_ge(s_y, done(n))
                        dve.wait_ge(s_pp, done(n - 1 - q))
                        dve.scalar_tensor_tensor(out=OT[:, q, :], in0=py[:, q, 0:M], scalar=g.vs[:, q:q + 1],
                                                 in1=DR[:, q, :], op0=ALU.add, op1=ALU.mult).then_inc(s_ot, 1)
                    for t in (0, 1):
                        n = i * 2 + t
                        dve.wait_ge(s_pp, done(n))
                        dve.tensor_tensor(out=cut(g.X, n * D, [1, D]), in0=pp[:, t, 0:D],
                                          in1=cut(g.X, n * D, [1, D]), op=ALU.add).then_inc(s_add, 1)
                dve.wait_ge(s_add, done(T - 1))

            @block.tensor
            def _(pe):
                for s in (s_u, s_y, s_d, s_pp):
                    pe.sem_inc(s, 2)
                pe.wait_ge(s_w, 16)
                with pe.Fori(0, T // 2) as i:
                    for q in (0, 1):
                        n = i * 2 + q
                        pe.wait_ge(s_l[q], landed(i))
                        pe.wait_ge(s_t, done(n - 2))
                        pe.matmul(pu[:, q, 0:M], g.GS[:, q, :], R[:, q, 0, :], start=True, stop=True).then_inc(s_u, 1)
                        pe.wait_ge(s_ot, done(n - 2))
                        pe.matmul(py[:, q, 0:M], g.WS[:, q, PAIRS, :], R[:, q, 0, :], start=True, stop=False)
                        pe.wait_ge(s_z, done(n))
                        for f in range(PAIRS):
                            last = pe.matmul(py[:, q, 0:M], g.WS[:, q, f, :], Z[:, q, f, :], start=False,
                                             stop=f == PAIRS - 1)
                        last.then_inc(s_y, 1)
                    for q in (0, 1):
                        n = i * 2 + q
                        pe.wait_ge(s_t, done(n))
                        pe.wait_ge(s_d2, done(n - 2))
                        pe.matmul(pd[:, q, 0:M], g.blk[:, :], TT[:, q, :], start=True, stop=True).then_inc(s_d, 1)
                    for t in (0, 1):
                        n = i * 2 + t
                        pe.wait_ge(s_ot, done(i * 2 + 1))
                        pe.wait_ge(s_add, done(n - 2))
                        for q in (0, 1):
                            last = pe.matmul(pp[:, t, 0:D], OT[:, q, t * P:(t + 1) * P], WP[:, q, :],
                                             start=q == 0, stop=q == 1)
                        last.then_inc(s_pp, 1)

AGGS = 4
AROWS = NP + P
BATCH = 8
SCOLS = SROWS // P


def steps_phase(nc, g):
    names = ["s_iota", "s_row", "s_bc", "s_sb", "s_k", "s_tk", "s_gf", "s_tp", "s_out", "s_fin"]
    with phase(nc, names, ["s_in", "s_st", "s_w"]) as (held, sems):
        s_iota, s_row, s_bc, s_sb, s_k, s_tk, s_gf, s_tp, s_out, s_fin, s_in, s_st, s_w = sems
        s_g, = pool_sems(nc, ["s_g"])

        def sb(name, shape, dt=F32):
            return held.enter_context(nc.sbuf_tensor(own(nc, name), shape, dt))

        lrow = sb("last_dst", [1, ET], I32)
        trow = sb("tile_no", [1, ET], I32)
        wrow = sb("last_win", [1, ET], I32)
        wf = sb("win_f", [1, ET])
        tf = sb("tile_f", [1, ET])
        srow = sb("s_sum", [1, ET])
        sall = sb("s_all", [P, ET])
        junk = sb("junk", [P, ET])
        ki = sb("k_i", [P, SCOLS], I32)
        kf = sb("k_f", [P, SCOLS])
        tk = sb("t_k", [P, SCOLS])
        tki = g.tki
        wk = sb("w_k", [P, SCOLS])
        wki = sb("w_ki", [P, SCOLS], I32)
        wb = sb("w_base", [P, SCOLS])
        gd = sb("g_dst", [P, SCOLS, P], I32)
        gs = sb("g_src", [P, SCOLS, P], I32)
        rf = sb("rel_f", [P, SCOLS, P])
        sf = sb("src_f", [P, SCOLS, P])
        pb = held.enter_context(nc.psum_tensor(own(nc, "pb"), [P, 1024], F32))
        tp = held.enter_context(nc.psum_tensor(own(nc, "tp"), [P, 2, 512], F32))
        with nc.Block() as block:
            @block.sync
            def _(sp):
                sp.dma_start(lrow[:, :], flat(g.edst, P - 1, [ET, 1], [P, ET]),
                             allow_slow_non_contiguous=True).then_inc(s_in, 16)
                sp.wait_ge(s_gf, 1)
                sp.dma_start(flat(g.srows, 0, [P, P], [P * P, SCOLS], [1, P]), sf[:, :, :]).then_inc(s_st, 16)
                sp.dma_start(flat(g.wsteps, 0, [1, P], [P, SCOLS]), wki[:, :],
                             allow_slow_non_contiguous=True).then_inc(s_w, 16)
                sp.wait_ge(s_w, 16)
                sp.dma_start(g.wrow[:, :], flat(g.wsteps, 0, [SROWS, 1], [1, SROWS])).then_inc(s_w, 16)
                sp.wait_ge(s_w, 32)
                sp.wait_ge(s_st, 16)

            @block.gpsimd
            def _(pool):
                pool.iota(trow[:, :], pattern=[[1, ET]], base=0, channel_multiplier=0).then_inc(s_iota, 1)
                pool.iota(ki[:, :], pattern=[[P, SCOLS]], base=0, channel_multiplier=1).then_inc(s_iota, 1)
                pool.wait_ge(s_tk, 1)
                for c in range(SCOLS):
                    for to, of in ((gd, g.edst), (gs, g.esrc)):
                        pool.indirect_dma_start(
                            out=to[:, c, :], out_offset=None, in_=flat(of, 0, [P, ET], [1, P]),
                            in_offset=bass.IndirectOffsetOnAxis(ap=tki[:, c:c + 1], axis=0)).then_inc(s_g, 16)
                pool.wait_ge(s_g, 32 * SCOLS)

            @block.vector
            def _(dve):
                dve.wait_ge(s_in, 16)
                dve.tensor_scalar(out=wrow[:, :], in0=lrow[:, :], scalar1=7, scalar2=None,
                                  op0=ALU.logical_shift_right).then_inc(s_row, 1)
                dve.wait_ge(s_iota, 2)
                dve.tensor_copy(tf[:, :], trow[:, :])
                dve.tensor_copy(kf[:, :], ki[:, :]).then_inc(s_k, 1)
                dve.wait_ge(s_row, 1)
                dve.tensor_copy(wf[:, :], wrow[:, :]).then_inc(s_row, 1)
                dve.wait_ge(s_row, 2)
                dve.tensor_tensor(out=srow[:, :], in0=wf[:, :], in1=tf[:, :], op=ALU.add).then_inc(s_row, 1)
                dve.wait_ge(s_bc, 1)
                dve.tensor_copy(sall[:, :], pb[:, 0:ET]).then_inc(s_sb, 1)
                dve.wait_ge(s_sb, 1)
                for c in range(SCOLS):
                    if c:
                        dve.wait_ge(s_k, c + 1)
                    dve.tensor_scalar(out=junk[:, :], in0=sall[:, :], scalar1=kf[:, c:c + 1], scalar2=0.0,
                                      op0=ALU.is_lt, op1=ALU.add, accum_out=tk[:, c:c + 1]).then_inc(s_k, 1)
                dve.wait_ge(s_k, SCOLS + 1)
                dve.tensor_scalar(out=tk[:, :], in0=tk[:, :], scalar1=float(ET - 1), scalar2=None,
                                  op0=ALU.min).then_inc(s_k, 1)
                dve.wait_ge(s_k, SCOLS + 2)
                dve.tensor_tensor(out=wk[:, :], in0=kf[:, :], in1=tk[:, :], op=ALU.subtract).then_inc(s_k, 1)
                dve.tensor_copy(tki[:, :], tk[:, :]).then_inc(s_tk, 1)
                dve.wait_ge(s_k, SCOLS + 3)
                dve.tensor_copy(wki[:, :], wk[:, :])
                dve.tensor_scalar(out=wb[:, :], in0=wk[:, :], scalar1=float(P), scalar2=None,
                                  op0=ALU.mult).then_inc(s_k, 1)
                dve.wait_ge(s_k, SCOLS + 4)
                dve.wait_ge(s_g, 32 * SCOLS)
                for c in range(SCOLS):
                    dve.tensor_scalar(out=rf[:, c, :], in0=gd[:, c, :], scalar1=wb[:, c:c + 1], scalar2=None,
                                      op0=ALU.subtract)
                dve.tensor_copy(sf[:, :, :], gs[:, :, :]).then_inc(s_gf, 1)
                for c in range(SCOLS):
                    for k, to in enumerate((g.rel, g.src)):
                        dve.wait_ge(s_tp, 2 * c + k + 1)
                        dve.tensor_copy(to[:, c * P:(c + 1) * P], tp[:, k, 0:P]).then_inc(s_out, 1)
                dve.wait_ge(s_out, 2 * SCOLS)
                dve.tensor_copy(g.srci[:, :], g.src[:, :]).then_inc(s_fin, 1)
                dve.wait_ge(s_fin, 1)

            @block.tensor
            def _(pe):
                pe.wait_ge(s_row, 3)
                pe.matmul(pb[:, 0:512], g.ones[0:1, :], srow[0:1, 0:512], start=True, stop=True)
                pe.matmul(pb[:, 512:ET], g.ones[0:1, :], srow[0:1, 512:ET], start=True, stop=True).then_inc(s_bc, 1)
                pe.wait_ge(s_gf, 1)
                for c in range(SCOLS):
                    for k, of in enumerate((rf, sf)):
                        if c:
                            pe.wait_ge(s_out, 2 * c + k - 1)
                        pe.transpose(tp[:, k, 0:P], of[:, c, :], g.ident[:, :]).then_inc(s_tp, 1)


def graph0_phase(nc, g):
    names = ["s_oh", "s_dup", "s_i1", "s_i2", "s_idx", "s_m", "s_mt", "s_r", "s_rc", "s_tr", "s_go"]
    with phase(nc, names, ["s_b0", "s_b1"]) as (held, sems):
        s_oh, s_dup, s_i1, s_i2, s_idx, s_m, s_mt, s_r, s_rc, s_tr, s_go, *s_b = sems
        s_c = pool_sems(nc, [f"s_c{a}" for a in range(AGGS)])

        def sb(name, shape, dt=F32):
            return held.enter_context(nc.sbuf_tensor(own(nc, name), shape, dt))

        U = 2 * BATCH
        TURNS = STEPS // U
        assert TURNS * U == STEPS
        KB = sb("src_rows", [P, 2, BATCH, P])
        OH = sb("one_hot", [P, 2, BATCH, P], BF16)
        S = sb("same_src", [P, 2, BATCH, P], BF16)
        ZC = AROWS * GW // P // 4
        zeros = sb("zeros", [P, ZC])
        junk = sb("junk", [P, P])
        DUP = sb("dup", [P, 2, BATCH])
        I1 = sb("i1", [P, 2, BATCH])
        I2 = sb("i2", [P, 2, BATCH])
        IDX = sb("idx", [P, 2, BATCH], I32)
        TR = sb("spare", [P, 1])
        MT = sb("mt", [P, 4, P])
        R = sb("rows", [P, BATCH, GW])
        pm = held.enter_context(nc.psum_tensor(own(nc, "pm"), [P, 2, 512], F32))
        pr = held.enter_context(nc.psum_tensor(own(nc, "pr"), [P, 4, 512], F32))

        def fin(k):
            return k + 1 + U

        with nc.Block() as block:
            @block.sync
            def _(sp):
                for s in s_b:
                    sp.sem_inc(s, 16)
                with sp.Fori(0, TURNS) as i:
                    for h in (0, 1):
                        sp.wait_ge(s_idx, i * 2 + h + 1)
                        sp.dma_start(KB[:, h, :, :], flat(g.srows, (i * U + h * BATCH) * P, [0, P], [1, BATCH * P])
                                     ).then_inc(s_b[h], 16)

            @block.vector
            def _(dve):
                dve.sem_inc(s_idx, 2)
                dve.sem_inc(s_oh, U)
                dve.sem_inc(s_dup, U)
                for s in (s_i1, s_i2):
                    dve.sem_inc(s, 2)
                dve.memset(zeros[:, :], 0.0)
                dve.tensor_scalar(out=TR[:, :], in0=g.pcol[:, :], scalar1=float(NP), scalar2=None,
                                  op0=ALU.add).then_inc(s_tr, 1)
                dve.wait_ge(s_tr, 1)
                with dve.Fori(0, TURNS) as i:
                    for h in (0, 1):
                        k0 = i * U + h * BATCH
                        dve.wait_ge(s_b[h], landed(i))
                        dve.wait_ge(s_m, fin(k0 - U + BATCH - 1))
                        for j in range(BATCH):
                            k = k0 + j
                            dve.tensor_scalar(out=OH[:, h, j, :], in0=g.iota[:, :], scalar1=cut(g.rel, k, [1, 1]),
                                              scalar2=None, op0=ALU.is_equal)
                            dve.tensor_scalar(out=S[:, h, j, :], in0=KB[:, h, j, :], scalar1=cut(g.src, k, [1, 1]),
                                              scalar2=None, op0=ALU.is_equal).then_inc(s_oh, 1)
                            dve.wait_ge(s_dup, fin(k - 1))
                            dve.scalar_tensor_tensor(out=junk[:, :], in0=KB[:, h, j, :],
                                                     scalar=cut(g.src, k, [1, 1]), in1=g.lower[:, :],
                                                     op0=ALU.is_equal, op1=ALU.mult,
                                                     accum_out=DUP[:, h, j:j + 1]).then_inc(s_dup, 1)
                        m = i * 2 + h
                        src = cut(g.src, k0, [1, BATCH])
                        dve.wait_ge(s_dup, fin(k0 + BATCH - 1))
                        dve.tensor_scalar(out=DUP[:, h, :], in0=DUP[:, h, :], scalar1=1.0, scalar2=None, op0=ALU.min)
                        dve.tensor_scalar(out=I1[:, h, :], in0=src, scalar1=-1.0, scalar2=TR[:, 0:1], op0=ALU.mult,
                                          op1=ALU.add).then_inc(s_i1, 1)
                        dve.wait_ge(s_i1, done(m))
                        dve.tensor_tensor(out=I2[:, h, :], in0=I1[:, h, :], in1=DUP[:, h, :],
                                          op=ALU.mult).then_inc(s_i2, 1)
                        dve.wait_ge(s_i2, done(m))
                        dve.wait_ge(s_go, fin(k0 - BATCH - 1 + AGGS))
                        dve.tensor_tensor(out=IDX[:, h, :], in0=I2[:, h, :], in1=src, op=ALU.add).then_inc(s_idx, 1)

            @block.scalar
            def _(act):
                def rows(i, h, j):
                    k = i * U + h * BATCH + j
                    act.wait_ge(s_r, fin(k))
                    act.wait_ge(s_go, fin(k - 4))
                    act.activation(R[:, j, :], pr[:, j % 4, 0:GW], ACT.Copy).then_inc(s_rc, 1)

                act.sem_inc(s_mt, U)
                act.sem_inc(s_rc, U)
                with act.Fori(0, TURNS) as i:
                    for h in (0, 1):
                        for j in range(BATCH):
                            k = i * U + h * BATCH + j
                            act.wait_ge(s_m, fin(k))
                            act.wait_ge(s_r, fin(k - 4))
                            act.activation(MT[:, j % 4, :], pm[:, j % 2, 0:P], ACT.Copy).then_inc(s_mt, 1)
                            if j:
                                rows(i, h, j - 1)
                        rows(i, h, BATCH - 1)
                for s in (s_rc,):
                    act.wait_ge(s, fin(STEPS - 1))

            @block.gpsimd
            def _(pool):
                pool.sem_inc(s_go, U)
                pool.wait_ge(s_tr, 1)
                for a in range(AGGS):
                    for q in range(4):
                        pool.dma_start(flat(g.agg[a], q * ZC, [4 * ZC, P], [1, ZC]), zeros[:, :]).then_inc(s_c[a], 16)
                with pool.Fori(0, TURNS) as i:
                    for h in (0, 1):
                        pool.wait_ge(s_idx, done(i * 2 + h))
                        for j in range(BATCH):
                            k = i * U + h * BATCH + j
                            a = j % AGGS
                            pool.wait_ge(s_rc, fin(k))
                            pool.wait_ge(s_c[a], 16 * (i * 4 + h * 2 + j // 4 - 1 + 5))
                            pool.sem_inc(s_go, 1)
                            pool.indirect_dma_start(
                                out=g.agg[a][:, :], out_offset=bass.IndirectOffsetOnAxis(ap=IDX[:, h, j:j + 1], axis=0),
                                in_=R[:, j, :], in_offset=None, compute_op=ALU.add).then_inc(s_c[a], 16)
                for s in s_c:
                    pool.wait_ge(s, 16 * (STEPS // AGGS - 1 + 5))

            @block.tensor
            def _(pe):
                pe.sem_inc(s_m, U)
                pe.sem_inc(s_r, U)

                def to_rows(i, h, j):
                    k = i * U + h * BATCH + j
                    at = pe.value_load(g.wrow[0:1, bass.ds(k, 1)], min_val=0, max_val=T - 1)
                    pe.wait_ge(s_mt, fin(k))
                    pe.wait_ge(s_rc, fin(k - 4))
                    pe.matmul(pr[:, j % 4, 0:GW], MT[:, j % 4, :], cut(g.XN, at * GW, [1, GW]), start=True,
                              stop=True).then_inc(s_r, 1)

                with pe.Fori(0, TURNS) as i:
                    for h in (0, 1):
                        for j in range(BATCH):
                            k = i * U + h * BATCH + j
                            pe.wait_ge(s_oh, fin(k))
                            pe.wait_ge(s_mt, fin(k - 2))
                            pe.matmul(pm[:, j % 2, 0:P], OH[:, h, j, :], S[:, h, j, :], start=True,
                                      stop=True).then_inc(s_m, 1)
                            if j:
                                to_rows(i, h, j - 1)
                        to_rows(i, h, BATCH - 1)

RING = 4


def join_phase(nc, g, w, layer, cfg):
    names = ["s_go", "s_a", "s_b", "s_cnt", "s_rec", "s_mn", "s_tp", "s_mt", "s_mm", "s_add", "s_st", "s_mv", "s_sd",
             "s_rs", "s_xs", "s_keep", "s_xtp", "s_xt", "s_lp", "s_lg", "s_mx", "s_ix", "s_ef", "s_oh",
             "s_e", "s_ex", "s_sum", "s_ri"]
    with phase(nc, names, ["s_w", "s_l0", "s_l1"]) as (held, sems):
        (s_go, s_a, s_b, s_cnt, s_rec, s_mn, s_tp, s_mt, s_mm, s_add, s_st, s_mv, s_sd, s_rs, s_xs, s_keep, s_xtp,
         s_xt, s_lp, s_lg, s_mx, s_ix, s_ef, s_oh, s_e, s_ex, s_sum, s_ri, s_w, s_l0, s_l1) = sems
        s_l = (s_l0, s_l1)

        def sb(name, shape, dt=F32):
            return held.enter_context(nc.sbuf_tensor(own(nc, name), shape, dt))

        NE, TOP = cfg.experts, cfg.top
        WR = sb("w_router", [P, 2, NE])
        BR = sb("b_router", [P, NE])
        if layer == 0:
            W2 = sb("w_nbr", [P, 2, D])
            AG = sb("agg_in", [P, 2, AGGS, GW])
            A2 = sb("agg_2", [P, 2, 2, GW])
            A1 = sb("agg_1", [P, 2, GW])
            MT = sb("mean_t", [P, 2, D])
        CN = sb("cnt", [P, 2, H])
        RC = sb("rcnt", [P, 2, H])
        MN = sb("mean", [P, 2, D])
        ST = sb("st", [P, 2, 6])
        MV = sb("mv", [P, 2, 2])
        SD = sb("sd", [P, 2, 1])
        RS = sb("rs", [P, 2, 1])
        XS = sb("xs", [P, 2, D])
        XT = sb("xt", [P, 2, D])
        LG = sb("logits", [P, 2, NE])
        MX = sb("max8", [P, 2, 8])
        MI = sb("max_i", [P, 2, 8], U32)
        EX = sb("exps", [P, 2, NE])
        SU = sb("sum", [P, 2, 1])
        RI = sb("rsum", [P, 2, 1])
        NX = sb("neg_max", [P, 2, 1])
        pt = held.enter_context(nc.psum_tensor(own(nc, "pt"), [P, 2, 512], F32))
        pm = held.enter_context(nc.psum_tensor(own(nc, "pm"), [P, 2, 512], F32))
        px = held.enter_context(nc.psum_tensor(own(nc, "px"), [P, 2, 512], F32))
        pl = held.enter_context(nc.psum_tensor(own(nc, "pl"), [P, 2, 512], F32))
        NWT = 16 * (3 if layer == 0 else 2)
        router_w, router_b = (w.L0_ffn_router_w, w.L0_ffn_router_b) if layer == 0 else (w.L1_ffn_gate_w, w.L1_ffn_gate_b)
        with nc.Block() as block:
            @block.sync
            def _(sp):
                sp.dma_start(WR[:, :, :], router_w.rearrange("(c p) o -> p c o", p=P)).then_inc(s_w, 16)
                sp.dma_start(BR[:, :], router_b.partition_broadcast(P)).then_inc(s_w, 16)
                if layer == 0:
                    sp.dma_start(W2[:, :, :], w.L0_gnn_W2.rearrange("(c p) o -> p c o", p=P)).then_inc(s_w, 16)
                    for s in s_l:
                        sp.sem_inc(s, 16 * AGGS)
                    with sp.Fori(0, T // 2) as i:
                        for u in (0, 1):
                            n = i * 2 + u
                            sp.wait_ge(s_a, done(n - 2))
                            for a in range(AGGS):
                                sp.dma_start(AG[:, u, a, :], flat(g.agg[a], n * (P * GW), [GW, P], [1, GW])
                                             ).then_inc(s_l[u], 16)

            @block.vector
            def _(dve):
                for s in (s_a, s_b, s_cnt, s_rec, s_mn, s_add, s_st, s_mv, s_rs, s_xs, s_lg, s_mx, s_ix, s_ef, s_oh, s_e,
                          s_ri):
                    dve.sem_inc(s, 2)
                dve.wait_ge(s_w, NWT)
                with dve.Fori(0, T // 2) as i:
                    if layer == 0:
                        for u in (0, 1):
                            n = i * 2 + u
                            dve.wait_ge(s_l[u], landed(i, AGGS))
                            dve.tensor_tensor(out=A2[:, u, :, :], in0=AG[:, u, 0:2, :], in1=AG[:, u, 2:4, :],
                                              op=ALU.add).then_inc(s_a, 1)
                        for u in (0, 1):
                            n = i * 2 + u
                            dve.wait_ge(s_a, done(n))
                            dve.tensor_tensor(out=A1[:, u, :], in0=A2[:, u, 0, :], in1=A2[:, u, 1, :],
                                              op=ALU.add).then_inc(s_b, 1)
                    for u in (0, 1):
                        n = i * 2 + u
                        if layer == 0:
                            dve.wait_ge(s_b, done(n))
                            dve.tensor_scalar(out=CN[:, u, 0:1], in0=A1[:, u, D:D + 1], scalar1=1.0, scalar2=None,
                                              op0=ALU.max).then_inc(s_cnt, 1)
                        else:
                            dve.tensor_scalar(out=CN[:, u, :], in0=cut(g.XN, n * AW + HD, [HW1, H]), scalar1=1e-16,
                                              scalar2=None, op0=ALU.add).then_inc(s_cnt, 1)
                    for u in (0, 1):
                        n = i * 2 + u
                        dve.wait_ge(s_cnt, done(n))
                        k = 1 if layer == 0 else H
                        dve.reciprocal(RC[:, u, 0:k], CN[:, u, 0:k]).then_inc(s_rec, 1)
                    for u in (0, 1):
                        n = i * 2 + u
                        dve.wait_ge(s_rec, done(n))
                        if layer == 0:
                            dve.wait_ge(s_tp, done(n - 2))
                            dve.tensor_scalar(out=MN[:, u, :], in0=A1[:, u, 0:D], scalar1=RC[:, u, 0:1], scalar2=None,
                                              op0=ALU.mult).then_inc(s_mn, 1)
                        else:
                            dve.tensor_tensor(out=MN[:, u, :].rearrange("p (h d) -> p h d", d=HD),
                                              in0=cut(g.XN, n * AW, [HW1, H], [1, HD]),
                                              in1=cut(RC, u * H, [1, H], [0, HD]), op=ALU.mult).then_inc(s_mn, 1)
                    for u in (0, 1):
                        n = i * 2 + u
                        if layer == 0:
                            dve.wait_ge(s_mm, done(n))
                            more = pm[:, u, 0:D]
                        else:
                            dve.wait_ge(s_mn, done(n))
                            more = MN[:, u, :]
                        dve.tensor_tensor(out=cut(g.X, n * D, [1, D]), in0=more, in1=cut(g.X, n * D, [1, D]),
                                          op=ALU.add).then_inc(s_add, 1)
                    for u in (0, 1):
                        n = i * 2 + u
                        dve.wait_ge(s_add, done(n))
                        dve.sem_inc(s_go, 1)
                        dve.bn_stats(out=ST[:, u, :], in_=cut(g.X, n * D, [1, D])).then_inc(s_st, 1)
                    for u in (0, 1):
                        n = i * 2 + u
                        dve.wait_ge(s_st, done(n))
                        dve.sem_inc(s_go, 1)
                        dve.bn_aggr(out=MV[:, u, :], in_=ST[:, u, :]).then_inc(s_mv, 1)
                    for u in (0, 1):
                        n = i * 2 + u
                        dve.wait_ge(s_sd, done(n))
                        dve.reciprocal(RS[:, u, :], SD[:, u, :]).then_inc(s_rs, 1)
                    for u in (0, 1):
                        n = i * 2 + u
                        dve.wait_ge(s_rs, done(n))
                        dve.wait_ge(s_keep, done(n - 2))
                        dve.wait_ge(s_xtp, done(n - 2))
                        dve.tensor_scalar(out=XS[:, u, :], in0=cut(g.X, n * D, [1, D]), scalar1=MV[:, u, 0:1],
                                          scalar2=RS[:, u, 0:1], op0=ALU.subtract, op1=ALU.mult).then_inc(s_xs, 1)
                    for u in (0, 1):
                        n = i * 2 + u
                        dve.wait_ge(s_lp, done(n))
                        dve.tensor_tensor(out=LG[:, u, :], in0=pl[:, u, 0:NE], in1=BR[:, :], op=ALU.add).then_inc(s_lg, 1)
                    values = LG
                    if layer:
                        for u in (0, 1):
                            n = i * 2 + u
                            dve.wait_ge(s_lg, done(n))
                            dve.tensor_reduce(out=NX[:, u, :], in_=LG[:, u, :], axis=AX.X, op=ALU.max,
                                              negate=True).then_inc(s_e, 1)
                        for u in (0, 1):
                            n = i * 2 + u
                            dve.wait_ge(s_ex, done(n))
                            dve.reciprocal(RI[:, u, :], SU[:, u, :]).then_inc(s_ri, 1)
                        for u in (0, 1):
                            n = i * 2 + u
                            dve.wait_ge(s_ri, done(n))
                            dve.tensor_scalar(out=LG[:, u, :], in0=EX[:, u, :], scalar1=RI[:, u, 0:1], scalar2=None,
                                              op0=ALU.mult).then_inc(s_sum, 1)
                    for u in (0, 1):
                        n = i * 2 + u
                        if layer:
                            dve.wait_ge(s_sum, n + 1)
                        else:
                            dve.wait_ge(s_lg, done(n))
                        dve.sem_inc(s_go, 1)
                        dve.max(MX[:, u, :], values[:, u, :]).then_inc(s_mx, 1)
                    for u in (0, 1):
                        n = i * 2 + u
                        dve.wait_ge(s_mx, done(n))
                        dve.sem_inc(s_go, 1)
                        dve.max_index(MI[:, u, :], MX[:, u, :], values[:, u, :]).then_inc(s_ix, 1)
                    for u in (0, 1):
                        n = i * 2 + u
                        dve.wait_ge(s_ix, done(n))
                        if layer:
                            dve.tensor_copy(cut(g.cw, n, [T, TOP]), MX[:, u, 0:TOP])
                        dve.tensor_copy(cut(g.eidx, n, [T, TOP]), MI[:, u, 0:TOP]).then_inc(s_ef, 1)
                    for u in (0, 1):
                        n = i * 2 + u
                        dve.wait_ge(s_ef, done(n))
                        for k in range(TOP):
                            last = dve.tensor_scalar(out=cut(g.choice, (k * T + n) * NE, [1, NE]), in0=g.iota[:, 0:NE],
                                                     scalar1=cut(g.eidx, k * T + n, [1, 1]), scalar2=None,
                                                     op0=ALU.is_equal)
                        last.then_inc(s_oh, 1)
                dve.wait_ge(s_oh, done(T - 1))

            @block.scalar
            def _(act):
                for s in (s_mt, s_sd, s_xt, s_ex):
                    act.sem_inc(s, 2)
                with act.Fori(0, T // 2) as i:
                    if layer == 0:
                        for u in (0, 1):
                            n = i * 2 + u
                            act.wait_ge(s_tp, done(n))
                            act.activation(MT[:, u, :], pt[:, u, 0:D], ACT.Copy).then_inc(s_mt, 1)
                    for u in (0, 1):
                        n = i * 2 + u
                        act.wait_ge(s_mv, done(n))
                        act.activation(SD[:, u, :], MV[:, u, 1:2], ACT.Sqrt, bias=g.eps[:, 0:1]).then_inc(s_sd, 1)
                    for u in (0, 1):
                        n = i * 2 + u
                        act.wait_ge(s_xtp, done(n))
                        act.activation(XT[:, u, :], px[:, u, 0:D], ACT.Copy).then_inc(s_xt, 1)
                    if layer:
                        for u in (0, 1):
                            n = i * 2 + u
                            act.wait_ge(s_e, done(n))
                            act.activation(EX[:, u, :], LG[:, u, :], ACT.Exp, bias=NX[:, u, 0:1],
                                           accum_out=SU[:, u, :]).then_inc(s_ex, 1)

            @block.gpsimd
            def _(pool):
                pool.sem_inc(s_keep, 2)
                with pool.Fori(0, T // 2) as i:
                    for u in (0, 1):
                        n = i * 2 + u
                        pool.wait_ge(s_xs, done(n))
                        if layer:
                            pool.wait_ge(s_mn, done(n))
                        pool.tensor_copy(cut(g.XN, n * (AW if layer else GW), [1, D]), XS[:, u, :]).then_inc(s_keep, 1)
                pool.wait_ge(s_keep, done(T - 1))

            @block.tensor
            def _(pe):
                for s in (s_tp, s_mm, s_xtp, s_lp):
                    pe.sem_inc(s, 2)
                pe.wait_ge(s_w, NWT)
                with pe.Fori(0, T // 2) as i:
                    if layer == 0:
                        for u in (0, 1):
                            n = i * 2 + u
                            pe.wait_ge(s_mn, done(n))
                            pe.wait_ge(s_mt, done(n - 2))
                            for c in (0, 1):
                                last = pe.transpose(pt[:, u, c * P:(c + 1) * P], MN[:, u, c * P:(c + 1) * P],
                                                    g.ident[:, :])
                            last.then_inc(s_tp, 1)
                        for u in (0, 1):
                            n = i * 2 + u
                            pe.wait_ge(s_mt, done(n))
                            pe.wait_ge(s_add, done(n - 2))
                            for c in (0, 1):
                                last = pe.matmul(pm[:, u, 0:D], MT[:, u, c * P:(c + 1) * P], W2[:, c, :],
                                                 start=c == 0, stop=c == 1)
                            last.then_inc(s_mm, 1)
                    for u in (0, 1):
                        n = i * 2 + u
                        pe.wait_ge(s_xs, done(n))
                        pe.wait_ge(s_xt, done(n - 2))
                        for c in (0, 1):
                            last = pe.transpose(px[:, u, c * P:(c + 1) * P], XS[:, u, c * P:(c + 1) * P], g.ident[:, :])
                        last.then_inc(s_xtp, 1)
                    for u in (0, 1):
                        n = i * 2 + u
                        pe.wait_ge(s_xt, done(n))
                        pe.wait_ge(s_lg, done(n - 2))
                        for c in (0, 1):
                            last = pe.matmul(pl[:, u, 0:NE], XT[:, u, c * P:(c + 1) * P], WR[:, c, :],
                                             start=c == 0, stop=c == 1)
                        last.then_inc(s_lp, 1)


def sort_phase(nc, g, layer, cfg):
    names = ["s_up", "s_pw", "s_cn", "s_inc", "s_exc", "s_a", "s_b", "s_pos", "s_row", "s_cmp", "s_le", "s_s",
             "s_tk", "s_ek", "s_er", "s_ei", "s_z"]
    with phase(nc, names, ["s_zero"]) as (held, sems):
        (s_up, s_pw, s_cn, s_inc, s_exc, s_a, s_b, s_pos, s_row, s_cmp, s_le, s_s, s_tk, s_ek, s_er, s_ei, s_z,
         s_zero) = sems
        s_sc, = pool_sems(nc, ["s_sc"])

        def sb(name, shape, dt=F32):
            return held.enter_context(nc.sbuf_tensor(own(nc, name), shape, dt))

        NE, TOP, STEPS_E = cfg.experts, cfg.top, cfg.steps
        J = TOP * T
        C = J * NE
        up = sb("before", [P, P], BF16)
        one = sb("one_bf", [P, P], BF16)
        CN = sb("counts", [P, C])
        INC = sb("inclusive", [P, C])
        A = sb("a", [P, C])
        Bf = sb("b", [P, C])
        zero = sb("zero_c", [P, C])
        POS = sb("pos", [P, J])
        LAST = sb("last_i", [P, J], I32)
        LASTF = sb("last_f", [P, J])
        LE = sb("le", [P, J])
        JN = sb("j_no", [P, J], I32)
        JF = sb("j_f", [P, J])
        junk = sb("junk", [P, J])
        TK = sb("tk", [P, 1])
        EK = sb("ek", [P, 1])
        pw = held.enter_context(nc.psum_tensor(own(nc, "pw"), [P, 2048], F32))
        pc = held.enter_context(nc.psum_tensor(own(nc, "pc"), [P, 2048], F32))
        XROWS = g.XN
        RW = AW if layer else GW
        with nc.Block() as block:
            @block.sync
            def _(sp):
                sp.wait_ge(s_z, 1)
                for k in range(0, STEPS_E, 4):
                    m = min(4, STEPS_E - k)
                    sp.dma_start(flat(g.xe, k * P * D, [m * D, P], [1, m * D]), g.zeros[:, 0:m * D]).then_inc(s_zero, 16)
                sp.wait_ge(s_zero, 16 * -(-STEPS_E // 4))

            @block.gpsimd
            def _(pool):
                pool.iota(LAST[:, :], pattern=[[P, J]], base=P - 1, channel_multiplier=0).then_inc(s_up, 1)
                pool.iota(JN[:, :], pattern=[[1, J]], base=0, channel_multiplier=0).then_inc(s_up, 1)
                pool.wait_ge(s_row, 1)
                pool.wait_ge(s_zero, 16 * -(-STEPS_E // 4))
                for j in range(J):
                    pool.indirect_dma_start(
                        out=flat(g.xe, 0, [D, STEPS_E * P], [1, D]),
                        out_offset=bass.IndirectOffsetOnAxis(ap=g.rowi[:, j:j + 1], axis=0),
                        in_=cut(XROWS, (j % T) * RW, [1, D]), in_offset=None).then_inc(s_sc, 16)
                pool.wait_ge(s_sc, 16 * J)

            @block.vector
            def _(dve):
                dve.memset(g.zeros[:, :], 0.0).then_inc(s_z, 1)
                dve.memset(one[:, :], 1.0)
                dve.memset(zero[:, :], 0.0)
                dve.tensor_scalar(out=up[:, :], in0=g.iota[:, :], scalar1=g.pcol[:, 0:1], scalar2=None,
                                  op0=ALU.is_gt).then_inc(s_cn, 1)
                dve.wait_ge(s_up, 2)
                dve.tensor_copy(LASTF[:, :], LAST[:, :])
                dve.tensor_copy(JF[:, :], JN[:, :]).then_inc(s_s, 1)
                dve.wait_ge(s_pw, 2)
                dve.tensor_copy(cut(CN, 0, [1, J], [J, NE]), pc[:, 0:C].rearrange("p (j e) -> p j e", e=NE)
                                ).then_inc(s_cn, 1)
                dve.wait_ge(s_cn, 2)
                dve.tensor_tensor_scan(out=INC[:, :], data0=CN[:, :], data1=zero[:, :], initial=0.0, op0=ALU.add,
                                       op1=ALU.add).then_inc(s_inc, 1)
                dve.wait_ge(s_inc, 1)
                dve.tensor_tensor(out=CN[:, :], in0=INC[:, :], in1=CN[:, :], op=ALU.subtract).then_inc(s_exc, 1)
                dve.wait_ge(s_exc, 1)
                dve.tensor_tensor(out=A[:, :].rearrange("p (j e) -> p j e", e=NE),
                                  in0=pw[:, 0:C].rearrange("p (j e) -> p j e", e=NE),
                                  in1=cut(CN, 0, [1, J], [J, NE]), op=ALU.add).then_inc(s_a, 1)
                dve.wait_ge(s_a, 1)
                dve.tensor_tensor(out=Bf[:, :], in0=A[:, :], in1=g.choice[:, 0:C], op=ALU.mult).then_inc(s_b, 1)
                dve.wait_ge(s_b, 1)
                dve.tensor_reduce(out=POS[:, :], in_=Bf[:, :].rearrange("p (j e) -> p j e", e=NE), axis=AX.X,
                                  op=ALU.add).then_inc(s_pos, 1)
                dve.wait_ge(s_pos, 1)
                dve.scalar_tensor_tensor(out=g.rowi[:, 0:J], in0=g.eidx[:, 0:J], scalar=float(P), in1=POS[:, :],
                                         op0=ALU.mult, op1=ALU.add).then_inc(s_row, 1)
                dve.wait_ge(s_s, 1)
                dve.tensor_tensor(out=A[:, :].rearrange("p (j e) -> p j e", e=NE), in0=cut(INC, J - 1, [0, J], [J, NE]),
                                  in1=cut(LASTF, 0, [1, J], [0, NE]), op=ALU.is_le).then_inc(s_cmp, 1)
                dve.wait_ge(s_cmp, 1)
                dve.tensor_reduce(out=LE[:, :], in_=A[:, :].rearrange("p (j e) -> p j e", e=NE), axis=AX.X,
                                  op=ALU.add).then_inc(s_le, 1)
                dve.wait_ge(s_le, 1)
                dve.tensor_tensor(out=LE[:, :], in0=LE[:, :], in1=JF[:, :], op=ALU.add).then_inc(s_s, 1)
                dve.wait_ge(s_s, 2)
                dve.tensor_scalar(out=junk[:, :], in0=LE[:, :], scalar1=g.pcol[:, 0:1], scalar2=0.0, op0=ALU.is_lt,
                                  op1=ALU.add, accum_out=TK[:, :]).then_inc(s_tk, 1)
                dve.wait_ge(s_tk, 1)
                dve.tensor_scalar(out=TK[:, :], in0=TK[:, :], scalar1=float(J - 1), scalar2=None,
                                  op0=ALU.min).then_inc(s_tk, 1)
                dve.wait_ge(s_tk, 2)
                dve.tensor_tensor(out=EK[:, :], in0=g.pcol[:, :], in1=TK[:, :], op=ALU.subtract).then_inc(s_ek, 1)
                dve.wait_ge(s_ek, 1)
                dve.tensor_scalar(out=EK[:, :], in0=EK[:, :], scalar1=float(NE - 1), scalar2=None,
                                  op0=ALU.min).then_inc(s_ek, 1)
                dve.wait_ge(s_er, 1)
                dve.tensor_copy(g.erow[:, :], pc[0:1, 0:P]).then_inc(s_ei, 1)
                dve.wait_ge(s_ei, 1)

            @block.tensor
            def _(pe):
                pe.wait_ge(s_cn, 1)
                for lhs, to in ((up, pw), (one, pc)):
                    for a in range(0, C, 512):
                        b = min(a + 512, C)
                        last = pe.matmul(to[:, a:b], lhs[:, :], g.choice[:, a:b], start=True, stop=True)
                    last.then_inc(s_pw, 1)
                pe.wait_ge(s_ek, 2)
                pe.matmul(pc[0:1, 0:P], EK[:, :], g.ident[:, :], start=True, stop=True).then_inc(s_er, 1)


def experts_phase(nc, g, w, layer, cfg):
    names = ["s_go", "s_xp", "s_xt", "s_h", "s_hb", "s_ha", "s_hp", "s_ht", "s_y", "s_yo"]
    with phase(nc, names, ["s_w", "s_l0", "s_l1", "s_o0", "s_o1"]) as (held, sems):
        s_go, s_xp, s_xt, s_h, s_hb, s_ha, s_hp, s_ht, s_y, s_yo, s_w, s_l0, s_l1, s_o0, s_o1 = sems
        s_l, s_o = (s_l0, s_l1), (s_o0, s_o1)

        def sb(name, shape, dt=F32):
            return held.enter_context(nc.sbuf_tensor(own(nc, name), shape, dt))

        NE, HID, TURNS = cfg.experts, cfg.hidden, cfg.steps // 2
        HC = max(1, HID // P)
        HR = min(HID, P)
        W1 = 0
        B1 = 2 * NE * HID
        assert B1 + NE * HID <= T * GW
        W2 = sb("w2", [HR, HC, NE, D])
        B2 = sb("b2", [P, NE, D])
        XI = sb("xi", [P, 2, D])
        XT = sb("xt", [P, 2, D])
        HB = sb("hb", [P, 2, HID])
        HA = sb("ha", [P, 2, HID])
        HT = sb("ht", [HR, 2, HC * P])
        YO = sb("yo", [P, 2, D])
        px = held.enter_context(nc.psum_tensor(own(nc, "px"), [P, 2, 512], F32))
        ph = held.enter_context(nc.psum_tensor(own(nc, "ph"), [P, 2, 512], F32))
        pt = held.enter_context(nc.psum_tensor(own(nc, "pt"), [P, 2, 512], F32))
        py = held.enter_context(nc.psum_tensor(own(nc, "py"), [P, 2, 512], F32))
        w1, b1, w2, b2 = ((w.L0_ffn_W1, w.L0_ffn_b1, w.L0_ffn_W2, w.L0_ffn_b2) if layer == 0 else
                          (w.L1_ffn_W1, w.L1_ffn_b1, w.L1_ffn_W2, w.L1_ffn_b2))
        NWT = 16 * (4 + HC)
        with nc.Block() as block:
            @block.sync
            def _(sp):
                for s in (*s_l, *s_o):
                    sp.sem_inc(s, 16)
                for c in (0, 1):
                    sp.dma_start(cut(g.XN, W1 + c * NE * HID, [HID, NE], [1, HID]),
                                 w1[:, c * P:(c + 1) * P, :].rearrange("e p h -> p e h")).then_inc(s_w, 16)
                sp.dma_start(cut(g.XN, B1, [1, NE * HID]), b1.rearrange("e h -> (e h)").partition_broadcast(P)
                             ).then_inc(s_w, 16)
                for c in range(HC):
                    sp.dma_start(W2[:, c, :, :], w2[:, c * HR:(c + 1) * HR, :].rearrange("e p d -> p e d")
                                 ).then_inc(s_w, 16)
                sp.dma_start(B2[:, :, :].rearrange("p e d -> p (e d)"), b2.rearrange("e d -> (e d)").partition_broadcast(P)
                             ).then_inc(s_w, 16)

                def store(k, i, u):
                    sp.wait_ge(s_yo, done(k))
                    sp.dma_start(flat(g.ye, k * P * D, [D, P], [1, D]), YO[:, u, :]).then_inc(s_o[u], 16)

                with sp.Fori(0, TURNS) as i:
                    for u in (0, 1):
                        k = i * 2 + u
                        sp.wait_ge(s_xp, done(k - 2))
                        sp.dma_start(XI[:, u, :], flat(g.xe, k * P * D, [D, P], [1, D])).then_inc(s_l[u], 16)
                    for u in (0, 1):
                        store(i * 2 + u, i, u)
                for s in s_o:
                    sp.wait_ge(s, landed(TURNS - 1))

            @block.scalar
            def _(act):
                for s in (s_xt, s_ha, s_ht):
                    act.sem_inc(s, 2)
                with act.Fori(0, TURNS) as i:
                    for u in (0, 1):
                        k = i * 2 + u
                        act.wait_ge(s_xp, done(k))
                        act.activation(XT[:, u, :], px[:, u, 0:D], ACT.Copy).then_inc(s_xt, 1)
                    for u in (0, 1):
                        k = i * 2 + u
                        act.wait_ge(s_hb, done(k))
                        act.wait_ge(s_hp, done(k - 2))
                        act.activation(HA[:, u, :], HB[:, u, :], ACT.Gelu if layer else ACT.Relu).then_inc(s_ha, 1)
                    for u in (0, 1):
                        k = i * 2 + u
                        act.wait_ge(s_hp, done(k))
                        act.activation(HT[:, u, :], pt[0:HR, u, 0:HC * P], ACT.Copy).then_inc(s_ht, 1)

            @block.vector
            def _(dve):
                for s in (s_hb, s_yo):
                    dve.sem_inc(s, 2)
                dve.wait_ge(s_w, NWT)
                with dve.Fori(0, TURNS) as i:
                    ex = []
                    for u in (0, 1):
                        k = i * 2 + u
                        ex.append(dve.value_load(g.erow[0:1, bass.ds(k, 1)], min_val=0, max_val=NE - 1))
                        dve.wait_ge(s_h, done(k))
                        dve.wait_ge(s_ha, done(k - 2))
                        dve.tensor_tensor(out=HB[:, u, :], in0=ph[:, u, 0:HID], in1=cut(g.XN, ex[u] * HID + B1, [1, HID]),
                                          op=ALU.add).then_inc(s_hb, 1)
                    for u in (0, 1):
                        k = i * 2 + u
                        dve.wait_ge(s_y, done(k))
                        dve.wait_ge(s_o[u], landed(i - 1))
                        dve.tensor_tensor(out=YO[:, u, :], in0=py[:, u, 0:D], in1=cut(B2, ex[u] * D, [1, D]),
                                          op=ALU.add).then_inc(s_yo, 1)

            @block.tensor
            def _(pe):
                for s in (s_xp, s_h, s_hp, s_y):
                    pe.sem_inc(s, 2)
                pe.wait_ge(s_w, NWT)
                with pe.Fori(0, TURNS) as i:
                    ex = []
                    for u in (0, 1):
                        k = i * 2 + u
                        pe.wait_ge(s_l[u], landed(i))
                        pe.wait_ge(s_xt, done(k - 2))
                        for c in (0, 1):
                            last = pe.transpose(px[:, u, c * P:(c + 1) * P], XI[:, u, c * P:(c + 1) * P], g.ident[:, :])
                        last.then_inc(s_xp, 1)
                    for u in (0, 1):
                        k = i * 2 + u
                        ex.append(pe.value_load(g.erow[0:1, bass.ds(k, 1)], min_val=0, max_val=NE - 1))
                        pe.wait_ge(s_xt, done(k))
                        pe.wait_ge(s_hb, done(k - 2))
                        for c in (0, 1):
                            last = pe.matmul(ph[:, u, 0:HID], XT[:, u, c * P:(c + 1) * P],
                                             cut(g.XN, ex[u] * HID + W1 + c * NE * HID, [1, HID]), start=c == 0, stop=c == 1)
                        last.then_inc(s_h, 1)
                    for u in (0, 1):
                        k = i * 2 + u
                        pe.wait_ge(s_ha, done(k))
                        pe.wait_ge(s_ht, done(k - 2))
                        pe.sem_inc(s_go, 1)
                        for c in range(HC):
                            last = pe.transpose(pt[0:HR, u, c * P:(c + 1) * P], HA[:, u, c * HR:(c + 1) * HR],
                                                g.ident[:, :])
                        last.then_inc(s_hp, 1)
                    for u in (0, 1):
                        k = i * 2 + u
                        pe.wait_ge(s_ht, done(k))
                        pe.wait_ge(s_yo, done(k - 2))
                        for c in range(HC):
                            last = pe.matmul(py[:, u, 0:D], HT[:, u, c * P:(c + 1) * P],
                                             cut(W2, ex[u] * D + c * NE * D, [1, D]), start=c == 0, stop=c == HC - 1)
                        last.then_inc(s_y, 1)


def merge_phase(nc, g, layer, cfg, out):
    names = ["s_add"]
    with phase(nc, names, ["s_out"]) as (held, sems):
        s_add, s_out = sems
        s_g = pool_sems(nc, [f"s_g{r}" for r in range(RING)])
        Y = held.enter_context(nc.sbuf_tensor(own(nc, "y_in"), [P, RING, D], F32))
        J = cfg.top * T
        NE = cfg.experts
        OUT_T = 7
        with nc.Block() as block:
            @block.gpsimd
            def _(pool):
                for q in range(J):
                    if q >= RING:
                        pool.wait_ge(s_add, q - RING + 1)
                    j = (q % cfg.top) * T + q // cfg.top
                    pool.indirect_dma_start(
                        out=Y[:, q % RING, :], out_offset=None, in_=flat(g.ye, 0, [D, cfg.steps * P], [1, D]),
                        in_offset=bass.IndirectOffsetOnAxis(ap=g.rowi[:, j:j + 1], axis=0)).then_inc(s_g[q % RING], 16)

            @block.vector
            def _(dve):
                for q in range(J):
                    j = (q % cfg.top) * T + q // cfg.top
                    t = q // cfg.top
                    dve.wait_ge(s_g[q % RING], 16 * (q // RING + 1))
                    if q % cfg.top:
                        dve.wait_ge(s_add, q)
                    dve.scalar_tensor_tensor(out=g.X[:, t, :], in0=Y[:, q % RING, :],
                                             scalar=g.cw[:, j:j + 1] if layer else 0.0, in1=g.X[:, t, :],
                                             op0=ALU.mult if layer else ALU.max, op1=ALU.add).then_inc(s_add, 1)
                dve.wait_ge(s_add, J)

            if layer:
                @block.sync
                def _(sp):
                    stores = 0
                    for t in range(0, FULL, OUT_T):
                        m = min(OUT_T, FULL - t)
                        sp.wait_ge(s_add, cfg.top * (t + m))
                        sp.dma_start(out[t * P:(t + m) * P, :].rearrange("(t p) d -> p t d", p=P),
                                     g.X[:, t:t + m, :]).then_inc(s_out, 16)
                        stores += 1
                    sp.wait_ge(s_add, cfg.top * (FULL + 1))
                    sp.dma_start(out[FULL * P:N, :], g.X[0:REST, FULL, :]).then_inc(s_out, 16)
                    sp.wait_ge(s_out, 16 * (stores + 1))

HW1 = HD + 1
PC = EP // P
DIV_EPS, NORM_EPS = 1e-7, 1e-12


def project1_phase(nc, g, w):
    names = ["s_go", "s_pre", "s_prep", "s_fold", "s_bias", "s_st", "s_mv", "s_sd", "s_rs", "s_xs", "s_xtp", "s_xt",
             "s_pp", "s_pj", "s_as", "s_red", "s_root", "s_keep"]
    with phase(nc, names, ["s_w", "s_t0", "s_t1", "s_p0", "s_p1"]) as (held, sems):
        (s_go, s_pre, s_prep, s_fold, s_bias, s_st, s_mv, s_sd, s_rs, s_xs, s_xtp, s_xt, s_pp, s_pj, s_as, s_red,
         s_root, s_keep, s_w, s_t0, s_t1, s_p0, s_p1) = sems
        s_t, s_p = (s_t0, s_t1), (s_p0, s_p1)

        def sb(name, shape, dt=F32):
            return held.enter_context(nc.sbuf_tensor(own(nc, name), shape, dt))

        WVT = sb("w_v_t", [P, 2, D])
        WO = sb("w_out", [P, 2, D])
        BV = sb("b_v", [P, 2])
        W = sb("w_both", [P, 2, 2 * D])
        RB = sb("res_bias", [P, 2, D])
        AB = sb("a_src", [P, D])
        ST = sb("st", [P, 2, 6])
        MV = sb("mv", [P, 2, 2])
        SD = sb("sd", [P, 2, 1])
        RS = sb("rs", [P, 2, 1])
        XS = sb("xs", [P, 2, D])
        XT = sb("xt", [P, 2, D])
        PJ = sb("proj", [P, 2, H, HW1])
        PA = sb("proj_a", [P, 2, D])
        AS = sb("score", [P, 2, H])
        pt = held.enter_context(nc.psum_tensor(own(nc, "pt"), [P, 2, 512], F32))
        pp = held.enter_context(nc.psum_tensor(own(nc, "pp"), [P, 2, 512], F32))
        pf = held.enter_context(nc.psum_tensor(own(nc, "pf"), [P, 2, 512], F32))
        NWT = 16 * 6
        with nc.Block() as block:
            @block.sync
            def _(sp):
                for s in s_t:
                    sp.sem_inc(s, 16)
                for s in s_p:
                    sp.sem_inc(s, 32)
                sp.dma_start(WVT[:, :, :], w.L1_mix_W_qkv_t[2 * D:3 * D, :].rearrange("(c p) o -> p c o", p=P)).then_inc(s_w, 16)
                sp.dma_start(WO[:, :, :], w.L1_mix_W_out.rearrange("(c p) o -> p c o", p=P)).then_inc(s_w, 16)
                sp.dma_start(W[:, :, 0:D], w.L1_gnn_W.rearrange("(c p) o -> p c o", p=P)).then_inc(s_w, 16)
                sp.dma_start(BV[:, :], w.L1_mix_b_qkv[2 * D:3 * D].rearrange("(c p) -> p c", p=P),
                             allow_slow_non_contiguous=True).then_inc(s_w, 16)
                sp.dma_start(RB[:, 0, :], w.L1_mix_b_out.partition_broadcast(P)).then_inc(s_w, 16)
                sp.dma_start(AB[:, :], w.L1_gnn_a_src.rearrange("h d -> (h d)").partition_broadcast(P)).then_inc(s_w, 16)
                with sp.Fori(0, T // 2) as i:
                    for u in (0, 1):
                        n = i * 2 + u
                        sp.wait_ge(s_xt, done(n))
                        sp.dma_start(flat(g.xT, n * P * D, [D, P], [1, D]), XT[:, u, :]).then_inc(s_t[u], 16)
                    for u in (0, 1):
                        n = i * 2 + u
                        sp.wait_ge(s_pj, done(n))
                        sp.dma_start(flat(g.xp, n * P * AW, [AW, P], [1, AW]),
                                     PJ[:, u, :, :].rearrange("p h d -> p (h d)")).then_inc(s_p[u], 16)
                        sp.wait_ge(s_red, done(n))
                        sp.dma_start(flat(g.score, n * P * H, [H, P], [1, H]), AS[:, u, :]).then_inc(s_p[u], 16)
                for s in s_t:
                    sp.wait_ge(s, landed(T // 2 - 1))
                for s in s_p:
                    sp.wait_ge(s, landed(T // 2 - 1, 2))

            @block.vector
            def _(dve):
                for s in (s_st, s_mv, s_rs, s_xs, s_as, s_red, s_root):
                    dve.sem_inc(s, 2)
                dve.memset(PJ[:, :, :, HD:HW1], 1.0).then_inc(s_pre, 1)
                dve.wait_ge(s_fold, 2)
                dve.tensor_copy(W[:, :, D:2 * D], pf[:, :, 0:D])
                dve.wait_ge(s_fold, 3)
                dve.tensor_tensor(out=RB[:, 1, :], in0=RB[:, 0, :], in1=pt[:, 0, 0:D], op=ALU.add).then_inc(s_prep, 1)
                with dve.Fori(0, T // 2) as i:
                    for u in (0, 1):
                        n = i * 2 + u
                        dve.bn_stats(out=ST[:, u, :], in_=cut(g.X, n * D, [1, D])).then_inc(s_st, 1)
                    for u in (0, 1):
                        n = i * 2 + u
                        dve.wait_ge(s_st, done(n))
                        dve.sem_inc(s_go, 1)
                        dve.bn_aggr(out=MV[:, u, :], in_=ST[:, u, :]).then_inc(s_mv, 1)
                    for u in (0, 1):
                        n = i * 2 + u
                        dve.wait_ge(s_sd, done(n))
                        dve.reciprocal(RS[:, u, :], SD[:, u, :]).then_inc(s_rs, 1)
                    for u in (0, 1):
                        n = i * 2 + u
                        dve.wait_ge(s_rs, done(n))
                        dve.wait_ge(s_xtp, done(n - 2))
                        dve.tensor_scalar(out=XS[:, u, :], in0=cut(g.X, n * D, [1, D]), scalar1=MV[:, u, 0:1],
                                          scalar2=RS[:, u, 0:1], op0=ALU.subtract, op1=ALU.mult).then_inc(s_xs, 1)
                    for u in (0, 1):
                        n = i * 2 + u
                        dve.wait_ge(s_pj, done(n))
                        dve.wait_ge(s_red, done(n - 2))
                        dve.tensor_tensor(out=PA[:, u, :].rearrange("p (h d) -> p h d", d=HD),
                                          in0=PJ[:, u, :, 0:HD], in1=AB[:, :].rearrange("p (h d) -> p h d", d=HD),
                                          op=ALU.mult).then_inc(s_as, 1)
                        dve.tensor_tensor(out=cut(g.X, n * D, [1, D]), in0=pp[:, u, D:2 * D],
                                          in1=cut(g.X, n * D, [1, D]), op=ALU.add).then_inc(s_root, 1)
                    for u in (0, 1):
                        n = i * 2 + u
                        dve.wait_ge(s_as, done(n))
                        dve.wait_ge(s_p[u], landed(i - 1, 2))
                        dve.tensor_reduce(out=AS[:, u, :], in_=PA[:, u, :].rearrange("p (h d) -> p h d", d=HD),
                                          axis=AX.X, op=ALU.add).then_inc(s_red, 1)

            @block.scalar
            def _(act):
                for s in (s_sd, s_xt, s_pj):
                    act.sem_inc(s, 2)
                act.wait_ge(s_pre, 1)
                with act.Fori(0, T // 2) as i:
                    for u in (0, 1):
                        n = i * 2 + u
                        act.wait_ge(s_mv, done(n))
                        act.activation(SD[:, u, :], MV[:, u, 1:2], ACT.Sqrt, bias=g.eps[:, 0:1]).then_inc(s_sd, 1)
                    for u in (0, 1):
                        n = i * 2 + u
                        act.wait_ge(s_xtp, done(n))
                        act.wait_ge(s_t[u], landed(i - 1))
                        act.activation(XT[:, u, :], pt[:, u, 0:D], ACT.Copy).then_inc(s_xt, 1)
                    for u in (0, 1):
                        n = i * 2 + u
                        act.wait_ge(s_pp, done(n))
                        act.wait_ge(s_as, done(n - 2))
                        act.wait_ge(s_p[u], landed(i - 1, 2))
                        act.activation(PJ[:, u, :, 0:HD], pp[:, u, 0:D].rearrange("p (h d) -> p h d", d=HD),
                                       ACT.Copy).then_inc(s_pj, 1)

            @block.gpsimd
            def _(pool):
                pool.sem_inc(s_keep, 2)
                pool.wait_ge(s_prep, 1)
                with pool.Fori(0, T // 2) as i:
                    for u in (0, 1):
                        n = i * 2 + u
                        pool.wait_ge(s_root, done(n))
                        pool.tensor_tensor(out=cut(g.X, n * D, [1, D]), in0=cut(g.X, n * D, [1, D]),
                                           in1=RB[:, 1, :], op=ALU.add).then_inc(s_keep, 1)
                pool.wait_ge(s_keep, done(T - 1))

            @block.tensor
            def _(pe):
                for s in (s_xtp, s_pp):
                    pe.sem_inc(s, 2)
                pe.wait_ge(s_w, NWT)
                for m in (0, 1):
                    for c in (0, 1):
                        last = pe.matmul(pf[:, m, 0:D], WVT[:, c, m * P:(m + 1) * P], WO[:, c, :], start=c == 0,
                                         stop=c == 1)
                    last.then_inc(s_fold, 1)
                for c in (0, 1):
                    last = pe.matmul(pt[:, 0, 0:D], cut(BV, c, [0, P]), WO[:, c, :], start=c == 0, stop=c == 1)
                last.then_inc(s_fold, 1)
                pe.wait_ge(s_prep, 1)
                with pe.Fori(0, T // 2) as i:
                    for u in (0, 1):
                        n = i * 2 + u
                        pe.wait_ge(s_xs, done(n))
                        pe.wait_ge(s_xt, done(n - 2))
                        for c in (0, 1):
                            last = pe.transpose(pt[:, u, c * P:(c + 1) * P], XS[:, u, c * P:(c + 1) * P], g.ident[:, :])
                        last.then_inc(s_xtp, 1)
                    for u in (0, 1):
                        n = i * 2 + u
                        pe.wait_ge(s_xt, done(n))
                        pe.wait_ge(s_pj, done(n - 2))
                        pe.wait_ge(s_root, done(n - 2))
                        for c in (0, 1):
                            last = pe.matmul(pp[:, u, :], XT[:, u, c * P:(c + 1) * P], W[:, c, :],
                                             start=c == 0, stop=c == 1)
                        last.then_inc(s_pp, 1)


def mix1_phase(nc, g, w):
    names = ["s_c1", "s_c2", "s_c3", "s_qkvp", "s_qkv", "s_sq", "s_sk", "s_s4", "s_a", "s_r", "s_rt", "s_m", "s_m2", "s_im",
             "s_fac", "s_n", "s_ksq", "s_acc", "s_qtp", "s_qt", "s_zero", "s_out", "s_kt", "s_kw", "s_ix", "s_mv",
             "s_add", "s_pp", "s_cp", "s_go"]
    with phase(nc, names, ["s_w", "s_l0", "s_l1", "s_q0", "s_q1", "s_r0", "s_r1", "s_ie"]) as (held, sems):
        (s_c1, s_c2, s_c3, s_qkvp, s_qkv, s_sq, s_sk, s_s4, s_a, s_r, s_rt, s_m, s_m2, s_im, s_fac, s_n, s_ksq, s_acc,
         s_qtp, s_qt, s_zero, s_out, s_kt, s_kw, s_ix, s_mv, s_add, s_pp, s_cp, s_go, s_w, s_l0, s_l1, s_q0, s_q1,
         s_r0, s_r1, s_ie) = sems
        s_g0, s_g1 = pool_sems(nc, ["s_g0", "s_g1"])
        s_l, s_q, s_rl, s_g = (s_l0, s_l1), (s_q0, s_q1), (s_r0, s_r1), (s_g0, s_g1)

        def sb(name, shape, dt=F32):
            return held.enter_context(nc.sbuf_tensor(own(nc, name), shape, dt))

        W = sb("w_qkv", [P, 2, 3 * D])
        B = sb("b_qkv", [P, 3 * D])
        WO = sb("w_out", [P, 2, D])
        MW = sb("mean_w", [P, 2, 2])
        MB = sb("mean_b", [P, 2])
        XT = sb("xt", [P, 2, D])
        QKV = sb("qkv", [P, 2, 3 * D])
        SQ = sb("squares", [P, 2, 2 * D])
        J4 = sb("fourth", [P, 2, D])
        SS = sb("sums", [P, 2, 2])
        S4 = sb("sum4", [P, 2, 1])
        A = sb("a", [P, 2, 2])
        R = sb("r", [P, 2, 2])
        RT = sb("root", [P, 2, 1])
        M = sb("m", [P, 2, 1])
        M2 = sb("m2", [P, 2, 1])
        IM = sb("im", [P, 2, 1])
        FA = sb("fac", [P, 2, 2])
        NQ = sb("norm", [P, 2, 2 * D])
        KSQ = sb("k_sq", [P, 2, D])
        QT = sb("qt", [P, 2, D])
        QL = sb("ql", [P, 2, D])
        KV = sb("kv", [P, 2, D])
        NR = sb("nr", [P, 2])
        NI = sb("ni", [P, 2])
        KT = sb("kt", [P, 2, D])
        KW = sb("kw", [P, 2, D])
        IE = sb("edge_src", [P, PC], I32)
        IX = sb("ix", [P, 2, BATCH], I32)
        RG = sb("ring", [P, 2, BATCH, H])
        pq = held.enter_context(nc.psum_tensor(own(nc, "pq"), [P, 2, 1024], F32))
        acc = held.enter_context(nc.psum_tensor(own(nc, "acc"), [P, 2, D], F32))
        nrm = held.enter_context(nc.psum_tensor(own(nc, "nrm"), [P, 512], F32))
        pr = held.enter_context(nc.psum_tensor(own(nc, "pr"), [P, 2, 512], F32))
        HT = T // 2
        with nc.Block() as block:
            @block.sync
            def _(sp):
                sp.dma_start(IE[:, :], flat(g.esrc, 0, [PC, P], [1, PC])).then_inc(s_ie, 16)
                for s in (*s_l, *s_q, *s_rl):
                    sp.sem_inc(s, 16)
                sp.dma_start(W[:, :, :], w.L1_mix_W_qkv.rearrange("(c p) o -> p c o", p=P)).then_inc(s_w, 16)
                sp.dma_start(B[:, :], w.L1_mix_b_qkv.partition_broadcast(P)).then_inc(s_w, 16)
                sp.dma_start(WO[:, :, :], w.L1_mix_W_out.rearrange("(c p) o -> p c o", p=P)).then_inc(s_w, 16)
                with sp.Fori(0, HT) as i:
                    for u in (0, 1):
                        n = i * 2 + u
                        sp.wait_ge(s_qkvp, done(n - 2))
                        sp.dma_start(XT[:, u, :], flat(g.xT, n * P * D, [D, P], [1, D])).then_inc(s_l[u], 16)
                    for u in (0, 1):
                        n = i * 2 + u
                        sp.wait_ge(s_qt, done(n))
                        sp.dma_start(flat(g.q1, n * P * D, [D, P], [1, D]), QT[:, u, :]).then_inc(s_q[u], 16)
                for s in s_q:
                    sp.wait_ge(s, landed(HT - 1))
                with sp.Fori(0, HT) as i:
                    for u in (0, 1):
                        n = i * 2 + u
                        sp.wait_ge(s_pp, done(n - 2))
                        sp.dma_start(QL[:, u, :], flat(g.q1, n * P * D, [D, P], [1, D])).then_inc(s_rl[u], 16)

            @block.gpsimd
            def _(pool):
                TURNS = PC // (2 * BATCH)
                pool.wait_ge(s_ie, 16)
                pool.sem_inc(s_ix, 2)
                pool.sem_inc(s_cp, 2)

                def fetch(i, h):
                    m = i * 2 + h
                    pool.tensor_copy(IX[:, h, :], cut(IE, m * BATCH, [1, BATCH])).then_inc(s_ix, 1)
                    pool.wait_ge(s_ix, done(m))
                    pool.sem_inc(s_go, 1)
                    for j in range(BATCH):
                        pool.indirect_dma_start(
                            out=RG[:, h, j, :], out_offset=None, in_=flat(g.score, 0, [H, NP], [1, H]),
                            in_offset=bass.IndirectOffsetOnAxis(ap=IX[:, h, j:j + 1], axis=0)).then_inc(s_g[h], 16)

                def keep(i, h):
                    m = i * 2 + h
                    pool.wait_ge(s_g[h], (i + 1) * (16 * BATCH))
                    pool.tensor_copy(cut(g.ES, m * BATCH * H, [1, BATCH * H]),
                                     RG[:, h, :, :].rearrange("p j h -> p (j h)")).then_inc(s_cp, 1)
                    pool.wait_ge(s_cp, done(m))

                fetch(0, 0)
                with pool.Fori(0, TURNS - 1) as i:
                    fetch(i, 1)
                    keep(i, 0)
                    pool.sem_inc(s_go, 1)
                    fetch(i + 1, 0)
                    keep(i, 1)
                    pool.sem_inc(s_go, 1)
                fetch(TURNS - 1, 1)
                keep(TURNS - 1, 0)
                keep(TURNS - 1, 1)

            @block.vector
            def _(dve):
                for s in (s_qkv, s_a, s_r, s_m, s_m2, s_im, s_fac, s_n, s_add):
                    dve.sem_inc(s, 2)
                dve.wait_ge(s_w, 48)
                dve.tensor_reduce(out=MW[:, :, :], in_=W[:, :, 0:2 * D].rearrange("p c (k d) -> p c k d", d=D),
                                  axis=AX.X, op=ALU.add)
                dve.tensor_reduce(out=MB[:, :], in_=B[:, 0:2 * D].rearrange("p (k d) -> p k d", d=D), axis=AX.X,
                                  op=ALU.add).then_inc(s_c1, 1)
                dve.wait_ge(s_c1, 1)
                dve.tensor_scalar(out=MW[:, :, :], in0=MW[:, :, :], scalar1=1.0 / D, scalar2=None, op0=ALU.mult)
                dve.tensor_scalar(out=MB[:, :], in0=MB[:, :], scalar1=1.0 / D, scalar2=None,
                                  op0=ALU.mult).then_inc(s_c2, 1)
                dve.wait_ge(s_c2, 1)
                for c in (0, 1):
                    for k in (0, 1):
                        dve.tensor_scalar(out=W[:, c, k * D:(k + 1) * D], in0=W[:, c, k * D:(k + 1) * D],
                                          scalar1=MW[:, c, k:k + 1], scalar2=None, op0=ALU.subtract)
                for k in (0, 1):
                    last = dve.tensor_scalar(out=B[:, k * D:(k + 1) * D], in0=B[:, k * D:(k + 1) * D],
                                             scalar1=MB[:, k:k + 1], scalar2=None, op0=ALU.subtract)
                last.then_inc(s_c3, 1)
                dve.wait_ge(s_c3, 1)
                with dve.Fori(0, HT) as i:
                    for u in (0, 1):
                        n = i * 2 + u
                        dve.wait_ge(s_qkvp, done(n))
                        dve.wait_ge(s_acc, done(n - 2))
                        dve.wait_ge(s_sk, done(n - 2))
                        dve.tensor_tensor(out=QKV[:, u, :], in0=pq[:, u, 0:3 * D], in1=B[:, :],
                                          op=ALU.add).then_inc(s_qkv, 1)
                    for u in (0, 1):
                        n = i * 2 + u
                        dve.wait_ge(s_sk, done(n))
                        dve.tensor_scalar(out=A[:, u, :], in0=SS[:, u, :], scalar1=DIV_EPS, scalar2=None,
                                          op0=ALU.add).then_inc(s_a, 1)
                    for u in (0, 1):
                        n = i * 2 + u
                        dve.wait_ge(s_a, done(n))
                        dve.reciprocal(R[:, u, :], A[:, u, :]).then_inc(s_r, 1)
                    for u in (0, 1):
                        n = i * 2 + u
                        dve.wait_ge(s_r, done(n))
                        dve.wait_ge(s_rt, done(n))
                        dve.tensor_tensor(out=M[:, u, :], in0=R[:, u, 0:1], in1=RT[:, u, :], op=ALU.mult).then_inc(s_m, 1)
                    for u in (0, 1):
                        n = i * 2 + u
                        dve.wait_ge(s_m, done(n))
                        dve.tensor_scalar(out=M2[:, u, :], in0=M[:, u, :], scalar1=NORM_EPS, scalar2=None,
                                          op0=ALU.max).then_inc(s_m2, 1)
                    for u in (0, 1):
                        n = i * 2 + u
                        dve.wait_ge(s_m2, done(n))
                        dve.reciprocal(IM[:, u, :], M2[:, u, :]).then_inc(s_im, 1)
                    for u in (0, 1):
                        n = i * 2 + u
                        dve.wait_ge(s_im, done(n))
                        dve.tensor_tensor(out=FA[:, u, 0:1], in0=R[:, u, 0:1], in1=IM[:, u, :], op=ALU.mult)
                        dve.tensor_tensor(out=FA[:, u, 1:2], in0=R[:, u, 1:2], in1=cut(g.valid, n, [1, 1]),
                                          op=ALU.mult).then_inc(s_fac, 1)
                    for u in (0, 1):
                        n = i * 2 + u
                        dve.wait_ge(s_fac, done(n))
                        dve.wait_ge(s_qtp, done(n - 2))
                        dve.wait_ge(s_ksq, done(n - 2))
                        for k in (0, 1):
                            last = dve.tensor_scalar(out=NQ[:, u, k * D:(k + 1) * D], in0=SQ[:, u, k * D:(k + 1) * D],
                                                     scalar1=FA[:, u, k:k + 1], scalar2=None, op0=ALU.mult)
                        last.then_inc(s_n, 1)
                dve.wait_ge(s_zero, 2)
                dve.tensor_copy(NR[:, :], nrm[:, 0:2]).then_inc(s_out, 1)
                dve.wait_ge(s_out, 2)
                dve.tensor_scalar(out=NI[:, :], in0=NR[:, :], scalar1=NORM_EPS, scalar2=None, op0=ALU.max
                                  ).then_inc(s_out, 1)
                dve.wait_ge(s_out, 3)
                dve.reciprocal(NR[:, :], NI[:, :]).then_inc(s_out, 1)
                dve.wait_ge(s_out, 4)
                for c in (0, 1):
                    last = dve.tensor_scalar(out=KV[:, c, :], in0=acc[:, c, :], scalar1=NR[:, c:c + 1], scalar2=None,
                                             op0=ALU.mult)
                last.then_inc(s_kt, 1)
                dve.wait_ge(s_kt, 2)
                dve.tensor_copy(KT[:, :, :], pr[:, :, 0:D]).then_inc(s_kt, 1)
                dve.wait_ge(s_kw, 1)
                dve.tensor_scalar(out=KW[:, :, :], in0=pq[:, 0:2, 0:D], scalar1=float(N) ** -0.5, scalar2=None,
                                  op0=ALU.mult).then_inc(s_kw, 1)
                with dve.Fori(0, HT) as i:
                    for u in (0, 1):
                        n = i * 2 + u
                        dve.wait_ge(s_pp, done(n))
                        dve.tensor_tensor(out=cut(g.X, n * D, [1, D]), in0=pr[:, u, 0:D],
                                          in1=cut(g.X, n * D, [1, D]), op=ALU.add).then_inc(s_add, 1)
                dve.wait_ge(s_add, done(T - 1))

            @block.scalar
            def _(act):
                for s in (s_sq, s_sk, s_s4, s_rt, s_ksq, s_qt):
                    act.sem_inc(s, 2)
                with act.Fori(0, HT) as i:
                    for u in (0, 1):
                        n = i * 2 + u
                        act.wait_ge(s_qkv, done(n))
                        act.wait_ge(s_n, done(n - 2))
                        act.activation(SQ[:, u, 0:D], QKV[:, u, 0:D], ACT.Square, accum_out=SS[:, u, 0:1]).then_inc(s_sq, 1)
                        act.activation(SQ[:, u, D:2 * D], QKV[:, u, D:2 * D], ACT.Square,
                                       accum_out=SS[:, u, 1:2]).then_inc(s_sk, 1)
                    for u in (0, 1):
                        n = i * 2 + u
                        act.wait_ge(s_sq, done(n))
                        act.activation(J4[:, u, :], SQ[:, u, 0:D], ACT.Square, accum_out=S4[:, u, :]).then_inc(s_s4, 1)
                    for u in (0, 1):
                        n = i * 2 + u
                        act.wait_ge(s_s4, done(n))
                        act.activation(RT[:, u, :], S4[:, u, :], ACT.Sqrt, bias=g.zero[:, 0:1]).then_inc(s_rt, 1)
                    for u in (0, 1):
                        n = i * 2 + u
                        act.wait_ge(s_n, done(n))
                        act.wait_ge(s_acc, done(n - 2))
                        act.activation(KSQ[:, u, :], NQ[:, u, D:2 * D], ACT.Square).then_inc(s_ksq, 1)
                    for u in (0, 1):
                        n = i * 2 + u
                        act.wait_ge(s_qtp, done(n))
                        act.wait_ge(s_q[u], landed(i - 1))
                        act.activation(QT[:, u, :], pr[:, u, 0:D], ACT.Copy).then_inc(s_qt, 1)
                act.wait_ge(s_zero, 2)
                act.wait_ge(s_out, 1)
                act.activation(NR[:, :], NR[:, :], ACT.Sqrt, bias=g.zero[:, 0:1]).then_inc(s_out, 1)

            @block.tensor
            def _(pe):
                for s in (s_qkvp, s_acc, s_qtp, s_pp):
                    pe.sem_inc(s, 2)

                def zero(start, stop):
                    pe.matmul(acc[:, :, :], g.zrow[0:1, 0:P], g.zrow[0:1, :], start=start, stop=stop)
                    pe.matmul(nrm[:, :], g.zrow[0:1, 0:P], g.zrow[0:1, :], start=start, stop=stop).then_inc(s_zero, 1)

                zero(True, False)
                pe.wait_ge(s_c3, 1)
                with pe.Fori(0, HT) as i:
                    for u in (0, 1):
                        n = i * 2 + u
                        pe.wait_ge(s_l[u], landed(i))
                        pe.wait_ge(s_qkv, done(n - 2))
                        for c in (0, 1):
                            for a, b in ((0, 512), (512, 768)):
                                last = pe.matmul(pq[:, u, a:b], XT[:, u, c * P:(c + 1) * P], W[:, c, a:b],
                                                 start=c == 0, stop=c == 1)
                        last.then_inc(s_qkvp, 1)
                    for u in (0, 1):
                        n = i * 2 + u
                        pe.wait_ge(s_n, done(n))
                        pe.wait_ge(s_qt, done(n - 2))
                        for c in (0, 1):
                            last = pe.transpose(pr[:, u, c * P:(c + 1) * P], NQ[:, u, c * P:(c + 1) * P], g.ident[:, :])
                        last.then_inc(s_qtp, 1)
                        pe.wait_ge(s_ksq, done(n))
                        for c in (0, 1):
                            pe.matmul(acc[:, c, :], NQ[:, u, D + c * P:D + (c + 1) * P], QKV[:, u, 2 * D:3 * D],
                                      start=False, stop=False)
                        for c in (0, 1):
                            last = pe.matmul(nrm[:, c:c + 1], KSQ[:, u, c * P:(c + 1) * P], g.ones[:, 0:1],
                                             start=False, stop=False)
                        last.then_inc(s_acc, 1)
                zero(False, True)
                pe.wait_ge(s_kt, 1)
                pe.wait_ge(s_qt, done(T - 1))
                for c in (0, 1):
                    for d in (0, 1):
                        last = pe.transpose(pr[:, d, c * P:(c + 1) * P], KV[:, c, d * P:(d + 1) * P], g.ident[:, :])
                last.then_inc(s_kt, 1)
                pe.wait_ge(s_kt, 3)
                for c in (0, 1):
                    for d in (0, 1):
                        last = pe.matmul(pq[:, c, 0:D], KT[:, d, c * P:(c + 1) * P], WO[:, d, :], start=d == 0, stop=d == 1)
                last.then_inc(s_kw, 1)
                pe.wait_ge(s_kw, 2)
                with pe.Fori(0, HT) as i:
                    for u in (0, 1):
                        n = i * 2 + u
                        pe.wait_ge(s_rl[u], landed(i))
                        pe.wait_ge(s_add, done(n - 2))
                        for c in (0, 1):
                            last = pe.matmul(pr[:, u, 0:D], QL[:, u, c * P:(c + 1) * P], KW[:, c, :],
                                             start=c == 0, stop=c == 1)
                        last.then_inc(s_pp, 1)


def weights1_phase(nc, g):
    names = ["s_ms", "s_ne", "s_pen", "s_ps", "s_f", "s_fl", "s_t", "s_tc", "s_ch", "s_chb", "s_cb", "s_ci",
             "s_m", "s_exp", "s_wt", "s_wc"]
    with phase(nc, names, ["s_d", "s_we"]) as (held, sems):
        (s_ms, s_ne, s_pen, s_ps, s_f, s_fl, s_t, s_tc, s_ch, s_chb, s_cb, s_ci, s_m, s_exp, s_wt, s_wc,
         s_d, s_we) = sems
        s_g, = pool_sems(nc, ["s_g"])

        def sb(name, shape, dt=F32):
            return held.enter_context(nc.sbuf_tensor(own(nc, name), shape, dt))

        DI = sb("dst_i", [P, PC + 2], I32)
        PEN = sb("pen", [P, PC + 1])
        PS = sb("pen_sum", [P, 2])
        FL = sb("ends", [P, H])
        PB = sb("pen_b", [P, H])
        CH = sb("chain_in", [H, 2, P])
        CO = sb("chain_out", [H, P + 1])
        CI = sb("carry", [P, H])
        FO, BO = 0, H * PC
        pt = held.enter_context(nc.psum_tensor(own(nc, "pt"), [P, 2, 512], F32))
        pw = held.enter_context(nc.psum_tensor(own(nc, "pw"), [P, 4, 512], F32))
        W4 = sb("w_rows", [P, 2, P * H])
        with nc.Block() as block:
            @block.sync
            def _(sp):
                sp.wait_ge(s_ms, 1)
                sp.dma_start(DI[:, 1:PC + 1], flat(g.edst, 0, [PC, P], [1, PC])).then_inc(s_d, 16)
                sp.dma_start(DI[1:P, 0:1], flat(g.edst, PC - 1, [PC, P - 1], [1, 1]),
                             allow_slow_non_contiguous=True).then_inc(s_d, 16)
                sp.dma_start(DI[0:P - 1, PC + 1:PC + 2], flat(g.edst, PC, [PC, P - 1], [1, 1]),
                             allow_slow_non_contiguous=True).then_inc(s_d, 16)
                sp.wait_ge(s_exp, 1)
                sp.dma_start(flat(g.we, 0, [PC * H, P], [1, PC * H]), g.ES[:, :]).then_inc(s_we, 16)
                sp.wait_ge(s_we, 16)

            @block.gpsimd
            def _(pool):
                pool.wait_ge(s_we, 16)
                for c in range(SCOLS):
                    if c >= 2:
                        pool.wait_ge(s_wt, (c - 1) * H)
                    pool.indirect_dma_start(
                        out=W4[:, c % 2, :], out_offset=None, in_=flat(g.we, 0, [P * H, ET], [1, P * H]),
                        in_offset=bass.IndirectOffsetOnAxis(ap=g.tki[:, c:c + 1], axis=0)).then_inc(s_g, 16)
                    pool.wait_ge(s_g, 16 * (c + 1))

            @block.vector
            def _(dve):
                dve.memset(DI[:, :], -1).then_inc(s_ms, 1)
                dve.wait_ge(s_d, 48)
                dve.tensor_tensor(out=PEN[:, :], in0=DI[:, 0:PC + 1], in1=DI[:, 1:PC + 2],
                                  op=ALU.not_equal).then_inc(s_ne, 1)
                dve.wait_ge(s_ne, 1)
                dve.tensor_scalar(out=PEN[:, :], in0=PEN[:, :], scalar1=NEG, scalar2=None, op0=ALU.mult).then_inc(s_pen, 1)
                dve.memset(CO[:, :], NEG)
                dve.wait_ge(s_pen, 1)
                for b in (0, 1):
                    last = dve.tensor_reduce(out=PS[:, b:b + 1], in_=PEN[:, b:b + PC], axis=AX.X, op=ALU.add)
                last.then_inc(s_ps, 1)
                dve.wait_ge(s_ps, 1)
                for b in (0, 1):
                    def runs(h, first):
                        scores = cut(g.ES, h, [H, PC])
                        fwd = cut(g.XN, FO + h * PC, [1, PC])
                        bwd = cut(g.XN, BO + h * PC + PC - 1, [-1, PC])
                        start = NEG if first else CI[:, h:h + 1]
                        if b == 0:
                            return dve.tensor_tensor_scan(out=fwd, data0=PEN[:, 0:PC], data1=scores, initial=start,
                                                          op0=ALU.add, op1=ALU.max)
                        return dve.tensor_tensor_scan(out=bwd, data0=cut(PEN, PC, [-1, PC]),
                                                      data1=cut(g.XN, FO + h * PC + PC - 1, [-1, PC]),
                                                      initial=start, op0=ALU.add, op1=ALU.max)

                    for h in range(H):
                        last = runs(h, True)
                    last.then_inc(s_f, 1)
                    dve.wait_ge(s_f, 2 * b + 1)
                    dve.tensor_copy(FL[:, :], cut(g.XN, (FO + PC - 1) if b == 0 else BO, [PC, H]))
                    dve.tensor_copy(PB[:, :], cut(PS, b, [0, H])).then_inc(s_fl, 1)
                    dve.wait_ge(s_t, b + 1)
                    dve.tensor_copy(CH[:, :, :], pt[0:H, :, 0:P]).then_inc(s_tc, 1)
                    dve.wait_ge(s_tc, b + 1)
                    if b == 0:
                        dve.tensor_tensor_scan(out=CO[:, 1:P + 1], data0=CH[:, 1, :], data1=CH[:, 0, :], initial=NEG,
                                               op0=ALU.add, op1=ALU.max).then_inc(s_ch, 1)
                    else:
                        dve.memset(CO[:, P:P + 1], NEG)
                        dve.tensor_tensor_scan(out=cut(CO, P - 1, [-1, P]), data0=cut(CH, 2 * P - 1, [-1, P]),
                                               data1=cut(CH, P - 1, [-1, P]), initial=NEG, op0=ALU.add,
                                               op1=ALU.max).then_inc(s_ch, 1)
                    dve.wait_ge(s_cb, b + 1)
                    dve.tensor_copy(CI[:, :], pt[:, 0, 0:H]).then_inc(s_ci, 1)
                    dve.wait_ge(s_ci, b + 1)
                    for h in range(H):
                        last = runs(h, False)
                    last.then_inc(s_f, 1)
                    dve.wait_ge(s_f, 2 * b + 2)
                dve.tensor_tensor(out=cut(g.ES, 0, [H, PC], [1, H]), in0=cut(g.ES, 0, [H, PC], [1, H]),
                                  in1=cut(g.XN, BO, [1, PC], [PC, H]), op=ALU.subtract).then_inc(s_m, 1)
                for c in range(SCOLS):
                    for h in range(H):
                        k = c * H + h
                        dve.wait_ge(s_wt, k + 1)
                        dve.tensor_copy(cut(g.wst, c * P * H + h, [H, P]), pw[:, k % 4, 0:P]).then_inc(s_wc, 1)
                dve.wait_ge(s_wc, SCOLS * H)

            @block.scalar
            def _(act):
                act.wait_ge(s_m, 1)
                act.activation(g.ES[:, :], g.ES[:, :], ACT.Exp).then_inc(s_exp, 1)

            @block.tensor
            def _(pe):
                for b in (0, 1):
                    pe.wait_ge(s_fl, b + 1)
                    pe.transpose(pt[0:H, 0, 0:P], FL[:, :], g.ident[:, :])
                    pe.transpose(pt[0:H, 1, 0:P], PB[:, :], g.ident[:, :]).then_inc(s_t, 1)
                    pe.wait_ge(s_ch, b + 1)
                    pe.transpose(pt[:, 0, 0:H], CO[:, b:b + P], g.ident[0:H, 0:H]).then_inc(s_cb, 1)
                for c in range(SCOLS):
                    pe.wait_ge(s_g, 16 * (c + 1))
                    for h in range(H):
                        k = c * H + h
                        if k >= 4:
                            pe.wait_ge(s_wc, k - 3)
                        pe.transpose(pw[:, k % 4, 0:P], cut(W4, (c % 2) * P * H + h, [H, P]), g.ident[:, :]).then_inc(s_wt, 1)


def graph1_phase(nc, g):
    names = ["s_z", "s_ix", "s_go", "s_pr", "s_oh", "s_pa", "s_acc", "s_gd"]
    with phase(nc, names) as (held, sems):
        s_z, s_ix, s_go, s_pr, s_oh, s_pa, s_acc, s_gd = sems
        s_g = pool_sems(nc, ["s_g0", "s_g1"])

        def sb(name, shape, dt=F32):
            return held.enter_context(nc.sbuf_tensor(own(nc, name), shape, dt))

        U = 2 * BATCH
        TURNS = STEPS // U
        IX = sb("ix", [P, 2, BATCH], I32)
        RG = sb("ring", [P, 2, BATCH, AW])
        PR = sb("weighted", [P, 4, AW])
        OH = sb("one_hot", [P, 4, P])
        pa = held.enter_context(nc.psum_tensor(own(nc, "pa"), [P, 4, 512], F32))

        def fin(k):
            return k + 1 + U

        with nc.Block() as block:
            @block.gpsimd
            def _(pool):
                pool.sem_inc(s_ix, 2)
                with pool.Fori(0, TURNS) as i:
                    for h in (0, 1):
                        m = i * 2 + h
                        pool.wait_ge(s_pr, fin(m * BATCH - U + BATCH - 1))
                        pool.tensor_copy(IX[:, h, :], cut(g.srci, m * BATCH, [1, BATCH])).then_inc(s_ix, 1)
                        pool.wait_ge(s_ix, done(m))
                        pool.sem_inc(s_go, 1)
                        for j in range(BATCH):
                            pool.indirect_dma_start(
                                out=RG[:, h, j, :], out_offset=None, in_=flat(g.xp, 0, [AW, NP], [1, AW]),
                                in_offset=bass.IndirectOffsetOnAxis(ap=IX[:, h, j:j + 1], axis=0)).then_inc(s_g[h], 16)

            @block.vector
            def _(dve):
                for s in (s_pr, s_oh, s_acc):
                    dve.sem_inc(s, U)
                dve.memset(cut(g.XN, 0, [1, T * AW]), 0.0).then_inc(s_z, 1)
                dve.wait_ge(s_z, 1)

                def add(k, j, at):
                    dve.wait_ge(s_pa, fin(k))
                    dve.wait_ge(s_acc, fin(k - 1))
                    dve.tensor_tensor(out=cut(g.XN, at * AW, [1, AW]), in0=pa[:, j % 4, 0:AW],
                                      in1=cut(g.XN, at * AW, [1, AW]), op=ALU.add).then_inc(s_acc, 1)

                with dve.Fori(0, TURNS) as i:
                    for h in (0, 1):
                        k0 = i * U + h * BATCH
                        dve.wait_ge(s_g[h], (i + 1) * (16 * BATCH))
                        ats = []
                        for j in range(BATCH):
                            k = k0 + j
                            ats.append(dve.value_load(g.wrow[0:1, bass.ds(k, 1)], min_val=0, max_val=T - 1))
                            dve.wait_ge(s_pa, fin(k - 4))
                            dve.tensor_tensor(out=PR[:, j % 4, :].rearrange("p (h d) -> p h d", d=HW1),
                                              in0=RG[:, h, j, :].rearrange("p (h d) -> p h d", d=HW1),
                                              in1=cut(g.wst, k * H, [1, H], [0, HW1]), op=ALU.mult).then_inc(s_pr, 1)
                            dve.tensor_scalar(out=OH[:, j % 4, :], in0=g.iota[:, :], scalar1=cut(g.rel, k, [1, 1]),
                                              scalar2=None, op0=ALU.is_equal).then_inc(s_oh, 1)
                            if j >= 2:
                                add(k - 2, j - 2, ats[j - 2])
                        for j in (BATCH - 2, BATCH - 1):
                            add(k0 + j, j, ats[j])
                dve.wait_ge(s_acc, fin(STEPS - 1))

            @block.tensor
            def _(pe):
                pe.sem_inc(s_pa, U)
                with pe.Fori(0, TURNS) as i:
                    for h in (0, 1):
                        for j in range(BATCH):
                            k = i * U + h * BATCH + j
                            pe.wait_ge(s_oh, fin(k))
                            pe.wait_ge(s_acc, fin(k - 4))
                            pe.matmul(pa[:, j % 4, 0:AW], OH[:, j % 4, :], PR[:, j % 4, :], start=True,
                                      stop=True).then_inc(s_pa, 1)


class Bag:
    pass

WEIGHTS = ["L0_gnn_W1", "L0_gnn_b1", "L0_gnn_W2", "L0_gnn_b2", "L0_mix_Wqkv", "L0_mix_bqkv", "L0_mix_Wproj",
           "L0_mix_bproj", "L0_mix_temperature", "L0_ffn_router_w", "L0_ffn_router_b", "L0_ffn_W1", "L0_ffn_b1",
           "L0_ffn_W2", "L0_ffn_b2", "L1_gnn_W", "L1_gnn_a_src", "L1_mix_W_qkv", "L1_mix_b_qkv",
           "L1_mix_W_qkv_t", "L1_mix_W_out", "L1_mix_b_out", "L1_ffn_gate_w", "L1_ffn_gate_b", "L1_ffn_W1", "L1_ffn_b1", "L1_ffn_W2",
           "L1_ffn_b2"]
TRANSPOSED = ("L0_gnn_W1", "L0_gnn_W2", "L0_mix_Wqkv", "L0_mix_Wproj", "L0_ffn_router_w")
Weights = namedtuple("Weights", WEIGHTS)


def feed_forward(nc, g, w, layer, cfg, out):
    with ExitStack() as route:
        g.choice = route.enter_context(nc.sbuf_tensor(own(nc, "choice"), [P, T * 32], BF16))
        g.zeros = route.enter_context(nc.sbuf_tensor(own(nc, "zeros"), [P, 4 * D], F32))
        join_phase(nc, g, w, layer, cfg)
        sort_phase(nc, g, layer, cfg)
    experts_phase(nc, g, w, layer, cfg)
    merge_phase(nc, g, layer, cfg, out)


def gnn_kernel(nc, x, src, dst, w, out):
    g = Bag()
    g.esrc = nc.dram_tensor("esrc", [EP], I32)
    g.edst = nc.dram_tensor("edst", [EP], I32)
    g.kv = nc.dram_tensor("kv", [T, P, 2 * D], F32)
    g.qT = nc.dram_tensor("qT", [2, P, NP], F32)
    g.srows = nc.dram_tensor("srows", [SROWS, P], F32)
    g.wsteps = nc.dram_tensor("wsteps", [SROWS], I32)
    g.agg = [nc.dram_tensor(f"agg{a}", [AROWS, GW], F32) for a in range(AGGS)]
    ffn0, ffn1 = Bag(), Bag()
    ffn0.experts, ffn0.top, ffn0.hidden = 32, 1, 64
    ffn1.experts, ffn1.top, ffn1.hidden = 8, 2, 512
    for f in (ffn0, ffn1):
        f.steps = -(-(f.top * T + f.experts - 1) // 2) * 2
    g.xT = nc.dram_tensor("xn1_t", [NP * D], F32)
    g.q1 = nc.dram_tensor("q1_t", [NP * D], F32)
    g.xp = nc.dram_tensor("projected", [NP * AW], F32)
    g.score = nc.dram_tensor("source_score", [NP * H], F32)
    g.we = nc.dram_tensor("edge_weight", [EP * H], F32)
    g.xe = nc.dram_tensor("expert_in", [ffn1.steps * P, D], F32)
    g.ye = nc.dram_tensor("expert_out", [ffn1.steps * P, D], F32)
    with ExitStack() as held:
        def sb(name, shape, dt=F32):
            return held.enter_context(nc.sbuf_tensor(name, shape, dt))

        g.X = sb("X", [P, T, D])
        g.XN = sb("XN", [P, 2 * H * PC])
        g.iota = sb("iota", [P, P])
        g.pcol = sb("pcol", [P, 1])
        g.ident = sb("ident", [P, P])
        g.lower = sb("lower", [P, P])
        g.valid = sb("valid", [P, T])
        g.eps = sb("eps", [P, 1])
        g.zero = sb("zero", [P, 1])
        g.ones = sb("ones", [P, P])
        g.zrow = sb("zrow", [1, 512])
        g.blk = sb("blk", [P, P])
        g.head = sb("head", [P, 1])
        g.rel = sb("step_rel", [P, SROWS])
        g.src = sb("step_src", [P, SROWS])
        g.srci = sb("step_srci", [P, SROWS], I32)
        g.tki = sb("step_tile", [P, SCOLS], I32)
        g.wrow = sb("step_wrow", [1, SROWS], I32)
        g.cw = sb("expert_weight", [P, 2 * T])
        g.eidx = sb("expert_no", [P, 2 * T])
        g.rowi = sb("expert_row", [P, 2 * T], I32)
        g.erow = sb("expert_of_step", [1, P], I32)
        setup_phase(nc, g, x, src, dst)
        with ExitStack() as mix0:
            def sb0(name, shape):
                return mix0.enter_context(nc.sbuf_tensor(name, shape, F32))

            g.WS = sb0("WS", [P, 2, PAIRS + 1, P])
            g.GS = sb0("GS", [P, 2, P])
            g.ks = sb0("ks", [P, 2])
            g.vs = sb0("vs", [P, 2])
            qkv0_phase(nc, g, w)
            keys0_phase(nc, g)
            queries0_phase(nc, g, w)
        steps_phase(nc, g)
        graph0_phase(nc, g)
        feed_forward(nc, g, w, 0, ffn0, out)
        project1_phase(nc, g, w)
        with ExitStack() as edges:
            g.ES = edges.enter_context(nc.sbuf_tensor("edge_score", [P, PC * H], F32))
            mix1_phase(nc, g, w)
            g.wst = edges.enter_context(nc.sbuf_tensor("step_weight", [P, SROWS * H], F32))
            weights1_phase(nc, g)
            graph1_phase(nc, g)
        feed_forward(nc, g, w, 1, ffn1, out)

def kernel(**inputs):
    import numpy as _np
    import concourse.bacc as _bacc
    from concourse import mybir as _mybir
    from concourse.bass_utils import run_bass_kernel_spmd as _run

    nc = _bacc.Bacc("TRN2", target_bir_lowering=False, num_devices=1)
    arrays = {}

    def given(name, a):
        a = _np.ascontiguousarray(a)
        arrays[f"in_{name}_dram"] = a
        return nc.dram_tensor(f"in_{name}_dram", a.shape, _mybir.dt.from_np(a.dtype), kind="ExternalInput").ap()

    x, src, dst = (given(name, inputs[name]) for name in ("x", "src", "dst"))
    params = {}
    for name in WEIGHTS:
        if name == "L1_mix_W_qkv_t":
            a = _np.asarray(inputs["L1_mix_W_qkv"]).T
        elif name in TRANSPOSED:
            a = _np.asarray(inputs[name]).T
        elif name == "L0_mix_temperature":
            a = _np.asarray(inputs[name]).reshape(H)
        else:
            a = _np.asarray(inputs[name])
        params[name] = given(name, a)
    out = nc.dram_tensor("out_0_dram", (N, D), _mybir.dt.from_np(_np.dtype("float32")), kind="ExternalOutput").ap()
    gnn_kernel(nc, x, src, dst, Weights(**params), out)
    r = _run(nc, [arrays], core_ids=[0])
    return r.results[0]["out_0_dram"]
```

```python
from collections import namedtuple
from contextlib import ExitStack, contextmanager

import concourse.bass as bass
from concourse import mybir

F32 = mybir.dt.float32
BF16 = mybir.dt.bfloat16
I32 = mybir.dt.int32
U32 = mybir.dt.uint32
ALU = mybir.AluOpType
ACT = mybir.ActivationFunctionType
AX = mybir.AxisListType

P = 128
N = 6250
D = 256
T = 50
NP = T * P
FULL = N // P
REST = N - FULL * P
H, HD = 8, 32
E = 106250
ET = -(-E // (16 * P)) * 16
EP = ET * P
WIN = -(-N // P)
STEPS = ET + WIN - 1
SROWS = -(-STEPS // P) * P
PAD_NODE = WIN * P - 1
GW = 260
AW = GW + 4
LN_EPS = 1e-5
NEG = -1.0e30


def cut(buf, at, *dims):
    whole = buf[tuple([slice(None)] * len(buf.shape))]
    return bass.AP(whole.tensor, whole.offset + at, [list(whole.ap[0]), *[list(d) for d in dims]])


def sub(ap, at, *dims):
    return bass.AP(ap.tensor, ap.offset + at, [list(ap.ap[0]), *[list(d) for d in dims]])


def flat(buf, at, *dims):
    whole = buf[tuple([slice(None)] * len(buf.shape))]
    return bass.AP(whole.tensor, whole.offset + at, [list(d) for d in dims])


def own(nc, name):
    return f"{name}_{nc.next_id()}"


def done(n):
    return n + 3


def landed(i, k=1):
    return 16 * k * (i + 2)


def pool_sems(nc, names):
    return [nc.alloc_semaphore(own(nc, n)) for n in names]


@contextmanager
def phase(nc, names, dma_names=()):
    with ExitStack() as held:
        sems = [held.enter_context(nc.semaphore(own(nc, n))) for n in (*names, *dma_names)]
        yield held, sems
        with nc.Block() as block:
            @block.gpsimd
            def _(pool):
                for s in sems:
                    pool.sem_clear(s)


def setup_phase(nc, g, x, src, dst):
    names = ["s_x0", "s_iota", "s_pad", "s_f", "s_z", "s_blk", "s_const"]
    with phase(nc, names, ["s_in", "s_edge"]) as (held, sems):
        s_x0, s_iota, s_pad, s_f, s_z, s_blk, s_const, s_in, s_edge = sems
        blk_i = held.enter_context(nc.sbuf_tensor(own(nc, "blk_i"), [P, P], I32))
        row_i = held.enter_context(nc.sbuf_tensor(own(nc, "row_i"), [P, 1], I32))
        iota_i = held.enter_context(nc.sbuf_tensor(own(nc, "iota_i"), [P, P], I32))
        col_i = held.enter_context(nc.sbuf_tensor(own(nc, "col_i"), [P, 1], I32))
        node_i = held.enter_context(nc.sbuf_tensor(own(nc, "node_i"), [P, T], I32))
        node_f = held.enter_context(nc.sbuf_tensor(own(nc, "node_f"), [P, T], F32))
        pad_i = held.enter_context(nc.sbuf_tensor(own(nc, "pad_i"), [1, EP - E], I32))
        with nc.Block() as block:
            @block.sync
            def _(sp):
                for t in range(0, FULL, 12):
                    sp.dma_start(g.X[:, t:t + 12, :],
                                 x[t * P:(t + 12) * P, :].rearrange("(t p) d -> p t d", p=P)).then_inc(s_in, 16)
                sp.wait_ge(s_x0, 1)
                sp.dma_start(g.X[0:REST, FULL, :], x[FULL * P:N, :]).then_inc(s_in, 16)
                for to, of in ((g.esrc, src), (g.edst, dst)):
                    sp.dma_start(flat(to, 0, [E // 10, 10], [1, E // 10]),
                                 of.rearrange("(a b) -> a b", a=10)).then_inc(s_edge, 16)
                sp.wait_ge(s_pad, 1)
                for to in (g.esrc, g.edst):
                    sp.dma_start(flat(to, E, [EP - E, 1], [1, EP - E]), pad_i[:, :]).then_inc(s_edge, 16)
                sp.wait_ge(s_in, 16 * (FULL // 12 + 1))
                sp.wait_ge(s_edge, 64)

            @block.gpsimd
            def _(pool):
                pool.iota(iota_i[:, :], pattern=[[1, P]], base=0, channel_multiplier=0).then_inc(s_iota, 1)
                pool.iota(col_i[:, :], pattern=[[1, 1]], base=0, channel_multiplier=1).then_inc(s_iota, 1)
                pool.iota(node_i[:, :], pattern=[[P, T]], base=0, channel_multiplier=1).then_inc(s_iota, 1)
                pool.memset(pad_i[:, :], PAD_NODE).then_inc(s_pad, 1)
                pool.wait_ge(s_z, 1)
                for a in range(AGGS):
                    pool.dma_start(g.agg[a][NP:AROWS, :], g.zeros0[:, 0:GW]).then_inc(g.s_c[a], 16)

            @block.vector
            def _(dve):
                dve.memset(g.X[:, FULL:T, :], 0.0).then_inc(s_x0, 1)
                dve.memset(g.zeros0[:, :], 0.0).then_inc(s_z, 1)
                dve.memset(cut(g.XN, D, [GW, T], [1, 1]), 1.0)
                dve.memset(cut(g.XN, D + 1, [GW, T], [1, GW - D - 1]), 0.0)
                dve.memset(g.eps[:, :], LN_EPS)
                dve.memset(g.zero[:, :], 0.0)
                dve.memset(g.zrow[:, :], 0.0)
                dve.memset(g.ones[:, :], 1.0)
                dve.wait_ge(s_iota, 3)
                dve.tensor_copy(g.iota[:, :], iota_i[:, :]).then_inc(s_f, 1)
                dve.tensor_copy(g.pcol[:, :], col_i[:, :]).then_inc(s_f, 1)
                dve.tensor_copy(node_f[:, :], node_i[:, :]).then_inc(s_f, 1)
                dve.tensor_scalar(out=blk_i[:, :], in0=iota_i[:, :], scalar1=5, scalar2=None,
                                  op0=ALU.logical_shift_right)
                dve.tensor_scalar(out=row_i[:, :], in0=col_i[:, :], scalar1=5, scalar2=None,
                                  op0=ALU.logical_shift_right).then_inc(s_blk, 1)
                dve.wait_ge(s_blk, 1)
                dve.tensor_copy(g.blk[:, :], blk_i[:, :])
                dve.tensor_copy(g.head[:, :], row_i[:, :]).then_inc(s_blk, 1)
                dve.wait_ge(s_blk, 2)
                dve.tensor_scalar(out=g.blk[:, :], in0=g.blk[:, :], scalar1=g.head[:, 0:1], scalar2=None,
                                  op0=ALU.is_equal)
                dve.wait_ge(s_f, 3)
                dve.tensor_scalar(out=g.ident[:, :], in0=g.iota[:, :], scalar1=g.pcol[:, 0:1], scalar2=None,
                                  op0=ALU.is_equal)
                dve.tensor_scalar(out=g.lower[:, :], in0=g.iota[:, :], scalar1=g.pcol[:, 0:1], scalar2=None,
                                  op0=ALU.is_lt)
                dve.tensor_scalar(out=g.valid[:, :], in0=node_f[:, :], scalar1=float(N), scalar2=None,
                                  op0=ALU.is_lt).then_inc(s_const, 1)
                dve.wait_ge(s_const, 1)


def norms_phase(nc, g):
    with phase(nc, ["s_st", "s_mv", "s_turn", "s_keep", "s_sd", "s_rs"]) as (held, sems):
        s_st, s_mv, s_turn, s_keep, s_sd, s_rs = sems
        G = 5
        assert T % G == 0
        ST = held.enter_context(nc.sbuf_tensor(own(nc, "st"), [P, G, 6], F32))
        MV = held.enter_context(nc.sbuf_tensor(own(nc, "mv"), [P, G, 2], F32))
        SD = held.enter_context(nc.sbuf_tensor(own(nc, "sd"), [P, T], F32))
        with nc.Block() as block:
            @block.vector
            def _(dve):
                with dve.Fori(0, T // G) as i:
                    for u in range(G):
                        last = dve.bn_stats(out=ST[:, u, :], in_=cut(g.X, (i * G + u) * D, [1, D]))
                    last.then_inc(s_st, 1)
                    dve.wait_ge(s_st, i + 1)
                    dve.sem_inc(s_turn, 1)
                    for u in range(G):
                        last = dve.bn_aggr(out=MV[:, u, :], in_=ST[:, u, :])
                    last.then_inc(s_mv, 1)
                    dve.wait_ge(s_mv, i + 1)
                    dve.tensor_copy(cut(g.mv, i * G * 2, [1, G * 2]), MV[:, :, :].rearrange("p g m -> p (g m)")
                                    ).then_inc(s_keep, 1)
                    dve.wait_ge(s_keep, i + 1)
                    dve.sem_inc(s_turn, 1)
                dve.wait_ge(s_sd, 1)
                dve.reciprocal(cut(g.mv, 1, [2, T]), SD[:, :]).then_inc(s_rs, 1)
                dve.wait_ge(s_rs, 1)

            @block.scalar
            def _(act):
                act.wait_ge(s_keep, T // G)
                act.activation(SD[:, :], cut(g.mv, 1, [2, T]), ACT.Sqrt, bias=g.eps[:, 0:1]).then_inc(s_sd, 1)


def qkv0_phase(nc, g, w):
    names = ["s_res", "s_xs", "s_keep", "s_xtp", "s_xt", "s_qkvp", "s_qkv", "s_sq", "s_ss",
             "s_sc", "s_nm", "s_fac", "s_fac2", "s_fac3", "s_qk", "s_qtp", "s_qt", "s_bias", "s_cf", "s_root", "s_turn"]
    with phase(nc, names, ["s_w", "s_kv0", "s_kv1", "s_qo0", "s_qo1", "s_agg"]) as (held, sems):
        (s_res, s_xs, s_keep, s_xtp, s_xt, s_qkvp, s_qkv, s_sq, s_ss, s_sc, s_nm, s_fac, s_fac2,
         s_fac3, s_qk, s_qtp, s_qt, s_bias, s_cf, s_root, s_turn, s_w, s_kv0, s_kv1, s_qo0, s_qo1, s_agg) = sems
        s_kv, s_qo = (s_kv0, s_kv1), (s_qo0, s_qo1)

        def sb(name, shape, dt=F32):
            return held.enter_context(nc.sbuf_tensor(own(nc, name), shape, dt))

        W = sb("w_qkv", [P, 2, 4 * D])
        B = sb("b_qkv", [P, 3 * D])
        RB = sb("res_bias", [P, 3, D])
        C = sb("ss_scale", [P, 2 * H])
        F = sb("norm_scale", [P, 2 * H])
        XS = sb("xs", [P, 2, D])
        XT = sb("xt", [P, 2, D])
        QKV = sb("qkv", [P, 2, 3 * D])
        SQ = sb("sq", [P, 2, 2 * D])
        SS = sb("ss", [P, 2, 2 * H])
        SC = sb("sc", [P, 2, 2 * H])
        NM = sb("nm", [P, 2, 2 * H])
        FA = sb("fa", [P, 2, 2 * H])
        FB = sb("fb", [P, 2, 2 * H])
        QK = sb("qk", [P, 2, 2 * D])
        QT = sb("qt", [P, 2, D])
        pt = held.enter_context(nc.psum_tensor(own(nc, "pt"), [P, 2, 512], F32))
        pq = held.enter_context(nc.psum_tensor(own(nc, "pq"), [P, 2, 1024], F32))
        pr = held.enter_context(nc.psum_tensor(own(nc, "pr"), [P, 2, 512], F32))
        QSCALE = float(HD) ** 0.25
        NW = 16 * 7
        with nc.Block() as block:
            @block.sync
            def _(sp):
                for s in (*s_kv, *s_qo):
                    sp.sem_inc(s, 32)
                sp.dma_start(W[:, :, 0:3 * D], w.L0_mix_Wqkv.rearrange("(c p) o -> p c o", p=P)).then_inc(s_w, 16)
                sp.dma_start(W[:, :, 3 * D:4 * D], w.L0_gnn_W1.rearrange("(c p) o -> p c o", p=P)).then_inc(s_w, 16)
                sp.dma_start(B[:, :], w.L0_mix_bqkv.partition_broadcast(P)).then_inc(s_w, 16)
                for k, b in enumerate((w.L0_gnn_b1, w.L0_gnn_b2, w.L0_mix_bproj)):
                    sp.dma_start(RB[:, k, :], b.partition_broadcast(P)).then_inc(s_w, 16)
                sp.dma_start(C[:, 0:H], w.L0_mix_temperature.partition_broadcast(P)).then_inc(s_w, 16)
                for a in range(AGGS):
                    for q in range(4):
                        sp.dma_start(flat(g.agg[a], q * ZC, [4 * ZC, P], [1, ZC]), g.zeros0[:, :]).then_inc(s_agg, 16)
                with sp.Fori(0, T // 2) as i:
                    for u in (0, 1):
                        n = i * 2 + u
                        sp.wait_ge(s_qk, done(n))
                        sp.dma_start(flat(g.kv, n * (P * 2 * D), [2 * D, P], [1, D]),
                                     QK[:, u, D:2 * D]).then_inc(s_kv[u], 16)
                        sp.dma_start(flat(g.kv, n * (P * 2 * D) + D, [2 * D, P], [1, D]),
                                     QKV[:, u, 2 * D:3 * D]).then_inc(s_kv[u], 16)
                        sp.wait_ge(s_qt, done(n))
                        for c in (0, 1):
                            sp.dma_start(flat(g.qT, c * P * NP + n * P, [NP, P], [1, P]),
                                         QT[:, u, c * P:(c + 1) * P]).then_inc(s_qo[u], 16)
                for s in (*s_kv, *s_qo):
                    sp.wait_ge(s, landed(T // 2 - 1, 2))
                sp.wait_ge(s_agg, 16 * 4 * AGGS)

            @block.vector
            def _(dve):
                for s in (s_root, s_xs, s_qkv, s_ss, s_sc, s_fac, s_fac2, s_fac3, s_qk):
                    dve.sem_inc(s, 2)
                dve.wait_ge(s_w, NW)
                dve.tensor_scalar(out=F[:, 0:H], in0=C[:, 0:H], scalar1=QSCALE * QSCALE, scalar2=None,
                                  op0=ALU.mult).then_inc(s_cf, 1)
                dve.memset(F[:, H:2 * H], QSCALE)
                dve.wait_ge(s_cf, 1)
                dve.memset(C[:, 0:H], QSCALE * QSCALE)
                dve.memset(C[:, H:2 * H], 1.0)
                dve.tensor_tensor(out=RB[:, 0, :], in0=RB[:, 0, :], in1=RB[:, 1, :], op=ALU.add).then_inc(s_cf, 1)
                dve.wait_ge(s_cf, 2)
                dve.tensor_tensor(out=RB[:, 0, :], in0=RB[:, 0, :], in1=RB[:, 2, :], op=ALU.add).then_inc(s_bias, 1)

                def normed(i):
                    for u in (0, 1):
                        n = i * 2 + u
                        dve.wait_ge(s_keep, done(n - 2))
                        dve.wait_ge(s_xtp, done(n - 2))
                        dve.tensor_scalar(out=XS[:, u, :], in0=cut(g.X, n * D, [1, D]), scalar1=cut(g.mv, n * 2, [1, 1]),
                                          scalar2=cut(g.mv, n * 2 + 1, [1, 1]), op0=ALU.subtract, op1=ALU.mult).then_inc(s_xs, 1)

                def biased(i):
                    for u in (0, 1):
                        n = i * 2 + u
                        dve.wait_ge(s_qkvp, done(n))
                        dve.wait_ge(s_qk, done(n - 2))
                        dve.wait_ge(s_kv[u], landed(i - 1, 2))
                        dve.tensor_tensor(out=QKV[:, u, :], in0=pq[:, u, 0:3 * D], in1=B[:, :],
                                          op=ALU.add).then_inc(s_qkv, 1)
                        dve.tensor_tensor(out=cut(g.X, n * D, [1, D]), in0=pq[:, u, 3 * D:4 * D],
                                          in1=cut(g.X, n * D, [1, D]), op=ALU.add).then_inc(s_root, 1)

                def scaled(i):
                    for u in (0, 1):
                        n = i * 2 + u
                        dve.wait_ge(s_sq, done(n))
                        dve.tensor_reduce(out=SS[:, u, :], in_=SQ[:, u, :].rearrange("p (h d) -> p h d", d=HD),
                                          axis=AX.X, op=ALU.add).then_inc(s_ss, 1)
                    for u in (0, 1):
                        n = i * 2 + u
                        dve.wait_ge(s_ss, done(n))
                        dve.tensor_tensor(out=SC[:, u, :], in0=SS[:, u, :], in1=C[:, :], op=ALU.mult).then_inc(s_sc, 1)
                    for u in (0, 1):
                        n = i * 2 + u
                        dve.wait_ge(s_sc, done(n))
                        dve.tensor_scalar(out=SS[:, u, :], in0=SC[:, u, :], scalar1=1e-24, scalar2=None,
                                          op0=ALU.max).then_inc(s_fac, 1)

                def divided(i):
                    for u in (0, 1):
                        n = i * 2 + u
                        dve.wait_ge(s_nm, done(n))
                        dve.reciprocal(FA[:, u, :], NM[:, u, :]).then_inc(s_fac2, 1)
                    for u in (0, 1):
                        n = i * 2 + u
                        dve.wait_ge(s_fac2, done(n))
                        dve.tensor_tensor(out=FB[:, u, 0:H], in0=FA[:, u, 0:H], in1=F[:, 0:H], op=ALU.mult)
                        dve.scalar_tensor_tensor(out=FB[:, u, H:2 * H], in0=FA[:, u, H:2 * H],
                                                 scalar=cut(g.valid, n, [1, 1]), in1=F[:, H:2 * H],
                                                 op0=ALU.mult, op1=ALU.mult).then_inc(s_fac3, 1)
                    for u in (0, 1):
                        n = i * 2 + u
                        dve.wait_ge(s_fac3, done(n))
                        dve.wait_ge(s_qtp, done(n - 2))
                        dve.wait_ge(s_kv[u], landed(i - 1, 2))
                        dve.tensor_tensor(out=QK[:, u, :].rearrange("p (h d) -> p h d", d=HD),
                                          in0=QKV[:, u, 0:2 * D].rearrange("p (h d) -> p h d", d=HD),
                                          in1=cut(FB, u * 2 * H, [1, 2 * H], [0, HD]), op=ALU.mult).then_inc(s_qk, 1)

                def turn(i, first, last):
                    if not last:
                        normed(i + 1)
                    if not first:
                        scaled(i - 1)
                        divided(i - 1)
                    biased(i)

                normed(0)
                turn(0, True, False)
                with dve.Fori(1, T // 2 - 1) as i:
                    turn(i, False, False)
                turn(T // 2 - 1, False, True)
                scaled(T // 2 - 1)
                divided(T // 2 - 1)
                dve.wait_ge(s_qk, done(T - 1))

            @block.scalar
            def _(act):
                for s in (s_xt, s_sq, s_nm, s_qt):
                    act.sem_inc(s, 2)

                def turned(i):
                    for u in (0, 1):
                        n = i * 2 + u
                        act.wait_ge(s_xtp, done(n))
                        act.wait_ge(s_qkvp, done(n - 2))
                        act.activation(XT[:, u, :], pt[:, u, 0:D], ACT.Copy).then_inc(s_xt, 1)

                def squares(i):
                    for u in (0, 1):
                        n = i * 2 + u
                        act.wait_ge(s_qkv, done(n))
                        act.wait_ge(s_ss, done(n - 2))
                        act.activation(SQ[:, u, :], QKV[:, u, 0:2 * D], ACT.Square).then_inc(s_sq, 1)

                def roots(i):
                    for u in (0, 1):
                        n = i * 2 + u
                        act.wait_ge(s_fac, done(n))
                        act.wait_ge(s_fac2, done(n - 2))
                        act.activation(NM[:, u, :], SS[:, u, :], ACT.Sqrt, bias=g.zero[:, 0:1]).then_inc(s_nm, 1)

                def q_out(i):
                    for u in (0, 1):
                        n = i * 2 + u
                        act.wait_ge(s_qtp, done(n))
                        act.wait_ge(s_qo[u], landed(i - 1, 2))
                        act.activation(QT[:, u, :], pr[:, u, 0:D], ACT.Copy).then_inc(s_qt, 1)

                def turn(i, first, last):
                    if not first:
                        roots(i - 1)
                    if not last:
                        turned(i + 1)
                    if not first:
                        q_out(i - 1)
                    squares(i)

                turned(0)
                turn(0, True, False)
                with act.Fori(1, T // 2 - 1) as i:
                    turn(i, False, False)
                turn(T // 2 - 1, False, True)
                roots(T // 2 - 1)
                q_out(T // 2 - 1)
                act.wait_ge(s_qt, done(T - 1))

            @block.gpsimd
            def _(pool):
                pool.sem_inc(s_keep, 2)
                pool.wait_ge(s_bias, 1)

                def copied(i):
                    for u in (0, 1):
                        n = i * 2 + u
                        pool.wait_ge(s_xs, done(n))
                        pool.tensor_copy(cut(g.XN, n * GW, [1, D]), XS[:, u, :]).then_inc(s_keep, 1)

                def biased(i):
                    for u in (0, 1):
                        n = i * 2 + u
                        pool.wait_ge(s_root, done(n))
                        pool.tensor_tensor(out=cut(g.X, n * D, [1, D]), in0=cut(g.X, n * D, [1, D]),
                                           in1=RB[:, 0, :], op=ALU.add).then_inc(s_res, 1)

                copied(0)
                with pool.Fori(0, T // 2 - 1) as i:
                    copied(i + 1)
                    biased(i)
                biased(T // 2 - 1)
                pool.wait_ge(s_res, T)
                for s in g.s_c:
                    pool.wait_ge(s, 16)

            @block.tensor
            def _(pe):
                for s in (s_xtp, s_qkvp, s_qtp):
                    pe.sem_inc(s, 2)
                pe.wait_ge(s_w, NW)

                def turned(i):
                    for u in (0, 1):
                        n = i * 2 + u
                        pe.wait_ge(s_xs, done(n))
                        pe.wait_ge(s_xt, done(n - 2))
                        for c in (0, 1):
                            last = pe.transpose(pt[:, u, c * P:(c + 1) * P], XS[:, u, c * P:(c + 1) * P], g.ident[:, :])
                        last.then_inc(s_xtp, 1)

                def products(i, u):
                    n = i * 2 + u
                    pe.wait_ge(s_xt, done(n))
                    pe.wait_ge(s_qkv, done(n - 2))
                    pe.wait_ge(s_root, done(n - 2))
                    for c in (0, 1):
                        for a, b in ((0, 512), (512, 1024)):
                            last = pe.matmul(pq[:, u, a:b], XT[:, u, c * P:(c + 1) * P], W[:, c, a:b],
                                             start=c == 0, stop=c == 1)
                    last.then_inc(s_qkvp, 1)

                def q_turned(i):
                    for u in (0, 1):
                        n = i * 2 + u
                        pe.wait_ge(s_qk, done(n))
                        pe.wait_ge(s_qt, done(n - 2))
                        for c in (0, 1):
                            last = pe.transpose(pr[:, u, c * P:(c + 1) * P], QK[:, u, c * P:(c + 1) * P], g.ident[:, :])
                        last.then_inc(s_qtp, 1)

                def turn(i, first, last):
                    products(i, 0)
                    if not last:
                        turned(i + 1)
                    products(i, 1)
                    if not first:
                        q_turned(i - 1)

                turned(0)
                turn(0, True, False)
                with pe.Fori(1, T // 2 - 1) as i:
                    turn(i, False, False)
                turn(T // 2 - 1, False, True)
                q_turned(T // 2 - 1)

AGGS = 4
AROWS = NP + P
BATCH = 8
U = 2 * BATCH
TURNS = STEPS // U
assert TURNS * U == STEPS
ZC = NP * GW // P // 4


class Graph0:

    def __init__(self, nc, g, held):
        def sb(name, shape, dt=F32):
            return held.enter_context(nc.sbuf_tensor(own(nc, name), shape, dt))

        self.g = g
        self.KB = sb("src_rows", [P, 2, BATCH, P])
        self.OH = sb("one_hot", [P, 2, BATCH, P], BF16)
        self.S = sb("same_src", [P, 2, BATCH, P], BF16)
        self.junk = sb("junk", [P, P], BF16)
        self.DUP = sb("dup", [P, 2, BATCH])
        self.I1 = sb("i1", [P, 2, BATCH])
        self.I2 = sb("i2", [P, 2, BATCH])
        self.IDX = sb("idx", [P, 2, BATCH], I32)
        self.TR = sb("spare", [P, 1])
        self.MT = sb("mt", [P, 4, P])
        self.R = sb("rows", [P, BATCH, GW])
        self.pm = held.enter_context(nc.psum_tensor(own(nc, "pm"), [P, 512], F32))
        self.pr = held.enter_context(nc.psum_tensor(own(nc, "pr"), [P, 2, 512], F32))
        self.sems = [held.enter_context(nc.semaphore(own(nc, n))) for n in (
            "s_oh", "s_dup", "s_i1", "s_i2", "s_idx", "s_m", "s_mt", "s_r", "s_rc", "s_tr", "s_go", "s_b0", "s_b1")]
        (self.s_oh, self.s_dup, self.s_i1, self.s_i2, self.s_idx, self.s_m, self.s_mt, self.s_r, self.s_rc,
         self.s_tr, self.s_go, *self.s_b) = self.sems
        with nc.Block() as block:
            @block.sync
            def _(sp):
                for s in self.s_b:
                    sp.sem_inc(s, 16)

            @block.vector
            def _(dve):
                dve.sem_inc(self.s_oh, U)
                dve.sem_inc(self.s_dup, U)
                for s in (self.s_idx, self.s_i1, self.s_i2):
                    dve.sem_inc(s, 2)
                dve.tensor_scalar(out=self.TR[:, :], in0=g.pcol[:, :], scalar1=float(NP), scalar2=None,
                                  op0=ALU.add).then_inc(self.s_tr, 1)
                dve.wait_ge(self.s_tr, 1)

            @block.scalar
            def _(act):
                act.sem_inc(self.s_mt, U)
                act.sem_inc(self.s_rc, U)

            @block.gpsimd
            def _(pool):
                pool.sem_inc(self.s_go, U)

            @block.tensor
            def _(pe):
                pe.sem_inc(self.s_m, U)
                pe.sem_inc(self.s_r, U)

    def fin(self, k):
        return k + 1 + U

    def sync_half(self, sp, i, h):
        sp.wait_ge(self.s_idx, i * 2 + h + 1)
        sp.dma_start(self.KB[:, h, :, :], flat(self.g.srows, (i * U + h * BATCH) * P, [0, P], [1, BATCH * P])
                     ).then_inc(self.s_b[h], 16)

    def vector_half(self, dve, i, h):
        g, fin = self.g, self.fin
        k0 = i * U + h * BATCH
        dve.wait_ge(self.s_b[h], landed(i))
        dve.wait_ge(self.s_m, fin(k0 - U + BATCH - 1))
        for j in range(BATCH):
            k = k0 + j
            dve.tensor_scalar(out=self.OH[:, h, j, :], in0=g.iota[:, :], scalar1=cut(g.rel, k, [1, 1]),
                              scalar2=None, op0=ALU.is_equal)
            dve.tensor_scalar(out=self.S[:, h, j, :], in0=self.KB[:, h, j, :], scalar1=cut(g.src, k, [1, 1]),
                              scalar2=None, op0=ALU.is_equal).then_inc(self.s_oh, 1)
            dve.wait_ge(self.s_dup, fin(k - 1))
            dve.scalar_tensor_tensor(out=self.junk[:, :], in0=self.KB[:, h, j, :], scalar=cut(g.src, k, [1, 1]),
                                     in1=g.lower[:, :], op0=ALU.is_equal, op1=ALU.mult,
                                     accum_out=self.DUP[:, h, j:j + 1]).then_inc(self.s_dup, 1)
        m = i * 2 + h
        src = cut(g.src, k0, [1, BATCH])
        dve.wait_ge(self.s_dup, fin(k0 + BATCH - 1))
        dve.tensor_scalar(out=self.DUP[:, h, :], in0=self.DUP[:, h, :], scalar1=1.0, scalar2=None, op0=ALU.min)
        dve.tensor_scalar(out=self.I1[:, h, :], in0=src, scalar1=-1.0, scalar2=self.TR[:, 0:1], op0=ALU.mult,
                          op1=ALU.add).then_inc(self.s_i1, 1)
        dve.wait_ge(self.s_i1, done(m))
        dve.tensor_tensor(out=self.I2[:, h, :], in0=self.I1[:, h, :], in1=self.DUP[:, h, :],
                          op=ALU.mult).then_inc(self.s_i2, 1)
        dve.wait_ge(self.s_i2, done(m))
        dve.wait_ge(self.s_go, fin(k0 - BATCH - 1 + AGGS))
        dve.tensor_tensor(out=self.IDX[:, h, :], in0=self.I2[:, h, :], in1=src, op=ALU.add).then_inc(self.s_idx, 1)

    def scalar_steps(self, act, i, first, last):
        fin = self.fin

        def rows(j):
            k = i * U + j
            act.wait_ge(self.s_r, fin(k))
            act.wait_ge(self.s_go, fin(k - 4))
            act.activation(self.R[:, j % BATCH, :], self.pr[:, j % 2, 0:GW], ACT.Copy).then_inc(self.s_rc, 1)

        for j in range(first, last):
            k = i * U + j
            act.wait_ge(self.s_m, fin(k))
            act.wait_ge(self.s_r, fin(k - 4))
            act.activation(self.MT[:, j % 4, :], self.pm[:, 0:P], ACT.Copy).then_inc(self.s_mt, 1)
            if j:
                rows(j - 1)
        if last == U:
            rows(U - 1)

    def pool_half(self, pool, i, h):
        pool.wait_ge(self.s_idx, done(i * 2 + h))
        for j in range(BATCH):
            k = i * U + h * BATCH + j
            a = j % AGGS
            pool.wait_ge(self.s_rc, self.fin(k))
            pool.wait_ge(self.g.s_c[a], 16 * (i * 4 + h * 2 + j // 4 + 1))
            pool.sem_inc(self.s_go, 1)
            pool.indirect_dma_start(
                out=self.g.agg[a][:, :], out_offset=bass.IndirectOffsetOnAxis(ap=self.IDX[:, h, j:j + 1], axis=0),
                in_=self.R[:, j, :], in_offset=None, compute_op=ALU.add).then_inc(self.g.s_c[a], 16)

    def tensor_steps(self, pe, i, first, last):
        fin = self.fin

        def to_rows(j):
            k = i * U + j
            at = pe.value_load(self.g.wrow[0:1, bass.ds(k, 1)], min_val=0, max_val=T - 1)
            pe.wait_ge(self.s_mt, fin(k))
            pe.wait_ge(self.s_rc, fin(k - 2))
            pe.matmul(self.pr[:, j % 2, 0:GW], self.MT[:, j % 4, :], cut(self.g.XN, at * GW, [1, GW]), start=True,
                      stop=True).then_inc(self.s_r, 1)

        for j in range(first, last):
            k = i * U + j
            pe.wait_ge(self.s_oh, fin(k))
            pe.wait_ge(self.s_mt, fin(k - 1))
            pe.matmul(self.pm[:, 0:P], self.OH[:, j // BATCH, j % BATCH, :], self.S[:, j // BATCH, j % BATCH, :],
                      start=True, stop=True).then_inc(self.s_m, 1)
            if j:
                to_rows(j - 1)
        if last == U:
            to_rows(U - 1)

    def end(self, nc):
        with nc.Block() as block:
            @block.gpsimd
            def _(pool):
                for s in self.g.s_c:
                    pool.wait_ge(s, 16 * (STEPS // AGGS + 1))
                for s in self.sems:
                    pool.sem_clear(s)

SHIFTS = [(0, 0)] + [(a, b) for b in (4, 8, 12, 16) for a in range(4)]
PAIRS = len(SHIFTS)
TURNED = [0, 1, 2, 3, 4, 8, 12, 16]
SECOND = 0.5
GH = H // 2


def pair_weight(a, b):
    return 1.0 if b - a in (0, 16) else 2.0


def over_pairs(eng, q, pair):
    if q == 0:
        with eng.Fori(0, T // 2) as i:
            pair(i, i)
    else:
        with eng.Fori(0, LEFT) as a:
            pair(a * TAIL, a + T // 2)
            with eng.Fori(1, TAIL) as b:
                pair(a * TAIL + b, None)

LEFT = TURNS - T // 2 * 2
TAIL = T // 2 // LEFT
assert LEFT * TAIL == T // 2


def keys0_phase(nc, g, graph, q):
    names = ["s_dup", "s_z", "s_acc", "s_zero", "s_out", "s_tp", "s_m"]
    with phase(nc, names, ["s_l0", "s_l1"]) as (held, sems):
        s_dup, s_z, s_acc, s_zero, s_out, s_tp, s_m, s_l0, s_l1 = sems
        s_l = (s_l0, s_l1)

        def sb(name, shape, dt=F32):
            return held.enter_context(nc.sbuf_tensor(own(nc, name), shape, dt))

        LAST = PAIRS * P
        ZW = LAST + P + 1
        GRAM = ZW
        KV = sb("kv_in", [P, 2, 2, P])
        KD = sb("k_twice", [P, 2, GH, 2, HD])
        Z = sb("z", [P, 2, ZW + 3])
        S = sb("sums", [P, ZW + P + 1])
        acc = held.enter_context(nc.psum_tensor(own(nc, "acc"), [P, 2560], F32))
        assert GRAM + P + 1 <= 2560
        with nc.Block() as block:
            @block.sync
            def _(sp):
                for s in s_l:
                    sp.sem_inc(s, 32)

                def pair(i, turn):
                    for u in (0, 1):
                        if turn is not None:
                            graph.sync_half(sp, turn, u)
                        sp.wait_ge(s_acc, done(i * 2 + u - 2))
                        for c in (0, 1):
                            sp.dma_start(KV[:, u, c, :], flat(g.kv, (i * 2 + u) * (P * 2 * D) + c * D + q * P,
                                                              [2 * D, P], [1, P])).then_inc(s_l[u], 16)

                over_pairs(sp, q, pair)

            @block.scalar
            def _(act):
                act.sem_inc(s_dup, 2)

                def twice(i, u):
                    n = i * 2 + u
                    act.wait_ge(s_l[u], landed(i, 2))
                    act.wait_ge(s_z, done(n - 2))
                    act.wait_ge(s_acc, done(n - 2))
                    act.activation(KD[:, u, :, :, :], cut(KV, u * 2 * P, [HD, GH], [0, 2], [1, HD]), ACT.Copy)
                    act.activation(Z[:, u, LAST:LAST + P], KV[:, u, 0, :], ACT.Copy)
                    act.activation(Z[:, u, LAST + P:LAST + P + 1], cut(g.valid, n, [1, 1]),
                                   ACT.Copy).then_inc(s_dup, 1)

                if q == 0:
                    def turn(i, last):
                        graph.scalar_steps(act, i, 0, 3)
                        twice(i, 1)
                        graph.scalar_steps(act, i, 3, 12)
                        if not last:
                            twice(i + 1, 0)
                        graph.scalar_steps(act, i, 12, U)

                    twice(0, 0)
                    with act.Fori(0, T // 2 - 1) as i:
                        turn(i, False)
                    turn(T // 2 - 1, True)
                else:
                    def pair(i, turn):
                        for u in (0, 1):
                            twice(i, u)
                        if turn is not None:
                            graph.scalar_steps(act, turn, 0, U)

                    over_pairs(act, q, pair)

            @block.gpsimd
            def _(pool):
                def pair(i, turn):
                    if turn is not None:
                        graph.pool_half(pool, turn, 0)
                        graph.pool_half(pool, turn, 1)

                over_pairs(pool, q, pair)

            @block.vector
            def _(dve):
                dve.sem_inc(s_z, 2)

                def pair(i, turn):
                    for u in (0, 1):
                        n = i * 2 + u
                        if turn is not None:
                            graph.vector_half(dve, turn, u)
                        dve.wait_ge(s_dup, done(n))
                        dve.wait_ge(s_acc, done(n - 2))
                        dve.tensor_tensor(out=Z[:, u, 0:P].rearrange("p (h d) -> p h d", d=HD),
                                          in0=KD[:, u, :, 0, :], in1=KD[:, u, :, 0, :], op=ALU.mult)
                        for k, b in enumerate((4, 8, 12, 16)):
                            at = u * GH * 2 * HD
                            last = dve.tensor_tensor(
                                out=Z[:, u, (1 + 4 * k) * P:(5 + 4 * k) * P].rearrange("p (a h d) -> p a h d", a=4, d=HD),
                                in0=cut(KD, at, [1, 4], [2 * HD, GH], [1, HD]),
                                in1=cut(KD, at + b, [0, 4], [2 * HD, GH], [1, HD]), op=ALU.mult)
                        last.then_inc(s_z, 1)

                over_pairs(dve, q, pair)
                dve.wait_ge(s_zero, 2)
                dve.tensor_copy(S[:, :], acc[:, 0:ZW + P + 1]).then_inc(s_out, 1)
                dve.wait_ge(s_out, 1)
                for f in range(PAIRS + 1):
                    c = (SECOND * pair_weight(*SHIFTS[f]) if f < PAIRS else float(HD) ** 0.5) / N
                    dve.wait_ge(s_tp, f + 1)
                    dve.scalar_tensor_tensor(out=g.WS[:, q, f, :], in0=acc[:, f % 2 * 512:f % 2 * 512 + P], scalar=c,
                                             in1=g.blk[:, :], op0=ALU.mult, op1=ALU.mult).then_inc(s_m, 1)
                dve.scalar_tensor_tensor(out=g.GS[:, q, :], in0=S[:, GRAM:GRAM + P], scalar=SECOND / N,
                                         in1=g.blk[:, :], op0=ALU.mult, op1=ALU.mult)
                dve.tensor_scalar(out=g.ks[:, q:q + 1], in0=S[:, GRAM + P:GRAM + P + 1],
                                  scalar1=float(HD) ** 0.5 / N, scalar2=None, op0=ALU.mult)
                dve.tensor_scalar(out=g.vs[:, q:q + 1], in0=S[:, LAST + P:LAST + P + 1], scalar1=float(HD) / N,
                                  scalar2=None, op0=ALU.mult).then_inc(s_out, 1)

            @block.tensor
            def _(pe):
                pe.sem_inc(s_acc, 2)

                def zero(start, stop):
                    for b in range(5):
                        last = pe.matmul(acc[:, b * 512:(b + 1) * 512], g.zrow[0:1, 0:P], g.zrow[0:1, :],
                                         start=start, stop=stop)
                    return last

                def pair(i, turn):
                    for u in (0, 1):
                        pe.wait_ge(s_z, done(i * 2 + u))
                        for b in range(6):
                            if b < 5:
                                z0, z1 = b * 512, min(b * 512 + 512, ZW)
                                last = pe.matmul(acc[:, z0:z1], KV[:, u, 1, :], Z[:, u, z0:z1], start=False, stop=False)
                            else:
                                last = pe.matmul(acc[:, GRAM:GRAM + P + 1], KV[:, u, 0, :], Z[:, u, LAST:LAST + P + 1],
                                                 start=False, stop=False)
                                last.then_inc(s_acc, 1)
                            if turn is not None:
                                at = u * 6 + b
                                graph.tensor_steps(pe, turn, at * U // 12, (at + 1) * U // 12)

                zero(True, False).then_inc(s_zero, 1)
                over_pairs(pe, q, pair)
                zero(False, True).then_inc(s_zero, 1)
                pe.wait_ge(s_out, 1)
                for f in range(PAIRS + 1):
                    if f >= 2:
                        pe.wait_ge(s_m, f - 1)
                    pe.transpose(acc[:, f % 2 * 512:f % 2 * 512 + P], S[:, f * P:(f + 1) * P], g.ident[:, :]).then_inc(s_tp, 1)


def queries0_phase(nc, g, graph, w):
    names = ["s_go", "s_turn", "s_z", "s_zr", "s_u", "s_t", "s_d", "s_d2", "s_rec", "s_ot", "s_pp", "s_add"]
    with phase(nc, names, ["s_w", "s_l0", "s_l1"]) as (held, sems):
        s_go, s_turn, s_z, s_zr, s_u, s_t, s_d, s_d2, s_rec, s_ot, s_pp, s_add, s_w, s_l0, s_l1 = sems
        s_l = (s_l0, s_l1)

        def sb(name, shape, dt=F32):
            return held.enter_context(nc.sbuf_tensor(own(nc, name), shape, dt))

        M = 2 * P
        FIRST = T // 2 + LEFT
        WP = sb("w_proj", [P, 2, D])
        R = sb("turned", [P, 2, len(TURNED), M])
        Z = sb("z", [P, PAIRS, M])
        TT = sb("t", [P, 2, M])
        DE = sb("den", [P, 2, M])
        OT = TT
        py = held.enter_context(nc.psum_tensor(own(nc, "py"), [P, 2, 512], F32))
        pu = held.enter_context(nc.psum_tensor(own(nc, "pu"), [P, 2, 512], F32))
        pp = held.enter_context(nc.psum_tensor(own(nc, "pp"), [P, 512], F32))
        CHUNKS = [(0, 5), (5, 9), (9, 13), (13, 17)]

        def pd(q):
            return cut(pu, q * 512 + M, [1, M])

        def chunk(n, c):
            return n * 4 + c + 9
        with nc.Block() as block:
            @block.sync
            def _(sp):
                for s in s_l:
                    sp.sem_inc(s, 16)
                sp.dma_start(WP[:, :, :], w.L0_mix_Wproj.rearrange("(c p) o -> p c o", p=P)).then_inc(s_w, 16)
                with sp.Fori(0, T // 2) as i:
                    for q in (0, 1):
                        n = i * 2 + q
                        graph.sync_half(sp, i + FIRST, q)
                        sp.wait_ge(s_t, done(n - 2))
                        sp.wait_ge(s_zr, chunk(n - 2, 3))
                        sp.wait_ge(s_z, chunk(n - 2, 3))
                        sp.dma_start(R[:, q, 0, :], flat(g.qT, q * P * NP + i * M, [NP, P], [1, M])).then_inc(s_l[q], 16)

            @block.vector
            def _(dve):
                for s in (s_turn, s_t, s_d2, s_rec, s_ot, s_add):
                    dve.sem_inc(s, 2)
                dve.sem_inc(s_z, 8)

                def turned(i, q):
                    dve.wait_ge(s_l[q], landed(i))
                    dve.sem_inc(s_go, 1)
                    for k, r in enumerate(TURNED[1:]):
                        last = dve.stream_shuffle(out=R[:, q, k + 1, :], in_=R[:, q, 0, :],
                                                  mask=[(j + r) % HD for j in range(HD)])
                    last.then_inc(s_turn, 1)

                def pairs(i, q):
                    n = i * 2 + q
                    dve.wait_ge(s_turn, done(n))
                    for k in range(4):
                        dve.wait_ge(s_zr, chunk(n - 1, k))
                        if k == 0:
                            dve.tensor_tensor(out=Z[:, 0, :], in0=R[:, q, 0, :], in1=R[:, q, 0, :], op=ALU.mult)
                        dve.tensor_tensor(out=Z[:, 1 + 4 * k:5 + 4 * k, :], in0=R[:, q, 0:4, :],
                                          in1=cut(R, (q * 8 + 4 + k) * M, [0, 4], [1, M]),
                                          op=ALU.mult).then_inc(s_z, 1)
                    dve.wait_ge(s_u, done(n))
                    dve.wait_ge(s_pp, i + 1)
                    dve.scalar_tensor_tensor(out=TT[:, q, :], in0=pu[:, q, 0:M], scalar=g.ks[:, q:q + 1],
                                             in1=R[:, q, 0, :], op0=ALU.add, op1=ALU.mult).then_inc(s_t, 1)

                def divide(i):
                    for q in (0, 1):
                        n = i * 2 + q
                        dve.wait_ge(s_d, done(n))
                        dve.tensor_scalar(out=DE[:, q, :], in0=pd(q), scalar1=float(HD), scalar2=None,
                                          op0=ALU.add).then_inc(s_d2, 1)
                    for q in (0, 1):
                        n = i * 2 + q
                        dve.wait_ge(s_d2, done(n))
                        dve.reciprocal(DE[:, q, :], DE[:, q, :]).then_inc(s_rec, 1)
                    for q in (0, 1):
                        n = i * 2 + q
                        dve.wait_ge(s_rec, done(n))
                        dve.wait_ge(s_zr, chunk(n, 3))
                        dve.scalar_tensor_tensor(out=OT[:, q, :], in0=py[:, q, 0:M], scalar=g.vs[:, q:q + 1],
                                                 in1=DE[:, q, :], op0=ALU.add, op1=ALU.mult).then_inc(s_ot, 1)

                def add(i):
                    dve.wait_ge(s_pp, i + 2)
                    x = cut(g.X, i * 2 * D, [1, 2 * D])
                    dve.tensor_tensor(out=x, in0=pp[:, :], in1=x, op=ALU.add).then_inc(s_add, 1)

                def pair(i, before):
                    graph.vector_half(dve, i + FIRST, 0)
                    turned(i, 0)
                    if before:
                        divide(i - 1)
                    pairs(i, 0)
                    if before:
                        add(i - 1)
                    graph.vector_half(dve, i + FIRST, 1)
                    turned(i, 1)
                    pairs(i, 1)

                pair(0, False)
                with dve.Fori(1, T // 2) as i:
                    pair(i, True)
                divide(T // 2 - 1)
                add(T // 2 - 1)
                dve.wait_ge(s_add, 2 + T // 2)

            @block.scalar
            def _(act):
                with act.Fori(0, T // 2) as i:
                    graph.scalar_steps(act, i + FIRST, 0, U)

            @block.gpsimd
            def _(pool):
                with pool.Fori(0, T // 2) as i:
                    for h in (0, 1):
                        graph.pool_half(pool, i + FIRST, h)

            @block.tensor
            def _(pe):
                for s in (s_u, s_d):
                    pe.sem_inc(s, 2)
                pe.sem_inc(s_pp, 1)
                pe.sem_inc(s_zr, 8)
                pe.wait_ge(s_w, 16)

                def heads(i):
                    for q in (0, 1):
                        pe.wait_ge(s_t, done(i * 2 + q))
                        pe.matmul(pd(q), g.blk[:, :], TT[:, q, :], start=True, stop=True).then_inc(s_d, 1)

                def project(i):
                    pe.wait_ge(s_ot, done(i * 2 + 1))
                    pe.wait_ge(s_add, i + 2)
                    for t in (0, 1):
                        for q in (0, 1):
                            last = pe.matmul(pp[:, t * D:(t + 1) * D], OT[:, q, t * P:(t + 1) * P], WP[:, q, :],
                                             start=q == 0, stop=q == 1)
                    last.then_inc(s_pp, 1)

                def group(i, q, at):
                    n = i * 2 + q
                    pe.wait_ge(s_l[q], landed(i))
                    pe.wait_ge(s_d2, done(n - 2))
                    pe.matmul(pu[:, q, 0:M], g.GS[:, q, :], R[:, q, 0, :], start=True, stop=True).then_inc(s_u, 1)
                    pe.wait_ge(s_ot, done(n - 2))
                    pe.matmul(py[:, q, 0:M], g.WS[:, q, PAIRS, :], R[:, q, 0, :], start=True, stop=False)
                    for c, (f0, f1) in enumerate(CHUNKS):
                        pe.wait_ge(s_z, chunk(n, c))
                        for f in range(f0, f1):
                            last = pe.matmul(py[:, q, 0:M], g.WS[:, q, f, :], Z[:, f, :], start=False,
                                             stop=f == PAIRS - 1)
                        last.then_inc(s_zr, 1)
                        graph.tensor_steps(pe, i + FIRST, at + c, at + c + 1)

                def pair(i, before):
                    if before:
                        heads(i - 1)
                    graph.tensor_steps(pe, i + FIRST, 0, 5)
                    if before:
                        project(i - 1)
                    group(i, 0, 5)
                    graph.tensor_steps(pe, i + FIRST, 9, 12)
                    group(i, 1, 12)

                pair(0, False)
                with pe.Fori(1, T // 2) as i:
                    pair(i, True)
                heads(T // 2 - 1)
                project(T // 2 - 1)

SCOLS = SROWS // P


def steps_phase(nc, g):
    names = ["s_iota", "s_row", "s_bc", "s_sb", "s_k", "s_tk", "s_gf", "s_tp", "s_out", "s_fin"]
    with phase(nc, names, ["s_in", "s_st", "s_w"]) as (held, sems):
        s_iota, s_row, s_bc, s_sb, s_k, s_tk, s_gf, s_tp, s_out, s_fin, s_in, s_st, s_w = sems
        s_g, = pool_sems(nc, ["s_g"])

        def sb(name, shape, dt=F32):
            return held.enter_context(nc.sbuf_tensor(own(nc, name), shape, dt))

        lrow = sb("last_dst", [1, ET], I32)
        trow = sb("tile_no", [1, ET], I32)
        wrow = sb("last_win", [1, ET], I32)
        wf = sb("win_f", [1, ET])
        tf = sb("tile_f", [1, ET])
        srow = sb("s_sum", [1, ET])
        sall = sb("s_all", [P, ET])
        junk = sb("junk", [P, ET])
        ki = sb("k_i", [P, SCOLS], I32)
        kf = sb("k_f", [P, SCOLS])
        tk = sb("t_k", [P, SCOLS])
        tki = g.tki
        wk = sb("w_k", [P, SCOLS])
        wki = sb("w_ki", [P, SCOLS], I32)
        wb = sb("w_base", [P, SCOLS])
        gd = sb("g_dst", [P, SCOLS, P], I32)
        gs = sb("g_src", [P, SCOLS, P], I32)
        rf = sb("rel_f", [P, SCOLS, P])
        sf = sb("src_f", [P, SCOLS, P])
        pb = held.enter_context(nc.psum_tensor(own(nc, "pb"), [P, 1024], F32))
        tp = held.enter_context(nc.psum_tensor(own(nc, "tp"), [P, 2, 512], F32))
        with nc.Block() as block:
            @block.sync
            def _(sp):
                sp.dma_start(lrow[:, :], flat(g.edst, P - 1, [ET, 1], [P, ET]),
                             allow_slow_non_contiguous=True).then_inc(s_in, 16)
                sp.wait_ge(s_gf, 1)
                sp.dma_start(flat(g.srows, 0, [P, P], [P * P, SCOLS], [1, P]), sf[:, :, :]).then_inc(s_st, 16)
                sp.dma_start(flat(g.wsteps, 0, [1, P], [P, SCOLS]), wki[:, :],
                             allow_slow_non_contiguous=True).then_inc(s_w, 16)
                sp.wait_ge(s_w, 16)
                sp.dma_start(g.wrow[:, :], flat(g.wsteps, 0, [SROWS, 1], [1, SROWS])).then_inc(s_w, 16)
                sp.wait_ge(s_w, 32)
                sp.wait_ge(s_st, 16)

            @block.gpsimd
            def _(pool):
                pool.iota(trow[:, :], pattern=[[1, ET]], base=0, channel_multiplier=0).then_inc(s_iota, 1)
                pool.iota(ki[:, :], pattern=[[P, SCOLS]], base=0, channel_multiplier=1).then_inc(s_iota, 1)
                pool.wait_ge(s_tk, 1)
                for c in range(SCOLS):
                    for to, of in ((gd, g.edst), (gs, g.esrc)):
                        pool.indirect_dma_start(
                            out=to[:, c, :], out_offset=None, in_=flat(of, 0, [P, ET], [1, P]),
                            in_offset=bass.IndirectOffsetOnAxis(ap=tki[:, c:c + 1], axis=0)).then_inc(s_g, 16)
                pool.wait_ge(s_g, 32 * SCOLS)

            @block.vector
            def _(dve):
                dve.wait_ge(s_in, 16)
                dve.tensor_scalar(out=wrow[:, :], in0=lrow[:, :], scalar1=7, scalar2=None,
                                  op0=ALU.logical_shift_right).then_inc(s_row, 1)
                dve.wait_ge(s_iota, 2)
                dve.tensor_copy(tf[:, :], trow[:, :])
                dve.tensor_copy(kf[:, :], ki[:, :]).then_inc(s_k, 1)
                dve.wait_ge(s_row, 1)
                dve.tensor_copy(wf[:, :], wrow[:, :]).then_inc(s_row, 1)
                dve.wait_ge(s_row, 2)
                dve.tensor_tensor(out=srow[:, :], in0=wf[:, :], in1=tf[:, :], op=ALU.add).then_inc(s_row, 1)
                dve.wait_ge(s_bc, 1)
                dve.tensor_copy(sall[:, :], pb[:, 0:ET]).then_inc(s_sb, 1)
                dve.wait_ge(s_sb, 1)
                for c in range(SCOLS):
                    if c:
                        dve.wait_ge(s_k, c + 1)
                    dve.tensor_scalar(out=junk[:, :], in0=sall[:, :], scalar1=kf[:, c:c + 1], scalar2=0.0,
                                      op0=ALU.is_lt, op1=ALU.add, accum_out=tk[:, c:c + 1]).then_inc(s_k, 1)
                dve.wait_ge(s_k, SCOLS + 1)
                dve.tensor_scalar(out=tk[:, :], in0=tk[:, :], scalar1=float(ET - 1), scalar2=None,
                                  op0=ALU.min).then_inc(s_k, 1)
                dve.wait_ge(s_k, SCOLS + 2)
                dve.tensor_tensor(out=wk[:, :], in0=kf[:, :], in1=tk[:, :], op=ALU.subtract).then_inc(s_k, 1)
                dve.tensor_copy(tki[:, :], tk[:, :]).then_inc(s_tk, 1)
                dve.wait_ge(s_k, SCOLS + 3)
                dve.tensor_copy(wki[:, :], wk[:, :])
                dve.tensor_scalar(out=wb[:, :], in0=wk[:, :], scalar1=float(P), scalar2=None,
                                  op0=ALU.mult).then_inc(s_k, 1)
                dve.wait_ge(s_k, SCOLS + 4)
                dve.wait_ge(s_g, 32 * SCOLS)
                for c in range(SCOLS):
                    dve.tensor_scalar(out=rf[:, c, :], in0=gd[:, c, :], scalar1=wb[:, c:c + 1], scalar2=None,
                                      op0=ALU.subtract)
                dve.tensor_copy(sf[:, :, :], gs[:, :, :]).then_inc(s_gf, 1)
                for c in range(SCOLS):
                    for k, to in enumerate((g.rel, g.src)):
                        dve.wait_ge(s_tp, 2 * c + k + 1)
                        dve.tensor_copy(to[:, c * P:(c + 1) * P], tp[:, k, 0:P]).then_inc(s_out, 1)
                dve.wait_ge(s_out, 2 * SCOLS)
                dve.tensor_copy(g.srci[:, :], g.src[:, :]).then_inc(s_fin, 1)
                dve.wait_ge(s_fin, 1)

            @block.tensor
            def _(pe):
                pe.wait_ge(s_row, 3)
                pe.matmul(pb[:, 0:512], g.ones[0:1, :], srow[0:1, 0:512], start=True, stop=True)
                pe.matmul(pb[:, 512:ET], g.ones[0:1, :], srow[0:1, 512:ET], start=True, stop=True).then_inc(s_bc, 1)
                pe.wait_ge(s_gf, 1)
                for c in range(SCOLS):
                    for k, of in enumerate((rf, sf)):
                        if c:
                            pe.wait_ge(s_out, 2 * c + k - 1)
                        pe.transpose(tp[:, k, 0:P], of[:, c, :], g.ident[:, :]).then_inc(s_tp, 1)

RING = 4


def join_phase(nc, g, w, layer, cfg):
    names = ["s_go", "s_a", "s_b", "s_cnt", "s_rec", "s_mn", "s_tp", "s_mt", "s_mm", "s_add", "s_st", "s_mv", "s_sd",
             "s_rs", "s_xs", "s_keep", "s_xtp", "s_xt", "s_lp", "s_lg", "s_mx", "s_ix", "s_ef", "s_oh",
             "s_e", "s_ex", "s_sum", "s_ri"]
    with phase(nc, names, ["s_w", "s_l0", "s_l1"]) as (held, sems):
        (s_go, s_a, s_b, s_cnt, s_rec, s_mn, s_tp, s_mt, s_mm, s_add, s_st, s_mv, s_sd, s_rs, s_xs, s_keep, s_xtp,
         s_xt, s_lp, s_lg, s_mx, s_ix, s_ef, s_oh, s_e, s_ex, s_sum, s_ri, s_w, s_l0, s_l1) = sems
        s_l = (s_l0, s_l1)

        def sb(name, shape, dt=F32):
            return held.enter_context(nc.sbuf_tensor(own(nc, name), shape, dt))

        NE, TOP = cfg.experts, cfg.top
        WR = sb("w_router", [P, 2, NE])
        BR = sb("b_router", [P, NE])
        if layer == 0:
            W2 = sb("w_nbr", [P, 2, D])
            AG = sb("agg_in", [P, 2, AGGS, GW])
            A2 = sb("agg_2", [P, 2, 2, GW])
            A1 = sb("agg_1", [P, 2, GW])
            MT = sb("mean_t", [P, 2, D])
        CN = sb("cnt", [P, 2, H])
        RC = sb("rcnt", [P, 2, H])
        MN = sb("mean", [P, 2, D])
        ST = sb("st", [P, 2, 6])
        MV = sb("mv", [P, 2, 2])
        SD = sb("sd", [P, 2, 1])
        RS = sb("rs", [P, 2, 1])
        XS = sb("xs", [P, 2, D])
        XT = sb("xt", [P, 2, D])
        LG = sb("logits", [P, 2, NE])
        MX = sb("max8", [P, 2, 8])
        MI = sb("max_i", [P, 2, 8], U32)
        EX = sb("exps", [P, 2, NE])
        SU = sb("sum", [P, 2, 1])
        RI = sb("rsum", [P, 2, 1])
        NX = sb("neg_max", [P, 2, 1])
        pt = held.enter_context(nc.psum_tensor(own(nc, "pt"), [P, 2, 512], F32))
        pm = held.enter_context(nc.psum_tensor(own(nc, "pm"), [P, 2, 512], F32))
        px = held.enter_context(nc.psum_tensor(own(nc, "px"), [P, 2, 512], F32))
        pl = held.enter_context(nc.psum_tensor(own(nc, "pl"), [P, 2, 512], F32))
        NWT = 16 * (3 if layer == 0 else 2)
        router_w, router_b = (w.L0_ffn_router_w, w.L0_ffn_router_b) if layer == 0 else (w.L1_ffn_gate_w, w.L1_ffn_gate_b)
        with nc.Block() as block:
            @block.sync
            def _(sp):
                sp.dma_start(WR[:, :, :], router_w.rearrange("(c p) o -> p c o", p=P)).then_inc(s_w, 16)
                sp.dma_start(BR[:, :], router_b.partition_broadcast(P)).then_inc(s_w, 16)
                if layer == 0:
                    sp.dma_start(W2[:, :, :], w.L0_gnn_W2.rearrange("(c p) o -> p c o", p=P)).then_inc(s_w, 16)
                    for s in s_l:
                        sp.sem_inc(s, 16 * AGGS)
                    with sp.Fori(0, T // 2) as i:
                        for u in (0, 1):
                            n = i * 2 + u
                            sp.wait_ge(s_a, done(n - 2))
                            for a in range(AGGS):
                                sp.dma_start(AG[:, u, a, :], flat(g.agg[a], n * (P * GW), [GW, P], [1, GW])
                                             ).then_inc(s_l[u], 16)

            @block.vector
            def _(dve):
                for s in (s_a, s_b, s_cnt, s_rec, s_mn, s_add, s_st, s_mv, s_rs, s_xs, s_lg, s_mx, s_ix, s_ef, s_oh, s_e,
                          s_ri):
                    dve.sem_inc(s, 2)
                dve.wait_ge(s_w, NWT)
                with dve.Fori(0, T // 2) as i:
                    if layer == 0:
                        for u in (0, 1):
                            n = i * 2 + u
                            dve.wait_ge(s_l[u], landed(i, AGGS))
                            dve.tensor_tensor(out=A2[:, u, :, :], in0=AG[:, u, 0:2, :], in1=AG[:, u, 2:4, :],
                                              op=ALU.add).then_inc(s_a, 1)
                        for u in (0, 1):
                            n = i * 2 + u
                            dve.wait_ge(s_a, done(n))
                            dve.tensor_tensor(out=A1[:, u, :], in0=A2[:, u, 0, :], in1=A2[:, u, 1, :],
                                              op=ALU.add).then_inc(s_b, 1)
                    for u in (0, 1):
                        n = i * 2 + u
                        if layer == 0:
                            dve.wait_ge(s_b, done(n))
                            dve.tensor_scalar(out=CN[:, u, 0:1], in0=A1[:, u, D:D + 1], scalar1=1.0, scalar2=None,
                                              op0=ALU.max).then_inc(s_cnt, 1)
                        else:
                            dve.tensor_scalar(out=CN[:, u, :], in0=cut(g.XN, n * AW + HD, [HW1, H]), scalar1=1e-16,
                                              scalar2=None, op0=ALU.add).then_inc(s_cnt, 1)
                    for u in (0, 1):
                        n = i * 2 + u
                        dve.wait_ge(s_cnt, done(n))
                        k = 1 if layer == 0 else H
                        dve.reciprocal(RC[:, u, 0:k], CN[:, u, 0:k]).then_inc(s_rec, 1)
                    for u in (0, 1):
                        n = i * 2 + u
                        dve.wait_ge(s_rec, done(n))
                        if layer == 0:
                            dve.wait_ge(s_tp, done(n - 2))
                            dve.tensor_scalar(out=MN[:, u, :], in0=A1[:, u, 0:D], scalar1=RC[:, u, 0:1], scalar2=None,
                                              op0=ALU.mult).then_inc(s_mn, 1)
                        else:
                            dve.tensor_tensor(out=MN[:, u, :].rearrange("p (h d) -> p h d", d=HD),
                                              in0=cut(g.XN, n * AW, [HW1, H], [1, HD]),
                                              in1=cut(RC, u * H, [1, H], [0, HD]), op=ALU.mult).then_inc(s_mn, 1)
                    for u in (0, 1):
                        n = i * 2 + u
                        if layer == 0:
                            dve.wait_ge(s_mm, done(n))
                            more = pm[:, u, 0:D]
                        else:
                            dve.wait_ge(s_mn, done(n))
                            more = MN[:, u, :]
                        dve.tensor_tensor(out=cut(g.X, n * D, [1, D]), in0=more, in1=cut(g.X, n * D, [1, D]),
                                          op=ALU.add).then_inc(s_add, 1)
                    for u in (0, 1):
                        n = i * 2 + u
                        dve.wait_ge(s_add, done(n))
                        dve.sem_inc(s_go, 1)
                        dve.bn_stats(out=ST[:, u, :], in_=cut(g.X, n * D, [1, D])).then_inc(s_st, 1)
                    for u in (0, 1):
                        n = i * 2 + u
                        dve.wait_ge(s_st, done(n))
                        dve.sem_inc(s_go, 1)
                        dve.bn_aggr(out=MV[:, u, :], in_=ST[:, u, :]).then_inc(s_mv, 1)
                    for u in (0, 1):
                        n = i * 2 + u
                        dve.wait_ge(s_sd, done(n))
                        dve.reciprocal(RS[:, u, :], SD[:, u, :]).then_inc(s_rs, 1)
                    for u in (0, 1):
                        n = i * 2 + u
                        dve.wait_ge(s_rs, done(n))
                        dve.wait_ge(s_keep, done(n - 2))
                        dve.wait_ge(s_xtp, done(n - 2))
                        dve.tensor_scalar(out=XS[:, u, :], in0=cut(g.X, n * D, [1, D]), scalar1=MV[:, u, 0:1],
                                          scalar2=RS[:, u, 0:1], op0=ALU.subtract, op1=ALU.mult).then_inc(s_xs, 1)
                    for u in (0, 1):
                        n = i * 2 + u
                        dve.wait_ge(s_lp, done(n))
                        dve.tensor_tensor(out=LG[:, u, :], in0=pl[:, u, 0:NE], in1=BR[:, :], op=ALU.add).then_inc(s_lg, 1)
                    values = LG
                    if layer:
                        for u in (0, 1):
                            n = i * 2 + u
                            dve.wait_ge(s_lg, done(n))
                            dve.tensor_reduce(out=NX[:, u, :], in_=LG[:, u, :], axis=AX.X, op=ALU.max,
                                              negate=True).then_inc(s_e, 1)
                        for u in (0, 1):
                            n = i * 2 + u
                            dve.wait_ge(s_ex, done(n))
                            dve.reciprocal(RI[:, u, :], SU[:, u, :]).then_inc(s_ri, 1)
                        for u in (0, 1):
                            n = i * 2 + u
                            dve.wait_ge(s_ri, done(n))
                            dve.tensor_scalar(out=LG[:, u, :], in0=EX[:, u, :], scalar1=RI[:, u, 0:1], scalar2=None,
                                              op0=ALU.mult).then_inc(s_sum, 1)
                    for u in (0, 1):
                        n = i * 2 + u
                        if layer:
                            dve.wait_ge(s_sum, n + 1)
                        else:
                            dve.wait_ge(s_lg, done(n))
                        dve.sem_inc(s_go, 1)
                        dve.max(MX[:, u, :], values[:, u, :]).then_inc(s_mx, 1)
                    for u in (0, 1):
                        n = i * 2 + u
                        dve.wait_ge(s_mx, done(n))
                        dve.sem_inc(s_go, 1)
                        dve.max_index(MI[:, u, :], MX[:, u, :], values[:, u, :]).then_inc(s_ix, 1)
                    for u in (0, 1):
                        n = i * 2 + u
                        dve.wait_ge(s_ix, done(n))
                        if layer:
                            dve.tensor_copy(cut(g.cw, n, [T, TOP]), MX[:, u, 0:TOP])
                        dve.tensor_copy(cut(g.eidx, n, [T, TOP]), MI[:, u, 0:TOP]).then_inc(s_ef, 1)
                    for u in (0, 1):
                        n = i * 2 + u
                        dve.wait_ge(s_ef, done(n))
                        for k in range(TOP):
                            last = dve.tensor_scalar(out=cut(g.choice, (k * T + n) * NE, [1, NE]), in0=g.iota[:, 0:NE],
                                                     scalar1=cut(g.eidx, k * T + n, [1, 1]), scalar2=None,
                                                     op0=ALU.is_equal)
                        last.then_inc(s_oh, 1)
                dve.wait_ge(s_oh, done(T - 1))

            @block.scalar
            def _(act):
                for s in (s_mt, s_sd, s_xt, s_ex):
                    act.sem_inc(s, 2)
                with act.Fori(0, T // 2) as i:
                    if layer == 0:
                        for u in (0, 1):
                            n = i * 2 + u
                            act.wait_ge(s_tp, done(n))
                            act.activation(MT[:, u, :], pt[:, u, 0:D], ACT.Copy).then_inc(s_mt, 1)
                    for u in (0, 1):
                        n = i * 2 + u
                        act.wait_ge(s_mv, done(n))
                        act.activation(SD[:, u, :], MV[:, u, 1:2], ACT.Sqrt, bias=g.eps[:, 0:1]).then_inc(s_sd, 1)
                    for u in (0, 1):
                        n = i * 2 + u
                        act.wait_ge(s_xtp, done(n))
                        act.activation(XT[:, u, :], px[:, u, 0:D], ACT.Copy).then_inc(s_xt, 1)
                    if layer:
                        for u in (0, 1):
                            n = i * 2 + u
                            act.wait_ge(s_e, done(n))
                            act.activation(EX[:, u, :], LG[:, u, :], ACT.Exp, bias=NX[:, u, 0:1],
                                           accum_out=SU[:, u, :]).then_inc(s_ex, 1)

            @block.gpsimd
            def _(pool):
                pool.sem_inc(s_keep, 2)
                with pool.Fori(0, T // 2) as i:
                    for u in (0, 1):
                        n = i * 2 + u
                        pool.wait_ge(s_xs, done(n))
                        if layer:
                            pool.wait_ge(s_mn, done(n))
                        pool.tensor_copy(cut(g.XN, n * (AW if layer else GW), [1, D]), XS[:, u, :]).then_inc(s_keep, 1)
                pool.wait_ge(s_keep, done(T - 1))

            @block.tensor
            def _(pe):
                for s in (s_tp, s_mm, s_xtp, s_lp):
                    pe.sem_inc(s, 2)
                pe.wait_ge(s_w, NWT)
                with pe.Fori(0, T // 2) as i:
                    if layer == 0:
                        for u in (0, 1):
                            n = i * 2 + u
                            pe.wait_ge(s_mn, done(n))
                            pe.wait_ge(s_mt, done(n - 2))
                            for c in (0, 1):
                                last = pe.transpose(pt[:, u, c * P:(c + 1) * P], MN[:, u, c * P:(c + 1) * P],
                                                    g.ident[:, :])
                            last.then_inc(s_tp, 1)
                        for u in (0, 1):
                            n = i * 2 + u
                            pe.wait_ge(s_mt, done(n))
                            pe.wait_ge(s_add, done(n - 2))
                            for c in (0, 1):
                                last = pe.matmul(pm[:, u, 0:D], MT[:, u, c * P:(c + 1) * P], W2[:, c, :],
                                                 start=c == 0, stop=c == 1)
                            last.then_inc(s_mm, 1)
                    for u in (0, 1):
                        n = i * 2 + u
                        pe.wait_ge(s_xs, done(n))
                        pe.wait_ge(s_xt, done(n - 2))
                        for c in (0, 1):
                            last = pe.transpose(px[:, u, c * P:(c + 1) * P], XS[:, u, c * P:(c + 1) * P], g.ident[:, :])
                        last.then_inc(s_xtp, 1)
                    for u in (0, 1):
                        n = i * 2 + u
                        pe.wait_ge(s_xt, done(n))
                        pe.wait_ge(s_lg, done(n - 2))
                        for c in (0, 1):
                            last = pe.matmul(pl[:, u, 0:NE], XT[:, u, c * P:(c + 1) * P], WR[:, c, :],
                                             start=c == 0, stop=c == 1)
                        last.then_inc(s_lp, 1)


def sort_phase(nc, g, layer, cfg):
    names = ["s_up", "s_pw", "s_cn", "s_inc", "s_exc", "s_a", "s_b", "s_pos", "s_row", "s_cmp", "s_le", "s_s",
             "s_tk", "s_ek", "s_er", "s_ei", "s_z"]
    with phase(nc, names, ["s_zero"]) as (held, sems):
        (s_up, s_pw, s_cn, s_inc, s_exc, s_a, s_b, s_pos, s_row, s_cmp, s_le, s_s, s_tk, s_ek, s_er, s_ei, s_z,
         s_zero) = sems
        s_sc, = pool_sems(nc, ["s_sc"])

        def sb(name, shape, dt=F32):
            return held.enter_context(nc.sbuf_tensor(own(nc, name), shape, dt))

        NE, TOP, STEPS_E = cfg.experts, cfg.top, cfg.steps
        J = TOP * T
        C = J * NE
        up = sb("before", [P, P], BF16)
        one = sb("one_bf", [P, P], BF16)
        CN = sb("counts", [P, C])
        INC = sb("inclusive", [P, C])
        A = sb("a", [P, C])
        Bf = sb("b", [P, C])
        zero = sb("zero_c", [P, C])
        POS = sb("pos", [P, J])
        LAST = sb("last_i", [P, J], I32)
        LASTF = sb("last_f", [P, J])
        LE = sb("le", [P, J])
        JN = sb("j_no", [P, J], I32)
        JF = sb("j_f", [P, J])
        junk = sb("junk", [P, J])
        TK = sb("tk", [P, 1])
        EK = sb("ek", [P, 1])
        pw = held.enter_context(nc.psum_tensor(own(nc, "pw"), [P, 2048], F32))
        pc = held.enter_context(nc.psum_tensor(own(nc, "pc"), [P, 2048], F32))
        XROWS = g.XN
        RW = AW if layer else GW
        with nc.Block() as block:
            @block.sync
            def _(sp):
                sp.wait_ge(s_z, 1)
                for k in range(0, STEPS_E, 4):
                    m = min(4, STEPS_E - k)
                    sp.dma_start(flat(g.xe, k * P * D, [m * D, P], [1, m * D]), g.zeros[:, 0:m * D]).then_inc(s_zero, 16)
                sp.wait_ge(s_zero, 16 * -(-STEPS_E // 4))

            @block.gpsimd
            def _(pool):
                pool.iota(LAST[:, :], pattern=[[P, J]], base=P - 1, channel_multiplier=0).then_inc(s_up, 1)
                pool.iota(JN[:, :], pattern=[[1, J]], base=0, channel_multiplier=0).then_inc(s_up, 1)
                pool.wait_ge(s_row, 1)
                pool.wait_ge(s_zero, 16 * -(-STEPS_E // 4))
                for j in range(J):
                    pool.indirect_dma_start(
                        out=flat(g.xe, 0, [D, STEPS_E * P], [1, D]),
                        out_offset=bass.IndirectOffsetOnAxis(ap=g.rowi[:, j:j + 1], axis=0),
                        in_=cut(XROWS, (j % T) * RW, [1, D]), in_offset=None).then_inc(s_sc, 16)
                pool.wait_ge(s_sc, 16 * J)

            @block.vector
            def _(dve):
                dve.memset(g.zeros[:, :], 0.0).then_inc(s_z, 1)
                dve.memset(one[:, :], 1.0)
                dve.memset(zero[:, :], 0.0)
                dve.tensor_scalar(out=up[:, :], in0=g.iota[:, :], scalar1=g.pcol[:, 0:1], scalar2=None,
                                  op0=ALU.is_gt).then_inc(s_cn, 1)
                dve.wait_ge(s_up, 2)
                dve.tensor_copy(LASTF[:, :], LAST[:, :])
                dve.tensor_copy(JF[:, :], JN[:, :]).then_inc(s_s, 1)
                dve.wait_ge(s_pw, 2)
                dve.tensor_copy(cut(CN, 0, [1, J], [J, NE]), pc[:, 0:C].rearrange("p (j e) -> p j e", e=NE)
                                ).then_inc(s_cn, 1)
                dve.wait_ge(s_cn, 2)
                dve.tensor_tensor_scan(out=INC[:, :], data0=CN[:, :], data1=zero[:, :], initial=0.0, op0=ALU.add,
                                       op1=ALU.add).then_inc(s_inc, 1)
                dve.wait_ge(s_inc, 1)
                dve.tensor_tensor(out=CN[:, :], in0=INC[:, :], in1=CN[:, :], op=ALU.subtract).then_inc(s_exc, 1)
                dve.wait_ge(s_exc, 1)
                dve.tensor_tensor(out=A[:, :].rearrange("p (j e) -> p j e", e=NE),
                                  in0=pw[:, 0:C].rearrange("p (j e) -> p j e", e=NE),
                                  in1=cut(CN, 0, [1, J], [J, NE]), op=ALU.add).then_inc(s_a, 1)
                dve.wait_ge(s_a, 1)
                dve.tensor_tensor(out=Bf[:, :], in0=A[:, :], in1=g.choice[:, 0:C], op=ALU.mult).then_inc(s_b, 1)
                dve.wait_ge(s_b, 1)
                dve.tensor_reduce(out=POS[:, :], in_=Bf[:, :].rearrange("p (j e) -> p j e", e=NE), axis=AX.X,
                                  op=ALU.add).then_inc(s_pos, 1)
                dve.wait_ge(s_pos, 1)
                dve.scalar_tensor_tensor(out=g.rowi[:, 0:J], in0=g.eidx[:, 0:J], scalar=float(P), in1=POS[:, :],
                                         op0=ALU.mult, op1=ALU.add).then_inc(s_row, 1)
                dve.wait_ge(s_s, 1)
                dve.tensor_tensor(out=A[:, :].rearrange("p (j e) -> p j e", e=NE), in0=cut(INC, J - 1, [0, J], [J, NE]),
                                  in1=cut(LASTF, 0, [1, J], [0, NE]), op=ALU.is_le).then_inc(s_cmp, 1)
                dve.wait_ge(s_cmp, 1)
                dve.tensor_reduce(out=LE[:, :], in_=A[:, :].rearrange("p (j e) -> p j e", e=NE), axis=AX.X,
                                  op=ALU.add).then_inc(s_le, 1)
                dve.wait_ge(s_le, 1)
                dve.tensor_tensor(out=LE[:, :], in0=LE[:, :], in1=JF[:, :], op=ALU.add).then_inc(s_s, 1)
                dve.wait_ge(s_s, 2)
                dve.tensor_scalar(out=junk[:, :], in0=LE[:, :], scalar1=g.pcol[:, 0:1], scalar2=0.0, op0=ALU.is_lt,
                                  op1=ALU.add, accum_out=TK[:, :]).then_inc(s_tk, 1)
                dve.wait_ge(s_tk, 1)
                dve.tensor_scalar(out=TK[:, :], in0=TK[:, :], scalar1=float(J - 1), scalar2=None,
                                  op0=ALU.min).then_inc(s_tk, 1)
                dve.wait_ge(s_tk, 2)
                dve.tensor_tensor(out=EK[:, :], in0=g.pcol[:, :], in1=TK[:, :], op=ALU.subtract).then_inc(s_ek, 1)
                dve.wait_ge(s_ek, 1)
                dve.tensor_scalar(out=EK[:, :], in0=EK[:, :], scalar1=float(NE - 1), scalar2=None,
                                  op0=ALU.min).then_inc(s_ek, 1)
                dve.wait_ge(s_er, 1)
                dve.tensor_copy(g.erow[:, :], pc[0:1, 0:P]).then_inc(s_ei, 1)
                dve.wait_ge(s_ei, 1)

            @block.tensor
            def _(pe):
                pe.wait_ge(s_cn, 1)
                for lhs, to in ((up, pw), (one, pc)):
                    for a in range(0, C, 512):
                        b = min(a + 512, C)
                        last = pe.matmul(to[:, a:b], lhs[:, :], g.choice[:, a:b], start=True, stop=True)
                    last.then_inc(s_pw, 1)
                pe.wait_ge(s_ek, 2)
                pe.matmul(pc[0:1, 0:P], EK[:, :], g.ident[:, :], start=True, stop=True).then_inc(s_er, 1)


def experts_phase(nc, g, w, layer, cfg):
    names = ["s_go", "s_xp", "s_xt", "s_h", "s_hb", "s_ha", "s_hp", "s_ht", "s_y", "s_yo"]
    with phase(nc, names, ["s_w", "s_l0", "s_l1", "s_o0", "s_o1"]) as (held, sems):
        s_go, s_xp, s_xt, s_h, s_hb, s_ha, s_hp, s_ht, s_y, s_yo, s_w, s_l0, s_l1, s_o0, s_o1 = sems
        s_l, s_o = (s_l0, s_l1), (s_o0, s_o1)

        def sb(name, shape, dt=F32):
            return held.enter_context(nc.sbuf_tensor(own(nc, name), shape, dt))

        NE, HID, TURNS = cfg.experts, cfg.hidden, cfg.steps // 2
        HC = max(1, HID // P)
        HR = min(HID, P)
        W1 = 0
        B1 = 2 * NE * HID
        assert B1 + NE * HID <= T * GW
        W2 = sb("w2", [HR, HC, NE, D])
        B2 = sb("b2", [P, NE, D])
        XI = sb("xi", [P, 2, D])
        XT = sb("xt", [P, 2, D])
        HB = sb("hb", [P, 2, HID])
        HA = sb("ha", [P, 2, HID])
        HT = sb("ht", [HR, 2, HC * P])
        YO = sb("yo", [P, 2, D])
        px = held.enter_context(nc.psum_tensor(own(nc, "px"), [P, 2, 512], F32))
        ph = held.enter_context(nc.psum_tensor(own(nc, "ph"), [P, 2, 512], F32))
        pt = held.enter_context(nc.psum_tensor(own(nc, "pt"), [P, 2, 512], F32))
        py = held.enter_context(nc.psum_tensor(own(nc, "py"), [P, 2, 512], F32))
        w1, b1, w2, b2 = ((w.L0_ffn_W1, w.L0_ffn_b1, w.L0_ffn_W2, w.L0_ffn_b2) if layer == 0 else
                          (w.L1_ffn_W1, w.L1_ffn_b1, w.L1_ffn_W2, w.L1_ffn_b2))
        NWT = 16 * (4 + HC)
        with nc.Block() as block:
            @block.sync
            def _(sp):
                for s in (*s_l, *s_o):
                    sp.sem_inc(s, 16)
                for c in (0, 1):
                    sp.dma_start(cut(g.XN, W1 + c * NE * HID, [HID, NE], [1, HID]),
                                 w1[:, c * P:(c + 1) * P, :].rearrange("e p h -> p e h")).then_inc(s_w, 16)
                sp.dma_start(cut(g.XN, B1, [1, NE * HID]), b1.rearrange("e h -> (e h)").partition_broadcast(P)
                             ).then_inc(s_w, 16)
                for c in range(HC):
                    sp.dma_start(W2[:, c, :, :], w2[:, c * HR:(c + 1) * HR, :].rearrange("e p d -> p e d")
                                 ).then_inc(s_w, 16)
                sp.dma_start(B2[:, :, :].rearrange("p e d -> p (e d)"), b2.rearrange("e d -> (e d)").partition_broadcast(P)
                             ).then_inc(s_w, 16)

                def load(i):
                    for u in (0, 1):
                        k = i * 2 + u
                        sp.wait_ge(s_xp, done(k - 2))
                        sp.dma_start(XI[:, u, :], flat(g.xe, k * P * D, [D, P], [1, D])).then_inc(s_l[u], 16)

                def store(i):
                    for u in (0, 1):
                        k = i * 2 + u
                        sp.wait_ge(s_yo, done(k))
                        sp.dma_start(flat(g.ye, k * P * D, [D, P], [1, D]), YO[:, u, :]).then_inc(s_o[u], 16)

                load(0)
                load(1)
                with sp.Fori(1, TURNS - 1) as i:
                    load(i + 1)
                    store(i - 1)
                store(TURNS - 2)
                store(TURNS - 1)
                for s in s_o:
                    sp.wait_ge(s, landed(TURNS - 1))

            @block.scalar
            def _(act):
                act.sem_inc(s_ha, 2)
                with act.Fori(0, TURNS) as i:
                    for u in (0, 1):
                        k = i * 2 + u
                        act.wait_ge(s_hb, done(k))
                        act.wait_ge(s_hp, done(k - 2))
                        act.activation(HA[:, u, :], HB[:, u, :], ACT.Gelu if layer else ACT.Relu).then_inc(s_ha, 1)

            @block.vector
            def _(dve):
                for s in (s_xt, s_hb, s_ht, s_yo):
                    dve.sem_inc(s, 2)

                def hidden(i):
                    for u in (0, 1):
                        k = i * 2 + u
                        e = dve.value_load(g.erow[0:1, bass.ds(k, 1)], min_val=0, max_val=NE - 1)
                        dve.wait_ge(s_h, done(k))
                        dve.wait_ge(s_ha, done(k - 2))
                        dve.tensor_tensor(out=HB[:, u, :], in0=ph[:, u, 0:HID], in1=cut(g.XN, e * HID + B1, [1, HID]),
                                          op=ALU.add).then_inc(s_hb, 1)

                def inputs(i):
                    for u in (0, 1):
                        k = i * 2 + u
                        dve.wait_ge(s_xp, done(k))
                        dve.wait_ge(s_h, done(k - 2))
                        dve.tensor_copy(XT[:, u, :], px[:, u, 0:D]).then_inc(s_xt, 1)

                def outputs(i):
                    for u in (0, 1):
                        k = i * 2 + u
                        e = dve.value_load(g.erow[0:1, bass.ds(k, 1)], min_val=0, max_val=NE - 1)
                        dve.wait_ge(s_y, done(k))
                        dve.wait_ge(s_o[u], landed(i - 1))
                        dve.tensor_tensor(out=YO[:, u, :], in0=py[:, u, 0:D], in1=cut(B2, e * D, [1, D]),
                                          op=ALU.add).then_inc(s_yo, 1)

                def turned(i):
                    for u in (0, 1):
                        k = i * 2 + u
                        dve.wait_ge(s_hp, done(k))
                        dve.wait_ge(s_y, done(k - 2))
                        dve.tensor_copy(HT[:, u, :], pt[0:HR, u, 0:HC * P]).then_inc(s_ht, 1)

                inputs(0)
                dve.wait_ge(s_w, NWT)
                hidden(0)
                inputs(1)
                turned(0)
                with dve.Fori(1, TURNS - 1) as i:
                    hidden(i)
                    inputs(i + 1)
                    outputs(i - 1)
                    turned(i)
                hidden(TURNS - 1)
                outputs(TURNS - 2)
                turned(TURNS - 1)
                outputs(TURNS - 1)

            @block.tensor
            def _(pe):
                for s in (s_xp, s_h, s_hp, s_y):
                    pe.sem_inc(s, 2)

                def inputs(i):
                    for u in (0, 1):
                        k = i * 2 + u
                        pe.wait_ge(s_l[u], landed(i))
                        pe.wait_ge(s_xt, done(k - 2))
                        for c in (0, 1):
                            last = pe.transpose(px[:, u, c * P:(c + 1) * P], XI[:, u, c * P:(c + 1) * P], g.ident[:, :])
                        last.then_inc(s_xp, 1)

                def hidden(i):
                    for u in (0, 1):
                        k = i * 2 + u
                        e = pe.value_load(g.erow[0:1, bass.ds(k, 1)], min_val=0, max_val=NE - 1)
                        pe.wait_ge(s_xt, done(k))
                        pe.wait_ge(s_hb, done(k - 2))
                        for c in (0, 1):
                            last = pe.matmul(ph[:, u, 0:HID], XT[:, u, c * P:(c + 1) * P],
                                             cut(g.XN, e * HID + W1 + c * NE * HID, [1, HID]), start=c == 0, stop=c == 1)
                        last.then_inc(s_h, 1)

                def turned(i):
                    for u in (0, 1):
                        k = i * 2 + u
                        pe.wait_ge(s_ha, done(k))
                        pe.wait_ge(s_ht, done(k - 2))
                        pe.sem_inc(s_go, 1)
                        for c in range(HC):
                            last = pe.transpose(pt[0:HR, u, c * P:(c + 1) * P], HA[:, u, c * HR:(c + 1) * HR],
                                                g.ident[:, :])
                        last.then_inc(s_hp, 1)

                def outputs(i):
                    for u in (0, 1):
                        k = i * 2 + u
                        e = pe.value_load(g.erow[0:1, bass.ds(k, 1)], min_val=0, max_val=NE - 1)
                        pe.wait_ge(s_ht, done(k))
                        pe.wait_ge(s_yo, done(k - 2))
                        for c in range(HC):
                            last = pe.matmul(py[:, u, 0:D], HT[:, u, c * P:(c + 1) * P],
                                             cut(W2, e * D + c * NE * D, [1, D]), start=c == 0, stop=c == HC - 1)
                        last.then_inc(s_y, 1)

                inputs(0)
                pe.wait_ge(s_w, NWT)
                hidden(0)
                inputs(1)
                turned(0)
                with pe.Fori(1, TURNS - 1) as i:
                    hidden(i)
                    inputs(i + 1)
                    outputs(i - 1)
                    turned(i)
                hidden(TURNS - 1)
                outputs(TURNS - 2)
                turned(TURNS - 1)
                outputs(TURNS - 1)


def merge_phase(nc, g, layer, cfg, out):
    names = ["s_add"]
    with phase(nc, names, ["s_out"]) as (held, sems):
        s_add, s_out = sems
        s_g = pool_sems(nc, [f"s_g{r}" for r in range(RING)])
        Y = held.enter_context(nc.sbuf_tensor(own(nc, "y_in"), [P, RING, D], F32))
        J = cfg.top * T
        NE = cfg.experts
        OUT_T = 7
        with nc.Block() as block:
            @block.gpsimd
            def _(pool):
                for q in range(J):
                    if q >= RING:
                        pool.wait_ge(s_add, q - RING + 1)
                    j = (q % cfg.top) * T + q // cfg.top
                    pool.indirect_dma_start(
                        out=Y[:, q % RING, :], out_offset=None, in_=flat(g.ye, 0, [D, cfg.steps * P], [1, D]),
                        in_offset=bass.IndirectOffsetOnAxis(ap=g.rowi[:, j:j + 1], axis=0)).then_inc(s_g[q % RING], 16)

            @block.vector
            def _(dve):
                for q in range(J):
                    j = (q % cfg.top) * T + q // cfg.top
                    t = q // cfg.top
                    dve.wait_ge(s_g[q % RING], 16 * (q // RING + 1))
                    if q % cfg.top:
                        dve.wait_ge(s_add, q)
                    dve.scalar_tensor_tensor(out=g.X[:, t, :], in0=Y[:, q % RING, :],
                                             scalar=g.cw[:, j:j + 1] if layer else 0.0, in1=g.X[:, t, :],
                                             op0=ALU.mult if layer else ALU.max, op1=ALU.add).then_inc(s_add, 1)
                dve.wait_ge(s_add, J)

            if layer:
                @block.sync
                def _(sp):
                    stores = 0
                    for t in range(0, FULL, OUT_T):
                        m = min(OUT_T, FULL - t)
                        sp.wait_ge(s_add, cfg.top * (t + m))
                        sp.dma_start(out[t * P:(t + m) * P, :].rearrange("(t p) d -> p t d", p=P),
                                     g.X[:, t:t + m, :]).then_inc(s_out, 16)
                        stores += 1
                    sp.wait_ge(s_add, cfg.top * (FULL + 1))
                    sp.dma_start(out[FULL * P:N, :], g.X[0:REST, FULL, :]).then_inc(s_out, 16)
                    sp.wait_ge(s_out, 16 * (stores + 1))

HW1 = HD + 1
PC = EP // P
DIV_EPS, NORM_EPS = 1e-7, 1e-12


def project1_phase(nc, g, w):
    names = ["s_go", "s_pre", "s_prep", "s_fold", "s_bias", "s_st", "s_mv", "s_sd", "s_rs", "s_xs", "s_xtp", "s_xt",
             "s_pp", "s_pj", "s_as", "s_red", "s_root", "s_keep"]
    with phase(nc, names, ["s_w", "s_t0", "s_t1", "s_p0", "s_p1"]) as (held, sems):
        (s_go, s_pre, s_prep, s_fold, s_bias, s_st, s_mv, s_sd, s_rs, s_xs, s_xtp, s_xt, s_pp, s_pj, s_as, s_red,
         s_root, s_keep, s_w, s_t0, s_t1, s_p0, s_p1) = sems
        s_t, s_p = (s_t0, s_t1), (s_p0, s_p1)

        def sb(name, shape, dt=F32):
            return held.enter_context(nc.sbuf_tensor(own(nc, name), shape, dt))

        WVT = sb("w_v_t", [P, 2, D])
        WO = sb("w_out", [P, 2, D])
        BV = sb("b_v", [P, 2])
        W = sb("w_both", [P, 2, 2 * D])
        RB = sb("res_bias", [P, 2, D])
        AB = sb("a_src", [P, D])
        ST = sb("st", [P, 2, 6])
        MV = sb("mv", [P, 2, 2])
        SD = sb("sd", [P, 2, 1])
        RS = sb("rs", [P, 2, 1])
        XS = sb("xs", [P, 2, D])
        XT = sb("xt", [P, 2, D])
        PJ = sb("proj", [P, 2, H, HW1])
        PA = sb("proj_a", [P, 2, D])
        AS = sb("score", [P, 2, H])
        pt = held.enter_context(nc.psum_tensor(own(nc, "pt"), [P, 2, 512], F32))
        pp = held.enter_context(nc.psum_tensor(own(nc, "pp"), [P, 2, 512], F32))
        pf = held.enter_context(nc.psum_tensor(own(nc, "pf"), [P, 2, 512], F32))
        NWT = 16 * 6
        with nc.Block() as block:
            @block.sync
            def _(sp):
                for s in s_t:
                    sp.sem_inc(s, 16)
                for s in s_p:
                    sp.sem_inc(s, 32)
                sp.dma_start(WVT[:, :, :], w.L1_mix_W_qkv_t[2 * D:3 * D, :].rearrange("(c p) o -> p c o", p=P)).then_inc(s_w, 16)
                sp.dma_start(WO[:, :, :], w.L1_mix_W_out.rearrange("(c p) o -> p c o", p=P)).then_inc(s_w, 16)
                sp.dma_start(W[:, :, 0:D], w.L1_gnn_W.rearrange("(c p) o -> p c o", p=P)).then_inc(s_w, 16)
                sp.dma_start(BV[:, :], w.L1_mix_b_qkv[2 * D:3 * D].rearrange("(c p) -> p c", p=P),
                             allow_slow_non_contiguous=True).then_inc(s_w, 16)
                sp.dma_start(RB[:, 0, :], w.L1_mix_b_out.partition_broadcast(P)).then_inc(s_w, 16)
                sp.dma_start(AB[:, :], w.L1_gnn_a_src.rearrange("h d -> (h d)").partition_broadcast(P)).then_inc(s_w, 16)
                with sp.Fori(0, T // 2) as i:
                    for u in (0, 1):
                        n = i * 2 + u
                        sp.wait_ge(s_xt, done(n))
                        sp.dma_start(flat(g.xT, n * P * D, [D, P], [1, D]), XT[:, u, :]).then_inc(s_t[u], 16)
                    for u in (0, 1):
                        n = i * 2 + u
                        sp.wait_ge(s_pj, done(n))
                        sp.dma_start(flat(g.xp, n * P * AW, [AW, P], [1, AW]),
                                     PJ[:, u, :, :].rearrange("p h d -> p (h d)")).then_inc(s_p[u], 16)
                        sp.wait_ge(s_red, done(n))
                        sp.dma_start(flat(g.score, n * P * H, [H, P], [1, H]), AS[:, u, :]).then_inc(s_p[u], 16)
                for s in s_t:
                    sp.wait_ge(s, landed(T // 2 - 1))
                for s in s_p:
                    sp.wait_ge(s, landed(T // 2 - 1, 2))

            @block.vector
            def _(dve):
                for s in (s_st, s_mv, s_rs, s_xs, s_as, s_red, s_root):
                    dve.sem_inc(s, 2)
                dve.memset(PJ[:, :, :, HD:HW1], 1.0).then_inc(s_pre, 1)
                dve.wait_ge(s_fold, 2)
                dve.tensor_copy(W[:, :, D:2 * D], pf[:, :, 0:D])
                dve.wait_ge(s_fold, 3)
                dve.tensor_tensor(out=RB[:, 1, :], in0=RB[:, 0, :], in1=pt[:, 0, 0:D], op=ALU.add).then_inc(s_prep, 1)
                with dve.Fori(0, T // 2) as i:
                    for u in (0, 1):
                        n = i * 2 + u
                        dve.bn_stats(out=ST[:, u, :], in_=cut(g.X, n * D, [1, D])).then_inc(s_st, 1)
                    for u in (0, 1):
                        n = i * 2 + u
                        dve.wait_ge(s_st, done(n))
                        dve.sem_inc(s_go, 1)
                        dve.bn_aggr(out=MV[:, u, :], in_=ST[:, u, :]).then_inc(s_mv, 1)
                    for u in (0, 1):
                        n = i * 2 + u
                        dve.wait_ge(s_sd, done(n))
                        dve.reciprocal(RS[:, u, :], SD[:, u, :]).then_inc(s_rs, 1)
                    for u in (0, 1):
                        n = i * 2 + u
                        dve.wait_ge(s_rs, done(n))
                        dve.wait_ge(s_xtp, done(n - 2))
                        dve.tensor_scalar(out=XS[:, u, :], in0=cut(g.X, n * D, [1, D]), scalar1=MV[:, u, 0:1],
                                          scalar2=RS[:, u, 0:1], op0=ALU.subtract, op1=ALU.mult).then_inc(s_xs, 1)
                    for u in (0, 1):
                        n = i * 2 + u
                        dve.wait_ge(s_pj, done(n))
                        dve.wait_ge(s_red, done(n - 2))
                        dve.tensor_tensor(out=PA[:, u, :].rearrange("p (h d) -> p h d", d=HD),
                                          in0=PJ[:, u, :, 0:HD], in1=AB[:, :].rearrange("p (h d) -> p h d", d=HD),
                                          op=ALU.mult).then_inc(s_as, 1)
                        dve.tensor_tensor(out=cut(g.X, n * D, [1, D]), in0=pp[:, u, D:2 * D],
                                          in1=cut(g.X, n * D, [1, D]), op=ALU.add).then_inc(s_root, 1)
                    for u in (0, 1):
                        n = i * 2 + u
                        dve.wait_ge(s_as, done(n))
                        dve.wait_ge(s_p[u], landed(i - 1, 2))
                        dve.tensor_reduce(out=AS[:, u, :], in_=PA[:, u, :].rearrange("p (h d) -> p h d", d=HD),
                                          axis=AX.X, op=ALU.add).then_inc(s_red, 1)

            @block.scalar
            def _(act):
                for s in (s_sd, s_xt, s_pj):
                    act.sem_inc(s, 2)
                act.wait_ge(s_pre, 1)
                with act.Fori(0, T // 2) as i:
                    for u in (0, 1):
                        n = i * 2 + u
                        act.wait_ge(s_mv, done(n))
                        act.activation(SD[:, u, :], MV[:, u, 1:2], ACT.Sqrt, bias=g.eps[:, 0:1]).then_inc(s_sd, 1)
                    for u in (0, 1):
                        n = i * 2 + u
                        act.wait_ge(s_xtp, done(n))
                        act.wait_ge(s_t[u], landed(i - 1))
                        act.activation(XT[:, u, :], pt[:, u, 0:D], ACT.Copy).then_inc(s_xt, 1)
                    for u in (0, 1):
                        n = i * 2 + u
                        act.wait_ge(s_pp, done(n))
                        act.wait_ge(s_as, done(n - 2))
                        act.wait_ge(s_p[u], landed(i - 1, 2))
                        act.activation(PJ[:, u, :, 0:HD], pp[:, u, 0:D].rearrange("p (h d) -> p h d", d=HD),
                                       ACT.Copy).then_inc(s_pj, 1)

            @block.gpsimd
            def _(pool):
                pool.sem_inc(s_keep, 2)
                pool.wait_ge(s_prep, 1)
                with pool.Fori(0, T // 2) as i:
                    for u in (0, 1):
                        n = i * 2 + u
                        pool.wait_ge(s_root, done(n))
                        pool.tensor_tensor(out=cut(g.X, n * D, [1, D]), in0=cut(g.X, n * D, [1, D]),
                                           in1=RB[:, 1, :], op=ALU.add).then_inc(s_keep, 1)
                pool.wait_ge(s_keep, done(T - 1))

            @block.tensor
            def _(pe):
                for s in (s_xtp, s_pp):
                    pe.sem_inc(s, 2)
                pe.wait_ge(s_w, NWT)
                for m in (0, 1):
                    for c in (0, 1):
                        last = pe.matmul(pf[:, m, 0:D], WVT[:, c, m * P:(m + 1) * P], WO[:, c, :], start=c == 0,
                                         stop=c == 1)
                    last.then_inc(s_fold, 1)
                for c in (0, 1):
                    last = pe.matmul(pt[:, 0, 0:D], cut(BV, c, [0, P]), WO[:, c, :], start=c == 0, stop=c == 1)
                last.then_inc(s_fold, 1)
                pe.wait_ge(s_prep, 1)
                with pe.Fori(0, T // 2) as i:
                    for u in (0, 1):
                        n = i * 2 + u
                        pe.wait_ge(s_xs, done(n))
                        pe.wait_ge(s_xt, done(n - 2))
                        for c in (0, 1):
                            last = pe.transpose(pt[:, u, c * P:(c + 1) * P], XS[:, u, c * P:(c + 1) * P], g.ident[:, :])
                        last.then_inc(s_xtp, 1)
                    for u in (0, 1):
                        n = i * 2 + u
                        pe.wait_ge(s_xt, done(n))
                        pe.wait_ge(s_pj, done(n - 2))
                        pe.wait_ge(s_root, done(n - 2))
                        for c in (0, 1):
                            last = pe.matmul(pp[:, u, :], XT[:, u, c * P:(c + 1) * P], W[:, c, :],
                                             start=c == 0, stop=c == 1)
                        last.then_inc(s_pp, 1)


def mix1_phase(nc, g, w):
    names = ["s_c1", "s_c2", "s_c3", "s_qkvp", "s_qkv", "s_sq", "s_sk", "s_s4", "s_a", "s_r", "s_rt", "s_m", "s_m2", "s_im",
             "s_fac", "s_n", "s_ksq", "s_acc", "s_qtp", "s_qt", "s_zero", "s_out", "s_kt", "s_kw", "s_ix", "s_mv",
             "s_add", "s_pp", "s_cp", "s_go"]
    with phase(nc, names, ["s_w", "s_l0", "s_l1", "s_q0", "s_q1", "s_r0", "s_r1", "s_ie"]) as (held, sems):
        (s_c1, s_c2, s_c3, s_qkvp, s_qkv, s_sq, s_sk, s_s4, s_a, s_r, s_rt, s_m, s_m2, s_im, s_fac, s_n, s_ksq, s_acc,
         s_qtp, s_qt, s_zero, s_out, s_kt, s_kw, s_ix, s_mv, s_add, s_pp, s_cp, s_go, s_w, s_l0, s_l1, s_q0, s_q1,
         s_r0, s_r1, s_ie) = sems
        s_g0, s_g1 = pool_sems(nc, ["s_g0", "s_g1"])
        s_l, s_q, s_rl, s_g = (s_l0, s_l1), (s_q0, s_q1), (s_r0, s_r1), (s_g0, s_g1)

        def sb(name, shape, dt=F32):
            return held.enter_context(nc.sbuf_tensor(own(nc, name), shape, dt))

        W = sb("w_qkv", [P, 2, 3 * D])
        B = sb("b_qkv", [P, 3 * D])
        WO = sb("w_out", [P, 2, D])
        MW = sb("mean_w", [P, 2, 2])
        MB = sb("mean_b", [P, 2])
        XT = sb("xt", [P, 2, D])
        QKV = sb("qkv", [P, 2, 3 * D])
        SQ = sb("squares", [P, 2, 2 * D])
        J4 = sb("fourth", [P, 2, D])
        SS = sb("sums", [P, 2, 2])
        S4 = sb("sum4", [P, 2, 1])
        A = sb("a", [P, 2, 2])
        R = sb("r", [P, 2, 2])
        RT = sb("root", [P, 2, 1])
        M = sb("m", [P, 2, 1])
        M2 = sb("m2", [P, 2, 1])
        IM = sb("im", [P, 2, 1])
        FA = sb("fac", [P, 2, 2])
        NQ = sb("norm", [P, 2, 2 * D])
        KSQ = sb("k_sq", [P, 2, D])
        QT = sb("qt", [P, 2, D])
        QL = sb("ql", [P, 2, D])
        KV = sb("kv", [P, 2, D])
        NR = sb("nr", [P, 2])
        NI = sb("ni", [P, 2])
        KT = sb("kt", [P, 2, D])
        KW = sb("kw", [P, 2, D])
        IE = sb("edge_src", [P, PC], I32)
        IX = sb("ix", [P, 2, BATCH], I32)
        RG = sb("ring", [P, 2, BATCH, H])
        pq = held.enter_context(nc.psum_tensor(own(nc, "pq"), [P, 2, 1024], F32))
        acc = held.enter_context(nc.psum_tensor(own(nc, "acc"), [P, 2, D], F32))
        nrm = held.enter_context(nc.psum_tensor(own(nc, "nrm"), [P, 512], F32))
        pr = held.enter_context(nc.psum_tensor(own(nc, "pr"), [P, 2, 512], F32))
        HT = T // 2
        with nc.Block() as block:
            @block.sync
            def _(sp):
                sp.dma_start(IE[:, :], flat(g.esrc, 0, [PC, P], [1, PC])).then_inc(s_ie, 16)
                for s in (*s_l, *s_q, *s_rl):
                    sp.sem_inc(s, 16)
                sp.dma_start(W[:, :, :], w.L1_mix_W_qkv.rearrange("(c p) o -> p c o", p=P)).then_inc(s_w, 16)
                sp.dma_start(B[:, :], w.L1_mix_b_qkv.partition_broadcast(P)).then_inc(s_w, 16)
                sp.dma_start(WO[:, :, :], w.L1_mix_W_out.rearrange("(c p) o -> p c o", p=P)).then_inc(s_w, 16)
                with sp.Fori(0, HT) as i:
                    for u in (0, 1):
                        n = i * 2 + u
                        sp.wait_ge(s_qkvp, done(n - 2))
                        sp.dma_start(XT[:, u, :], flat(g.xT, n * P * D, [D, P], [1, D])).then_inc(s_l[u], 16)
                    for u in (0, 1):
                        n = i * 2 + u
                        sp.wait_ge(s_qt, done(n))
                        sp.dma_start(flat(g.q1, n * P * D, [D, P], [1, D]), QT[:, u, :]).then_inc(s_q[u], 16)
                for s in s_q:
                    sp.wait_ge(s, landed(HT - 1))
                with sp.Fori(0, HT) as i:
                    for u in (0, 1):
                        n = i * 2 + u
                        sp.wait_ge(s_pp, done(n - 2))
                        sp.dma_start(QL[:, u, :], flat(g.q1, n * P * D, [D, P], [1, D])).then_inc(s_rl[u], 16)

            @block.gpsimd
            def _(pool):
                TURNS = PC // (2 * BATCH)
                pool.wait_ge(s_ie, 16)
                pool.sem_inc(s_ix, 2)
                pool.sem_inc(s_cp, 2)

                def fetch(i, h):
                    m = i * 2 + h
                    pool.tensor_copy(IX[:, h, :], cut(IE, m * BATCH, [1, BATCH])).then_inc(s_ix, 1)
                    pool.wait_ge(s_ix, done(m))
                    pool.sem_inc(s_go, 1)
                    for j in range(BATCH):
                        pool.indirect_dma_start(
                            out=RG[:, h, j, :], out_offset=None, in_=flat(g.score, 0, [H, NP], [1, H]),
                            in_offset=bass.IndirectOffsetOnAxis(ap=IX[:, h, j:j + 1], axis=0)).then_inc(s_g[h], 16)

                def keep(i, h):
                    m = i * 2 + h
                    pool.wait_ge(s_g[h], (i + 1) * (16 * BATCH))
                    pool.tensor_copy(cut(g.ES, m * BATCH * H, [1, BATCH * H]),
                                     RG[:, h, :, :].rearrange("p j h -> p (j h)")).then_inc(s_cp, 1)
                    pool.wait_ge(s_cp, done(m))

                fetch(0, 0)
                with pool.Fori(0, TURNS - 1) as i:
                    fetch(i, 1)
                    keep(i, 0)
                    pool.sem_inc(s_go, 1)
                    fetch(i + 1, 0)
                    keep(i, 1)
                    pool.sem_inc(s_go, 1)
                fetch(TURNS - 1, 1)
                keep(TURNS - 1, 0)
                keep(TURNS - 1, 1)

            @block.vector
            def _(dve):
                for s in (s_qkv, s_a, s_r, s_m, s_m2, s_im, s_fac, s_n, s_add):
                    dve.sem_inc(s, 2)
                dve.wait_ge(s_w, 48)
                dve.tensor_reduce(out=MW[:, :, :], in_=W[:, :, 0:2 * D].rearrange("p c (k d) -> p c k d", d=D),
                                  axis=AX.X, op=ALU.add)
                dve.tensor_reduce(out=MB[:, :], in_=B[:, 0:2 * D].rearrange("p (k d) -> p k d", d=D), axis=AX.X,
                                  op=ALU.add).then_inc(s_c1, 1)
                dve.wait_ge(s_c1, 1)
                dve.tensor_scalar(out=MW[:, :, :], in0=MW[:, :, :], scalar1=1.0 / D, scalar2=None, op0=ALU.mult)
                dve.tensor_scalar(out=MB[:, :], in0=MB[:, :], scalar1=1.0 / D, scalar2=None,
                                  op0=ALU.mult).then_inc(s_c2, 1)
                dve.wait_ge(s_c2, 1)
                for c in (0, 1):
                    for k in (0, 1):
                        dve.tensor_scalar(out=W[:, c, k * D:(k + 1) * D], in0=W[:, c, k * D:(k + 1) * D],
                                          scalar1=MW[:, c, k:k + 1], scalar2=None, op0=ALU.subtract)
                for k in (0, 1):
                    last = dve.tensor_scalar(out=B[:, k * D:(k + 1) * D], in0=B[:, k * D:(k + 1) * D],
                                             scalar1=MB[:, k:k + 1], scalar2=None, op0=ALU.subtract)
                last.then_inc(s_c3, 1)
                dve.wait_ge(s_c3, 1)
                with dve.Fori(0, HT) as i:
                    for u in (0, 1):
                        n = i * 2 + u
                        dve.wait_ge(s_qkvp, done(n))
                        dve.wait_ge(s_acc, done(n - 2))
                        dve.wait_ge(s_sk, done(n - 2))
                        dve.tensor_tensor(out=QKV[:, u, :], in0=pq[:, u, 0:3 * D], in1=B[:, :],
                                          op=ALU.add).then_inc(s_qkv, 1)
                    for u in (0, 1):
                        n = i * 2 + u
                        dve.wait_ge(s_sk, done(n))
                        dve.tensor_scalar(out=A[:, u, :], in0=SS[:, u, :], scalar1=DIV_EPS, scalar2=None,
                                          op0=ALU.add).then_inc(s_a, 1)
                    for u in (0, 1):
                        n = i * 2 + u
                        dve.wait_ge(s_a, done(n))
                        dve.reciprocal(R[:, u, :], A[:, u, :]).then_inc(s_r, 1)
                    for u in (0, 1):
                        n = i * 2 + u
                        dve.wait_ge(s_r, done(n))
                        dve.wait_ge(s_rt, done(n))
                        dve.tensor_tensor(out=M[:, u, :], in0=R[:, u, 0:1], in1=RT[:, u, :], op=ALU.mult).then_inc(s_m, 1)
                    for u in (0, 1):
                        n = i * 2 + u
                        dve.wait_ge(s_m, done(n))
                        dve.tensor_scalar(out=M2[:, u, :], in0=M[:, u, :], scalar1=NORM_EPS, scalar2=None,
                                          op0=ALU.max).then_inc(s_m2, 1)
                    for u in (0, 1):
                        n = i * 2 + u
                        dve.wait_ge(s_m2, done(n))
                        dve.reciprocal(IM[:, u, :], M2[:, u, :]).then_inc(s_im, 1)
                    for u in (0, 1):
                        n = i * 2 + u
                        dve.wait_ge(s_im, done(n))
                        dve.tensor_tensor(out=FA[:, u, 0:1], in0=R[:, u, 0:1], in1=IM[:, u, :], op=ALU.mult)
                        dve.tensor_tensor(out=FA[:, u, 1:2], in0=R[:, u, 1:2], in1=cut(g.valid, n, [1, 1]),
                                          op=ALU.mult).then_inc(s_fac, 1)
                    for u in (0, 1):
                        n = i * 2 + u
                        dve.wait_ge(s_fac, done(n))
                        dve.wait_ge(s_qtp, done(n - 2))
                        dve.wait_ge(s_ksq, done(n - 2))
                        for k in (0, 1):
                            last = dve.tensor_scalar(out=NQ[:, u, k * D:(k + 1) * D], in0=SQ[:, u, k * D:(k + 1) * D],
                                                     scalar1=FA[:, u, k:k + 1], scalar2=None, op0=ALU.mult)
                        last.then_inc(s_n, 1)
                dve.wait_ge(s_zero, 2)
                dve.tensor_copy(NR[:, :], nrm[:, 0:2]).then_inc(s_out, 1)
                dve.wait_ge(s_out, 2)
                dve.tensor_scalar(out=NI[:, :], in0=NR[:, :], scalar1=NORM_EPS, scalar2=None, op0=ALU.max
                                  ).then_inc(s_out, 1)
                dve.wait_ge(s_out, 3)
                dve.reciprocal(NR[:, :], NI[:, :]).then_inc(s_out, 1)
                dve.wait_ge(s_out, 4)
                for c in (0, 1):
                    last = dve.tensor_scalar(out=KV[:, c, :], in0=acc[:, c, :], scalar1=NR[:, c:c + 1], scalar2=None,
                                             op0=ALU.mult)
                last.then_inc(s_kt, 1)
                dve.wait_ge(s_kt, 2)
                dve.tensor_copy(KT[:, :, :], pr[:, :, 0:D]).then_inc(s_kt, 1)
                dve.wait_ge(s_kw, 1)
                dve.tensor_scalar(out=KW[:, :, :], in0=pq[:, 0:2, 0:D], scalar1=float(N) ** -0.5, scalar2=None,
                                  op0=ALU.mult).then_inc(s_kw, 1)
                with dve.Fori(0, HT) as i:
                    for u in (0, 1):
                        n = i * 2 + u
                        dve.wait_ge(s_pp, done(n))
                        dve.tensor_tensor(out=cut(g.X, n * D, [1, D]), in0=pr[:, u, 0:D],
                                          in1=cut(g.X, n * D, [1, D]), op=ALU.add).then_inc(s_add, 1)
                dve.wait_ge(s_add, done(T - 1))

            @block.scalar
            def _(act):
                for s in (s_sq, s_sk, s_s4, s_rt, s_ksq, s_qt):
                    act.sem_inc(s, 2)
                with act.Fori(0, HT) as i:
                    for u in (0, 1):
                        n = i * 2 + u
                        act.wait_ge(s_qkv, done(n))
                        act.wait_ge(s_n, done(n - 2))
                        act.activation(SQ[:, u, 0:D], QKV[:, u, 0:D], ACT.Square, accum_out=SS[:, u, 0:1]).then_inc(s_sq, 1)
                        act.activation(SQ[:, u, D:2 * D], QKV[:, u, D:2 * D], ACT.Square,
                                       accum_out=SS[:, u, 1:2]).then_inc(s_sk, 1)
                    for u in (0, 1):
                        n = i * 2 + u
                        act.wait_ge(s_sq, done(n))
                        act.activation(J4[:, u, :], SQ[:, u, 0:D], ACT.Square, accum_out=S4[:, u, :]).then_inc(s_s4, 1)
                    for u in (0, 1):
                        n = i * 2 + u
                        act.wait_ge(s_s4, done(n))
                        act.activation(RT[:, u, :], S4[:, u, :], ACT.Sqrt, bias=g.zero[:, 0:1]).then_inc(s_rt, 1)
                    for u in (0, 1):
                        n = i * 2 + u
                        act.wait_ge(s_n, done(n))
                        act.wait_ge(s_acc, done(n - 2))
                        act.activation(KSQ[:, u, :], NQ[:, u, D:2 * D], ACT.Square).then_inc(s_ksq, 1)
                    for u in (0, 1):
                        n = i * 2 + u
                        act.wait_ge(s_qtp, done(n))
                        act.wait_ge(s_q[u], landed(i - 1))
                        act.activation(QT[:, u, :], pr[:, u, 0:D], ACT.Copy).then_inc(s_qt, 1)
                act.wait_ge(s_zero, 2)
                act.wait_ge(s_out, 1)
                act.activation(NR[:, :], NR[:, :], ACT.Sqrt, bias=g.zero[:, 0:1]).then_inc(s_out, 1)

            @block.tensor
            def _(pe):
                for s in (s_qkvp, s_acc, s_qtp, s_pp):
                    pe.sem_inc(s, 2)

                def zero(start, stop):
                    pe.matmul(acc[:, :, :], g.zrow[0:1, 0:P], g.zrow[0:1, :], start=start, stop=stop)
                    pe.matmul(nrm[:, :], g.zrow[0:1, 0:P], g.zrow[0:1, :], start=start, stop=stop).then_inc(s_zero, 1)

                zero(True, False)
                pe.wait_ge(s_c3, 1)
                with pe.Fori(0, HT) as i:
                    for u in (0, 1):
                        n = i * 2 + u
                        pe.wait_ge(s_l[u], landed(i))
                        pe.wait_ge(s_qkv, done(n - 2))
                        for c in (0, 1):
                            for a, b in ((0, 512), (512, 768)):
                                last = pe.matmul(pq[:, u, a:b], XT[:, u, c * P:(c + 1) * P], W[:, c, a:b],
                                                 start=c == 0, stop=c == 1)
                        last.then_inc(s_qkvp, 1)
                    for u in (0, 1):
                        n = i * 2 + u
                        pe.wait_ge(s_n, done(n))
                        pe.wait_ge(s_qt, done(n - 2))
                        for c in (0, 1):
                            last = pe.transpose(pr[:, u, c * P:(c + 1) * P], NQ[:, u, c * P:(c + 1) * P], g.ident[:, :])
                        last.then_inc(s_qtp, 1)
                        pe.wait_ge(s_ksq, done(n))
                        for c in (0, 1):
                            pe.matmul(acc[:, c, :], NQ[:, u, D + c * P:D + (c + 1) * P], QKV[:, u, 2 * D:3 * D],
                                      start=False, stop=False)
                        for c in (0, 1):
                            last = pe.matmul(nrm[:, c:c + 1], KSQ[:, u, c * P:(c + 1) * P], g.ones[:, 0:1],
                                             start=False, stop=False)
                        last.then_inc(s_acc, 1)
                zero(False, True)
                pe.wait_ge(s_kt, 1)
                pe.wait_ge(s_qt, done(T - 1))
                for c in (0, 1):
                    for d in (0, 1):
                        last = pe.transpose(pr[:, d, c * P:(c + 1) * P], KV[:, c, d * P:(d + 1) * P], g.ident[:, :])
                last.then_inc(s_kt, 1)
                pe.wait_ge(s_kt, 3)
                for c in (0, 1):
                    for d in (0, 1):
                        last = pe.matmul(pq[:, c, 0:D], KT[:, d, c * P:(c + 1) * P], WO[:, d, :], start=d == 0, stop=d == 1)
                last.then_inc(s_kw, 1)
                pe.wait_ge(s_kw, 2)
                with pe.Fori(0, HT) as i:
                    for u in (0, 1):
                        n = i * 2 + u
                        pe.wait_ge(s_rl[u], landed(i))
                        pe.wait_ge(s_add, done(n - 2))
                        for c in (0, 1):
                            last = pe.matmul(pr[:, u, 0:D], QL[:, u, c * P:(c + 1) * P], KW[:, c, :],
                                             start=c == 0, stop=c == 1)
                        last.then_inc(s_pp, 1)


def weights1_phase(nc, g):
    names = ["s_ms", "s_ne", "s_pen", "s_ps", "s_f", "s_fl", "s_t", "s_tc", "s_ch", "s_chb", "s_cb", "s_ci",
             "s_m", "s_exp", "s_wt", "s_wc"]
    with phase(nc, names, ["s_d", "s_we"]) as (held, sems):
        (s_ms, s_ne, s_pen, s_ps, s_f, s_fl, s_t, s_tc, s_ch, s_chb, s_cb, s_ci, s_m, s_exp, s_wt, s_wc,
         s_d, s_we) = sems
        s_g, = pool_sems(nc, ["s_g"])

        def sb(name, shape, dt=F32):
            return held.enter_context(nc.sbuf_tensor(own(nc, name), shape, dt))

        DI = sb("dst_i", [P, PC + 2], I32)
        PEN = sb("pen", [P, PC + 1])
        PS = sb("pen_sum", [P, 2])
        FL = sb("ends", [P, H])
        PB = sb("pen_b", [P, H])
        CH = sb("chain_in", [H, 2, P])
        CO = sb("chain_out", [H, P + 1])
        CI = sb("carry", [P, H])
        FO, BO = 0, H * PC
        pt = held.enter_context(nc.psum_tensor(own(nc, "pt"), [P, 2, 512], F32))
        pw = held.enter_context(nc.psum_tensor(own(nc, "pw"), [P, 4, 512], F32))
        W4 = sb("w_rows", [P, 2, P * H])
        with nc.Block() as block:
            @block.sync
            def _(sp):
                sp.wait_ge(s_ms, 1)
                sp.dma_start(DI[:, 1:PC + 1], flat(g.edst, 0, [PC, P], [1, PC])).then_inc(s_d, 16)
                sp.dma_start(DI[1:P, 0:1], flat(g.edst, PC - 1, [PC, P - 1], [1, 1]),
                             allow_slow_non_contiguous=True).then_inc(s_d, 16)
                sp.dma_start(DI[0:P - 1, PC + 1:PC + 2], flat(g.edst, PC, [PC, P - 1], [1, 1]),
                             allow_slow_non_contiguous=True).then_inc(s_d, 16)
                sp.wait_ge(s_exp, 1)
                sp.dma_start(flat(g.we, 0, [PC * H, P], [1, PC * H]), g.ES[:, :]).then_inc(s_we, 16)
                sp.wait_ge(s_we, 16)

            @block.gpsimd
            def _(pool):
                pool.wait_ge(s_we, 16)
                for c in range(SCOLS):
                    if c >= 2:
                        pool.wait_ge(s_wt, (c - 1) * H)
                    pool.indirect_dma_start(
                        out=W4[:, c % 2, :], out_offset=None, in_=flat(g.we, 0, [P * H, ET], [1, P * H]),
                        in_offset=bass.IndirectOffsetOnAxis(ap=g.tki[:, c:c + 1], axis=0)).then_inc(s_g, 16)
                    pool.wait_ge(s_g, 16 * (c + 1))

            @block.vector
            def _(dve):
                dve.memset(DI[:, :], -1).then_inc(s_ms, 1)
                dve.wait_ge(s_d, 48)
                dve.tensor_tensor(out=PEN[:, :], in0=DI[:, 0:PC + 1], in1=DI[:, 1:PC + 2],
                                  op=ALU.not_equal).then_inc(s_ne, 1)
                dve.wait_ge(s_ne, 1)
                dve.tensor_scalar(out=PEN[:, :], in0=PEN[:, :], scalar1=NEG, scalar2=None, op0=ALU.mult).then_inc(s_pen, 1)
                dve.memset(CO[:, :], NEG)
                dve.wait_ge(s_pen, 1)
                for b in (0, 1):
                    last = dve.tensor_reduce(out=PS[:, b:b + 1], in_=PEN[:, b:b + PC], axis=AX.X, op=ALU.add)
                last.then_inc(s_ps, 1)
                dve.wait_ge(s_ps, 1)
                for b in (0, 1):
                    def runs(h, first):
                        scores = cut(g.ES, h, [H, PC])
                        fwd = cut(g.XN, FO + h * PC, [1, PC])
                        bwd = cut(g.XN, BO + h * PC + PC - 1, [-1, PC])
                        start = NEG if first else CI[:, h:h + 1]
                        if b == 0:
                            return dve.tensor_tensor_scan(out=fwd, data0=PEN[:, 0:PC], data1=scores, initial=start,
                                                          op0=ALU.add, op1=ALU.max)
                        return dve.tensor_tensor_scan(out=bwd, data0=cut(PEN, PC, [-1, PC]),
                                                      data1=cut(g.XN, FO + h * PC + PC - 1, [-1, PC]),
                                                      initial=start, op0=ALU.add, op1=ALU.max)

                    for h in range(H):
                        last = runs(h, True)
                    last.then_inc(s_f, 1)
                    dve.wait_ge(s_f, 2 * b + 1)
                    dve.tensor_copy(FL[:, :], cut(g.XN, (FO + PC - 1) if b == 0 else BO, [PC, H]))
                    dve.tensor_copy(PB[:, :], cut(PS, b, [0, H])).then_inc(s_fl, 1)
                    dve.wait_ge(s_t, b + 1)
                    dve.tensor_copy(CH[:, :, :], pt[0:H, :, 0:P]).then_inc(s_tc, 1)
                    dve.wait_ge(s_tc, b + 1)
                    if b == 0:
                        dve.tensor_tensor_scan(out=CO[:, 1:P + 1], data0=CH[:, 1, :], data1=CH[:, 0, :], initial=NEG,
                                               op0=ALU.add, op1=ALU.max).then_inc(s_ch, 1)
                    else:
                        dve.memset(CO[:, P:P + 1], NEG)
                        dve.tensor_tensor_scan(out=cut(CO, P - 1, [-1, P]), data0=cut(CH, 2 * P - 1, [-1, P]),
                                               data1=cut(CH, P - 1, [-1, P]), initial=NEG, op0=ALU.add,
                                               op1=ALU.max).then_inc(s_ch, 1)
                    dve.wait_ge(s_cb, b + 1)
                    dve.tensor_copy(CI[:, :], pt[:, 0, 0:H]).then_inc(s_ci, 1)
                    dve.wait_ge(s_ci, b + 1)
                    for h in range(H):
                        last = runs(h, False)
                    last.then_inc(s_f, 1)
                    dve.wait_ge(s_f, 2 * b + 2)
                dve.tensor_tensor(out=cut(g.ES, 0, [H, PC], [1, H]), in0=cut(g.ES, 0, [H, PC], [1, H]),
                                  in1=cut(g.XN, BO, [1, PC], [PC, H]), op=ALU.subtract).then_inc(s_m, 1)
                for c in range(SCOLS):
                    for h in range(H):
                        k = c * H + h
                        dve.wait_ge(s_wt, k + 1)
                        dve.tensor_copy(cut(g.wst, c * P * H + h, [H, P]), pw[:, k % 4, 0:P]).then_inc(s_wc, 1)
                dve.wait_ge(s_wc, SCOLS * H)

            @block.scalar
            def _(act):
                act.wait_ge(s_m, 1)
                act.activation(g.ES[:, :], g.ES[:, :], ACT.Exp).then_inc(s_exp, 1)

            @block.tensor
            def _(pe):
                for b in (0, 1):
                    pe.wait_ge(s_fl, b + 1)
                    pe.transpose(pt[0:H, 0, 0:P], FL[:, :], g.ident[:, :])
                    pe.transpose(pt[0:H, 1, 0:P], PB[:, :], g.ident[:, :]).then_inc(s_t, 1)
                    pe.wait_ge(s_ch, b + 1)
                    pe.transpose(pt[:, 0, 0:H], CO[:, b:b + P], g.ident[0:H, 0:H]).then_inc(s_cb, 1)
                for c in range(SCOLS):
                    pe.wait_ge(s_g, 16 * (c + 1))
                    for h in range(H):
                        k = c * H + h
                        if k >= 4:
                            pe.wait_ge(s_wc, k - 3)
                        pe.transpose(pw[:, k % 4, 0:P], cut(W4, (c % 2) * P * H + h, [H, P]), g.ident[:, :]).then_inc(s_wt, 1)

QUARTERS = 4
QB = U // QUARTERS
PACK = 4


def graph1_phase(nc, g):
    names = ["s_z", "s_ix", "s_go", "s_pr", "s_df", "s_oh", "s_pa", "s_acc"]
    with phase(nc, names) as (held, sems):
        s_z, s_ix, s_go, s_pr, s_df, s_oh, s_pa, s_acc = sems
        s_g = pool_sems(nc, [f"s_g{x}" for x in range(QUARTERS)])

        def sb(name, shape, dt=F32):
            return held.enter_context(nc.sbuf_tensor(own(nc, name), shape, dt))

        IX = sb("ix", [P, U], I32)
        WP = sb("windows", [1, SROWS // PACK], I32)
        RG = sb("ring", [P, U, AW])
        PR = sb("weighted", [P, 4, AW])
        DF = sb("distance", [P, 4, P])
        OH = sb("one_hot", [P, 4, P])
        pa = held.enter_context(nc.psum_tensor(own(nc, "pa"), [P, 4, 512], F32))

        def fin(k):
            return k + 1 + U

        with nc.Block() as block:
            @block.gpsimd
            def _(pool):
                with pool.Fori(0, TURNS) as i:
                    for x in range(QUARTERS):
                        pool.wait_ge(s_ix, i * QUARTERS + x + 1)
                        pool.wait_ge(s_pr, fin(i * U + x * QB + QB - 1 - U))
                        pool.sem_inc(s_go, 1)
                        for j in range(x * QB, (x + 1) * QB):
                            pool.indirect_dma_start(
                                out=RG[:, j, :], out_offset=None, in_=flat(g.xp, 0, [AW, NP], [1, AW]),
                                in_offset=bass.IndirectOffsetOnAxis(ap=IX[:, j:j + 1], axis=0)).then_inc(s_g[x], 16)

            @block.vector
            def _(dve):
                for s in (s_pr, s_acc):
                    dve.sem_inc(s, U)
                dve.memset(cut(g.XN, 0, [1, T * AW]), 0.0).then_inc(s_z, 1)
                dve.tensor_copy(WP[:, :], sub(g.wrow[0:1, :], PACK - 1, [PACK, SROWS // PACK])).then_inc(s_z, 1)
                for p in range(PACK - 2, -1, -1):
                    dve.wait_ge(s_z, PACK - p)
                    dve.scalar_tensor_tensor(out=WP[:, :], in0=WP[:, :], scalar=float(T),
                                             in1=sub(g.wrow[0:1, :], p, [PACK, SROWS // PACK]), op0=ALU.mult,
                                             op1=ALU.add).then_inc(s_z, 1)
                dve.wait_ge(s_z, PACK + 1)

                def add(i, j, packs):
                    k = i * U + j
                    at = packs[j // PACK] // T ** (j % PACK) % T
                    dve.wait_ge(s_pa, fin(k))
                    dve.wait_ge(s_acc, fin(k - 1))
                    dve.tensor_tensor(out=cut(g.XN, at * AW, [1, AW]), in0=pa[:, j % 4, 0:AW],
                                      in1=cut(g.XN, at * AW, [1, AW]), op=ALU.add).then_inc(s_acc, 1)

                with dve.Fori(0, TURNS) as i:
                    _, packs = nc.values_load_multi_w_load_instructions(
                        WP[0:1, bass.ds(i * (U // PACK), U // PACK)], engines=(mybir.EngineType.DVE,), min_val=0,
                        max_val=T ** PACK - 1)
                    for j in range(U):
                        k = i * U + j
                        x = j // QB
                        if j % QB == 0:
                            dve.wait_ge(s_g[x], (i + 1) * (16 * QB))
                        dve.wait_ge(s_pa, fin(k - 4))
                        dve.tensor_tensor(out=PR[:, j % 4, :].rearrange("p (h d) -> p h d", d=HW1),
                                          in0=RG[:, j, :].rearrange("p (h d) -> p h d", d=HW1),
                                          in1=cut(g.wst, k * H, [1, H], [0, HW1]), op=ALU.mult).then_inc(s_pr, 1)
                        if j >= 2:
                            add(i, j - 2, packs)
                    for j in (U - 2, U - 1):
                        add(i, j, packs)
                dve.wait_ge(s_acc, fin(STEPS - 1))

            @block.scalar
            def _(act):
                act.sem_inc(s_df, U)
                act.sem_inc(s_oh, U)
                for x in range(QUARTERS):
                    act.activation(IX[:, x * QB:(x + 1) * QB], cut(g.srci, x * QB, [1, QB]), ACT.Copy).then_inc(s_ix, 1)
                with act.Fori(0, TURNS) as i:
                    for j in range(U):
                        k = i * U + j
                        act.wait_ge(s_oh, fin(k - 4))
                        act.activation(DF[:, j % 4, :], g.iota[:, :], ACT.Abs, bias=cut(g.rel, k, [1, 1]),
                                       scale=-1.0).then_inc(s_df, 1)
                        act.wait_ge(s_df, fin(k))
                        act.wait_ge(s_pa, fin(k - 4))
                        act.activation(OH[:, j % 4, :], DF[:, j % 4, :], ACT.Relu, bias=g.ones[:, 0:1],
                                       scale=-1.0).then_inc(s_oh, 1)
                        if j % QB == QB - 1:
                            x = j // QB
                            act.wait_ge(s_g[x], (i + 1) * (16 * QB))
                            act.wait_ge(s_ix, i * QUARTERS + x + QUARTERS)
                            act.activation(IX[:, x * QB:(x + 1) * QB], cut(g.srci, i * U + U + x * QB, [1, QB]),
                                           ACT.Copy).then_inc(s_ix, 1)

            @block.tensor
            def _(pe):
                pe.sem_inc(s_pa, U)
                with pe.Fori(0, TURNS) as i:
                    for h in (0, 1):
                        for j in range(BATCH):
                            k = i * U + h * BATCH + j
                            pe.wait_ge(s_oh, fin(k))
                            pe.wait_ge(s_pr, fin(k))
                            pe.wait_ge(s_acc, fin(k - 4))
                            pe.matmul(pa[:, j % 4, 0:AW], OH[:, j % 4, :], PR[:, j % 4, :], start=True,
                                      stop=True).then_inc(s_pa, 1)


class Bag:
    pass

WEIGHTS = ["L0_gnn_W1", "L0_gnn_b1", "L0_gnn_W2", "L0_gnn_b2", "L0_mix_Wqkv", "L0_mix_bqkv", "L0_mix_Wproj",
           "L0_mix_bproj", "L0_mix_temperature", "L0_ffn_router_w", "L0_ffn_router_b", "L0_ffn_W1", "L0_ffn_b1",
           "L0_ffn_W2", "L0_ffn_b2", "L1_gnn_W", "L1_gnn_a_src", "L1_mix_W_qkv", "L1_mix_b_qkv",
           "L1_mix_W_qkv_t", "L1_mix_W_out", "L1_mix_b_out", "L1_ffn_gate_w", "L1_ffn_gate_b", "L1_ffn_W1", "L1_ffn_b1", "L1_ffn_W2",
           "L1_ffn_b2"]
TRANSPOSED = ("L0_gnn_W1", "L0_gnn_W2", "L0_mix_Wqkv", "L0_mix_Wproj", "L0_ffn_router_w")
Weights = namedtuple("Weights", WEIGHTS)


def feed_forward(nc, g, w, layer, cfg, out):
    with ExitStack() as route:
        g.choice = route.enter_context(nc.sbuf_tensor(own(nc, "choice"), [P, T * 32], BF16))
        g.zeros = route.enter_context(nc.sbuf_tensor(own(nc, "zeros"), [P, 4 * D], F32))
        join_phase(nc, g, w, layer, cfg)
        sort_phase(nc, g, layer, cfg)
    experts_phase(nc, g, w, layer, cfg)
    merge_phase(nc, g, layer, cfg, out)


def gnn_kernel(nc, x, src, dst, w, out):
    g = Bag()
    g.esrc = nc.dram_tensor("esrc", [EP], I32)
    g.edst = nc.dram_tensor("edst", [EP], I32)
    g.kv = nc.dram_tensor("kv", [T, P, 2 * D], F32)
    g.qT = nc.dram_tensor("qT", [2, P, NP], F32)
    g.srows = nc.dram_tensor("srows", [SROWS, P], F32)
    g.wsteps = nc.dram_tensor("wsteps", [SROWS], I32)
    g.agg = [nc.dram_tensor(f"agg{a}", [AROWS, GW], F32) for a in range(AGGS)]
    ffn0, ffn1 = Bag(), Bag()
    ffn0.experts, ffn0.top, ffn0.hidden = 32, 1, 64
    ffn1.experts, ffn1.top, ffn1.hidden = 8, 2, 512
    for f in (ffn0, ffn1):
        f.steps = -(-(f.top * T + f.experts - 1) // 2) * 2
    g.xT = nc.dram_tensor("xn1_t", [NP * D], F32)
    g.q1 = nc.dram_tensor("q1_t", [NP * D], F32)
    g.xp = nc.dram_tensor("projected", [NP * AW], F32)
    g.score = nc.dram_tensor("source_score", [NP * H], F32)
    g.we = nc.dram_tensor("edge_weight", [EP * H], F32)
    g.xe = nc.dram_tensor("expert_in", [ffn1.steps * P, D], F32)
    g.ye = nc.dram_tensor("expert_out", [ffn1.steps * P, D], F32)
    with ExitStack() as held:
        def sb(name, shape, dt=F32):
            return held.enter_context(nc.sbuf_tensor(name, shape, dt))

        g.X = sb("X", [P, T, D])
        g.XN = sb("XN", [P, 2 * H * PC])
        g.iota = sb("iota", [P, P])
        g.pcol = sb("pcol", [P, 1])
        g.ident = sb("ident", [P, P])
        g.lower = sb("lower", [P, P])
        g.valid = sb("valid", [P, T])
        g.eps = sb("eps", [P, 1])
        g.mv = sb("mean_dev", [P, T, 2])
        g.zero = sb("zero", [P, 1])
        g.ones = sb("ones", [P, P])
        g.zrow = sb("zrow", [1, 512])
        g.blk = sb("blk", [P, P])
        g.head = sb("head", [P, 1])
        g.rel = sb("step_rel", [P, SROWS])
        g.src = sb("step_src", [P, SROWS])
        g.srci = sb("step_srci", [P, SROWS], I32)
        g.tki = sb("step_tile", [P, SCOLS], I32)
        g.wrow = sb("step_wrow", [1, SROWS], I32)
        g.cw = sb("expert_weight", [P, 2 * T])
        g.eidx = sb("expert_no", [P, 2 * T])
        g.rowi = sb("expert_row", [P, 2 * T], I32)
        g.erow = sb("expert_of_step", [1, P], I32)
        g.s_c = pool_sems(nc, [f"s_c{a}" for a in range(AGGS)])
        with ExitStack() as mix0, ExitStack() as zeroing:
            def sb0(name, shape):
                return mix0.enter_context(nc.sbuf_tensor(name, shape, F32))

            g.WS = sb0("WS", [P, 2, PAIRS + 1, P])
            g.GS = sb0("GS", [P, 2, P])
            g.ks = sb0("ks", [P, 2])
            g.vs = sb0("vs", [P, 2])
            g.zeros0 = zeroing.enter_context(nc.sbuf_tensor("zeros0", [P, ZC], F32))
            setup_phase(nc, g, x, src, dst)
            steps_phase(nc, g)
            norms_phase(nc, g)
            qkv0_phase(nc, g, w)
            zeroing.close()
            graph = Graph0(nc, g, mix0)
            for q in (0, 1):
                keys0_phase(nc, g, graph, q)
            queries0_phase(nc, g, graph, w)
            graph.end(nc)
        feed_forward(nc, g, w, 0, ffn0, out)
        project1_phase(nc, g, w)
        with ExitStack() as edges:
            g.ES = edges.enter_context(nc.sbuf_tensor("edge_score", [P, PC * H], F32))
            mix1_phase(nc, g, w)
            g.wst = edges.enter_context(nc.sbuf_tensor("step_weight", [P, SROWS * H], F32))
            weights1_phase(nc, g)
            graph1_phase(nc, g)
        feed_forward(nc, g, w, 1, ffn1, out)

def kernel(**inputs):
    import numpy as _np
    import concourse.bacc as _bacc
    from concourse import mybir as _mybir
    from concourse.bass_utils import run_bass_kernel_spmd as _run

    nc = _bacc.Bacc("TRN2", target_bir_lowering=False, num_devices=1)
    arrays = {}

    def given(name, a):
        a = _np.ascontiguousarray(a)
        arrays[f"in_{name}_dram"] = a
        return nc.dram_tensor(f"in_{name}_dram", a.shape, _mybir.dt.from_np(a.dtype), kind="ExternalInput").ap()

    x, src, dst = (given(name, inputs[name]) for name in ("x", "src", "dst"))
    params = {}
    for name in WEIGHTS:
        if name == "L1_mix_W_qkv_t":
            a = _np.asarray(inputs["L1_mix_W_qkv"]).T
        elif name in TRANSPOSED:
            a = _np.asarray(inputs[name]).T
        elif name == "L0_mix_temperature":
            a = _np.asarray(inputs[name]).reshape(H)
        else:
            a = _np.asarray(inputs[name])
        params[name] = given(name, a)
    out = nc.dram_tensor("out_0_dram", (N, D), _mybir.dt.from_np(_np.dtype("float32")), kind="ExternalOutput").ap()
    gnn_kernel(nc, x, src, dst, Weights(**params), out)
    r = _run(nc, [arrays], core_ids=[0])
    return r.results[0]["out_0_dram"]
```

```python
from collections import namedtuple
from contextlib import ExitStack, contextmanager

import concourse.bass as bass
from concourse import mybir

F32 = mybir.dt.float32
BF16 = mybir.dt.bfloat16
I32 = mybir.dt.int32
U32 = mybir.dt.uint32
ALU = mybir.AluOpType
ACT = mybir.ActivationFunctionType
AX = mybir.AxisListType

P = 128
N = 6250
D = 256
T = 50
NP = T * P
FULL = N // P
REST = N - FULL * P
H, HD = 8, 32
E = 106250
ET = -(-E // (16 * P)) * 16
EP = ET * P
WIN = -(-N // P)
STEPS = ET + WIN - 1
SROWS = -(-STEPS // P) * P
PAD_NODE = WIN * P - 1
GW = 260
AW = GW + 4
LN_EPS = 1e-5
NEG = -1.0e30


def cut(buf, at, *dims):
    whole = buf[tuple([slice(None)] * len(buf.shape))]
    return bass.AP(whole.tensor, whole.offset + at, [list(whole.ap[0]), *[list(d) for d in dims]])


def sub(ap, at, *dims):
    return bass.AP(ap.tensor, ap.offset + at, [list(ap.ap[0]), *[list(d) for d in dims]])


def flat(buf, at, *dims):
    whole = buf[tuple([slice(None)] * len(buf.shape))]
    return bass.AP(whole.tensor, whole.offset + at, [list(d) for d in dims])


def own(nc, name):
    return f"{name}_{nc.next_id()}"


def done(n):
    return n + 3


def landed(i, k=1):
    return 16 * k * (i + 2)


def pool_sems(nc, names):
    return [nc.alloc_semaphore(own(nc, n)) for n in names]


@contextmanager
def phase(nc, names, dma_names=()):
    with ExitStack() as held:
        sems = [held.enter_context(nc.semaphore(own(nc, n))) for n in (*names, *dma_names)]
        yield held, sems
        with nc.Block() as block:
            @block.gpsimd
            def _(pool):
                for s in sems:
                    pool.sem_clear(s)


def setup_phase(nc, g, x, src, dst):
    names = ["s_x0", "s_iota", "s_pad", "s_f", "s_z", "s_blk", "s_const"]
    with phase(nc, names, ["s_in", "s_edge"]) as (held, sems):
        s_x0, s_iota, s_pad, s_f, s_z, s_blk, s_const, s_in, s_edge = sems
        blk_i = held.enter_context(nc.sbuf_tensor(own(nc, "blk_i"), [P, P], I32))
        row_i = held.enter_context(nc.sbuf_tensor(own(nc, "row_i"), [P, 1], I32))
        iota_i = held.enter_context(nc.sbuf_tensor(own(nc, "iota_i"), [P, P], I32))
        col_i = held.enter_context(nc.sbuf_tensor(own(nc, "col_i"), [P, 1], I32))
        node_i = held.enter_context(nc.sbuf_tensor(own(nc, "node_i"), [P, T], I32))
        node_f = held.enter_context(nc.sbuf_tensor(own(nc, "node_f"), [P, T], F32))
        pad_i = held.enter_context(nc.sbuf_tensor(own(nc, "pad_i"), [1, EP - E], I32))
        with nc.Block() as block:
            @block.sync
            def _(sp):
                for t in range(0, FULL, 12):
                    sp.dma_start(g.X[:, t:t + 12, :],
                                 x[t * P:(t + 12) * P, :].rearrange("(t p) d -> p t d", p=P)).then_inc(s_in, 16)
                sp.wait_ge(s_x0, 1)
                sp.dma_start(g.X[0:REST, FULL, :], x[FULL * P:N, :]).then_inc(s_in, 16)
                for to, of in ((g.esrc, src), (g.edst, dst)):
                    sp.dma_start(flat(to, 0, [E // 10, 10], [1, E // 10]),
                                 of.rearrange("(a b) -> a b", a=10)).then_inc(s_edge, 16)
                sp.wait_ge(s_pad, 1)
                for to in (g.esrc, g.edst):
                    sp.dma_start(flat(to, E, [EP - E, 1], [1, EP - E]), pad_i[:, :]).then_inc(s_edge, 16)
                sp.wait_ge(s_in, 16 * (FULL // 12 + 1))
                sp.wait_ge(s_edge, 64)

            @block.gpsimd
            def _(pool):
                pool.iota(iota_i[:, :], pattern=[[1, P]], base=0, channel_multiplier=0).then_inc(s_iota, 1)
                pool.iota(col_i[:, :], pattern=[[1, 1]], base=0, channel_multiplier=1).then_inc(s_iota, 1)
                pool.iota(node_i[:, :], pattern=[[P, T]], base=0, channel_multiplier=1).then_inc(s_iota, 1)
                pool.memset(pad_i[:, :], PAD_NODE).then_inc(s_pad, 1)
                pool.wait_ge(s_z, 1)
                for a in range(AGGS):
                    pool.dma_start(g.agg[a][NP:AROWS, :], g.zeros0[:, 0:GW]).then_inc(g.s_c[a], 16)

            @block.vector
            def _(dve):
                dve.memset(g.X[:, FULL:T, :], 0.0).then_inc(s_x0, 1)
                dve.memset(g.zeros0[:, :], 0.0).then_inc(s_z, 1)
                dve.memset(cut(g.XN, D, [GW, T], [1, 1]), 1.0)
                dve.memset(cut(g.XN, D + 1, [GW, T], [1, GW - D - 1]), 0.0)
                dve.memset(g.eps[:, :], LN_EPS)
                dve.memset(g.zero[:, :], 0.0)
                dve.memset(g.zrow[:, :], 0.0)
                dve.memset(g.ones[:, :], 1.0)
                dve.wait_ge(s_iota, 3)
                dve.tensor_copy(g.iota_b[:, :], iota_i[:, :])
                dve.tensor_copy(g.iota[:, :], iota_i[:, :]).then_inc(s_f, 1)
                dve.tensor_copy(g.pcol[:, :], col_i[:, :]).then_inc(s_f, 1)
                dve.tensor_copy(node_f[:, :], node_i[:, :]).then_inc(s_f, 1)
                dve.tensor_scalar(out=blk_i[:, :], in0=iota_i[:, :], scalar1=5, scalar2=None,
                                  op0=ALU.logical_shift_right)
                dve.tensor_scalar(out=row_i[:, :], in0=col_i[:, :], scalar1=5, scalar2=None,
                                  op0=ALU.logical_shift_right).then_inc(s_blk, 1)
                dve.wait_ge(s_blk, 1)
                dve.tensor_copy(g.blk[:, :], blk_i[:, :])
                dve.tensor_copy(g.head[:, :], row_i[:, :]).then_inc(s_blk, 1)
                dve.wait_ge(s_blk, 2)
                dve.tensor_scalar(out=g.blk[:, :], in0=g.blk[:, :], scalar1=g.head[:, 0:1], scalar2=None,
                                  op0=ALU.is_equal)
                dve.wait_ge(s_f, 3)
                dve.tensor_scalar(out=g.ident[:, :], in0=g.iota[:, :], scalar1=g.pcol[:, 0:1], scalar2=None,
                                  op0=ALU.is_equal)
                dve.tensor_scalar(out=g.lower[:, :], in0=g.iota[:, :], scalar1=g.pcol[:, 0:1], scalar2=None,
                                  op0=ALU.is_lt)
                dve.tensor_scalar(out=g.valid[:, :], in0=node_f[:, :], scalar1=float(N), scalar2=None,
                                  op0=ALU.is_lt).then_inc(s_const, 1)
                dve.wait_ge(s_const, 1)


def norms_phase(nc, g, zero_agg=False):
    with phase(nc, ["s_st", "s_mv", "s_turn", "s_keep", "s_sd", "s_rs"]) as (held, sems):
        s_st, s_mv, s_turn, s_keep, s_sd, s_rs = sems
        G = 25
        assert T % G == 0
        ST = held.enter_context(nc.sbuf_tensor(own(nc, "st"), [P, G, 6], F32))
        MV = held.enter_context(nc.sbuf_tensor(own(nc, "mv"), [P, G, 2], F32))
        SD = held.enter_context(nc.sbuf_tensor(own(nc, "sd"), [P, T], F32))
        with nc.Block() as block:
            @block.vector
            def _(dve):
                with dve.Fori(0, T // G) as i:
                    for u in range(G):
                        last = dve.bn_stats(out=ST[:, u, :], in_=cut(g.X, (i * G + u) * D, [1, D]))
                    last.then_inc(s_st, 1)
                    dve.wait_ge(s_st, i + 1)
                    dve.sem_inc(s_turn, 1)
                    for u in range(G):
                        last = dve.bn_aggr(out=MV[:, u, :], in_=ST[:, u, :])
                    last.then_inc(s_mv, 1)
                    dve.wait_ge(s_mv, i + 1)
                    dve.tensor_copy(cut(g.mv, i * G * 2, [1, G * 2]), MV[:, :, :].rearrange("p g m -> p (g m)")
                                    ).then_inc(s_keep, 1)
                    dve.wait_ge(s_keep, i + 1)
                    dve.sem_inc(s_turn, 1)
                dve.wait_ge(s_sd, 1)
                dve.reciprocal(cut(g.mv, 1, [2, T]), SD[:, :]).then_inc(s_rs, 1)
                dve.wait_ge(s_rs, 1)

            @block.sync
            def _(sp):
                for q in range(4 if zero_agg else 0):
                    sp.dma_start(flat(g.agg[0], q * ZC, [4 * ZC, P], [1, ZC]), g.zeros0[:, :]).then_inc(g.s_agg, 16)

            @block.scalar
            def _(act):
                act.wait_ge(s_keep, T // G)
                act.activation(SD[:, :], cut(g.mv, 1, [2, T]), ACT.Sqrt, bias=g.eps[:, 0:1]).then_inc(s_sd, 1)


def qkv0_phase(nc, g, w):
    names = ["s_res", "s_xs", "s_keep", "s_xtp", "s_xt", "s_qkvp", "s_qkv", "s_sq", "s_ss",
             "s_sc", "s_nm", "s_fac", "s_fac2", "s_fac3", "s_qk", "s_qtp", "s_qt", "s_bias", "s_cf", "s_root", "s_turn"]
    with phase(nc, names, ["s_w", "s_kv0", "s_kv1", "s_qo0", "s_qo1"]) as (held, sems):
        (s_res, s_xs, s_keep, s_xtp, s_xt, s_qkvp, s_qkv, s_sq, s_ss, s_sc, s_nm, s_fac, s_fac2,
         s_fac3, s_qk, s_qtp, s_qt, s_bias, s_cf, s_root, s_turn, s_w, s_kv0, s_kv1, s_qo0, s_qo1) = sems
        sems.append(g.s_agg)
        s_kv, s_qo = (s_kv0, s_kv1), (s_qo0, s_qo1)

        def sb(name, shape, dt=F32):
            return held.enter_context(nc.sbuf_tensor(own(nc, name), shape, dt))

        W = sb("w_qkv", [P, 2, 4 * D])
        B = sb("b_qkv", [P, 3 * D])
        RB = sb("res_bias", [P, 3, D])
        C = sb("ss_scale", [P, 2 * H])
        F = sb("norm_scale", [P, 2 * H])
        XS = sb("xs", [P, 2, D])
        XT = sb("xt", [P, 2, D])
        QKV = sb("qkv", [P, 2, 3 * D])
        SQ = sb("sq", [P, 2, 2 * D])
        SS = sb("ss", [P, 2, 2 * H])
        SC = sb("sc", [P, 2, 2 * H])
        NM = sb("nm", [P, 2, 2 * H])
        FA = sb("fa", [P, 2, 2 * H])
        FB = sb("fb", [P, 2, 2 * H])
        QK = sb("qk", [P, 2, 2 * D])
        QT = sb("qt", [P, 2, D])
        pt = held.enter_context(nc.psum_tensor(own(nc, "pt"), [P, 2, 512], F32))
        pq = held.enter_context(nc.psum_tensor(own(nc, "pq"), [P, 2, 1024], F32))
        pr = held.enter_context(nc.psum_tensor(own(nc, "pr"), [P, 2, 512], F32))
        QSCALE = float(HD) ** 0.25
        NW = 16 * 7
        with nc.Block() as block:
            @block.sync
            def _(sp):
                for s in (*s_kv, *s_qo):
                    sp.sem_inc(s, 32)
                sp.dma_start(W[:, :, 0:3 * D], w.L0_mix_Wqkv.rearrange("(c p) o -> p c o", p=P)).then_inc(s_w, 16)
                sp.dma_start(W[:, :, 3 * D:4 * D], w.L0_gnn_W1.rearrange("(c p) o -> p c o", p=P)).then_inc(s_w, 16)
                sp.dma_start(B[:, :], w.L0_mix_bqkv.partition_broadcast(P)).then_inc(s_w, 16)
                for k, b in enumerate((w.L0_gnn_b1, w.L0_gnn_b2, w.L0_mix_bproj)):
                    sp.dma_start(RB[:, k, :], b.partition_broadcast(P)).then_inc(s_w, 16)
                sp.dma_start(C[:, 0:H], w.L0_mix_temperature.partition_broadcast(P)).then_inc(s_w, 16)
                with sp.Fori(0, T // 2) as i:
                    for a in range(1, AGGS):
                        sp.dma_start(flat(g.agg[a], i * (2 * P * GW), [2 * GW, P], [1, 2 * GW]),
                                     g.zeros0[:, 0:2 * GW]).then_inc(g.s_agg, 16)
                    for u in (0, 1):
                        n = i * 2 + u
                        sp.wait_ge(s_qk, done(n))
                        sp.dma_start(flat(g.kv, n * (P * 2 * D), [2 * D, P], [1, D]),
                                     QK[:, u, D:2 * D]).then_inc(s_kv[u], 16)
                        sp.dma_start(flat(g.kv, n * (P * 2 * D) + D, [2 * D, P], [1, D]),
                                     QKV[:, u, 2 * D:3 * D]).then_inc(s_kv[u], 16)
                        sp.wait_ge(s_qt, done(n))
                        for c in (0, 1):
                            sp.dma_start(flat(g.qT, c * P * NP + n * P, [NP, P], [1, P]),
                                         QT[:, u, c * P:(c + 1) * P]).then_inc(s_qo[u], 16)
                for s in (*s_kv, *s_qo):
                    sp.wait_ge(s, landed(T // 2 - 1, 2))
                sp.wait_ge(g.s_agg, 16 * (4 + (AGGS - 1) * (T // 2)))

            @block.vector
            def _(dve):
                for s in (s_root, s_xs, s_qkv, s_ss, s_sc, s_fac, s_fac2, s_fac3, s_qk):
                    dve.sem_inc(s, 2)
                dve.wait_ge(s_w, NW)
                dve.tensor_scalar(out=F[:, 0:H], in0=C[:, 0:H], scalar1=QSCALE * QSCALE, scalar2=None,
                                  op0=ALU.mult).then_inc(s_cf, 1)
                dve.memset(F[:, H:2 * H], QSCALE)
                dve.wait_ge(s_cf, 1)
                dve.memset(C[:, 0:H], QSCALE * QSCALE)
                dve.memset(C[:, H:2 * H], 1.0)
                dve.tensor_tensor(out=RB[:, 0, :], in0=RB[:, 0, :], in1=RB[:, 1, :], op=ALU.add).then_inc(s_cf, 1)
                dve.wait_ge(s_cf, 2)
                dve.tensor_tensor(out=RB[:, 0, :], in0=RB[:, 0, :], in1=RB[:, 2, :], op=ALU.add).then_inc(s_bias, 1)

                def normed(i):
                    for u in (0, 1):
                        n = i * 2 + u
                        dve.wait_ge(s_keep, done(n - 2))
                        dve.wait_ge(s_xtp, done(n - 2))
                        dve.tensor_scalar(out=XS[:, u, :], in0=cut(g.X, n * D, [1, D]), scalar1=cut(g.mv, n * 2, [1, 1]),
                                          scalar2=cut(g.mv, n * 2 + 1, [1, 1]), op0=ALU.subtract, op1=ALU.mult).then_inc(s_xs, 1)

                def biased(i, u):
                    n = i * 2 + u
                    dve.wait_ge(s_qkvp, done(n))
                    dve.wait_ge(s_qk, done(n - 2))
                    dve.wait_ge(s_kv[u], landed(i - 1, 2))
                    dve.tensor_tensor(out=QKV[:, u, :], in0=pq[:, u, 0:3 * D], in1=B[:, :],
                                      op=ALU.add).then_inc(s_qkv, 1)
                    dve.tensor_tensor(out=cut(g.X, n * D, [1, D]), in0=pq[:, u, 3 * D:4 * D],
                                      in1=cut(g.X, n * D, [1, D]), op=ALU.add).then_inc(s_root, 1)

                def scaled(i):
                    for u in (0, 1):
                        n = i * 2 + u
                        dve.wait_ge(s_sq, done(n))
                        dve.tensor_reduce(out=SS[:, u, :], in_=SQ[:, u, :].rearrange("p (h d) -> p h d", d=HD),
                                          axis=AX.X, op=ALU.add).then_inc(s_ss, 1)
                    for u in (0, 1):
                        n = i * 2 + u
                        dve.wait_ge(s_ss, done(n))
                        dve.tensor_tensor(out=SC[:, u, :], in0=SS[:, u, :], in1=C[:, :], op=ALU.mult).then_inc(s_sc, 1)
                    for u in (0, 1):
                        n = i * 2 + u
                        dve.wait_ge(s_sc, done(n))
                        dve.tensor_scalar(out=SS[:, u, :], in0=SC[:, u, :], scalar1=1e-24, scalar2=None,
                                          op0=ALU.max).then_inc(s_fac, 1)

                def divided(i):
                    for u in (0, 1):
                        n = i * 2 + u
                        dve.wait_ge(s_nm, done(n))
                        dve.reciprocal(FA[:, u, :], NM[:, u, :]).then_inc(s_fac2, 1)
                    for u in (0, 1):
                        n = i * 2 + u
                        dve.wait_ge(s_fac2, done(n))
                        dve.tensor_tensor(out=FB[:, u, 0:H], in0=FA[:, u, 0:H], in1=F[:, 0:H], op=ALU.mult)
                        dve.scalar_tensor_tensor(out=FB[:, u, H:2 * H], in0=FA[:, u, H:2 * H],
                                                 scalar=cut(g.valid, n, [1, 1]), in1=F[:, H:2 * H],
                                                 op0=ALU.mult, op1=ALU.mult).then_inc(s_fac3, 1)
                    for u in (0, 1):
                        n = i * 2 + u
                        dve.wait_ge(s_fac3, done(n))
                        dve.wait_ge(s_qtp, done(n - 2))
                        dve.wait_ge(s_kv[u], landed(i - 1, 2))
                        dve.tensor_tensor(out=QK[:, u, :].rearrange("p (h d) -> p h d", d=HD),
                                          in0=QKV[:, u, 0:2 * D].rearrange("p (h d) -> p h d", d=HD),
                                          in1=cut(FB, u * 2 * H, [1, 2 * H], [0, HD]), op=ALU.mult).then_inc(s_qk, 1)

                def turn(i, first, last):
                    if not first:
                        scaled(i - 1)
                        divided(i - 1)
                    biased(i, 0)
                    if not last:
                        normed(i + 2)
                    biased(i, 1)

                normed(0)
                normed(1)
                turn(0, True, False)
                with dve.Fori(1, T // 2 - 2) as i:
                    turn(i, False, False)
                turn(T // 2 - 2, False, True)
                turn(T // 2 - 1, False, True)
                scaled(T // 2 - 1)
                divided(T // 2 - 1)
                dve.wait_ge(s_qk, done(T - 1))

            @block.scalar
            def _(act):
                for s in (s_xt, s_sq, s_nm, s_qt):
                    act.sem_inc(s, 2)

                def turned(i):
                    for u in (0, 1):
                        n = i * 2 + u
                        act.wait_ge(s_xtp, done(n))
                        act.wait_ge(s_qkvp, done(n - 2))
                        act.activation(XT[:, u, :], pt[:, u, 0:D], ACT.Copy).then_inc(s_xt, 1)

                def squares(i):
                    for u in (0, 1):
                        n = i * 2 + u
                        act.wait_ge(s_qkv, done(n))
                        act.wait_ge(s_ss, done(n - 2))
                        act.activation(SQ[:, u, :], QKV[:, u, 0:2 * D], ACT.Square).then_inc(s_sq, 1)

                def roots(i):
                    for u in (0, 1):
                        n = i * 2 + u
                        act.wait_ge(s_fac, done(n))
                        act.wait_ge(s_fac2, done(n - 2))
                        act.activation(NM[:, u, :], SS[:, u, :], ACT.Sqrt, bias=g.zero[:, 0:1]).then_inc(s_nm, 1)

                def q_out(i):
                    for u in (0, 1):
                        n = i * 2 + u
                        act.wait_ge(s_qtp, done(n))
                        act.wait_ge(s_qo[u], landed(i - 1, 2))
                        act.activation(QT[:, u, :], pr[:, u, 0:D], ACT.Copy).then_inc(s_qt, 1)

                def turn(i, first, last):
                    if not first:
                        roots(i - 1)
                    if not last:
                        turned(i + 1)
                    if not first:
                        q_out(i - 1)
                    squares(i)

                turned(0)
                turn(0, True, False)
                with act.Fori(1, T // 2 - 1) as i:
                    turn(i, False, False)
                turn(T // 2 - 1, False, True)
                roots(T // 2 - 1)
                q_out(T // 2 - 1)
                act.wait_ge(s_qt, done(T - 1))

            @block.gpsimd
            def _(pool):
                pool.sem_inc(s_keep, 2)
                pool.wait_ge(s_bias, 1)

                def copied(i):
                    for u in (0, 1):
                        n = i * 2 + u
                        pool.wait_ge(s_xs, done(n))
                        pool.tensor_copy(cut(g.XN, n * GW, [1, D]), XS[:, u, :]).then_inc(s_keep, 1)

                def biased(i):
                    for u in (0, 1):
                        n = i * 2 + u
                        pool.wait_ge(s_root, done(n))
                        pool.tensor_tensor(out=cut(g.X, n * D, [1, D]), in0=cut(g.X, n * D, [1, D]),
                                           in1=RB[:, 0, :], op=ALU.add).then_inc(s_res, 1)

                copied(0)
                with pool.Fori(0, T // 2 - 1) as i:
                    copied(i + 1)
                    biased(i)
                biased(T // 2 - 1)
                pool.wait_ge(s_res, T)
                for s in g.s_c:
                    pool.wait_ge(s, 16)

            @block.tensor
            def _(pe):
                for s in (s_xtp, s_qkvp, s_qtp):
                    pe.sem_inc(s, 2)
                pe.wait_ge(s_w, NW)

                def turned(i):
                    for u in (0, 1):
                        n = i * 2 + u
                        pe.wait_ge(s_xs, done(n))
                        pe.wait_ge(s_xt, done(n - 2))
                        for c in (0, 1):
                            last = pe.transpose(pt[:, u, c * P:(c + 1) * P], XS[:, u, c * P:(c + 1) * P], g.ident[:, :])
                        last.then_inc(s_xtp, 1)

                def products(i, u):
                    n = i * 2 + u
                    pe.wait_ge(s_xt, done(n))
                    pe.wait_ge(s_qkv, done(n - 2))
                    pe.wait_ge(s_root, done(n - 2))
                    for c in (0, 1):
                        for a, b in ((0, 512), (512, 1024)):
                            last = pe.matmul(pq[:, u, a:b], XT[:, u, c * P:(c + 1) * P], W[:, c, a:b],
                                             start=c == 0, stop=c == 1)
                    last.then_inc(s_qkvp, 1)

                def q_turned(i):
                    for u in (0, 1):
                        n = i * 2 + u
                        pe.wait_ge(s_qk, done(n))
                        pe.wait_ge(s_qt, done(n - 2))
                        for c in (0, 1):
                            last = pe.transpose(pr[:, u, c * P:(c + 1) * P], QK[:, u, c * P:(c + 1) * P], g.ident[:, :])
                        last.then_inc(s_qtp, 1)

                def turn(i, first, last):
                    products(i, 0)
                    if not last:
                        turned(i + 1)
                    products(i, 1)
                    if not first:
                        q_turned(i - 1)

                turned(0)
                turn(0, True, False)
                with pe.Fori(1, T // 2 - 1) as i:
                    turn(i, False, False)
                turn(T // 2 - 1, False, True)
                q_turned(T // 2 - 1)

AGGS = 4
AROWS = NP + P
BATCH = 8
U = 2 * BATCH
TURNS = STEPS // U
assert TURNS * U == STEPS
ZC = NP * GW // P // 4

PACK = 4


def turn_windows(nc, g, i, engine):
    _, packs = nc.values_load_multi_w_load_instructions(
        g.windows[0:1, bass.ds(i * (U // PACK), U // PACK)], engines=(engine,), min_val=0, max_val=T ** PACK - 1)
    return packs


def window(packs, j):
    return packs[j // PACK] // T ** (j % PACK) % T


class Graph0:

    def __init__(self, nc, g, held):
        def sb(name, shape, dt=F32):
            return held.enter_context(nc.sbuf_tensor(own(nc, name), shape, dt))

        self.nc, self.g = nc, g
        self.KB = sb("src_rows", [P, 2, BATCH, P])
        self.OH = sb("one_hot", [P, 2, BATCH, P], BF16)
        self.S = sb("same_src", [P, 2, BATCH, P], BF16)
        self.junk = sb("junk", [P, P], BF16)
        self.DUP = sb("dup", [P, 2, BATCH])
        self.I1 = sb("i1", [P, 2, BATCH])
        self.I2 = sb("i2", [P, 2, BATCH])
        self.IDX = sb("idx", [P, 2, BATCH], I32)
        self.TR = sb("spare", [P, 1])
        self.MT = sb("mt", [P, 4, P])
        self.R = sb("rows", [P, BATCH, GW])
        self.pm = held.enter_context(nc.psum_tensor(own(nc, "pm"), [P, 512], F32))
        self.pr = held.enter_context(nc.psum_tensor(own(nc, "pr"), [P, 2, 512], F32))
        self.sems = [held.enter_context(nc.semaphore(own(nc, n))) for n in (
            "s_oh", "s_dup", "s_i1", "s_i2", "s_idx", "s_m", "s_mt", "s_r", "s_rc", "s_tr", "s_go", "s_b0", "s_b1")]
        (self.s_oh, self.s_dup, self.s_i1, self.s_i2, self.s_idx, self.s_m, self.s_mt, self.s_r, self.s_rc,
         self.s_tr, self.s_go, *self.s_b) = self.sems
        with nc.Block() as block:
            @block.sync
            def _(sp):
                for s in self.s_b:
                    sp.sem_inc(s, 16)

            @block.vector
            def _(dve):
                dve.sem_inc(self.s_oh, U)
                dve.sem_inc(self.s_dup, U)
                for s in (self.s_idx, self.s_i1, self.s_i2):
                    dve.sem_inc(s, 2)
                dve.tensor_scalar(out=self.TR[:, :], in0=g.pcol[:, :], scalar1=float(NP), scalar2=None,
                                  op0=ALU.add).then_inc(self.s_tr, 1)
                dve.wait_ge(self.s_tr, 1)

            @block.scalar
            def _(act):
                act.sem_inc(self.s_mt, U)
                act.sem_inc(self.s_rc, U)

            @block.gpsimd
            def _(pool):
                pool.sem_inc(self.s_go, U)

            @block.tensor
            def _(pe):
                pe.sem_inc(self.s_m, U)
                pe.sem_inc(self.s_r, U)

    def fin(self, k):
        return k + 1 + U

    def sync_half(self, sp, i, h):
        sp.wait_ge(self.s_idx, i * 2 + h + 1)
        sp.dma_start(self.KB[:, h, :, :], flat(self.g.srows, (i * U + h * BATCH) * P, [0, P], [1, BATCH * P])
                     ).then_inc(self.s_b[h], 16)

    def vector_masks(self, dve, i, h):
        g, fin = self.g, self.fin
        k0 = i * U + h * BATCH
        dve.wait_ge(self.s_b[h], landed(i))
        dve.wait_ge(self.s_m, fin(k0 - U + BATCH - 1))
        for j in range(BATCH):
            k = k0 + j
            dve.tensor_scalar(out=self.OH[:, h, j, :], in0=g.iota_b[:, :], scalar1=cut(g.rel, k, [1, 1]),
                              scalar2=None, op0=ALU.is_equal)
            dve.tensor_scalar(out=self.S[:, h, j, :], in0=self.KB[:, h, j, :], scalar1=cut(g.src, k, [1, 1]),
                              scalar2=None, op0=ALU.is_equal).then_inc(self.s_oh, 1)
            dve.wait_ge(self.s_dup, fin(k - 1))
            dve.scalar_tensor_tensor(out=self.junk[:, :], in0=self.KB[:, h, j, :], scalar=cut(g.src, k, [1, 1]),
                                     in1=g.lower[:, :], op0=ALU.is_equal, op1=ALU.mult,
                                     accum_out=self.DUP[:, h, j:j + 1]).then_inc(self.s_dup, 1)

    def vector_rows(self, dve, i, h):
        g, fin = self.g, self.fin
        k0 = i * U + h * BATCH
        m = i * 2 + h
        src = cut(g.src, k0, [1, BATCH])
        dve.wait_ge(self.s_dup, fin(k0 + BATCH - 1))
        dve.tensor_scalar(out=self.DUP[:, h, :], in0=self.DUP[:, h, :], scalar1=1.0, scalar2=None, op0=ALU.min)
        dve.tensor_scalar(out=self.I1[:, h, :], in0=src, scalar1=-1.0, scalar2=self.TR[:, 0:1], op0=ALU.mult,
                          op1=ALU.add).then_inc(self.s_i1, 1)
        dve.wait_ge(self.s_i1, done(m))
        dve.tensor_tensor(out=self.I2[:, h, :], in0=self.I1[:, h, :], in1=self.DUP[:, h, :],
                          op=ALU.mult).then_inc(self.s_i2, 1)
        dve.wait_ge(self.s_i2, done(m))
        dve.wait_ge(self.s_go, fin(k0 - BATCH - 1 + AGGS))
        dve.tensor_tensor(out=self.IDX[:, h, :], in0=self.I2[:, h, :], in1=src, op=ALU.add).then_inc(self.s_idx, 1)

    def scalar_steps(self, act, i, first, last):
        fin = self.fin

        def rows(j):
            k = i * U + j
            act.wait_ge(self.s_r, fin(k))
            act.wait_ge(self.s_go, fin(k - 4))
            act.activation(self.R[:, j % BATCH, :], self.pr[:, j % 2, 0:GW], ACT.Copy).then_inc(self.s_rc, 1)

        for j in range(first, last):
            k = i * U + j
            act.wait_ge(self.s_m, fin(k))
            act.wait_ge(self.s_r, fin(k - 4))
            act.activation(self.MT[:, j % 4, :], self.pm[:, 0:P], ACT.Copy).then_inc(self.s_mt, 1)
            if j:
                rows(j - 1)
        if last == U:
            rows(U - 1)

    def pool_half(self, pool, i, h):
        pool.wait_ge(self.s_idx, done(i * 2 + h))
        for j in range(BATCH):
            k = i * U + h * BATCH + j
            a = j % AGGS
            pool.wait_ge(self.s_rc, self.fin(k))
            pool.wait_ge(self.g.s_c[a], 16 * (i * 4 + h * 2 + j // 4 + 1))
            pool.sem_inc(self.s_go, 1)
            pool.indirect_dma_start(
                out=self.g.agg[a][:, :], out_offset=bass.IndirectOffsetOnAxis(ap=self.IDX[:, h, j:j + 1], axis=0),
                in_=self.R[:, j, :], in_offset=None, compute_op=ALU.add).then_inc(self.g.s_c[a], 16)

    def tensor_steps(self, pe, i, first, last):
        fin = self.fin

        def to_rows(j):
            k = i * U + j
            at = window(self.packs, j)
            pe.wait_ge(self.s_mt, fin(k))
            pe.wait_ge(self.s_rc, fin(k - 2))
            pe.matmul(self.pr[:, j % 2, 0:GW], self.MT[:, j % 4, :], cut(self.g.XN, at * GW, [1, GW]), start=True,
                      stop=True).then_inc(self.s_r, 1)

        if first == 0:
            self.packs = turn_windows(self.nc, self.g, i, mybir.EngineType.PE)
        for j in range(first, last):
            k = i * U + j
            pe.wait_ge(self.s_oh, fin(k))
            pe.wait_ge(self.s_mt, fin(k - 1))
            pe.matmul(self.pm[:, 0:P], self.OH[:, j // BATCH, j % BATCH, :], self.S[:, j // BATCH, j % BATCH, :],
                      start=True, stop=True).then_inc(self.s_m, 1)
            if j:
                to_rows(j - 1)
        if last == U:
            to_rows(U - 1)

    def end(self, nc):
        with nc.Block() as block:
            @block.gpsimd
            def _(pool):
                for s in self.g.s_c:
                    pool.wait_ge(s, 16 * (STEPS // AGGS + 1))
                for s in self.sems:
                    pool.sem_clear(s)

SHIFTS = [(0, 0)] + [(a, b) for b in (4, 8, 12, 16) for a in range(4)]
PAIRS = len(SHIFTS)
TURNED = [0, 1, 2, 3, 4, 8, 12, 16]
SECOND = 0.5
GH = H // 2


def pair_weight(a, b):
    return 1.0 if b - a in (0, 16) else 2.0


def over_pairs(eng, q, pair):
    if q == 0:
        with eng.Fori(0, T // 2) as i:
            pair(i, i)
    else:
        with eng.Fori(0, LEFT) as a:
            pair(a * TAIL, a + T // 2)
            with eng.Fori(1, TAIL) as b:
                pair(a * TAIL + b, None)

LEFT = TURNS - T // 2 * 2
TAIL = T // 2 // LEFT
assert LEFT * TAIL == T // 2


def keys0_phase(nc, g, graph, q):
    names = ["s_dup", "s_z", "s_acc", "s_zero", "s_out", "s_tp", "s_m"]
    with phase(nc, names, ["s_l0", "s_l1"]) as (held, sems):
        s_dup, s_z, s_acc, s_zero, s_out, s_tp, s_m, s_l0, s_l1 = sems
        s_l = (s_l0, s_l1)

        def sb(name, shape, dt=F32):
            return held.enter_context(nc.sbuf_tensor(own(nc, name), shape, dt))

        LAST = PAIRS * P
        ZW = LAST + P + 1
        GRAM = ZW
        KV = sb("kv_in", [P, 2, 2, P])
        V = sb("v", [P, 2, P])
        KD = sb("k_twice", [P, 2, GH, 2, HD])
        Z = sb("z", [P, 2, ZW + 3])
        S = sb("sums", [P, ZW + P + 1])
        acc = held.enter_context(nc.psum_tensor(own(nc, "acc"), [P, 2560], F32))
        assert GRAM + P + 1 <= 2560
        with nc.Block() as block:
            @block.sync
            def _(sp):
                for s in s_l:
                    sp.sem_inc(s, 32)

                def pair(i, turn):
                    for u in (0, 1):
                        if turn is not None:
                            graph.sync_half(sp, turn, u)
                        sp.wait_ge(s_dup, done(i * 2 + u - 2))
                        for c in (0, 1):
                            sp.dma_start(KV[:, u, c, :], flat(g.kv, (i * 2 + u) * (P * 2 * D) + c * D + q * P,
                                                              [2 * D, P], [1, P])).then_inc(s_l[u], 16)

                over_pairs(sp, q, pair)

            @block.scalar
            def _(act):
                act.sem_inc(s_dup, 2)

                def twice(i, u):
                    n = i * 2 + u
                    act.wait_ge(s_l[u], landed(i, 2))
                    act.wait_ge(s_z, done(n - 2))
                    act.wait_ge(s_acc, done(n - 2))
                    act.activation(KD[:, u, :, :, :], cut(KV, u * 2 * P, [HD, GH], [0, 2], [1, HD]), ACT.Copy)
                    act.activation(Z[:, u, LAST:LAST + P], KV[:, u, 0, :], ACT.Copy)
                    act.activation(V[:, u, :], KV[:, u, 1, :], ACT.Copy)
                    act.activation(Z[:, u, LAST + P:LAST + P + 1], cut(g.valid, n, [1, 1]),
                                   ACT.Copy).then_inc(s_dup, 1)

                def pair(i, turn, last=False):
                    if turn is not None:
                        graph.scalar_steps(act, turn, 0, 3)
                    twice(i, 1)
                    if turn is not None:
                        graph.scalar_steps(act, turn, 3, 12)
                    if not last:
                        twice(i + 1, 0)
                    if turn is not None:
                        graph.scalar_steps(act, turn, 12, U)

                twice(0, 0)
                if q == 0:
                    with act.Fori(0, T // 2 - 1) as i:
                        pair(i, i)
                    pair(T // 2 - 1, T // 2 - 1, True)
                else:
                    with act.Fori(0, LEFT - 1) as a:
                        pair(a * TAIL, a + T // 2)
                        with act.Fori(1, TAIL) as b:
                            pair(a * TAIL + b, None)
                    pair((LEFT - 1) * TAIL, LEFT - 1 + T // 2)
                    with act.Fori(1, TAIL - 1) as b:
                        pair((LEFT - 1) * TAIL + b, None)
                    pair(T // 2 - 1, None, True)

            @block.gpsimd
            def _(pool):
                def pair(i, turn):
                    if turn is not None:
                        graph.pool_half(pool, turn, 0)
                        graph.pool_half(pool, turn, 1)

                over_pairs(pool, q, pair)

            @block.vector
            def _(dve):
                dve.sem_inc(s_z, 2)

                def pair(i, turn):
                    for u in (0, 1):
                        n = i * 2 + u
                        if turn is not None:
                            graph.vector_masks(dve, turn, u)
                        dve.wait_ge(s_dup, done(n))
                        dve.wait_ge(s_acc, done(n - 2))
                        dve.tensor_tensor(out=Z[:, u, 0:P].rearrange("p (h d) -> p h d", d=HD),
                                          in0=KD[:, u, :, 0, :], in1=KD[:, u, :, 0, :], op=ALU.mult)
                        for k, b in enumerate((4, 8, 12, 16)):
                            at = u * GH * 2 * HD
                            last = dve.tensor_tensor(
                                out=Z[:, u, (1 + 4 * k) * P:(5 + 4 * k) * P].rearrange("p (a h d) -> p a h d", a=4, d=HD),
                                in0=cut(KD, at, [1, 4], [2 * HD, GH], [1, HD]),
                                in1=cut(KD, at + b, [0, 4], [2 * HD, GH], [1, HD]), op=ALU.mult)
                        last.then_inc(s_z, 1)
                        if turn is not None:
                            graph.vector_rows(dve, turn, u)

                over_pairs(dve, q, pair)
                dve.wait_ge(s_zero, 2)
                dve.tensor_copy(S[:, :], acc[:, 0:ZW + P + 1]).then_inc(s_out, 1)
                dve.wait_ge(s_out, 1)
                for f in range(PAIRS + 1):
                    c = (SECOND * pair_weight(*SHIFTS[f]) if f < PAIRS else float(HD) ** 0.5) / N
                    dve.wait_ge(s_tp, f + 1)
                    dve.scalar_tensor_tensor(out=g.WS[:, q, f, :], in0=acc[:, f % 2 * 512:f % 2 * 512 + P], scalar=c,
                                             in1=g.blk[:, :], op0=ALU.mult, op1=ALU.mult).then_inc(s_m, 1)
                dve.scalar_tensor_tensor(out=g.GS[:, q, :], in0=S[:, GRAM:GRAM + P], scalar=SECOND / N,
                                         in1=g.blk[:, :], op0=ALU.mult, op1=ALU.mult)
                dve.tensor_scalar(out=g.ks[:, q:q + 1], in0=S[:, GRAM + P:GRAM + P + 1],
                                  scalar1=float(HD) ** 0.5 / N, scalar2=None, op0=ALU.mult)
                dve.tensor_scalar(out=g.vs[:, q:q + 1], in0=S[:, LAST + P:LAST + P + 1], scalar1=float(HD) / N,
                                  scalar2=None, op0=ALU.mult).then_inc(s_out, 1)

            @block.tensor
            def _(pe):
                pe.sem_inc(s_acc, 2)

                def zero(start, stop):
                    for b in range(5):
                        last = pe.matmul(acc[:, b * 512:(b + 1) * 512], g.zrow[0:1, 0:P], g.zrow[0:1, :],
                                         start=start, stop=stop)
                    return last

                def pair(i, turn):
                    for u in (0, 1):
                        pe.wait_ge(s_z, done(i * 2 + u))
                        for b in range(6):
                            if b < 5:
                                z0, z1 = b * 512, min(b * 512 + 512, ZW)
                                last = pe.matmul(acc[:, z0:z1], V[:, u, :], Z[:, u, z0:z1], start=False, stop=False)
                            else:
                                last = pe.matmul(acc[:, GRAM:GRAM + P + 1], Z[:, u, LAST:LAST + P], Z[:, u, LAST:LAST + P + 1],
                                                 start=False, stop=False)
                                last.then_inc(s_acc, 1)
                            if turn is not None:
                                at = u * 6 + b
                                graph.tensor_steps(pe, turn, at * U // 12, (at + 1) * U // 12)

                zero(True, False).then_inc(s_zero, 1)
                over_pairs(pe, q, pair)
                zero(False, True).then_inc(s_zero, 1)
                pe.wait_ge(s_out, 1)
                for f in range(PAIRS + 1):
                    if f >= 2:
                        pe.wait_ge(s_m, f - 1)
                    pe.transpose(acc[:, f % 2 * 512:f % 2 * 512 + P], S[:, f * P:(f + 1) * P], g.ident[:, :]).then_inc(s_tp, 1)


def queries0_phase(nc, g, graph, w):
    names = ["s_go", "s_turn", "s_z", "s_zr", "s_u", "s_t", "s_d", "s_d2", "s_rec", "s_ot", "s_pp", "s_add"]
    with phase(nc, names, ["s_w", "s_l0", "s_l1"]) as (held, sems):
        s_go, s_turn, s_z, s_zr, s_u, s_t, s_d, s_d2, s_rec, s_ot, s_pp, s_add, s_w, s_l0, s_l1 = sems
        s_l = (s_l0, s_l1)

        def sb(name, shape, dt=F32):
            return held.enter_context(nc.sbuf_tensor(own(nc, name), shape, dt))

        M = 2 * P
        FIRST = T // 2 + LEFT
        WP = sb("w_proj", [P, 2, D])
        R = sb("turned", [P, 2, len(TURNED), M])
        Z = sb("z", [P, PAIRS, M])
        TT = sb("t", [P, 2, M])
        DE = sb("den", [P, 2, M])
        OT = TT
        py = held.enter_context(nc.psum_tensor(own(nc, "py"), [P, 2, 512], F32))
        pu = held.enter_context(nc.psum_tensor(own(nc, "pu"), [P, 2, 512], F32))
        pp = held.enter_context(nc.psum_tensor(own(nc, "pp"), [P, 512], F32))
        CHUNKS = [(0, 5), (5, 9), (9, 13), (13, 17)]

        def pd(q):
            return cut(pu, q * 512 + M, [1, M])

        def chunk(n, c):
            return n * 4 + c + 9
        with nc.Block() as block:
            @block.sync
            def _(sp):
                for s in s_l:
                    sp.sem_inc(s, 16)
                sp.dma_start(WP[:, :, :], w.L0_mix_Wproj.rearrange("(c p) o -> p c o", p=P)).then_inc(s_w, 16)
                with sp.Fori(0, T // 2) as i:
                    for q in (0, 1):
                        n = i * 2 + q
                        graph.sync_half(sp, i + FIRST, q)
                        sp.wait_ge(s_t, done(n - 2))
                        sp.wait_ge(s_zr, chunk(n - 2, 3))
                        sp.wait_ge(s_z, chunk(n - 2, 3))
                        sp.dma_start(R[:, q, 0, :], flat(g.qT, q * P * NP + i * M, [NP, P], [1, M])).then_inc(s_l[q], 16)

            @block.vector
            def _(dve):
                for s in (s_turn, s_t, s_d2, s_rec, s_ot, s_add):
                    dve.sem_inc(s, 2)
                dve.sem_inc(s_z, 8)

                def turned(i, q):
                    dve.wait_ge(s_l[q], landed(i))
                    dve.sem_inc(s_go, 1)
                    for k, r in enumerate(TURNED[1:]):
                        last = dve.stream_shuffle(out=R[:, q, k + 1, :], in_=R[:, q, 0, :],
                                                  mask=[(j + r) % HD for j in range(HD)])
                    last.then_inc(s_turn, 1)

                def pairs(i, q):
                    n = i * 2 + q
                    dve.wait_ge(s_turn, done(n))
                    for k in range(4):
                        dve.wait_ge(s_zr, chunk(n - 1, k))
                        if k == 0:
                            dve.tensor_tensor(out=Z[:, 0, :], in0=R[:, q, 0, :], in1=R[:, q, 0, :], op=ALU.mult)
                        dve.tensor_tensor(out=Z[:, 1 + 4 * k:5 + 4 * k, :], in0=R[:, q, 0:4, :],
                                          in1=cut(R, (q * 8 + 4 + k) * M, [0, 4], [1, M]),
                                          op=ALU.mult).then_inc(s_z, 1)
                    dve.wait_ge(s_u, done(n))
                    dve.wait_ge(s_pp, i + 1)
                    dve.scalar_tensor_tensor(out=TT[:, q, :], in0=pu[:, q, 0:M], scalar=g.ks[:, q:q + 1],
                                             in1=R[:, q, 0, :], op0=ALU.add, op1=ALU.mult).then_inc(s_t, 1)

                def divide(i):
                    for q in (0, 1):
                        n = i * 2 + q
                        dve.wait_ge(s_d, done(n))
                        dve.tensor_scalar(out=DE[:, q, :], in0=pd(q), scalar1=float(HD), scalar2=None,
                                          op0=ALU.add).then_inc(s_d2, 1)
                    for q in (0, 1):
                        n = i * 2 + q
                        dve.wait_ge(s_d2, done(n))
                        dve.reciprocal(DE[:, q, :], DE[:, q, :]).then_inc(s_rec, 1)
                    for q in (0, 1):
                        n = i * 2 + q
                        dve.wait_ge(s_rec, done(n))
                        dve.wait_ge(s_zr, chunk(n, 3))
                        dve.scalar_tensor_tensor(out=OT[:, q, :], in0=py[:, q, 0:M], scalar=g.vs[:, q:q + 1],
                                                 in1=DE[:, q, :], op0=ALU.add, op1=ALU.mult).then_inc(s_ot, 1)

                def add(i):
                    dve.wait_ge(s_pp, i + 2)
                    x = cut(g.X, i * 2 * D, [1, 2 * D])
                    dve.tensor_tensor(out=x, in0=pp[:, :], in1=x, op=ALU.add).then_inc(s_add, 1)

                def pair(i, before):
                    graph.vector_masks(dve, i + FIRST, 0)
                    graph.vector_rows(dve, i + FIRST, 0)
                    turned(i, 0)
                    if before:
                        divide(i - 1)
                    pairs(i, 0)
                    if before:
                        add(i - 1)
                    graph.vector_masks(dve, i + FIRST, 1)
                    graph.vector_rows(dve, i + FIRST, 1)
                    turned(i, 1)
                    pairs(i, 1)

                pair(0, False)
                with dve.Fori(1, T // 2) as i:
                    pair(i, True)
                divide(T // 2 - 1)
                add(T // 2 - 1)
                dve.wait_ge(s_add, 2 + T // 2)

            @block.scalar
            def _(act):
                with act.Fori(0, T // 2) as i:
                    graph.scalar_steps(act, i + FIRST, 0, U)

            @block.gpsimd
            def _(pool):
                with pool.Fori(0, T // 2) as i:
                    for h in (0, 1):
                        graph.pool_half(pool, i + FIRST, h)

            @block.tensor
            def _(pe):
                for s in (s_u, s_d):
                    pe.sem_inc(s, 2)
                pe.sem_inc(s_pp, 1)
                pe.sem_inc(s_zr, 8)
                pe.wait_ge(s_w, 16)

                def heads(i):
                    for q in (0, 1):
                        pe.wait_ge(s_t, done(i * 2 + q))
                        pe.matmul(pd(q), g.blk[:, :], TT[:, q, :], start=True, stop=True).then_inc(s_d, 1)

                def project(i):
                    pe.wait_ge(s_ot, done(i * 2 + 1))
                    pe.wait_ge(s_add, i + 2)
                    for t in (0, 1):
                        for q in (0, 1):
                            last = pe.matmul(pp[:, t * D:(t + 1) * D], OT[:, q, t * P:(t + 1) * P], WP[:, q, :],
                                             start=q == 0, stop=q == 1)
                    last.then_inc(s_pp, 1)

                def group(i, q, at):
                    n = i * 2 + q
                    pe.wait_ge(s_l[q], landed(i))
                    pe.wait_ge(s_d2, done(n - 2))
                    pe.matmul(pu[:, q, 0:M], g.GS[:, q, :], R[:, q, 0, :], start=True, stop=True).then_inc(s_u, 1)
                    pe.wait_ge(s_ot, done(n - 2))
                    pe.matmul(py[:, q, 0:M], g.WS[:, q, PAIRS, :], R[:, q, 0, :], start=True, stop=False)
                    for c, (f0, f1) in enumerate(CHUNKS):
                        pe.wait_ge(s_z, chunk(n, c))
                        for f in range(f0, f1):
                            last = pe.matmul(py[:, q, 0:M], g.WS[:, q, f, :], Z[:, f, :], start=False,
                                             stop=f == PAIRS - 1)
                        last.then_inc(s_zr, 1)
                        graph.tensor_steps(pe, i + FIRST, at + c, at + c + 1)

                def pair(i, before):
                    if before:
                        heads(i - 1)
                    graph.tensor_steps(pe, i + FIRST, 0, 5)
                    if before:
                        project(i - 1)
                    group(i, 0, 5)
                    graph.tensor_steps(pe, i + FIRST, 9, 12)
                    group(i, 1, 12)

                pair(0, False)
                with pe.Fori(1, T // 2) as i:
                    pair(i, True)
                heads(T // 2 - 1)
                project(T // 2 - 1)

SCOLS = SROWS // P


def steps_phase(nc, g):
    names = ["s_iota", "s_row", "s_bc", "s_sb", "s_k", "s_tk", "s_gf", "s_tp", "s_out", "s_fin", "s_pk"]
    with phase(nc, names, ["s_in", "s_st", "s_w"]) as (held, sems):
        s_iota, s_row, s_bc, s_sb, s_k, s_tk, s_gf, s_tp, s_out, s_fin, s_pk, s_in, s_st, s_w = sems
        s_g, = pool_sems(nc, ["s_g"])

        def sb(name, shape, dt=F32):
            return held.enter_context(nc.sbuf_tensor(own(nc, name), shape, dt))

        lrow = sb("last_dst", [1, ET], I32)
        wrow_k = sb("windows_k", [1, SROWS], I32)
        trow = sb("tile_no", [1, ET], I32)
        wrow = sb("last_win", [1, ET], I32)
        wf = sb("win_f", [1, ET])
        tf = sb("tile_f", [1, ET])
        srow = sb("s_sum", [1, ET])
        sall = sb("s_all", [P, ET])
        junk = sb("junk", [P, ET])
        ki = sb("k_i", [P, SCOLS], I32)
        kf = sb("k_f", [P, SCOLS])
        tk = sb("t_k", [P, SCOLS])
        tki = g.tki
        wk = sb("w_k", [P, SCOLS])
        wki = sb("w_ki", [P, SCOLS], I32)
        wb = sb("w_base", [P, SCOLS])
        gd = sb("g_dst", [P, SCOLS, P], I32)
        gs = sb("g_src", [P, SCOLS, P], I32)
        rf = sb("rel_f", [P, SCOLS, P])
        sf = sb("src_f", [P, SCOLS, P])
        pb = held.enter_context(nc.psum_tensor(own(nc, "pb"), [P, 1024], F32))
        tp = held.enter_context(nc.psum_tensor(own(nc, "tp"), [P, 2, 512], F32))
        with nc.Block() as block:
            @block.sync
            def _(sp):
                sp.dma_start(lrow[:, :], flat(g.edst, P - 1, [ET, 1], [P, ET]),
                             allow_slow_non_contiguous=True).then_inc(s_in, 16)
                sp.wait_ge(s_gf, 1)
                sp.dma_start(flat(g.srows, 0, [P, P], [P * P, SCOLS], [1, P]), sf[:, :, :]).then_inc(s_st, 16)
                sp.dma_start(flat(g.wsteps, 0, [1, P], [P, SCOLS]), wki[:, :],
                             allow_slow_non_contiguous=True).then_inc(s_w, 16)
                sp.wait_ge(s_w, 16)
                sp.dma_start(wrow_k[:, :], flat(g.wsteps, 0, [SROWS, 1], [1, SROWS])).then_inc(s_w, 16)
                sp.wait_ge(s_w, 32)
                sp.wait_ge(s_st, 16)

            @block.gpsimd
            def _(pool):
                pool.iota(trow[:, :], pattern=[[1, ET]], base=0, channel_multiplier=0).then_inc(s_iota, 1)
                pool.iota(ki[:, :], pattern=[[P, SCOLS]], base=0, channel_multiplier=1).then_inc(s_iota, 1)
                pool.wait_ge(s_tk, 1)
                for c in range(SCOLS):
                    for to, of in ((gd, g.edst), (gs, g.esrc)):
                        pool.indirect_dma_start(
                            out=to[:, c, :], out_offset=None, in_=flat(of, 0, [P, ET], [1, P]),
                            in_offset=bass.IndirectOffsetOnAxis(ap=tki[:, c:c + 1], axis=0)).then_inc(s_g, 16)
                pool.wait_ge(s_g, 32 * SCOLS)

            @block.vector
            def _(dve):
                dve.wait_ge(s_in, 16)
                dve.tensor_scalar(out=wrow[:, :], in0=lrow[:, :], scalar1=7, scalar2=None,
                                  op0=ALU.logical_shift_right).then_inc(s_row, 1)
                dve.wait_ge(s_iota, 2)
                dve.tensor_copy(tf[:, :], trow[:, :])
                dve.tensor_copy(kf[:, :], ki[:, :]).then_inc(s_k, 1)
                dve.wait_ge(s_row, 1)
                dve.tensor_copy(wf[:, :], wrow[:, :]).then_inc(s_row, 1)
                dve.wait_ge(s_row, 2)
                dve.tensor_tensor(out=srow[:, :], in0=wf[:, :], in1=tf[:, :], op=ALU.add).then_inc(s_row, 1)
                dve.wait_ge(s_bc, 1)
                dve.tensor_copy(sall[:, :], pb[:, 0:ET]).then_inc(s_sb, 1)
                dve.wait_ge(s_sb, 1)
                for c in range(SCOLS):
                    if c:
                        dve.wait_ge(s_k, c + 1)
                    dve.tensor_scalar(out=junk[:, :], in0=sall[:, :], scalar1=kf[:, c:c + 1], scalar2=0.0,
                                      op0=ALU.is_lt, op1=ALU.add, accum_out=tk[:, c:c + 1]).then_inc(s_k, 1)
                dve.wait_ge(s_k, SCOLS + 1)
                dve.tensor_scalar(out=tk[:, :], in0=tk[:, :], scalar1=float(ET - 1), scalar2=None,
                                  op0=ALU.min).then_inc(s_k, 1)
                dve.wait_ge(s_k, SCOLS + 2)
                dve.tensor_tensor(out=wk[:, :], in0=kf[:, :], in1=tk[:, :], op=ALU.subtract).then_inc(s_k, 1)
                dve.tensor_copy(tki[:, :], tk[:, :]).then_inc(s_tk, 1)
                dve.wait_ge(s_k, SCOLS + 3)
                dve.tensor_copy(wki[:, :], wk[:, :])
                dve.tensor_scalar(out=wb[:, :], in0=wk[:, :], scalar1=float(P), scalar2=None,
                                  op0=ALU.mult).then_inc(s_k, 1)
                dve.wait_ge(s_k, SCOLS + 4)
                dve.wait_ge(s_g, 32 * SCOLS)
                for c in range(SCOLS):
                    dve.tensor_scalar(out=rf[:, c, :], in0=gd[:, c, :], scalar1=wb[:, c:c + 1], scalar2=None,
                                      op0=ALU.subtract)
                dve.tensor_copy(sf[:, :, :], gs[:, :, :]).then_inc(s_gf, 1)
                for c in range(SCOLS):
                    for k, to in enumerate((g.rel, g.src)):
                        dve.wait_ge(s_tp, 2 * c + k + 1)
                        dve.tensor_copy(to[:, c * P:(c + 1) * P], tp[:, k, 0:P]).then_inc(s_out, 1)
                dve.wait_ge(s_w, 32)
                dve.tensor_copy(g.windows[:, :], cut(wrow_k, PACK - 1, [PACK, SROWS // PACK])).then_inc(s_pk, 1)
                for p in range(PACK - 2, -1, -1):
                    dve.wait_ge(s_pk, PACK - 1 - p)
                    dve.scalar_tensor_tensor(out=g.windows[:, :], in0=g.windows[:, :], scalar=float(T),
                                             in1=cut(wrow_k, p, [PACK, SROWS // PACK]), op0=ALU.mult,
                                             op1=ALU.add).then_inc(s_pk, 1)
                dve.wait_ge(s_out, 2 * SCOLS)
                dve.tensor_copy(g.srci[:, :], g.src[:, :]).then_inc(s_fin, 1)
                dve.wait_ge(s_fin, 1)
                dve.wait_ge(s_pk, PACK)

            @block.tensor
            def _(pe):
                pe.wait_ge(s_row, 3)
                pe.matmul(pb[:, 0:512], g.ones[0:1, :], srow[0:1, 0:512], start=True, stop=True)
                pe.matmul(pb[:, 512:ET], g.ones[0:1, :], srow[0:1, 512:ET], start=True, stop=True).then_inc(s_bc, 1)
                pe.wait_ge(s_gf, 1)
                for c in range(SCOLS):
                    for k, of in enumerate((rf, sf)):
                        if c:
                            pe.wait_ge(s_out, 2 * c + k - 1)
                        pe.transpose(tp[:, k, 0:P], of[:, c, :], g.ident[:, :]).then_inc(s_tp, 1)

RING = 4


def mean0_phase(nc, g, w):
    names = ["s_a", "s_b", "s_cnt", "s_rec", "s_mn", "s_tp", "s_mt", "s_mm", "s_add"]
    with phase(nc, names, ["s_w", "s_l0", "s_l1"]) as (held, sems):
        s_a, s_b, s_cnt, s_rec, s_mn, s_tp, s_mt, s_mm, s_add, s_w, s_l0, s_l1 = sems
        s_l = (s_l0, s_l1)

        def sb(name, shape, dt=F32):
            return held.enter_context(nc.sbuf_tensor(own(nc, name), shape, dt))

        G = 5
        GROUPS = T // G
        assert T == G * GROUPS and GROUPS % 2 == 0
        W2 = sb("w_nbr", [P, 2, D])
        AG = sb("agg_in", [P, 2, AGGS, G * GW])
        A2 = sb("agg_2", [P, 2, G * GW])
        A1 = sb("agg_1", [P, 2, G * GW])
        CN = sb("cnt", [P, 2, G])
        RC = sb("rcnt", [P, 2, G])
        MN = sb("mean", [P, 2, G * D])
        MT = sb("mean_t", [P, 2, D])
        pt = held.enter_context(nc.psum_tensor(own(nc, "pt"), [P, 2, 512], F32))
        pm = held.enter_context(nc.psum_tensor(own(nc, "pm"), [P, G, 512], F32))
        with nc.Block() as block:
            @block.sync
            def _(sp):
                sp.dma_start(W2[:, :, :], w.L0_gnn_W2.rearrange("(c p) o -> p c o", p=P)).then_inc(s_w, 16)
                for s in s_l:
                    sp.sem_inc(s, 16 * AGGS)
                with sp.Fori(0, GROUPS // 2) as i:
                    for v in (0, 1):
                        m = i * 2 + v
                        sp.wait_ge(s_a, done(m - 2))
                        for a in range(AGGS):
                            sp.dma_start(AG[:, v, a, :].rearrange("p (g e) -> p g e", e=GW),
                                         flat(g.agg[a], m * (G * P * GW), [GW, P], [P * GW, G], [1, GW])
                                         ).then_inc(s_l[v], 16)

            @block.vector
            def _(dve):
                for s in (s_a, s_b, s_cnt, s_rec, s_mn, s_add):
                    dve.sem_inc(s, 2)

                def mean(i, v, first=False):
                    m = i * 2 + v
                    dve.wait_ge(s_l[v], landed(i, AGGS))
                    dve.tensor_tensor(out=A2[:, :, :], in0=AG[:, v, 0:2, :], in1=AG[:, v, 2:4, :],
                                      op=ALU.add).then_inc(s_a, 1)
                    dve.wait_ge(s_a, done(m))
                    dve.tensor_tensor(out=A1[:, v, :], in0=A2[:, 0, :], in1=A2[:, 1, :],
                                      op=ALU.add).then_inc(s_b, 1)
                    dve.wait_ge(s_b, done(m))
                    dve.tensor_scalar(out=CN[:, v, :], in0=cut(A1, v * G * GW + D, [GW, G]), scalar1=1.0,
                                      scalar2=None, op0=ALU.max).then_inc(s_cnt, 1)
                    dve.wait_ge(s_cnt, done(m))
                    dve.reciprocal(RC[:, v, :], CN[:, v, :]).then_inc(s_rec, 1)
                    dve.wait_ge(s_rec, done(m))
                    if not first:
                        dve.wait_ge(s_tp, done(m * G - G - 1))
                    dve.tensor_tensor(out=cut(MN, v * G * D, [D, G], [1, D]), in0=cut(A1, v * G * GW, [GW, G], [1, D]),
                                      in1=cut(RC, v * G, [1, G], [0, D]), op=ALU.mult).then_inc(s_mn, 1)

                def add(m):
                    dve.wait_ge(s_mm, done(m * G + G - 1))
                    x = cut(g.X, m * G * D, [D, G], [1, D])
                    dve.tensor_tensor(out=x, in0=pm[:, :, 0:D], in1=x, op=ALU.add).then_inc(s_add, 1)

                mean(0, 0, first=True)
                mean(0, 1, first=True)
                add(0)
                with dve.Fori(1, GROUPS // 2) as i:
                    for v in (0, 1):
                        mean(i, v)
                        add(i * 2 + v - 1)
                add(GROUPS - 1)
                dve.wait_ge(s_add, done(GROUPS - 1))

            @block.scalar
            def _(act):
                act.sem_inc(s_mt, 2)
                with act.Fori(0, T // 2) as i:
                    for u in (0, 1):
                        n = i * 2 + u
                        act.wait_ge(s_tp, done(n))
                        act.wait_ge(s_mm, done(n - 2))
                        act.activation(MT[:, u, :], pt[:, u, 0:D], ACT.Copy).then_inc(s_mt, 1)

            @block.tensor
            def _(pe):
                for s in (s_tp, s_mm):
                    pe.sem_inc(s, 2)
                pe.wait_ge(s_w, 16)
                with pe.Fori(0, GROUPS // 2) as i:
                    for k in range(0, 2 * G, 2):
                        for u in (0, 1):
                            n, v, t = i * (2 * G) + k + u, (k + u) // G, (k + u) % G
                            pe.wait_ge(s_mn, done(i * 2 + v))
                            pe.wait_ge(s_mt, done(n - 2))
                            for c in (0, 1):
                                last = pe.transpose(pt[:, u, c * P:(c + 1) * P],
                                                    MN[:, v, t * D + c * P:t * D + (c + 1) * P], g.ident[:, :])
                            last.then_inc(s_tp, 1)
                        for u in (0, 1):
                            n, v, t = i * (2 * G) + k + u, (k + u) // G, (k + u) % G
                            pe.wait_ge(s_mt, done(n))
                            pe.wait_ge(s_add, done(i * 2 + v - 1))
                            for c in (0, 1):
                                last = pe.matmul(pm[:, t, 0:D], MT[:, u, c * P:(c + 1) * P], W2[:, c, :],
                                                 start=c == 0, stop=c == 1)
                            last.then_inc(s_mm, 1)


def attend1_phase(nc, g):
    with phase(nc, ["s_cnt", "s_rec", "s_mn", "s_add"]) as (held, sems):
        s_cnt, s_rec, s_mn, s_add = sems
        G = 5
        CN = held.enter_context(nc.sbuf_tensor(own(nc, "weights"), [P, T * H], F32))
        MN = held.enter_context(nc.sbuf_tensor(own(nc, "mean"), [P, 2, G * D], F32))
        with nc.Block() as block:
            @block.vector
            def _(dve):
                dve.sem_inc(s_mn, 2)
                dve.sem_inc(s_add, 2)
                dve.tensor_scalar(out=CN[:, :], in0=cut(g.XN, HD, [HW1, T * H]), scalar1=1e-16, scalar2=None,
                                  op0=ALU.add).then_inc(s_cnt, 1)
                dve.wait_ge(s_cnt, 1)
                dve.reciprocal(CN[:, :], CN[:, :]).then_inc(s_rec, 1)
                dve.wait_ge(s_rec, 1)
                with dve.Fori(0, T // G // 2) as i:
                    for u in (0, 1):
                        m = i * 2 + u
                        dve.wait_ge(s_add, done(m - 2))
                        dve.tensor_tensor(out=cut(MN, u * G * D, [HD, G * H], [1, HD]),
                                          in0=cut(g.XN, m * G * AW, [HW1, G * H], [1, HD]),
                                          in1=cut(CN, m * G * H, [1, G * H], [0, HD]), op=ALU.mult).then_inc(s_mn, 1)
                    for u in (0, 1):
                        m = i * 2 + u
                        dve.wait_ge(s_mn, done(m))
                        x = cut(g.X, m * G * D, [1, G * D])
                        dve.tensor_tensor(out=x, in0=MN[:, u, :], in1=x, op=ALU.add).then_inc(s_add, 1)
                dve.wait_ge(s_add, done(T // G - 1))


def route_phase(nc, g, w, layer, cfg):
    names = ["s_go", "s_xs", "s_keep", "s_xtp", "s_xt", "s_lp", "s_lg", "s_mx", "s_ix", "s_ef", "s_oh", "s_e", "s_sub",
             "s_ex", "s_sum", "s_ri"]
    with phase(nc, names, ["s_w"]) as (held, sems):
        (s_go, s_xs, s_keep, s_xtp, s_xt, s_lp, s_lg, s_mx, s_ix, s_ef, s_oh, s_e, s_sub, s_ex, s_sum, s_ri,
         s_w) = sems

        def sb(name, shape, dt=F32):
            return held.enter_context(nc.sbuf_tensor(own(nc, name), shape, dt))

        NE, TOP = cfg.experts, cfg.top
        LAST = T // 2 - 1
        WR = sb("w_router", [P, 2, NE])
        BR = sb("b_router", [P, NE])
        XS = sb("xs", [P, 2, D])
        XT = sb("xt", [P, 2, D])
        LG = sb("logits", [P, T * NE])
        MX = sb("max8", [P, T * 8])
        MI = sb("max_i", [P, T * 8], U32)
        SU = sb("sum", [P, T])
        px = held.enter_context(nc.psum_tensor(own(nc, "px"), [P, 2, 512], F32))
        pl = held.enter_context(nc.psum_tensor(own(nc, "pl"), [P, 2, 512], F32))
        router_w, router_b = (w.L0_ffn_router_w, w.L0_ffn_router_b) if layer == 0 else (w.L1_ffn_gate_w, w.L1_ffn_gate_b)
        by_tile = ([1, T], [0, NE])
        with nc.Block() as block:
            @block.sync
            def _(sp):
                sp.dma_start(WR[:, :, :], router_w.rearrange("(c p) o -> p c o", p=P)).then_inc(s_w, 16)
                sp.dma_start(BR[:, :], router_b.partition_broadcast(P)).then_inc(s_w, 16)

            @block.vector
            def _(dve):
                for s in (s_xs, s_lg):
                    dve.sem_inc(s, 2)
                dve.wait_ge(s_w, 32)

                def normed(i):
                    for u in (0, 1):
                        n = i * 2 + u
                        dve.wait_ge(s_keep, done(n - 2))
                        dve.wait_ge(s_xtp, done(n - 2))
                        dve.tensor_scalar(out=XS[:, u, :], in0=cut(g.X, n * D, [1, D]), scalar1=cut(g.mv, n * 2, [1, 1]),
                                          scalar2=cut(g.mv, n * 2 + 1, [1, 1]), op0=ALU.subtract,
                                          op1=ALU.mult).then_inc(s_xs, 1)

                def logits(i):
                    for u in (0, 1):
                        n = i * 2 + u
                        dve.wait_ge(s_lp, done(n))
                        dve.tensor_tensor(out=cut(LG, n * NE, [1, NE]), in0=pl[:, u, 0:NE], in1=BR[:, :],
                                          op=ALU.add).then_inc(s_lg, 1)

                normed(0)
                normed(1)
                with dve.Fori(1, LAST) as i:
                    normed(i + 1)
                    logits(i - 1)
                logits(LAST - 1)
                logits(LAST)
                dve.wait_ge(s_lg, done(T - 1))
                every = cut(LG, 0, [NE, T], [1, NE])
                if layer:
                    dve.tensor_reduce(out=SU[:, :], in_=every, axis=AX.X, op=ALU.max).then_inc(s_e, 1)
                    dve.wait_ge(s_e, 1)
                    dve.tensor_tensor(out=every, in0=every, in1=cut(SU, 0, *by_tile), op=ALU.subtract).then_inc(s_sub, 1)
                    dve.wait_ge(s_ex, 1)
                    dve.tensor_reduce(out=SU[:, :], in_=every, axis=AX.X, op=ALU.add).then_inc(s_sum, 1)
                    dve.wait_ge(s_sum, 1)
                    dve.reciprocal(SU[:, :], SU[:, :]).then_inc(s_ri, 1)
                    dve.wait_ge(s_ri, 1)
                    dve.tensor_tensor(out=every, in0=every, in1=cut(SU, 0, *by_tile), op=ALU.mult).then_inc(s_sum, 1)
                    dve.wait_ge(s_sum, 2)
                for n in range(T):
                    last = dve.max(MX[:, n * 8:n * 8 + 8], LG[:, n * NE:(n + 1) * NE])
                last.then_inc(s_mx, 1)
                dve.wait_ge(s_mx, 1)
                for n in range(T):
                    last = dve.max_index(MI[:, n * 8:n * 8 + 8], MX[:, n * 8:n * 8 + 8], LG[:, n * NE:(n + 1) * NE])
                last.then_inc(s_ix, 1)
                dve.wait_ge(s_ix, 1)
                if layer:
                    dve.tensor_copy(cut(g.cw, 0, [T, TOP], [1, T]), cut(MX, 0, [1, TOP], [8, T]))
                dve.tensor_copy(cut(g.eidx, 0, [T, TOP], [1, T]), cut(MI, 0, [1, TOP], [8, T])).then_inc(s_ef, 1)
                dve.wait_ge(s_ef, 1)
                for k in range(TOP):
                    last = dve.tensor_tensor(out=cut(g.choice, k * T * NE, [NE, T], [1, NE]),
                                             in0=cut(g.iota, 0, [0, T], [1, NE]), in1=cut(g.eidx, k * T, *by_tile),
                                             op=ALU.is_equal)
                last.then_inc(s_oh, 1)
                dve.wait_ge(s_oh, 1)

            @block.scalar
            def _(act):
                act.sem_inc(s_xt, 2)
                with act.Fori(0, T // 2) as i:
                    for u in (0, 1):
                        n = i * 2 + u
                        act.wait_ge(s_xtp, done(n))
                        act.wait_ge(s_lp, done(n - 2))
                        act.activation(XT[:, u, :], px[:, u, 0:D], ACT.Copy).then_inc(s_xt, 1)
                if layer:
                    act.wait_ge(s_sub, 1)
                    act.activation(LG[:, :], LG[:, :], ACT.Exp).then_inc(s_ex, 1)

            @block.gpsimd
            def _(pool):
                pool.sem_inc(s_keep, 2)
                with pool.Fori(0, T // 2) as i:
                    for u in (0, 1):
                        n = i * 2 + u
                        pool.wait_ge(s_xs, done(n))
                        pool.tensor_copy(cut(g.XN, n * (AW if layer else GW), [1, D]), XS[:, u, :]).then_inc(s_keep, 1)
                pool.wait_ge(s_keep, done(T - 1))

            @block.tensor
            def _(pe):
                for s in (s_xtp, s_lp):
                    pe.sem_inc(s, 2)
                pe.wait_ge(s_w, 32)

                def turned(i):
                    for u in (0, 1):
                        n = i * 2 + u
                        pe.wait_ge(s_xs, done(n))
                        pe.wait_ge(s_xt, done(n - 2))
                        for c in (0, 1):
                            last = pe.transpose(px[:, u, c * P:(c + 1) * P], XS[:, u, c * P:(c + 1) * P], g.ident[:, :])
                        last.then_inc(s_xtp, 1)

                def logits(i):
                    for u in (0, 1):
                        n = i * 2 + u
                        pe.wait_ge(s_xt, done(n))
                        pe.wait_ge(s_lg, done(n - 2))
                        for c in (0, 1):
                            last = pe.matmul(pl[:, u, 0:NE], XT[:, u, c * P:(c + 1) * P], WR[:, c, :],
                                             start=c == 0, stop=c == 1)
                        last.then_inc(s_lp, 1)

                turned(0)
                with pe.Fori(0, LAST) as i:
                    turned(i + 1)
                    logits(i)
                logits(LAST)


def sort_phase(nc, g, layer, cfg):
    names = ["s_up", "s_pw", "s_cn", "s_inc", "s_exc", "s_a", "s_b", "s_pos", "s_row", "s_cmp", "s_le", "s_s",
             "s_tk", "s_ek", "s_er", "s_ei", "s_z"]
    with phase(nc, names, ["s_zero"]) as (held, sems):
        (s_up, s_pw, s_cn, s_inc, s_exc, s_a, s_b, s_pos, s_row, s_cmp, s_le, s_s, s_tk, s_ek, s_er, s_ei, s_z,
         s_zero) = sems
        s_sc, = pool_sems(nc, ["s_sc"])

        def sb(name, shape, dt=F32):
            return held.enter_context(nc.sbuf_tensor(own(nc, name), shape, dt))

        NE, TOP, STEPS_E = cfg.experts, cfg.top, cfg.steps
        J = TOP * T
        C = J * NE
        up = sb("before", [P, P], BF16)
        one = sb("one_bf", [P, P], BF16)
        CN = sb("counts", [P, C])
        INC = sb("inclusive", [P, C])
        A = sb("a", [P, C])
        Bf = sb("b", [P, C])
        zero = sb("zero_c", [P, C])
        POS = sb("pos", [P, J])
        LAST = sb("last_i", [P, J], I32)
        LASTF = sb("last_f", [P, J])
        LE = sb("le", [P, J])
        JN = sb("j_no", [P, J], I32)
        JF = sb("j_f", [P, J])
        junk = sb("junk", [P, J])
        TK = sb("tk", [P, 1])
        EK = sb("ek", [P, 1])
        pw = held.enter_context(nc.psum_tensor(own(nc, "pw"), [P, 2048], F32))
        pc = held.enter_context(nc.psum_tensor(own(nc, "pc"), [P, 2048], F32))
        XROWS = g.XN
        RW = AW if layer else GW
        with nc.Block() as block:
            @block.sync
            def _(sp):
                sp.wait_ge(s_z, 1)
                for k in range(0, STEPS_E, 4):
                    m = min(4, STEPS_E - k)
                    sp.dma_start(flat(g.xe, k * P * D, [m * D, P], [1, m * D]), g.zeros[:, 0:m * D]).then_inc(s_zero, 16)
                sp.wait_ge(s_zero, 16 * -(-STEPS_E // 4))

            @block.gpsimd
            def _(pool):
                pool.iota(LAST[:, :], pattern=[[P, J]], base=P - 1, channel_multiplier=0).then_inc(s_up, 1)
                pool.iota(JN[:, :], pattern=[[1, J]], base=0, channel_multiplier=0).then_inc(s_up, 1)
                pool.wait_ge(s_row, 1)
                pool.wait_ge(s_zero, 16 * -(-STEPS_E // 4))
                for j in range(J):
                    pool.indirect_dma_start(
                        out=flat(g.xe, 0, [D, STEPS_E * P], [1, D]),
                        out_offset=bass.IndirectOffsetOnAxis(ap=g.rowi[:, j:j + 1], axis=0),
                        in_=cut(XROWS, (j % T) * RW, [1, D]), in_offset=None).then_inc(s_sc, 16)
                pool.wait_ge(s_sc, 16 * J)

            @block.vector
            def _(dve):
                dve.memset(g.zeros[:, :], 0.0).then_inc(s_z, 1)
                dve.memset(one[:, :], 1.0)
                dve.memset(zero[:, :], 0.0)
                dve.tensor_scalar(out=up[:, :], in0=g.iota[:, :], scalar1=g.pcol[:, 0:1], scalar2=None,
                                  op0=ALU.is_gt).then_inc(s_cn, 1)
                dve.wait_ge(s_up, 2)
                dve.tensor_copy(LASTF[:, :], LAST[:, :])
                dve.tensor_copy(JF[:, :], JN[:, :]).then_inc(s_s, 1)
                dve.wait_ge(s_pw, 2)
                dve.tensor_copy(cut(CN, 0, [1, J], [J, NE]), pc[:, 0:C].rearrange("p (j e) -> p j e", e=NE)
                                ).then_inc(s_cn, 1)
                dve.wait_ge(s_cn, 2)
                dve.tensor_tensor_scan(out=INC[:, :], data0=CN[:, :], data1=zero[:, :], initial=0.0, op0=ALU.add,
                                       op1=ALU.add).then_inc(s_inc, 1)
                dve.wait_ge(s_inc, 1)
                dve.tensor_tensor(out=CN[:, :], in0=INC[:, :], in1=CN[:, :], op=ALU.subtract).then_inc(s_exc, 1)
                dve.wait_ge(s_exc, 1)
                dve.tensor_tensor(out=A[:, :].rearrange("p (j e) -> p j e", e=NE),
                                  in0=pw[:, 0:C].rearrange("p (j e) -> p j e", e=NE),
                                  in1=cut(CN, 0, [1, J], [J, NE]), op=ALU.add).then_inc(s_a, 1)
                dve.wait_ge(s_a, 1)
                dve.tensor_tensor(out=Bf[:, :], in0=A[:, :], in1=g.choice[:, 0:C], op=ALU.mult).then_inc(s_b, 1)
                dve.wait_ge(s_b, 1)
                dve.tensor_reduce(out=POS[:, :], in_=Bf[:, :].rearrange("p (j e) -> p j e", e=NE), axis=AX.X,
                                  op=ALU.add).then_inc(s_pos, 1)
                dve.wait_ge(s_pos, 1)
                dve.scalar_tensor_tensor(out=g.rowi[:, 0:J], in0=g.eidx[:, 0:J], scalar=float(P), in1=POS[:, :],
                                         op0=ALU.mult, op1=ALU.add).then_inc(s_row, 1)
                dve.wait_ge(s_s, 1)
                dve.tensor_tensor(out=A[:, :].rearrange("p (j e) -> p j e", e=NE), in0=cut(INC, J - 1, [0, J], [J, NE]),
                                  in1=cut(LASTF, 0, [1, J], [0, NE]), op=ALU.is_le).then_inc(s_cmp, 1)
                dve.wait_ge(s_cmp, 1)
                dve.tensor_reduce(out=LE[:, :], in_=A[:, :].rearrange("p (j e) -> p j e", e=NE), axis=AX.X,
                                  op=ALU.add).then_inc(s_le, 1)
                dve.wait_ge(s_le, 1)
                dve.tensor_tensor(out=LE[:, :], in0=LE[:, :], in1=JF[:, :], op=ALU.add).then_inc(s_s, 1)
                dve.wait_ge(s_s, 2)
                dve.tensor_scalar(out=junk[:, :], in0=LE[:, :], scalar1=g.pcol[:, 0:1], scalar2=0.0, op0=ALU.is_lt,
                                  op1=ALU.add, accum_out=TK[:, :]).then_inc(s_tk, 1)
                dve.wait_ge(s_tk, 1)
                dve.tensor_scalar(out=TK[:, :], in0=TK[:, :], scalar1=float(J - 1), scalar2=None,
                                  op0=ALU.min).then_inc(s_tk, 1)
                dve.wait_ge(s_tk, 2)
                dve.tensor_tensor(out=EK[:, :], in0=g.pcol[:, :], in1=TK[:, :], op=ALU.subtract).then_inc(s_ek, 1)
                dve.wait_ge(s_ek, 1)
                dve.tensor_scalar(out=EK[:, :], in0=EK[:, :], scalar1=float(NE - 1), scalar2=None,
                                  op0=ALU.min).then_inc(s_ek, 1)
                dve.wait_ge(s_er, 1)
                dve.tensor_copy(g.erow[:, :], pc[0:1, 0:P]).then_inc(s_ei, 1)
                dve.wait_ge(s_ei, 1)

            @block.tensor
            def _(pe):
                pe.wait_ge(s_cn, 1)
                for lhs, to in ((up, pw), (one, pc)):
                    for a in range(0, C, 512):
                        b = min(a + 512, C)
                        last = pe.matmul(to[:, a:b], lhs[:, :], g.choice[:, a:b], start=True, stop=True)
                    last.then_inc(s_pw, 1)
                pe.wait_ge(s_ek, 2)
                pe.matmul(pc[0:1, 0:P], EK[:, :], g.ident[:, :], start=True, stop=True).then_inc(s_er, 1)


def experts_phase(nc, g, w, layer, cfg):
    names = ["s_go", "s_xp", "s_xt", "s_h", "s_hb", "s_ha", "s_hp", "s_ht", "s_y", "s_yo"]
    with phase(nc, names, ["s_w", "s_l0", "s_l1", "s_o0", "s_o1"]) as (held, sems):
        s_go, s_xp, s_xt, s_h, s_hb, s_ha, s_hp, s_ht, s_y, s_yo, s_w, s_l0, s_l1, s_o0, s_o1 = sems
        s_l, s_o = (s_l0, s_l1), (s_o0, s_o1)

        def sb(name, shape, dt=F32):
            return held.enter_context(nc.sbuf_tensor(own(nc, name), shape, dt))

        NE, HID, TURNS = cfg.experts, cfg.hidden, cfg.steps // 2
        HC = max(1, HID // P)
        HR = min(HID, P)
        W1 = 0
        B1 = 2 * NE * HID
        assert B1 + NE * HID <= T * GW
        W2 = sb("w2", [HR, HC, NE, D])
        B2 = sb("b2", [P, NE, D])
        XI = sb("xi", [P, 2, D])
        XT = sb("xt", [P, 2, D])
        HB = sb("hb", [P, 2, HID])
        HA = sb("ha", [P, 2, HID])
        HT = sb("ht", [HR, 2, HC * P])
        YO = sb("yo", [P, 2, D])
        px = held.enter_context(nc.psum_tensor(own(nc, "px"), [P, 2, 512], F32))
        ph = held.enter_context(nc.psum_tensor(own(nc, "ph"), [P, 2, 512], F32))
        pt = held.enter_context(nc.psum_tensor(own(nc, "pt"), [P, 2, 512], F32))
        py = held.enter_context(nc.psum_tensor(own(nc, "py"), [P, 2, 512], F32))
        w1, b1, w2, b2 = ((w.L0_ffn_W1, w.L0_ffn_b1, w.L0_ffn_W2, w.L0_ffn_b2) if layer == 0 else
                          (w.L1_ffn_W1, w.L1_ffn_b1, w.L1_ffn_W2, w.L1_ffn_b2))
        NWT = 16 * (4 + HC)
        with nc.Block() as block:
            @block.sync
            def _(sp):
                for s in s_l:
                    sp.sem_inc(s, 16)
                for c in (0, 1):
                    sp.dma_start(cut(g.XN, W1 + c * NE * HID, [HID, NE], [1, HID]),
                                 w1[:, c * P:(c + 1) * P, :].rearrange("e p h -> p e h")).then_inc(s_w, 16)
                sp.dma_start(cut(g.XN, B1, [1, NE * HID]), b1.rearrange("e h -> (e h)").partition_broadcast(P)
                             ).then_inc(s_w, 16)
                for c in range(HC):
                    sp.dma_start(W2[:, c, :, :], w2[:, c * HR:(c + 1) * HR, :].rearrange("e p d -> p e d")
                                 ).then_inc(s_w, 16)
                sp.dma_start(B2[:, :, :].rearrange("p e d -> p (e d)"), b2.rearrange("e d -> (e d)").partition_broadcast(P)
                             ).then_inc(s_w, 16)

                def load(i):
                    for u in (0, 1):
                        k = i * 2 + u
                        sp.wait_ge(s_xp, done(k - 2))
                        sp.dma_start(XI[:, u, :], flat(g.xe, k * P * D, [D, P], [1, D])).then_inc(s_l[u], 16)

                with sp.Fori(0, TURNS) as i:
                    load(i)

            @block.scalar
            def _(act):
                act.sem_inc(s_ha, 2)
                for s in s_o:
                    act.sem_inc(s, 16)

                def hidden(i):
                    for u in (0, 1):
                        k = i * 2 + u
                        act.wait_ge(s_hb, done(k))
                        act.wait_ge(s_hp, done(k - 2))
                        act.activation(HA[:, u, :], HB[:, u, :], ACT.Gelu if layer else ACT.Relu).then_inc(s_ha, 1)

                def store(i):
                    for u in (0, 1):
                        k = i * 2 + u
                        act.wait_ge(s_yo, done(k))
                        act.dma_start(flat(g.ye, k * P * D, [D, P], [1, D]), YO[:, u, :]).then_inc(s_o[u], 16)

                hidden(0)
                with act.Fori(1, TURNS) as i:
                    hidden(i)
                    store(i - 1)
                store(TURNS - 1)
                for s in s_o:
                    act.wait_ge(s, landed(TURNS - 1))

            @block.vector
            def _(dve):
                for s in (s_xt, s_hb, s_ht, s_yo):
                    dve.sem_inc(s, 2)

                def of_steps(k, count):
                    _, ex = nc.values_load_multi_w_load_instructions(
                        g.erow[0:1, bass.ds(k, count)], engines=(mybir.EngineType.DVE,), min_val=0, max_val=NE - 1)
                    return ex

                def hidden(i, ex):
                    for u in (0, 1):
                        k = i * 2 + u
                        e = ex[u]
                        dve.wait_ge(s_h, done(k))
                        dve.wait_ge(s_ha, done(k - 2))
                        dve.tensor_tensor(out=HB[:, u, :], in0=ph[:, u, 0:HID], in1=cut(g.XN, e * HID + B1, [1, HID]),
                                          op=ALU.add).then_inc(s_hb, 1)

                def inputs(i):
                    for u in (0, 1):
                        k = i * 2 + u
                        dve.wait_ge(s_xp, done(k))
                        dve.wait_ge(s_h, done(k - 2))
                        dve.tensor_copy(XT[:, u, :], px[:, u, 0:D]).then_inc(s_xt, 1)

                def outputs(i, ex):
                    for u in (0, 1):
                        k = i * 2 + u
                        e = ex[u]
                        dve.wait_ge(s_y, done(k))
                        dve.wait_ge(s_o[u], landed(i - 1))
                        dve.tensor_tensor(out=YO[:, u, :], in0=py[:, u, 0:D], in1=cut(B2, e * D, [1, D]),
                                          op=ALU.add).then_inc(s_yo, 1)

                def turned(i):
                    for u in (0, 1):
                        k = i * 2 + u
                        dve.wait_ge(s_hp, done(k))
                        dve.wait_ge(s_y, done(k - 2))
                        dve.tensor_copy(HT[:, u, :], pt[0:HR, u, 0:HC * P]).then_inc(s_ht, 1)

                inputs(0)
                dve.wait_ge(s_w, NWT)
                hidden(0, of_steps(0, 2))
                inputs(1)
                turned(0)
                with dve.Fori(1, TURNS - 1) as i:
                    ex = of_steps(i * 2 - 2, 4)
                    hidden(i, ex[2:4])
                    inputs(i + 1)
                    outputs(i - 1, ex[0:2])
                    turned(i)
                ex = of_steps(TURNS * 2 - 4, 4)
                hidden(TURNS - 1, ex[2:4])
                outputs(TURNS - 2, ex[0:2])
                turned(TURNS - 1)
                outputs(TURNS - 1, ex[2:4])

            @block.tensor
            def _(pe):
                for s in (s_xp, s_h, s_hp, s_y):
                    pe.sem_inc(s, 2)

                def of_steps(k, count):
                    _, ex = nc.values_load_multi_w_load_instructions(
                        g.erow[0:1, bass.ds(k, count)], engines=(mybir.EngineType.PE,), min_val=0, max_val=NE - 1)
                    return ex

                def inputs(i):
                    for u in (0, 1):
                        k = i * 2 + u
                        pe.wait_ge(s_l[u], landed(i))
                        pe.wait_ge(s_xt, done(k - 2))
                        for c in (0, 1):
                            last = pe.transpose(px[:, u, c * P:(c + 1) * P], XI[:, u, c * P:(c + 1) * P], g.ident[:, :])
                        last.then_inc(s_xp, 1)

                def hidden(i, ex):
                    for u in (0, 1):
                        k = i * 2 + u
                        e = ex[u]
                        pe.wait_ge(s_xt, done(k))
                        pe.wait_ge(s_hb, done(k - 2))
                        for c in (0, 1):
                            last = pe.matmul(ph[:, u, 0:HID], XT[:, u, c * P:(c + 1) * P],
                                             cut(g.XN, e * HID + W1 + c * NE * HID, [1, HID]), start=c == 0, stop=c == 1)
                        last.then_inc(s_h, 1)

                def turned(i):
                    for u in (0, 1):
                        k = i * 2 + u
                        pe.wait_ge(s_ha, done(k))
                        pe.wait_ge(s_ht, done(k - 2))
                        pe.sem_inc(s_go, 1)
                        for c in range(HC):
                            last = pe.transpose(pt[0:HR, u, c * P:(c + 1) * P], HA[:, u, c * HR:(c + 1) * HR],
                                                g.ident[:, :])
                        last.then_inc(s_hp, 1)

                def outputs(i, ex):
                    for u in (0, 1):
                        k = i * 2 + u
                        e = ex[u]
                        pe.wait_ge(s_ht, done(k))
                        pe.wait_ge(s_yo, done(k - 2))
                        for c in range(HC):
                            last = pe.matmul(py[:, u, 0:D], HT[:, u, c * P:(c + 1) * P],
                                             cut(W2, e * D + c * NE * D, [1, D]), start=c == 0, stop=c == HC - 1)
                        last.then_inc(s_y, 1)

                inputs(0)
                pe.wait_ge(s_w, NWT)
                hidden(0, of_steps(0, 2))
                inputs(1)
                turned(0)
                with pe.Fori(1, TURNS - 1) as i:
                    ex = of_steps(i * 2 - 2, 4)
                    hidden(i, ex[2:4])
                    inputs(i + 1)
                    outputs(i - 1, ex[0:2])
                    turned(i)
                ex = of_steps(TURNS * 2 - 4, 4)
                hidden(TURNS - 1, ex[2:4])
                outputs(TURNS - 2, ex[0:2])
                turned(TURNS - 1)
                outputs(TURNS - 1, ex[2:4])


def merge_phase(nc, g, layer, cfg, out):
    names = ["s_add", "s_st", "s_mv", "s_sd", "s_rs"]
    with phase(nc, names, ["s_out"]) as (held, sems):
        s_add, s_st, s_mv, s_sd, s_rs, s_out = sems
        ST = held.enter_context(nc.sbuf_tensor(own(nc, "st"), [P, T, 6], F32))
        SD = held.enter_context(nc.sbuf_tensor(own(nc, "sd"), [P, T], F32))
        s_g = pool_sems(nc, [f"s_g{r}" for r in range(RING)])
        Y = held.enter_context(nc.sbuf_tensor(own(nc, "y_in"), [P, RING, D], F32))
        J = cfg.top * T
        NE = cfg.experts
        OUT_T = 7
        with nc.Block() as block:
            @block.gpsimd
            def _(pool):
                for q in range(J):
                    if q >= RING:
                        pool.wait_ge(s_add, q - RING + 1)
                    j = (q % cfg.top) * T + q // cfg.top
                    pool.indirect_dma_start(
                        out=Y[:, q % RING, :], out_offset=None, in_=flat(g.ye, 0, [D, cfg.steps * P], [1, D]),
                        in_offset=bass.IndirectOffsetOnAxis(ap=g.rowi[:, j:j + 1], axis=0)).then_inc(s_g[q % RING], 16)

            @block.vector
            def _(dve):
                def stats(t):
                    dve.wait_ge(s_add, t + 1)
                    dve.bn_stats(out=ST[:, t, :], in_=g.X[:, t, :]).then_inc(s_st, 1)

                def mean(t):
                    dve.wait_ge(s_st, t + 1)
                    dve.bn_aggr(out=cut(g.mv, 2 * t, [1, 2]), in_=ST[:, t, :]).then_inc(s_mv, 1)

                for q in range(J):
                    j = (q % cfg.top) * T + q // cfg.top
                    t = q // cfg.top
                    dve.wait_ge(s_g[q % RING], 16 * (q // RING + 1))
                    if q % cfg.top:
                        dve.wait_ge(s_add, q)
                    dve.scalar_tensor_tensor(out=g.X[:, t, :], in0=Y[:, q % RING, :],
                                             scalar=g.cw[:, j:j + 1] if layer else 0.0, in1=g.X[:, t, :],
                                             op0=ALU.mult if layer else ALU.max, op1=ALU.add).then_inc(s_add, 1)
                    if not layer and t >= 1:
                        stats(t - 1)
                    if not layer and t >= 2:
                        mean(t - 2)
                dve.wait_ge(s_add, J)
                if not layer:
                    stats(T - 1)
                    mean(T - 2)
                    mean(T - 1)
                    dve.wait_ge(s_sd, 1)
                    dve.reciprocal(cut(g.mv, 1, [2, T]), SD[:, :]).then_inc(s_rs, 1)
                    dve.wait_ge(s_rs, 1)

            if not layer:
                @block.scalar
                def _(act):
                    act.wait_ge(s_mv, T)
                    act.activation(SD[:, :], cut(g.mv, 1, [2, T]), ACT.Sqrt, bias=g.eps[:, 0:1]).then_inc(s_sd, 1)

            if layer:
                @block.sync
                def _(sp):
                    stores = 0
                    for t in range(0, FULL, OUT_T):
                        m = min(OUT_T, FULL - t)
                        sp.wait_ge(s_add, cfg.top * (t + m))
                        sp.dma_start(out[t * P:(t + m) * P, :].rearrange("(t p) d -> p t d", p=P),
                                     g.X[:, t:t + m, :]).then_inc(s_out, 16)
                        stores += 1
                    sp.wait_ge(s_add, cfg.top * (FULL + 1))
                    sp.dma_start(out[FULL * P:N, :], g.X[0:REST, FULL, :]).then_inc(s_out, 16)
                    sp.wait_ge(s_out, 16 * (stores + 1))

HW1 = HD + 1
PC = EP // P
DIV_EPS, NORM_EPS = 1e-7, 1e-12


def project1_phase(nc, g, w):
    names = ["s_pre", "s_xs", "s_xtp", "s_xt", "s_pp", "s_pj", "s_as", "s_red"]
    with phase(nc, names, ["s_w", "s_t0", "s_t1", "s_p0", "s_p1"]) as (held, sems):
        s_pre, s_xs, s_xtp, s_xt, s_pp, s_pj, s_as, s_red, s_w, s_t0, s_t1, s_p0, s_p1 = sems
        s_t, s_p = (s_t0, s_t1), (s_p0, s_p1)

        def sb(name, shape, dt=F32):
            return held.enter_context(nc.sbuf_tensor(own(nc, name), shape, dt))

        LAST = T // 2 - 1
        W = sb("w_project", [P, 2, D])
        AB = sb("a_src", [P, D])
        XS = sb("xs", [P, 2, D])
        XT = sb("xt", [P, 2, D])
        PJ = sb("proj", [P, 2, H, HW1])
        PA = sb("proj_a", [P, 2, D])
        AS = sb("score", [P, 2, H])
        pt = held.enter_context(nc.psum_tensor(own(nc, "pt"), [P, 2, 512], F32))
        pp = held.enter_context(nc.psum_tensor(own(nc, "pp"), [P, 2, 512], F32))
        with nc.Block() as block:
            @block.sync
            def _(sp):
                for s in s_t:
                    sp.sem_inc(s, 16)
                for s in s_p:
                    sp.sem_inc(s, 32)
                sp.dma_start(W[:, :, :], w.L1_gnn_W.rearrange("(c p) o -> p c o", p=P)).then_inc(s_w, 16)
                sp.dma_start(AB[:, :], w.L1_gnn_a_src.rearrange("h d -> (h d)").partition_broadcast(P)).then_inc(s_w, 16)

                def stored(i):
                    for u in (0, 1):
                        n = i * 2 + u
                        sp.wait_ge(s_pj, done(n))
                        sp.dma_start(flat(g.xp, n * P * AW, [AW, P], [1, AW]),
                                     PJ[:, u, :, :].rearrange("p h d -> p (h d)")).then_inc(s_p[u], 16)
                        sp.wait_ge(s_red, done(n))
                        sp.dma_start(flat(g.score, n * P * H, [H, P], [1, H]), AS[:, u, :]).then_inc(s_p[u], 16)

                def turned(i):
                    for u in (0, 1):
                        n = i * 2 + u
                        sp.wait_ge(s_xt, done(n))
                        sp.dma_start(flat(g.xT, n * P * D, [D, P], [1, D]), XT[:, u, :]).then_inc(s_t[u], 16)

                turned(0)
                with sp.Fori(0, LAST) as i:
                    turned(i + 1)
                    stored(i)
                stored(LAST)
                for s in s_t:
                    sp.wait_ge(s, landed(LAST))
                for s in s_p:
                    sp.wait_ge(s, landed(LAST, 2))

            @block.vector
            def _(dve):
                for s in (s_xs, s_as, s_red):
                    dve.sem_inc(s, 2)
                dve.memset(PJ[:, :, :, HD:HW1], 1.0).then_inc(s_pre, 1)
                dve.wait_ge(s_w, 32)

                def normed(i):
                    for u in (0, 1):
                        n = i * 2 + u
                        dve.wait_ge(s_xtp, done(n - 2))
                        dve.tensor_scalar(out=XS[:, u, :], in0=cut(g.X, n * D, [1, D]), scalar1=cut(g.mv, n * 2, [1, 1]),
                                          scalar2=cut(g.mv, n * 2 + 1, [1, 1]), op0=ALU.subtract,
                                          op1=ALU.mult).then_inc(s_xs, 1)

                def scores(i):
                    for u in (0, 1):
                        n = i * 2 + u
                        dve.wait_ge(s_pj, done(n))
                        dve.wait_ge(s_red, done(n - 2))
                        dve.tensor_tensor(out=PA[:, u, :].rearrange("p (h d) -> p h d", d=HD),
                                          in0=PJ[:, u, :, 0:HD], in1=AB[:, :].rearrange("p (h d) -> p h d", d=HD),
                                          op=ALU.mult).then_inc(s_as, 1)
                    for u in (0, 1):
                        n = i * 2 + u
                        dve.wait_ge(s_as, done(n))
                        dve.wait_ge(s_p[u], landed(i - 1, 2))
                        dve.tensor_reduce(out=AS[:, u, :], in_=PA[:, u, :].rearrange("p (h d) -> p h d", d=HD),
                                          axis=AX.X, op=ALU.add).then_inc(s_red, 1)

                normed(0)
                normed(1)
                with dve.Fori(1, LAST) as i:
                    normed(i + 1)
                    scores(i - 1)
                scores(LAST - 1)
                scores(LAST)

            @block.scalar
            def _(act):
                for s in (s_xt, s_pj):
                    act.sem_inc(s, 2)
                act.wait_ge(s_pre, 1)

                def turned(i):
                    for u in (0, 1):
                        n = i * 2 + u
                        act.wait_ge(s_xtp, done(n))
                        act.wait_ge(s_pp, done(n - 2))
                        act.wait_ge(s_t[u], landed(i - 1))
                        act.activation(XT[:, u, :], pt[:, u, 0:D], ACT.Copy).then_inc(s_xt, 1)

                def projected(i):
                    for u in (0, 1):
                        n = i * 2 + u
                        act.wait_ge(s_pp, done(n))
                        act.wait_ge(s_as, done(n - 2))
                        act.wait_ge(s_p[u], landed(i - 1, 2))
                        act.activation(PJ[:, u, :, 0:HD], pp[:, u, 0:D].rearrange("p (h d) -> p h d", d=HD),
                                       ACT.Copy).then_inc(s_pj, 1)

                turned(0)
                with act.Fori(0, LAST) as i:
                    turned(i + 1)
                    projected(i)
                projected(LAST)

            @block.tensor
            def _(pe):
                for s in (s_xtp, s_pp):
                    pe.sem_inc(s, 2)
                pe.wait_ge(s_w, 32)

                def turned(i):
                    for u in (0, 1):
                        n = i * 2 + u
                        pe.wait_ge(s_xs, done(n))
                        pe.wait_ge(s_xt, done(n - 2))
                        for c in (0, 1):
                            last = pe.transpose(pt[:, u, c * P:(c + 1) * P], XS[:, u, c * P:(c + 1) * P], g.ident[:, :])
                        last.then_inc(s_xtp, 1)

                def projected(i):
                    for u in (0, 1):
                        n = i * 2 + u
                        pe.wait_ge(s_xt, done(n))
                        pe.wait_ge(s_pj, done(n - 2))
                        for c in (0, 1):
                            last = pe.matmul(pp[:, u, 0:D], XT[:, u, c * P:(c + 1) * P], W[:, c, :],
                                             start=c == 0, stop=c == 1)
                        last.then_inc(s_pp, 1)

                turned(0)
                with pe.Fori(0, LAST) as i:
                    turned(i + 1)
                    projected(i)
                projected(LAST)


def mix1_phase(nc, g, w):
    names = ["s_z", "s_fold", "s_root", "s_c1", "s_c2", "s_c3", "s_qkvp", "s_qkv", "s_sq", "s_sk", "s_s4", "s_a", "s_r", "s_rt", "s_m", "s_m2", "s_im",
             "s_fac", "s_n", "s_ksq", "s_acc", "s_qtp", "s_qt", "s_zero", "s_out", "s_kt", "s_kw", "s_ix", "s_mv",
             "s_add", "s_pp", "s_cp", "s_go"]
    with phase(nc, names, ["s_w", "s_l0", "s_l1", "s_q0", "s_q1", "s_r0", "s_r1", "s_ie"]) as (held, sems):
        (s_z, s_fold, s_root, s_c1, s_c2, s_c3, s_qkvp, s_qkv, s_sq, s_sk, s_s4, s_a, s_r, s_rt, s_m, s_m2, s_im, s_fac, s_n, s_ksq, s_acc,
         s_qtp, s_qt, s_zero, s_out, s_kt, s_kw, s_ix, s_mv, s_add, s_pp, s_cp, s_go, s_w, s_l0, s_l1, s_q0, s_q1,
         s_r0, s_r1, s_ie) = sems
        s_g0, s_g1 = pool_sems(nc, ["s_g0", "s_g1"])
        s_l, s_q, s_rl, s_g = (s_l0, s_l1), (s_q0, s_q1), (s_r0, s_r1), (s_g0, s_g1)

        def sb(name, shape, dt=F32):
            return held.enter_context(nc.sbuf_tensor(own(nc, name), shape, dt))

        W = sb("w_qkv", [P, 2, 4 * D])
        B = sb("b_qkv", [P, 3 * D])
        WVT = sb("w_v_t", [P, 2, D])
        BV = sb("b_v", [P, 2])
        BO = sb("b_out", [1, D])
        RB = sb("res_bias", [1, D])
        WO = sb("w_out", [P, 2, D])
        MW = sb("mean_w", [P, 2, 2])
        MB = sb("mean_b", [P, 2])
        XT = sb("xt", [P, 2, D])
        QKV = sb("qkv", [P, 2, 3 * D])
        SQ = sb("squares", [P, 2, 2 * D])
        J4 = sb("fourth", [P, 2, D])
        SS = sb("sums", [P, 2, 2])
        S4 = sb("sum4", [P, 2, 1])
        A = sb("a", [P, 2, 2])
        R = sb("r", [P, 2, 2])
        RT = sb("root", [P, 2, 1])
        M = sb("m", [P, 2, 1])
        M2 = sb("m2", [P, 2, 1])
        IM = sb("im", [P, 2, 1])
        FA = sb("fac", [P, 2, 2])
        NQ = sb("norm", [P, 2, 2 * D])
        KSQ = sb("k_sq", [P, 2, D])
        QT = sb("qt", [P, 2, D])
        QL = sb("ql", [P, 2, D])
        KV = sb("kv", [P, 2, D])
        NR = sb("nr", [P, 2])
        NI = sb("ni", [P, 2])
        KT = sb("kt", [P, 2, D])
        KW = sb("kw", [P, 2, D])
        IE = sb("edge_src", [P, PC + U], I32)
        IX = sb("ix", [P, 2, BATCH], I32)
        RG = sb("ring", [P, 2, BATCH, H])
        pq = held.enter_context(nc.psum_tensor(own(nc, "pq"), [P, 2, 1024], F32))
        acc = held.enter_context(nc.psum_tensor(own(nc, "acc"), [P, 2, D], F32))
        nrm = held.enter_context(nc.psum_tensor(own(nc, "nrm"), [P, 512], F32))
        pr = held.enter_context(nc.psum_tensor(own(nc, "pr"), [P, 2, 512], F32))
        HT = T // 2
        NWT = 16 * 6
        GATHERS = PC // U
        assert GATHERS * U == PC and GATHERS > HT
        with nc.Block() as block:
            @block.sync
            def _(sp):
                sp.dma_start(IE[:, 0:PC], flat(g.esrc, 0, [PC, P], [1, PC])).then_inc(s_ie, 16)
                for s in (*s_l, *s_q, *s_rl):
                    sp.sem_inc(s, 16)
                sp.dma_start(WVT[:, :, :], w.L1_mix_W_qkv_t[2 * D:3 * D, :].rearrange("(c p) o -> p c o", p=P)).then_inc(s_w, 16)
                sp.dma_start(BV[:, :], w.L1_mix_b_qkv[2 * D:3 * D].rearrange("(c p) -> p c", p=P),
                             allow_slow_non_contiguous=True).then_inc(s_w, 16)
                sp.dma_start(BO[:, :], w.L1_mix_b_out.partition_broadcast(1)).then_inc(s_w, 16)
                sp.dma_start(W[:, :, 0:3 * D], w.L1_mix_W_qkv.rearrange("(c p) o -> p c o", p=P)).then_inc(s_w, 16)
                sp.dma_start(B[:, :], w.L1_mix_b_qkv.partition_broadcast(P)).then_inc(s_w, 16)
                sp.dma_start(WO[:, :, :], w.L1_mix_W_out.rearrange("(c p) o -> p c o", p=P)).then_inc(s_w, 16)

                def load(i):
                    for u in (0, 1):
                        n = i * 2 + u
                        sp.wait_ge(s_qkvp, done(n - 2))
                        sp.dma_start(XT[:, u, :], flat(g.xT, n * P * D, [D, P], [1, D])).then_inc(s_l[u], 16)

                def store(i):
                    for u in (0, 1):
                        n = i * 2 + u
                        sp.wait_ge(s_qt, done(n))
                        sp.dma_start(flat(g.q1, n * P * D, [D, P], [1, D]), QT[:, u, :]).then_inc(s_q[u], 16)

                load(0)
                load(1)
                with sp.Fori(0, HT - 2) as i:
                    load(i + 2)
                    store(i)
                store(HT - 2)
                store(HT - 1)
                for s in s_q:
                    sp.wait_ge(s, landed(HT - 1))
                with sp.Fori(0, HT) as i:
                    for u in (0, 1):
                        n = i * 2 + u
                        sp.wait_ge(s_pp, done(n - 2))
                        sp.dma_start(QL[:, u, :], flat(g.q1, n * P * D, [D, P], [1, D])).then_inc(s_rl[u], 16)

            @block.gpsimd
            def _(pool):
                with pool.Fori(0, GATHERS) as i:
                    for h in (0, 1):
                        m = i * 2 + h
                        pool.wait_ge(s_ix, m + 1)
                        pool.wait_ge(s_cp, m + 1)
                        pool.sem_inc(s_go, 1)
                        for j in range(BATCH):
                            pool.indirect_dma_start(
                                out=RG[:, h, j, :], out_offset=None, in_=flat(g.score, 0, [H, NP], [1, H]),
                                in_offset=bass.IndirectOffsetOnAxis(ap=IX[:, h, j:j + 1], axis=0)).then_inc(s_g[h], 16)

            @block.vector
            def _(dve):
                for s in (s_root, s_qkv, s_a, s_r, s_m, s_m2, s_im, s_fac, s_n, s_add):
                    dve.sem_inc(s, 2)
                dve.memset(IE[:, PC:PC + U], 0).then_inc(s_z, 1)
                dve.wait_ge(s_w, NWT)
                dve.tensor_reduce(out=MW[:, :, :], in_=W[:, :, 0:2 * D].rearrange("p c (k d) -> p c k d", d=D),
                                  axis=AX.X, op=ALU.add)
                dve.tensor_reduce(out=MB[:, :], in_=B[:, 0:2 * D].rearrange("p (k d) -> p k d", d=D), axis=AX.X,
                                  op=ALU.add).then_inc(s_c1, 1)
                dve.wait_ge(s_c1, 1)
                dve.tensor_scalar(out=MW[:, :, :], in0=MW[:, :, :], scalar1=1.0 / D, scalar2=None, op0=ALU.mult)
                dve.tensor_scalar(out=MB[:, :], in0=MB[:, :], scalar1=1.0 / D, scalar2=None,
                                  op0=ALU.mult).then_inc(s_c2, 1)
                dve.wait_ge(s_c2, 1)
                for c in (0, 1):
                    for k in (0, 1):
                        dve.tensor_scalar(out=W[:, c, k * D:(k + 1) * D], in0=W[:, c, k * D:(k + 1) * D],
                                          scalar1=MW[:, c, k:k + 1], scalar2=None, op0=ALU.subtract)
                for k in (0, 1):
                    last = dve.tensor_scalar(out=B[:, k * D:(k + 1) * D], in0=B[:, k * D:(k + 1) * D],
                                             scalar1=MB[:, k:k + 1], scalar2=None, op0=ALU.subtract)
                last.then_inc(s_c3, 1)
                dve.wait_ge(s_fold, 1)
                dve.tensor_copy(W[:, :, 3 * D:4 * D], pr[:, :, 0:D])
                dve.tensor_tensor(out=RB[:, :], in0=BO[:, :], in1=nrm[0:1, 0:D], op=ALU.add).then_inc(s_c3, 1)
                dve.wait_ge(s_c3, 2)

                def biased(i):
                    for u in (0, 1):
                        n = i * 2 + u
                        dve.wait_ge(s_qkvp, done(n))
                        dve.wait_ge(s_acc, done(n - 2))
                        dve.wait_ge(s_sk, done(n - 2))
                        dve.tensor_tensor(out=QKV[:, u, :], in0=pq[:, u, 0:3 * D], in1=B[:, :],
                                          op=ALU.add).then_inc(s_qkv, 1)
                    for u in (0, 1):
                        n = i * 2 + u
                        x = cut(g.X, n * D, [1, D])
                        dve.tensor_tensor(out=x, in0=pq[:, u, 3 * D:4 * D], in1=x, op=ALU.add).then_inc(s_root, 1)

                def normed(i):
                    for u in (0, 1):
                        n = i * 2 + u
                        dve.wait_ge(s_sk, done(n))
                        dve.tensor_scalar(out=A[:, u, :], in0=SS[:, u, :], scalar1=DIV_EPS, scalar2=None,
                                          op0=ALU.add).then_inc(s_a, 1)
                    for u in (0, 1):
                        n = i * 2 + u
                        dve.wait_ge(s_a, done(n))
                        dve.reciprocal(R[:, u, :], A[:, u, :]).then_inc(s_r, 1)
                    for u in (0, 1):
                        n = i * 2 + u
                        dve.wait_ge(s_r, done(n))
                        dve.wait_ge(s_rt, done(n))
                        dve.tensor_tensor(out=M[:, u, :], in0=R[:, u, 0:1], in1=RT[:, u, :], op=ALU.mult).then_inc(s_m, 1)
                    for u in (0, 1):
                        n = i * 2 + u
                        dve.wait_ge(s_m, done(n))
                        dve.tensor_scalar(out=M2[:, u, :], in0=M[:, u, :], scalar1=NORM_EPS, scalar2=None,
                                          op0=ALU.max).then_inc(s_m2, 1)
                    for u in (0, 1):
                        n = i * 2 + u
                        dve.wait_ge(s_m2, done(n))
                        dve.reciprocal(IM[:, u, :], M2[:, u, :]).then_inc(s_im, 1)
                    for u in (0, 1):
                        n = i * 2 + u
                        dve.wait_ge(s_im, done(n))
                        dve.tensor_tensor(out=FA[:, u, 0:1], in0=R[:, u, 0:1], in1=IM[:, u, :], op=ALU.mult)
                        dve.tensor_tensor(out=FA[:, u, 1:2], in0=R[:, u, 1:2], in1=cut(g.valid, n, [1, 1]),
                                          op=ALU.mult).then_inc(s_fac, 1)
                    for u in (0, 1):
                        n = i * 2 + u
                        dve.wait_ge(s_fac, done(n))
                        dve.wait_ge(s_qtp, done(n - 2))
                        dve.wait_ge(s_ksq, done(n - 2))
                        for k in (0, 1):
                            last = dve.tensor_scalar(out=NQ[:, u, k * D:(k + 1) * D], in0=SQ[:, u, k * D:(k + 1) * D],
                                                     scalar1=FA[:, u, k:k + 1], scalar2=None, op0=ALU.mult)
                        last.then_inc(s_n, 1)

                biased(0)
                with dve.Fori(0, HT - 1) as i:
                    normed(i)
                    biased(i + 1)
                normed(HT - 1)
                dve.wait_ge(s_zero, 2)
                dve.tensor_copy(NR[:, :], nrm[:, 0:2]).then_inc(s_out, 1)
                dve.wait_ge(s_out, 2)
                dve.tensor_scalar(out=NI[:, :], in0=NR[:, :], scalar1=NORM_EPS, scalar2=None, op0=ALU.max
                                  ).then_inc(s_out, 1)
                dve.wait_ge(s_out, 3)
                dve.reciprocal(NR[:, :], NI[:, :]).then_inc(s_out, 1)
                dve.wait_ge(s_out, 4)
                for c in (0, 1):
                    last = dve.tensor_scalar(out=KV[:, c, :], in0=acc[:, c, :], scalar1=NR[:, c:c + 1], scalar2=None,
                                             op0=ALU.mult)
                last.then_inc(s_kt, 1)
                dve.wait_ge(s_kt, 2)
                dve.tensor_copy(KT[:, :, :], pr[:, :, 0:D]).then_inc(s_kt, 1)
                dve.wait_ge(s_kw, 1)
                dve.tensor_scalar(out=KW[:, :, :], in0=pq[:, 0:2, 0:D], scalar1=float(N) ** -0.5, scalar2=None,
                                  op0=ALU.mult).then_inc(s_kw, 1)
                dve.wait_ge(s_root, done(T - 1))
                with dve.Fori(0, HT) as i:
                    for u in (0, 1):
                        n = i * 2 + u
                        dve.wait_ge(s_pp, done(n))
                        dve.tensor_tensor(out=cut(g.X, n * D, [1, D]), in0=pr[:, u, 0:D],
                                          in1=cut(g.X, n * D, [1, D]), op=ALU.add).then_inc(s_add, 1)
                dve.wait_ge(s_add, done(T - 1))

            @block.scalar
            def _(act):
                for s in (s_sq, s_sk, s_s4, s_rt, s_ksq, s_qt, s_cp):
                    act.sem_inc(s, 2)
                act.wait_ge(s_ie, 16)
                act.wait_ge(s_z, 1)
                for h in (0, 1):
                    act.activation(IX[:, h, :], IE[:, h * BATCH:(h + 1) * BATCH], ACT.Copy).then_inc(s_ix, 1)

                def keep(i):
                    for h in (0, 1):
                        m = i * 2 + h
                        act.wait_ge(s_g[h], (i + 1) * (16 * BATCH))
                        act.wait_ge(s_ix, m + 1)
                        act.activation(IX[:, h, :], cut(IE, (m + 2) * BATCH, [1, BATCH]), ACT.Copy).then_inc(s_ix, 1)
                        act.activation(cut(g.ES, m * BATCH * H, [1, BATCH * H]),
                                       RG[:, h, :, :].rearrange("p j h -> p (j h)"), ACT.Copy).then_inc(s_cp, 1)

                with act.Fori(0, HT) as i:
                    for u in (0, 1):
                        n = i * 2 + u
                        act.wait_ge(s_qkv, done(n))
                        act.wait_ge(s_n, done(n - 2))
                        act.activation(SQ[:, u, 0:D], QKV[:, u, 0:D], ACT.Square, accum_out=SS[:, u, 0:1]).then_inc(s_sq, 1)
                        act.activation(SQ[:, u, D:2 * D], QKV[:, u, D:2 * D], ACT.Square,
                                       accum_out=SS[:, u, 1:2]).then_inc(s_sk, 1)
                    for u in (0, 1):
                        n = i * 2 + u
                        act.wait_ge(s_sq, done(n))
                        act.activation(J4[:, u, :], SQ[:, u, 0:D], ACT.Square, accum_out=S4[:, u, :]).then_inc(s_s4, 1)
                    for u in (0, 1):
                        n = i * 2 + u
                        act.wait_ge(s_s4, done(n))
                        act.activation(RT[:, u, :], S4[:, u, :], ACT.Sqrt, bias=g.zero[:, 0:1]).then_inc(s_rt, 1)
                    for u in (0, 1):
                        n = i * 2 + u
                        act.wait_ge(s_n, done(n))
                        act.wait_ge(s_acc, done(n - 2))
                        act.activation(KSQ[:, u, :], NQ[:, u, D:2 * D], ACT.Square).then_inc(s_ksq, 1)
                    keep(i)
                    for u in (0, 1):
                        n = i * 2 + u
                        act.wait_ge(s_qtp, done(n))
                        act.wait_ge(s_q[u], landed(i - 1))
                        act.activation(QT[:, u, :], pr[:, u, 0:D], ACT.Copy).then_inc(s_qt, 1)
                act.wait_ge(s_zero, 2)
                act.wait_ge(s_out, 1)
                act.activation(NR[:, :], NR[:, :], ACT.Sqrt, bias=g.zero[:, 0:1]).then_inc(s_out, 1)
                with act.Fori(HT, GATHERS) as i:
                    keep(i)

            @block.tensor
            def _(pe):
                for s in (s_qkvp, s_acc, s_qtp, s_pp):
                    pe.sem_inc(s, 2)

                def zero(start, stop):
                    pe.matmul(acc[:, :, :], g.zrow[0:1, 0:P], g.zrow[0:1, :], start=start, stop=stop)
                    pe.matmul(nrm[:, :], g.zrow[0:1, 0:P], g.zrow[0:1, :], start=start, stop=stop).then_inc(s_zero, 1)

                pe.wait_ge(s_w, NWT)
                for m in (0, 1):
                    for c in (0, 1):
                        pe.matmul(pr[:, m, 0:D], WVT[:, c, m * P:(m + 1) * P], WO[:, c, :], start=c == 0, stop=c == 1)
                for c in (0, 1):
                    last = pe.matmul(nrm[0:1, 0:D], BV[:, c:c + 1], WO[:, c, :], start=c == 0, stop=c == 1)
                last.then_inc(s_fold, 1)
                pe.wait_ge(s_c3, 2)
                zero(True, False)

                def products(i):
                    for u in (0, 1):
                        n = i * 2 + u
                        pe.wait_ge(s_l[u], landed(i))
                        pe.wait_ge(s_qkv, done(n - 2))
                        pe.wait_ge(s_root, done(n - 2))
                        for c in (0, 1):
                            for a, b in ((0, 512), (512, 1024)):
                                pe.matmul(pq[:, u, a:b], XT[:, u, c * P:(c + 1) * P], W[:, c, a:b],
                                          start=c == 0, stop=c == 1 and a == 0)
                        pe.matmul(pq[:, u, 3 * D:4 * D], g.ones[0:1, 0:P], RB[0:1, :], start=False,
                                  stop=True).then_inc(s_qkvp, 1)

                def sums(i):
                    for u in (0, 1):
                        n = i * 2 + u
                        pe.wait_ge(s_n, done(n))
                        pe.wait_ge(s_qt, done(n - 2))
                        for c in (0, 1):
                            last = pe.transpose(pr[:, u, c * P:(c + 1) * P], NQ[:, u, c * P:(c + 1) * P], g.ident[:, :])
                        last.then_inc(s_qtp, 1)
                        pe.wait_ge(s_ksq, done(n))
                        for c in (0, 1):
                            pe.matmul(acc[:, c, :], NQ[:, u, D + c * P:D + (c + 1) * P], QKV[:, u, 2 * D:3 * D],
                                      start=False, stop=False)
                        for c in (0, 1):
                            last = pe.matmul(nrm[:, c:c + 1], KSQ[:, u, c * P:(c + 1) * P], g.ones[:, 0:1],
                                             start=False, stop=False)
                        last.then_inc(s_acc, 1)

                products(0)
                with pe.Fori(0, HT - 1) as i:
                    products(i + 1)
                    sums(i)
                sums(HT - 1)
                zero(False, True)
                pe.wait_ge(s_kt, 1)
                pe.wait_ge(s_qt, done(T - 1))
                for c in (0, 1):
                    for d in (0, 1):
                        last = pe.transpose(pr[:, d, c * P:(c + 1) * P], KV[:, c, d * P:(d + 1) * P], g.ident[:, :])
                last.then_inc(s_kt, 1)
                pe.wait_ge(s_kt, 3)
                for c in (0, 1):
                    for d in (0, 1):
                        last = pe.matmul(pq[:, c, 0:D], KT[:, d, c * P:(c + 1) * P], WO[:, d, :], start=d == 0, stop=d == 1)
                last.then_inc(s_kw, 1)
                pe.wait_ge(s_kw, 2)
                with pe.Fori(0, HT) as i:
                    for u in (0, 1):
                        n = i * 2 + u
                        pe.wait_ge(s_rl[u], landed(i))
                        pe.wait_ge(s_add, done(n - 2))
                        for c in (0, 1):
                            last = pe.matmul(pr[:, u, 0:D], QL[:, u, c * P:(c + 1) * P], KW[:, c, :],
                                             start=c == 0, stop=c == 1)
                        last.then_inc(s_pp, 1)


def weights1_phase(nc, g):
    names = ["s_ms", "s_ne", "s_pen", "s_ps", "s_f", "s_fl", "s_t", "s_tc", "s_ch", "s_chb", "s_cb", "s_ci",
             "s_m", "s_exp", "s_wt", "s_wc"]
    with phase(nc, names, ["s_d", "s_we"]) as (held, sems):
        (s_ms, s_ne, s_pen, s_ps, s_f, s_fl, s_t, s_tc, s_ch, s_chb, s_cb, s_ci, s_m, s_exp, s_wt, s_wc,
         s_d, s_we) = sems
        s_g, = pool_sems(nc, ["s_g"])

        def sb(name, shape, dt=F32):
            return held.enter_context(nc.sbuf_tensor(own(nc, name), shape, dt))

        DI = sb("dst_i", [P, PC + 2], I32)
        PEN = sb("pen", [P, PC + 1])
        PS = sb("pen_sum", [P, 2])
        FL = sb("ends", [P, H])
        PB = sb("pen_b", [P, H])
        CH = sb("chain_in", [H, 2, P])
        CO = sb("chain_out", [H, P + 1])
        CI = sb("carry", [P, H])
        FO, BO = 0, H * PC
        pt = held.enter_context(nc.psum_tensor(own(nc, "pt"), [P, 2, 512], F32))
        pw = held.enter_context(nc.psum_tensor(own(nc, "pw"), [P, 4, 512], F32))
        W4 = sb("w_rows", [P, 2, P * H])
        with nc.Block() as block:
            @block.sync
            def _(sp):
                sp.wait_ge(s_ms, 1)
                sp.dma_start(DI[:, 1:PC + 1], flat(g.edst, 0, [PC, P], [1, PC])).then_inc(s_d, 16)
                sp.dma_start(DI[1:P, 0:1], flat(g.edst, PC - 1, [PC, P - 1], [1, 1]),
                             allow_slow_non_contiguous=True).then_inc(s_d, 16)
                sp.dma_start(DI[0:P - 1, PC + 1:PC + 2], flat(g.edst, PC, [PC, P - 1], [1, 1]),
                             allow_slow_non_contiguous=True).then_inc(s_d, 16)
                sp.wait_ge(s_exp, 1)
                sp.dma_start(flat(g.we, 0, [PC * H, P], [1, PC * H]), g.ES[:, :]).then_inc(s_we, 16)
                sp.wait_ge(s_we, 16)

            @block.gpsimd
            def _(pool):
                pool.wait_ge(s_we, 16)
                for c in range(SCOLS):
                    if c >= 2:
                        pool.wait_ge(s_wt, (c - 1) * H)
                    pool.indirect_dma_start(
                        out=W4[:, c % 2, :], out_offset=None, in_=flat(g.we, 0, [P * H, ET], [1, P * H]),
                        in_offset=bass.IndirectOffsetOnAxis(ap=g.tki[:, c:c + 1], axis=0)).then_inc(s_g, 16)
                    pool.wait_ge(s_g, 16 * (c + 1))

            @block.vector
            def _(dve):
                dve.memset(DI[:, :], -1).then_inc(s_ms, 1)
                dve.wait_ge(s_d, 48)
                dve.tensor_tensor(out=PEN[:, :], in0=DI[:, 0:PC + 1], in1=DI[:, 1:PC + 2],
                                  op=ALU.not_equal).then_inc(s_ne, 1)
                dve.wait_ge(s_ne, 1)
                dve.tensor_scalar(out=PEN[:, :], in0=PEN[:, :], scalar1=NEG, scalar2=None, op0=ALU.mult).then_inc(s_pen, 1)
                dve.memset(CO[:, :], NEG)
                dve.wait_ge(s_pen, 1)
                for b in (0, 1):
                    last = dve.tensor_reduce(out=PS[:, b:b + 1], in_=PEN[:, b:b + PC], axis=AX.X, op=ALU.add)
                last.then_inc(s_ps, 1)
                dve.wait_ge(s_ps, 1)
                for b in (0, 1):
                    def runs(h, first):
                        scores = cut(g.ES, h, [H, PC])
                        fwd = cut(g.XN, FO + h * PC, [1, PC])
                        bwd = cut(g.XN, BO + h * PC + PC - 1, [-1, PC])
                        start = NEG if first else CI[:, h:h + 1]
                        if b == 0:
                            return dve.tensor_tensor_scan(out=fwd, data0=PEN[:, 0:PC], data1=scores, initial=start,
                                                          op0=ALU.add, op1=ALU.max)
                        return dve.tensor_tensor_scan(out=bwd, data0=cut(PEN, PC, [-1, PC]),
                                                      data1=cut(g.XN, FO + h * PC + PC - 1, [-1, PC]),
                                                      initial=start, op0=ALU.add, op1=ALU.max)

                    for h in range(H):
                        last = runs(h, True)
                    last.then_inc(s_f, 1)
                    dve.wait_ge(s_f, 2 * b + 1)
                    dve.tensor_copy(FL[:, :], cut(g.XN, (FO + PC - 1) if b == 0 else BO, [PC, H]))
                    dve.tensor_copy(PB[:, :], cut(PS, b, [0, H])).then_inc(s_fl, 1)
                    dve.wait_ge(s_t, b + 1)
                    dve.tensor_copy(CH[:, :, :], pt[0:H, :, 0:P]).then_inc(s_tc, 1)
                    dve.wait_ge(s_tc, b + 1)
                    if b == 0:
                        dve.tensor_tensor_scan(out=CO[:, 1:P + 1], data0=CH[:, 1, :], data1=CH[:, 0, :], initial=NEG,
                                               op0=ALU.add, op1=ALU.max).then_inc(s_ch, 1)
                    else:
                        dve.memset(CO[:, P:P + 1], NEG)
                        dve.tensor_tensor_scan(out=cut(CO, P - 1, [-1, P]), data0=cut(CH, 2 * P - 1, [-1, P]),
                                               data1=cut(CH, P - 1, [-1, P]), initial=NEG, op0=ALU.add,
                                               op1=ALU.max).then_inc(s_ch, 1)
                    dve.wait_ge(s_cb, b + 1)
                    dve.tensor_copy(CI[:, :], pt[:, 0, 0:H]).then_inc(s_ci, 1)
                    dve.wait_ge(s_ci, b + 1)
                    for h in range(H):
                        last = runs(h, False)
                    last.then_inc(s_f, 1)
                    dve.wait_ge(s_f, 2 * b + 2)
                dve.tensor_tensor(out=cut(g.ES, 0, [H, PC], [1, H]), in0=cut(g.ES, 0, [H, PC], [1, H]),
                                  in1=cut(g.XN, BO, [1, PC], [PC, H]), op=ALU.subtract).then_inc(s_m, 1)
                for c in range(SCOLS):
                    for h in range(H):
                        k = c * H + h
                        dve.wait_ge(s_wt, k + 1)
                        dve.tensor_copy(cut(g.wst, c * P * H + h, [H, P]), pw[:, k % 4, 0:P]).then_inc(s_wc, 1)
                dve.wait_ge(s_wc, SCOLS * H)

            @block.scalar
            def _(act):
                act.wait_ge(s_m, 1)
                act.activation(g.ES[:, :], g.ES[:, :], ACT.Exp).then_inc(s_exp, 1)

            @block.tensor
            def _(pe):
                for b in (0, 1):
                    pe.wait_ge(s_fl, b + 1)
                    pe.transpose(pt[0:H, 0, 0:P], FL[:, :], g.ident[:, :])
                    pe.transpose(pt[0:H, 1, 0:P], PB[:, :], g.ident[:, :]).then_inc(s_t, 1)
                    pe.wait_ge(s_ch, b + 1)
                    pe.transpose(pt[:, 0, 0:H], CO[:, b:b + P], g.ident[0:H, 0:H]).then_inc(s_cb, 1)
                for c in range(SCOLS):
                    pe.wait_ge(s_g, 16 * (c + 1))
                    for h in range(H):
                        k = c * H + h
                        if k >= 4:
                            pe.wait_ge(s_wc, k - 3)
                        pe.transpose(pw[:, k % 4, 0:P], cut(W4, (c % 2) * P * H + h, [H, P]), g.ident[:, :]).then_inc(s_wt, 1)

QUARTERS = 4
QB = U // QUARTERS


def graph1_phase(nc, g):
    names = ["s_z", "s_ix", "s_go", "s_pr", "s_df", "s_oh", "s_pa", "s_acc"]
    with phase(nc, names) as (held, sems):
        s_z, s_ix, s_go, s_pr, s_df, s_oh, s_pa, s_acc = sems
        s_g = pool_sems(nc, [f"s_g{x}" for x in range(QUARTERS)])

        def sb(name, shape, dt=F32):
            return held.enter_context(nc.sbuf_tensor(own(nc, name), shape, dt))

        IX = sb("ix", [P, U], I32)
        RG = sb("ring", [P, U, AW])
        PR = sb("weighted", [P, 4, AW])
        DF = sb("distance", [P, 4, P])
        OH = sb("one_hot", [P, 4, P])
        pa = held.enter_context(nc.psum_tensor(own(nc, "pa"), [P, 4, 512], F32))

        def fin(k):
            return k + 1 + U

        with nc.Block() as block:
            @block.gpsimd
            def _(pool):
                with pool.Fori(0, TURNS) as i:
                    for x in range(QUARTERS):
                        pool.wait_ge(s_ix, i * QUARTERS + x + 1)
                        pool.wait_ge(s_pr, fin(i * U + x * QB + QB - 1 - U))
                        pool.sem_inc(s_go, 1)
                        for j in range(x * QB, (x + 1) * QB):
                            pool.indirect_dma_start(
                                out=RG[:, j, :], out_offset=None, in_=flat(g.xp, 0, [AW, NP], [1, AW]),
                                in_offset=bass.IndirectOffsetOnAxis(ap=IX[:, j:j + 1], axis=0)).then_inc(s_g[x], 16)

            @block.vector
            def _(dve):
                for s in (s_pr, s_acc):
                    dve.sem_inc(s, U)
                dve.memset(cut(g.XN, 0, [1, T * AW]), 0.0).then_inc(s_z, 1)
                dve.wait_ge(s_z, 1)

                def add(i, j, packs):
                    k = i * U + j
                    at = window(packs, j)
                    dve.wait_ge(s_pa, fin(k))
                    dve.wait_ge(s_acc, fin(k - 1))
                    dve.tensor_tensor(out=cut(g.XN, at * AW, [1, AW]), in0=pa[:, j % 4, 0:AW],
                                      in1=cut(g.XN, at * AW, [1, AW]), op=ALU.add).then_inc(s_acc, 1)

                with dve.Fori(0, TURNS) as i:
                    packs = turn_windows(nc, g, i, mybir.EngineType.DVE)
                    for j in range(U):
                        k = i * U + j
                        x = j // QB
                        if j % QB == 0:
                            dve.wait_ge(s_g[x], (i + 1) * (16 * QB))
                        dve.wait_ge(s_pa, fin(k - 4))
                        dve.tensor_tensor(out=PR[:, j % 4, :].rearrange("p (h d) -> p h d", d=HW1),
                                          in0=RG[:, j, :].rearrange("p (h d) -> p h d", d=HW1),
                                          in1=cut(g.wst, k * H, [1, H], [0, HW1]), op=ALU.mult).then_inc(s_pr, 1)
                        if j >= 2:
                            add(i, j - 2, packs)
                    for j in (U - 2, U - 1):
                        add(i, j, packs)
                dve.wait_ge(s_acc, fin(STEPS - 1))

            @block.scalar
            def _(act):
                act.sem_inc(s_df, U)
                act.sem_inc(s_oh, U)
                for x in range(QUARTERS):
                    act.activation(IX[:, x * QB:(x + 1) * QB], cut(g.srci, x * QB, [1, QB]), ACT.Copy).then_inc(s_ix, 1)
                with act.Fori(0, TURNS) as i:
                    for j in range(U):
                        k = i * U + j
                        act.wait_ge(s_oh, fin(k - 4))
                        act.activation(DF[:, j % 4, :], g.iota[:, :], ACT.Abs, bias=cut(g.rel, k, [1, 1]),
                                       scale=-1.0).then_inc(s_df, 1)
                        act.wait_ge(s_df, fin(k))
                        act.wait_ge(s_pa, fin(k - 4))
                        act.activation(OH[:, j % 4, :], DF[:, j % 4, :], ACT.Relu, bias=g.ones[:, 0:1],
                                       scale=-1.0).then_inc(s_oh, 1)
                        if j % QB == QB - 1:
                            x = j // QB
                            act.wait_ge(s_g[x], (i + 1) * (16 * QB))
                            act.wait_ge(s_ix, i * QUARTERS + x + QUARTERS)
                            act.activation(IX[:, x * QB:(x + 1) * QB], cut(g.srci, i * U + U + x * QB, [1, QB]),
                                           ACT.Copy).then_inc(s_ix, 1)

            @block.tensor
            def _(pe):
                pe.sem_inc(s_pa, U)
                with pe.Fori(0, TURNS) as i:
                    for h in (0, 1):
                        for j in range(BATCH):
                            k = i * U + h * BATCH + j
                            pe.wait_ge(s_oh, fin(k))
                            pe.wait_ge(s_pr, fin(k))
                            pe.wait_ge(s_acc, fin(k - 4))
                            pe.matmul(pa[:, j % 4, 0:AW], OH[:, j % 4, :], PR[:, j % 4, :], start=True,
                                      stop=True).then_inc(s_pa, 1)


class Bag:
    pass

WEIGHTS = ["L0_gnn_W1", "L0_gnn_b1", "L0_gnn_W2", "L0_gnn_b2", "L0_mix_Wqkv", "L0_mix_bqkv", "L0_mix_Wproj",
           "L0_mix_bproj", "L0_mix_temperature", "L0_ffn_router_w", "L0_ffn_router_b", "L0_ffn_W1", "L0_ffn_b1",
           "L0_ffn_W2", "L0_ffn_b2", "L1_gnn_W", "L1_gnn_a_src", "L1_mix_W_qkv", "L1_mix_b_qkv",
           "L1_mix_W_qkv_t", "L1_mix_W_out", "L1_mix_b_out", "L1_ffn_gate_w", "L1_ffn_gate_b", "L1_ffn_W1", "L1_ffn_b1", "L1_ffn_W2",
           "L1_ffn_b2"]
TRANSPOSED = ("L0_gnn_W1", "L0_gnn_W2", "L0_mix_Wqkv", "L0_mix_Wproj", "L0_ffn_router_w")
Weights = namedtuple("Weights", WEIGHTS)


def feed_forward(nc, g, w, layer, cfg, out):
    with ExitStack() as route:
        g.choice = route.enter_context(nc.sbuf_tensor(own(nc, "choice"), [P, T * 32], BF16))
        g.zeros = route.enter_context(nc.sbuf_tensor(own(nc, "zeros"), [P, 4 * D], F32))
        if layer == 0:
            mean0_phase(nc, g, w)
        else:
            attend1_phase(nc, g)
        norms_phase(nc, g)
        route_phase(nc, g, w, layer, cfg)
        sort_phase(nc, g, layer, cfg)
    experts_phase(nc, g, w, layer, cfg)
    merge_phase(nc, g, layer, cfg, out)


def gnn_kernel(nc, x, src, dst, w, out):
    g = Bag()
    g.esrc = nc.dram_tensor("esrc", [EP], I32)
    g.edst = nc.dram_tensor("edst", [EP], I32)
    g.kv = nc.dram_tensor("kv", [T, P, 2 * D], F32)
    g.qT = nc.dram_tensor("qT", [2, P, NP], F32)
    g.srows = nc.dram_tensor("srows", [SROWS, P], F32)
    g.wsteps = nc.dram_tensor("wsteps", [SROWS], I32)
    g.agg = [nc.dram_tensor(f"agg{a}", [AROWS, GW], F32) for a in range(AGGS)]
    ffn0, ffn1 = Bag(), Bag()
    ffn0.experts, ffn0.top, ffn0.hidden = 32, 1, 64
    ffn1.experts, ffn1.top, ffn1.hidden = 8, 2, 512
    for f in (ffn0, ffn1):
        f.steps = -(-(f.top * T + f.experts - 1) // 2) * 2
    g.xT = nc.dram_tensor("xn1_t", [NP * D], F32)
    g.q1 = nc.dram_tensor("q1_t", [NP * D], F32)
    g.xp = nc.dram_tensor("projected", [NP * AW], F32)
    g.score = nc.dram_tensor("source_score", [NP * H], F32)
    g.we = nc.dram_tensor("edge_weight", [EP * H], F32)
    g.xe = nc.dram_tensor("expert_in", [ffn1.steps * P, D], F32)
    g.ye = nc.dram_tensor("expert_out", [ffn1.steps * P, D], F32)
    with ExitStack() as held:
        def sb(name, shape, dt=F32):
            return held.enter_context(nc.sbuf_tensor(name, shape, dt))

        g.X = sb("X", [P, T, D])
        g.XN = sb("XN", [P, 2 * H * PC])
        g.iota = sb("iota", [P, P])
        g.iota_b = sb("iota_b", [P, P], BF16)
        g.pcol = sb("pcol", [P, 1])
        g.ident = sb("ident", [P, P])
        g.lower = sb("lower", [P, P])
        g.valid = sb("valid", [P, T])
        g.eps = sb("eps", [P, 1])
        g.mv = sb("mean_dev", [P, T, 2])
        g.zero = sb("zero", [P, 1])
        g.ones = sb("ones", [P, P])
        g.zrow = sb("zrow", [1, 512])
        g.blk = sb("blk", [P, P])
        g.head = sb("head", [P, 1])
        g.rel = sb("step_rel", [P, SROWS])
        g.src = sb("step_src", [P, SROWS])
        g.srci = sb("step_srci", [P, SROWS], I32)
        g.tki = sb("step_tile", [P, SCOLS], I32)
        g.windows = sb("step_windows", [1, SROWS // PACK], I32)
        g.cw = sb("expert_weight", [P, 2 * T])
        g.eidx = sb("expert_no", [P, 2 * T])
        g.rowi = sb("expert_row", [P, 2 * T], I32)
        g.erow = sb("expert_of_step", [1, P], I32)
        g.s_agg = nc.alloc_semaphore("s_agg")
        g.s_c = pool_sems(nc, [f"s_c{a}" for a in range(AGGS)])
        with ExitStack() as mix0, ExitStack() as zeroing:
            def sb0(name, shape):
                return mix0.enter_context(nc.sbuf_tensor(name, shape, F32))

            g.WS = sb0("WS", [P, 2, PAIRS + 1, P])
            g.GS = sb0("GS", [P, 2, P])
            g.ks = sb0("ks", [P, 2])
            g.vs = sb0("vs", [P, 2])
            g.zeros0 = zeroing.enter_context(nc.sbuf_tensor("zeros0", [P, ZC], F32))
            setup_phase(nc, g, x, src, dst)
            steps_phase(nc, g)
            norms_phase(nc, g, zero_agg=True)
            qkv0_phase(nc, g, w)
            zeroing.close()
            graph = Graph0(nc, g, mix0)
            for q in (0, 1):
                keys0_phase(nc, g, graph, q)
            queries0_phase(nc, g, graph, w)
            graph.end(nc)
        feed_forward(nc, g, w, 0, ffn0, out)
        project1_phase(nc, g, w)
        with ExitStack() as edges:
            g.ES = edges.enter_context(nc.sbuf_tensor("edge_score", [P, PC * H], F32))
            mix1_phase(nc, g, w)
            g.wst = edges.enter_context(nc.sbuf_tensor("step_weight", [P, SROWS * H], F32))
            weights1_phase(nc, g)
            graph1_phase(nc, g)
        feed_forward(nc, g, w, 1, ffn1, out)

def kernel(**inputs):
    import numpy as _np
    import concourse.bacc as _bacc
    from concourse import mybir as _mybir
    from concourse.bass_utils import run_bass_kernel_spmd as _run

    nc = _bacc.Bacc("TRN2", target_bir_lowering=False, num_devices=1)
    arrays = {}

    def given(name, a):
        a = _np.ascontiguousarray(a)
        arrays[f"in_{name}_dram"] = a
        return nc.dram_tensor(f"in_{name}_dram", a.shape, _mybir.dt.from_np(a.dtype), kind="ExternalInput").ap()

    x, src, dst = (given(name, inputs[name]) for name in ("x", "src", "dst"))
    params = {}
    for name in WEIGHTS:
        if name == "L1_mix_W_qkv_t":
            a = _np.asarray(inputs["L1_mix_W_qkv"]).T
        elif name in TRANSPOSED:
            a = _np.asarray(inputs[name]).T
        elif name == "L0_mix_temperature":
            a = _np.asarray(inputs[name]).reshape(H)
        else:
            a = _np.asarray(inputs[name])
        params[name] = given(name, a)
    out = nc.dram_tensor("out_0_dram", (N, D), _mybir.dt.from_np(_np.dtype("float32")), kind="ExternalOutput").ap()
    gnn_kernel(nc, x, src, dst, Weights(**params), out)
    r = _run(nc, [arrays], core_ids=[0])
    return r.results[0]["out_0_dram"]
```
